# Optimizing a Trainium2 kernel written in Bass

```python
import numpy as np
import jax
import jax.numpy as jnp

def _softmax(x, axis=-1):
    return jax.nn.softmax(x, axis=axis)

def _gelu(x):
    return jax.nn.gelu(x, approximate=True)

def _silu(x):
    return jax.nn.silu(x)

def _sigmoid(x):
    return jax.nn.sigmoid(x)

def _layernorm(x, axis=-1, eps=1e-05):
    m = jnp.mean(x, axis=axis, keepdims=True)
    v = jnp.var(x, axis=axis, keepdims=True)
    return (x - m) / jnp.sqrt(v + eps)

def _scatter_add(tgt, idx, src, axis=0):
    return tgt.at[idx].add(src)

def _segment_sum(src, seg, n):
    return jax.ops.segment_sum(src, seg, n)
kernel_name = 'mk_seq_postln_d4_jaxref_r8_ac17f0'

def setup_inputs(seed: int=0):
    np.random.seed(seed)
    _w = jnp.asarray

    def _L0_attn_setup():
        import jax, jax.numpy as jnp
        import numpy as np
        MIN_RAD, MAX_RAD, EPS = (0.9, 0.999, 1e-08)

        def block_diag_linear(x, w, b):
            h, bw, _ = w.shape
            xb = x.reshape(x.shape[0], x.shape[1], h, bw)
            y = jnp.einsum('bthi,hij->bthj', xb, w) + b
            return y.reshape(x.shape)
        key = jax.random.key(seed)
        kx, kw1, kw2, ka = jax.random.split(key, 4)
        B, T, width, num_heads = (8, 512, 128, 8)
        bw = width // num_heads
        std = np.sqrt(1.0 / bw)
        x = jax.random.normal(kx, (B, T, width), dtype=jnp.float32)
        ig_w = std * jax.random.normal(kw1, (num_heads, bw, bw), dtype=jnp.float32)
        ig_b = jnp.zeros((num_heads, bw), dtype=jnp.float32)
        ag_w = std * jax.random.normal(kw2, (num_heads, bw, bw), dtype=jnp.float32)
        ag_b = jnp.zeros((num_heads, bw), dtype=jnp.float32)
        u = jax.random.uniform(ka, (width,), dtype=jnp.float32, minval=MIN_RAD ** 2 + EPS, maxval=MAX_RAD ** 2 + EPS)
        a_param = jnp.log(jnp.exp(-0.5 * jnp.log(u)) - 1.0)
        return {'x': x, 'ig_w': ig_w, 'ig_b': ig_b, 'ag_w': ag_w, 'ag_b': ag_b, 'a_param': a_param}
    _L0_attn_in = _L0_attn_setup()

    def _L0_ffn_setup():
        import jax, jax.numpy as jnp
        import numpy as np
        DIM = 128
        DEPTH = 2
        HEADS = 8
        DIM_HEAD = 64
        WINDOW = 64
        INNER = HEADS * DIM_HEAD
        HID = int(DIM * 4 * 2 / 3)
        B, N = (2, 1024)
        QK_SCALE = 8.0

        def shift_token(t):
            t1, t2 = jnp.split(t, 2, axis=-1)
            t2 = jnp.pad(t2, ((0, 0), (1, 0), (0, 0)))[:, :-1]
            return jnp.concatenate([t1, t2], axis=-1)

        def l2norm(t):
            return t / jnp.clip(jnp.linalg.norm(t, axis=-1, keepdims=True), 1e-12)

        def rotate_half(x):
            x1, x2 = jnp.split(x, 2, axis=-1)
            return jnp.concatenate([-x2, x1], axis=-1)

        def rotary_xpos(q, k):
            n = q.shape[-2]
            half_idx = jnp.arange(0, DIM_HEAD, 2, dtype=jnp.float32)
            inv_freq = 1.0 / 10000.0 ** (half_idx / DIM_HEAD)
            t = jnp.arange(n, dtype=jnp.float32)
            freqs = t[:, None] * inv_freq[None, :]
            freqs = jnp.concatenate([freqs, freqs], axis=-1)
            base = (half_idx + 0.4 * DIM_HEAD) / (1.4 * DIM_HEAD)
            power = (t - n // 2) / float(WINDOW // 2)
            scale = base[None, :] ** power[:, None]
            scale = jnp.concatenate([scale, scale], axis=-1)
            cos, sin = (jnp.cos(freqs), jnp.sin(freqs))
            q = q * cos * scale + rotate_half(q) * sin * scale
            k = k * cos / scale + rotate_half(k) * sin / scale
            return (q, k)

        def local_attention(q, k, v):
            b, h, n, d = q.shape
            w = n // WINDOW
            bq = q.reshape(b, h, w, WINDOW, d) * QK_SCALE
            bk = k.reshape(b, h, w, WINDOW, d)
            bv = v.reshape(b, h, w, WINDOW, d)

            def look_around(t):
                p = jnp.pad(t, ((0, 0), (0, 0), (1, 0), (0, 0), (0, 0)))
                return jnp.concatenate([p[:, :, :w], p[:, :, 1:]], axis=3)
            bk, bv = (look_around(bk), look_around(bv))
            bt = jnp.arange(n).reshape(w, WINDOW)
            btp = jnp.pad(bt, ((1, 0), (0, 0)), constant_values=-1)
            btk = jnp.concatenate([btp[:w], btp[1:]], axis=1)
            sim = jnp.einsum('bhwid,bhwjd->bhwij', bq, bk)
            i = bt[:, :, None]
            j = btk[:, None, :]
            mask = (i < j) | (i > j + WINDOW) | (j == -1)
            sim = jnp.where(mask, -jnp.finfo(sim.dtype).max, sim)
            attn = jax.nn.softmax(sim, axis=-1)
            out = jnp.einsum('bhwij,bhwjd->bhwid', attn, bv)
            return out.reshape(b, h, n, d)

        def _layer(x, wqkv, qs, ksc, wo, lg, lb, w1, b1, w2, b2):
            b, n, _ = x.shape
            h = shift_token(x)
            qkv = h @ wqkv
            q, k, v = jnp.split(qkv, 3, axis=-1)
            to_heads = lambda t: t.reshape(b, n, HEADS, DIM_HEAD).transpose(0, 2, 1, 3)
            q, k, v = (to_heads(q), to_heads(k), to_heads(v))
            q = l2norm(q) * qs
            k = l2norm(k) * ksc
            q, k = rotary_xpos(q, k)
            o = local_attention(q, k, v)
            o = o.transpose(0, 2, 1, 3).reshape(b, n, INNER)
            x = x + o @ wo
            h = shift_token(x)
            mu = h.mean(-1, keepdims=True)
            var = h.var(-1, keepdims=True)
            h = (h - mu) / jnp.sqrt(var + 1e-05) * lg + lb
            h = h @ w1 + b1
            a, g = jnp.split(h, 2, axis=-1)
            h = a * jax.nn.gelu(g, approximate=False)
            x = x + h @ w2 + b2
            return x
        key = jax.random.key(seed)
        ks = jax.random.split(key, 6)
        return {'x': jax.random.normal(ks[0], (B, N, DIM), jnp.float32), 'wqkv': jax.random.normal(ks[1], (DEPTH, DIM, 3 * INNER), jnp.float32) * 0.02, 'q_scale': jnp.ones((DEPTH, DIM_HEAD), jnp.float32), 'k_scale': jnp.ones((DEPTH, DIM_HEAD), jnp.float32), 'wo': jax.random.normal(ks[2], (DEPTH, INNER, DIM), jnp.float32) * 0.02, 'ln_g': jnp.ones((DEPTH, DIM), jnp.float32), 'ln_b': jnp.zeros((DEPTH, DIM), jnp.float32), 'w1': jax.random.normal(ks[3], (DEPTH, DIM, 2 * HID), jnp.float32) * 0.02, 'b1': jnp.zeros((DEPTH, 2 * HID), jnp.float32), 'w2': jax.random.normal(ks[4], (DEPTH, HID, DIM), jnp.float32) * 0.02, 'b2': jnp.zeros((DEPTH, DIM), jnp.float32)}
    _L0_ffn_in = _L0_ffn_setup()

    def _L1_attn_setup():
        import jax, jax.numpy as jnp
        import numpy as np
        BATCH, SEQ = (2, 256)
        D_MODEL, D_STATE, D_CONV, EXPAND = (128, 16, 4, 2)
        D_INNER = EXPAND * D_MODEL

        def _selective_scan(xc, delta, A, Bm, Cm):
            dA = jnp.exp(delta[..., None] * A)
            dBx = delta[..., None] * Bm[:, :, None, :] * xc[..., None]
            h0 = jnp.zeros((xc.shape[0], xc.shape[2], A.shape[1]), xc.dtype)

            def step(h, inp):
                dA_t, dBx_t, c_t = inp
                h = dA_t * h + dBx_t
                y = jnp.einsum('bdn,bn->bd', h, c_t)
                return (h, y)
            _, ys = jax.lax.scan(step, h0, (dA.swapaxes(0, 1), dBx.swapaxes(0, 1), Cm.swapaxes(0, 1)))
            return ys.swapaxes(0, 1)

        def _forward(x, W_in, conv_w, conv_b, W_xproj, w_dt, b_dt, A_log, D_param, W_out):
            xz = x @ W_in
            x_inner, z = jnp.split(xz, 2, axis=-1)
            xc = jax.lax.conv_general_dilated(x_inner.swapaxes(1, 2), conv_w, window_strides=(1,), padding=[(D_CONV - 1, 0)], dimension_numbers=('NCH', 'OIH', 'NCH'), feature_group_count=D_INNER) + conv_b[None, :, None]
            xc = jax.nn.silu(xc.swapaxes(1, 2))
            x_ssm = xc @ W_xproj
            delta_raw = x_ssm[..., :1]
            Bm = x_ssm[..., 1:1 + D_STATE]
            Cm = x_ssm[..., 1 + D_STATE:]
            delta = jax.nn.softplus(delta_raw * w_dt + b_dt)
            A = -jnp.exp(A_log)
            y = _selective_scan(xc, delta, A, Bm, Cm)
            y = y + xc * D_param
            y = y * jax.nn.silu(z)
            return y @ W_out
        key = jax.random.key(seed)
        ks = jax.random.split(key, 8)
        x = jax.random.normal(ks[0], (BATCH, SEQ, D_MODEL), jnp.float32)
        W_in = jax.random.normal(ks[1], (D_MODEL, 2 * D_INNER), jnp.float32) * D_MODEL ** (-0.5)
        conv_w = jax.random.normal(ks[2], (D_INNER, 1, D_CONV), jnp.float32) * D_CONV ** (-0.5)
        conv_b = jnp.zeros((D_INNER,), jnp.float32)
        W_xproj = jax.random.normal(ks[3], (D_INNER, 2 * D_STATE + 1), jnp.float32) * D_INNER ** (-0.5)
        w_dt = jax.random.normal(ks[4], (D_INNER,), jnp.float32)
        b_dt = jnp.zeros((D_INNER,), jnp.float32)
        A_log = jnp.log(jnp.tile(jnp.arange(1, D_STATE + 1, dtype=jnp.float32), (D_INNER, 1)))
        D_param = jnp.ones((D_INNER,), jnp.float32)
        W_out = jax.random.normal(ks[5], (D_INNER, D_MODEL), jnp.float32) * D_INNER ** (-0.5)
        return dict(x=x, W_in=W_in, conv_w=conv_w, conv_b=conv_b, W_xproj=W_xproj, w_dt=w_dt, b_dt=b_dt, A_log=A_log, D_param=D_param, W_out=W_out)
    _L1_attn_in = _L1_attn_setup()

    def _L1_ffn_setup():
        import math
        import jax, jax.numpy as jnp
        import numpy as np
        CAPACITY_FACTOR = 1.25
        key = jax.random.key(seed)
        ks = jax.random.split(key, 5)
        B, S, H, F, E = (4, 512, 128, 128, 32)
        scale_in = 1.0 / math.sqrt(H)
        scale_mid = 1.0 / math.sqrt(F)
        return {'x': jax.random.normal(ks[0], (B, S, H), dtype=jnp.float32), 'w_router': jax.random.normal(ks[1], (H, E), dtype=jnp.float32) * scale_in, 'w_gate': jax.random.normal(ks[2], (E, H, F), dtype=jnp.float32) * scale_in, 'w_up': jax.random.normal(ks[3], (E, H, F), dtype=jnp.float32) * scale_in, 'w_down': jax.random.normal(ks[4], (E, F, H), dtype=jnp.float32) * scale_mid}
    _L1_ffn_in = _L1_ffn_setup()

    def _L2_attn_setup():
        import jax, jax.numpy as jnp
        import numpy as np
        B, L, D, H, DK, DV, DI, NL = (8, 256, 128, 16, 64, 64, 512, 32)
        EPS = 1e-05

        def _layernorm(x, g, b):
            mu = jnp.mean(x, axis=-1, keepdims=True)
            var = jnp.mean(jnp.square(x - mu), axis=-1, keepdims=True)
            return (x - mu) * jax.lax.rsqrt(var + EPS) * g + b

        def _mha(x, wqs, wks, wvs, pw, pb, g, b):
            dk = wqs.shape[-1]
            q = jnp.einsum('mld,hdk->mhlk', x, wqs)
            k = jnp.einsum('mld,hdk->mhlk', x, wks)
            v = jnp.einsum('mld,hdv->mhlv', x, wvs)
            scores = jnp.einsum('mhqk,mhsk->mhqs', q, k) / jnp.sqrt(jnp.asarray(dk, x.dtype))
            attn = jax.nn.softmax(scores, axis=-1)
            out = jnp.einsum('mhqs,mhsv->mhqv', attn, v) - v
            m, h, l, dv = out.shape
            out = out.transpose(0, 2, 1, 3).reshape(m, l, h * dv)
            out = out @ pw + pb
            return _layernorm(out + x, g, b)

        def _ffn(x, w1, b1, w2, b2, g, b):
            h = jax.nn.relu(x @ w1 + b1)
            return _layernorm(h @ w2 + b2 + x, g, b)
        key = jax.random.key(seed)
        inp = {'enc_input': jax.random.normal(key, (B, L, D), jnp.float32)}
        shapes = {}
        for p in ['la', 'sa']:
            shapes[p + '_wqs'] = (H, D, DK)
            shapes[p + '_wks'] = (H, D, DK)
            shapes[p + '_wvs'] = (H, D, DV)
            shapes[p + '_pw'] = (H * DV, D)
            shapes[p + '_pb'] = (D,)
            shapes[p + '_g'] = (D,)
            shapes[p + '_b'] = (D,)
        for p in ['lf', 'pf']:
            shapes[p + '_w1'] = (D, DI)
            shapes[p + '_b1'] = (DI,)
            shapes[p + '_w2'] = (DI, D)
            shapes[p + '_b2'] = (D,)
            shapes[p + '_g'] = (D,)
            shapes[p + '_b'] = (D,)
        for i, (name, shp) in enumerate(shapes.items()):
            k = jax.random.fold_in(key, i + 1)
            if name.endswith('_g'):
                inp[name] = jnp.ones(shp, jnp.float32)
            elif name.endswith(('_b', '_pb', '_b1', '_b2')):
                inp[name] = jnp.zeros(shp, jnp.float32)
            else:
                inp[name] = jax.random.normal(k, shp, jnp.float32) * 0.02
        return inp
    _L2_attn_in = _L2_attn_setup()

    def _L2_ffn_setup():
        import jax, jax.numpy as jnp
        import numpy as np
        B, S, H = (4, 256, 128)
        E, K = (8, 2)
        I_R, I_S = (4 * H, 8 * H)
        CAP_FACTOR = 1.25
        SCALE = 1.0
        key = jax.random.key(seed)
        ks = jax.random.split(key, 9)
        std = 0.02
        return {'x': jax.random.normal(ks[0], (B, S, H), jnp.float32), 'router_w': std * jax.random.normal(ks[1], (E, H), jnp.float32), 'rg': std * jax.random.normal(ks[2], (E, H, I_R), jnp.float32), 'ru': std * jax.random.normal(ks[3], (E, H, I_R), jnp.float32), 'rd': std * jax.random.normal(ks[4], (E, I_R, H), jnp.float32), 'sg': std * jax.random.normal(ks[5], (H, I_S), jnp.float32), 'su': std * jax.random.normal(ks[6], (H, I_S), jnp.float32), 'sd': std * jax.random.normal(ks[7], (I_S, H), jnp.float32)}
    _L2_ffn_in = _L2_ffn_setup()

    def _L3_attn_setup():
        import jax, jax.numpy as jnp
        import numpy as np
        import math
        D_MODEL = 128
        N_HEADS = 16
        D_HEAD = D_MODEL // N_HEADS
        BLOCK = 256
        ROPE_BASE = 10000.0
        B, N = (2, 256)
        HEAD_TYPES = np.arange(N_HEADS) % 4
        PI_BITS = (HEAD_TYPES >> 1 & 1).astype(np.float32)
        E_BITS = (HEAD_TYPES & 1).astype(np.float32)

        def _rotate(t, cos, sin):
            t1 = t[..., 0::2]
            t2 = t[..., 1::2]
            r1 = t1 * cos - t2 * sin
            r2 = t1 * sin + t2 * cos
            return jnp.stack([r1, r2], axis=-1).reshape(t.shape)
        key = jax.random.key(seed)
        k1, k2, k3 = jax.random.split(key, 3)
        x = jax.random.normal(k1, (B, N, D_MODEL), dtype=jnp.float32)
        w_qkv = jax.random.normal(k2, (D_MODEL, 3 * D_MODEL), dtype=jnp.float32) * D_MODEL ** (-0.5)
        w_o = jax.random.normal(k3, (D_MODEL, D_MODEL), dtype=jnp.float32) * D_MODEL ** (-0.5)
        log_xi = jnp.full((N_HEADS,), math.log(BLOCK / 8.0), dtype=jnp.float32)
        return {'x': x, 'w_qkv': w_qkv, 'w_o': w_o, 'log_xi': log_xi}
    _L3_attn_in = _L3_attn_setup()

    def _L3_ffn_setup():
        import jax, jax.numpy as jnp
        import numpy as np
        THRESH_FACTOR = 0.7

        def ternary_quantize(w):
            delta = THRESH_FACTOR * jnp.mean(jnp.abs(w))
            return jnp.where(w > delta, 1.0, jnp.where(w < -delta, -1.0, 0.0)).astype(w.dtype)
        key = jax.random.key(seed)
        k1, k2, k3 = jax.random.split(key, 3)
        B, S, D_IN, D_OUT = (8, 512, 128, 128)
        inp = {'input': jax.random.normal(k1, (B, S, D_IN), dtype=jnp.float32), 'weight': jax.random.normal(k2, (D_OUT, D_IN), dtype=jnp.float32) * (1.0 / np.sqrt(D_IN)), 'alpha': jnp.ones((1,), dtype=jnp.float32), 'bias': jax.random.normal(k3, (D_OUT,), dtype=jnp.float32) * (1.0 / np.sqrt(D_IN))}
        return inp
    _L3_ffn_in = _L3_ffn_setup()
    _d = {'L0_attn_x': _L0_attn_in['x'], 'L0_attn_ig_w': _L0_attn_in['ig_w'], 'L0_attn_ig_b': _L0_attn_in['ig_b'], 'L0_attn_ag_w': _L0_attn_in['ag_w'], 'L0_attn_ag_b': _L0_attn_in['ag_b'], 'L0_attn_a_param': _L0_attn_in['a_param'], 'L0_ffn_wqkv': _L0_ffn_in['wqkv'], 'L0_ffn_q_scale': _L0_ffn_in['q_scale'], 'L0_ffn_k_scale': _L0_ffn_in['k_scale'], 'L0_ffn_wo': _L0_ffn_in['wo'], 'L0_ffn_ln_g': _L0_ffn_in['ln_g'], 'L0_ffn_ln_b': _L0_ffn_in['ln_b'], 'L0_ffn_w1': _L0_ffn_in['w1'], 'L0_ffn_b1': _L0_ffn_in['b1'], 'L0_ffn_w2': _L0_ffn_in['w2'], 'L0_ffn_b2': _L0_ffn_in['b2'], 'L1_attn_W_in': _L1_attn_in['W_in'], 'L1_attn_conv_w': _L1_attn_in['conv_w'], 'L1_attn_conv_b': _L1_attn_in['conv_b'], 'L1_attn_W_xproj': _L1_attn_in['W_xproj'], 'L1_attn_w_dt': _L1_attn_in['w_dt'], 'L1_attn_b_dt': _L1_attn_in['b_dt'], 'L1_attn_A_log': _L1_attn_in['A_log'], 'L1_attn_D_param': _L1_attn_in['D_param'], 'L1_attn_W_out': _L1_attn_in['W_out'], 'L1_ffn_w_router': _L1_ffn_in['w_router'], 'L1_ffn_w_gate': _L1_ffn_in['w_gate'], 'L1_ffn_w_up': _L1_ffn_in['w_up'], 'L1_ffn_w_down': _L1_ffn_in['w_down'], 'L2_attn_la_wqs': _L2_attn_in['la_wqs'], 'L2_attn_la_wks': _L2_attn_in['la_wks'], 'L2_attn_la_wvs': _L2_attn_in['la_wvs'], 'L2_attn_la_pw': _L2_attn_in['la_pw'], 'L2_attn_la_pb': _L2_attn_in['la_pb'], 'L2_attn_la_g': _L2_attn_in['la_g'], 'L2_attn_la_b': _L2_attn_in['la_b'], 'L2_attn_lf_w1': _L2_attn_in['lf_w1'], 'L2_attn_lf_b1': _L2_attn_in['lf_b1'], 'L2_attn_lf_w2': _L2_attn_in['lf_w2'], 'L2_attn_lf_b2': _L2_attn_in['lf_b2'], 'L2_attn_lf_g': _L2_attn_in['lf_g'], 'L2_attn_lf_b': _L2_attn_in['lf_b'], 'L2_attn_sa_wqs': _L2_attn_in['sa_wqs'], 'L2_attn_sa_wks': _L2_attn_in['sa_wks'], 'L2_attn_sa_wvs': _L2_attn_in['sa_wvs'], 'L2_attn_sa_pw': _L2_attn_in['sa_pw'], 'L2_attn_sa_pb': _L2_attn_in['sa_pb'], 'L2_attn_sa_g': _L2_attn_in['sa_g'], 'L2_attn_sa_b': _L2_attn_in['sa_b'], 'L2_attn_pf_w1': _L2_attn_in['pf_w1'], 'L2_attn_pf_b1': _L2_attn_in['pf_b1'], 'L2_attn_pf_w2': _L2_attn_in['pf_w2'], 'L2_attn_pf_b2': _L2_attn_in['pf_b2'], 'L2_attn_pf_g': _L2_attn_in['pf_g'], 'L2_attn_pf_b': _L2_attn_in['pf_b'], 'L2_ffn_router_w': _L2_ffn_in['router_w'], 'L2_ffn_rg': _L2_ffn_in['rg'], 'L2_ffn_ru': _L2_ffn_in['ru'], 'L2_ffn_rd': _L2_ffn_in['rd'], 'L2_ffn_sg': _L2_ffn_in['sg'], 'L2_ffn_su': _L2_ffn_in['su'], 'L2_ffn_sd': _L2_ffn_in['sd'], 'L3_attn_w_qkv': _L3_attn_in['w_qkv'], 'L3_attn_w_o': _L3_attn_in['w_o'], 'L3_attn_log_xi': _L3_attn_in['log_xi'], 'L3_ffn_weight': _L3_ffn_in['weight'], 'L3_ffn_alpha': _L3_ffn_in['alpha'], 'L3_ffn_bias': _L3_ffn_in['bias']}
    _x0 = _d['L0_attn_x']
    _d['L0_attn_x'] = jax.random.normal(jax.random.fold_in(jax.random.key(seed), 1), (8, 256, 128), dtype=_x0.dtype)
    del _x0
    return _d

def reference(L0_attn_x, L0_attn_ig_w, L0_attn_ig_b, L0_attn_ag_w, L0_attn_ag_b, L0_attn_a_param, L0_ffn_wqkv, L0_ffn_q_scale, L0_ffn_k_scale, L0_ffn_wo, L0_ffn_ln_g, L0_ffn_ln_b, L0_ffn_w1, L0_ffn_b1, L0_ffn_w2, L0_ffn_b2, L1_attn_W_in, L1_attn_conv_w, L1_attn_conv_b, L1_attn_W_xproj, L1_attn_w_dt, L1_attn_b_dt, L1_attn_A_log, L1_attn_D_param, L1_attn_W_out, L1_ffn_w_router, L1_ffn_w_gate, L1_ffn_w_up, L1_ffn_w_down, L2_attn_la_wqs, L2_attn_la_wks, L2_attn_la_wvs, L2_attn_la_pw, L2_attn_la_pb, L2_attn_la_g, L2_attn_la_b, L2_attn_lf_w1, L2_attn_lf_b1, L2_attn_lf_w2, L2_attn_lf_b2, L2_attn_lf_g, L2_attn_lf_b, L2_attn_sa_wqs, L2_attn_sa_wks, L2_attn_sa_wvs, L2_attn_sa_pw, L2_attn_sa_pb, L2_attn_sa_g, L2_attn_sa_b, L2_attn_pf_w1, L2_attn_pf_b1, L2_attn_pf_w2, L2_attn_pf_b2, L2_attn_pf_g, L2_attn_pf_b, L2_ffn_router_w, L2_ffn_rg, L2_ffn_ru, L2_ffn_rd, L2_ffn_sg, L2_ffn_su, L2_ffn_sd, L3_attn_w_qkv, L3_attn_w_o, L3_attn_log_xi, L3_ffn_weight, L3_ffn_alpha, L3_ffn_bias):

    def _L0_attn_ref(x, ig_w, ig_b, ag_w, ag_b, a_param):
        import jax, jax.numpy as jnp
        import numpy as np
        MIN_RAD, MAX_RAD, EPS = (0.9, 0.999, 1e-08)

        def block_diag_linear(x, w, b):
            h, bw, _ = w.shape
            xb = x.reshape(x.shape[0], x.shape[1], h, bw)
            y = jnp.einsum('bthi,hij->bthj', xb, w) + b
            return y.reshape(x.shape)
        gate_x = jax.nn.sigmoid(block_diag_linear(x, ig_w, ig_b))
        gate_a = jax.nn.sigmoid(block_diag_linear(x, ag_w, ag_b))
        log_a = -8.0 * gate_a * jax.nn.softplus(a_param)
        a = jnp.exp(log_a)
        a2 = jnp.exp(2.0 * log_a)
        gated_x = x * gate_x
        multiplier = jnp.sqrt(jnp.clip(1.0 - a2, 1e-07))
        normed_x = gated_x * multiplier
        B, T, D = x.shape
        p = jnp.cumprod(a, axis=1)
        p_prefix = jnp.concatenate([jnp.ones((B, 1, D), x.dtype), p[:, :-1]], axis=1)
        p_prefix = jnp.clip(p_prefix, 1e-07)
        w = normed_x / p_prefix
        S = jnp.cumsum(w, axis=1)
        h = p_prefix * S
        return h

    def _L0_ffn_ref(x, wqkv, q_scale, k_scale, wo, ln_g, ln_b, w1, b1, w2, b2):
        import jax, jax.numpy as jnp
        import numpy as np
        DIM = 128
        DEPTH = 2
        HEADS = 8
        DIM_HEAD = 64
        WINDOW = 64
        INNER = HEADS * DIM_HEAD
        HID = int(DIM * 4 * 2 / 3)
        B, N = (2, 1024)
        QK_SCALE = 8.0

        def shift_token(t):
            t1, t2 = jnp.split(t, 2, axis=-1)
            t2 = jnp.pad(t2, ((0, 0), (1, 0), (0, 0)))[:, :-1]
            return jnp.concatenate([t1, t2], axis=-1)

        def l2norm(t):
            return t / jnp.clip(jnp.linalg.norm(t, axis=-1, keepdims=True), 1e-12)

        def rotate_half(x):
            x1, x2 = jnp.split(x, 2, axis=-1)
            return jnp.concatenate([-x2, x1], axis=-1)

        def rotary_xpos(q, k):
            n = q.shape[-2]
            half_idx = jnp.arange(0, DIM_HEAD, 2, dtype=jnp.float32)
            inv_freq = 1.0 / 10000.0 ** (half_idx / DIM_HEAD)
            t = jnp.arange(n, dtype=jnp.float32)
            freqs = t[:, None] * inv_freq[None, :]
            freqs = jnp.concatenate([freqs, freqs], axis=-1)
            base = (half_idx + 0.4 * DIM_HEAD) / (1.4 * DIM_HEAD)
            power = (t - n // 2) / float(WINDOW // 2)
            scale = base[None, :] ** power[:, None]
            scale = jnp.concatenate([scale, scale], axis=-1)
            cos, sin = (jnp.cos(freqs), jnp.sin(freqs))
            q = q * cos * scale + rotate_half(q) * sin * scale
            k = k * cos / scale + rotate_half(k) * sin / scale
            return (q, k)

        def local_attention(q, k, v):
            b, h, n, d = q.shape
            w = n // WINDOW
            bq = q.reshape(b, h, w, WINDOW, d) * QK_SCALE
            bk = k.reshape(b, h, w, WINDOW, d)
            bv = v.reshape(b, h, w, WINDOW, d)

            def look_around(t):
                p = jnp.pad(t, ((0, 0), (0, 0), (1, 0), (0, 0), (0, 0)))
                return jnp.concatenate([p[:, :, :w], p[:, :, 1:]], axis=3)
            bk, bv = (look_around(bk), look_around(bv))
            bt = jnp.arange(n).reshape(w, WINDOW)
            btp = jnp.pad(bt, ((1, 0), (0, 0)), constant_values=-1)
            btk = jnp.concatenate([btp[:w], btp[1:]], axis=1)
            sim = jnp.einsum('bhwid,bhwjd->bhwij', bq, bk)
            i = bt[:, :, None]
            j = btk[:, None, :]
            mask = (i < j) | (i > j + WINDOW) | (j == -1)
            sim = jnp.where(mask, -jnp.finfo(sim.dtype).max, sim)
            attn = jax.nn.softmax(sim, axis=-1)
            out = jnp.einsum('bhwij,bhwjd->bhwid', attn, bv)
            return out.reshape(b, h, n, d)

        def _layer(x, wqkv, qs, ksc, wo, lg, lb, w1, b1, w2, b2):
            b, n, _ = x.shape
            h = shift_token(x)
            qkv = h @ wqkv
            q, k, v = jnp.split(qkv, 3, axis=-1)
            to_heads = lambda t: t.reshape(b, n, HEADS, DIM_HEAD).transpose(0, 2, 1, 3)
            q, k, v = (to_heads(q), to_heads(k), to_heads(v))
            q = l2norm(q) * qs
            k = l2norm(k) * ksc
            q, k = rotary_xpos(q, k)
            o = local_attention(q, k, v)
            o = o.transpose(0, 2, 1, 3).reshape(b, n, INNER)
            x = x + o @ wo
            h = shift_token(x)
            mu = h.mean(-1, keepdims=True)
            var = h.var(-1, keepdims=True)
            h = (h - mu) / jnp.sqrt(var + 1e-05) * lg + lb
            h = h @ w1 + b1
            a, g = jnp.split(h, 2, axis=-1)
            h = a * jax.nn.gelu(g, approximate=False)
            x = x + h @ w2 + b2
            return x
        for l in range(DEPTH):
            x = _layer(x, wqkv[l], q_scale[l], k_scale[l], wo[l], ln_g[l], ln_b[l], w1[l], b1[l], w2[l], b2[l])
        return x

    def _L1_attn_ref(x, W_in, conv_w, conv_b, W_xproj, w_dt, b_dt, A_log, D_param, W_out):
        import jax, jax.numpy as jnp
        import numpy as np
        BATCH, SEQ = (2, 256)
        D_MODEL, D_STATE, D_CONV, EXPAND = (128, 16, 4, 2)
        D_INNER = EXPAND * D_MODEL

        def _selective_scan(xc, delta, A, Bm, Cm):
            dA = jnp.exp(delta[..., None] * A)
            dBx = delta[..., None] * Bm[:, :, None, :] * xc[..., None]
            h0 = jnp.zeros((xc.shape[0], xc.shape[2], A.shape[1]), xc.dtype)

            def step(h, inp):
                dA_t, dBx_t, c_t = inp
                h = dA_t * h + dBx_t
                y = jnp.einsum('bdn,bn->bd', h, c_t)
                return (h, y)
            _, ys = jax.lax.scan(step, h0, (dA.swapaxes(0, 1), dBx.swapaxes(0, 1), Cm.swapaxes(0, 1)))
            return ys.swapaxes(0, 1)

        def _forward(x, W_in, conv_w, conv_b, W_xproj, w_dt, b_dt, A_log, D_param, W_out):
            xz = x @ W_in
            x_inner, z = jnp.split(xz, 2, axis=-1)
            xc = jax.lax.conv_general_dilated(x_inner.swapaxes(1, 2), conv_w, window_strides=(1,), padding=[(D_CONV - 1, 0)], dimension_numbers=('NCH', 'OIH', 'NCH'), feature_group_count=D_INNER) + conv_b[None, :, None]
            xc = jax.nn.silu(xc.swapaxes(1, 2))
            x_ssm = xc @ W_xproj
            delta_raw = x_ssm[..., :1]
            Bm = x_ssm[..., 1:1 + D_STATE]
            Cm = x_ssm[..., 1 + D_STATE:]
            delta = jax.nn.softplus(delta_raw * w_dt + b_dt)
            A = -jnp.exp(A_log)
            y = _selective_scan(xc, delta, A, Bm, Cm)
            y = y + xc * D_param
            y = y * jax.nn.silu(z)
            return y @ W_out
        return _forward(x, W_in, conv_w, conv_b, W_xproj, w_dt, b_dt, A_log, D_param, W_out)

    def _L1_ffn_ref(x, w_router, w_gate, w_up, w_down):
        import math
        import jax, jax.numpy as jnp
        import numpy as np
        CAPACITY_FACTOR = 1.25
        B, S, H = x.shape
        E = w_gate.shape[0]
        T = B * S
        C = int(math.ceil(CAPACITY_FACTOR * T / E))
        xt = x.reshape(T, H)
        logits = xt @ w_router
        probs = jax.nn.softmax(logits, axis=-1)
        top1 = jnp.argmax(probs, axis=-1)
        gate = jnp.take_along_axis(probs, top1[:, None], axis=1)[:, 0]
        onehot = jax.nn.one_hot(top1, E, dtype=jnp.int32)
        pos = jnp.cumsum(onehot, axis=0)[jnp.arange(T), top1] - 1
        accepted = pos < C
        slot = jnp.where(accepted, top1 * C + pos, E * C)
        buf = jnp.zeros((E * C + 1, H), dtype=x.dtype).at[slot].set(xt)
        buf = buf[:E * C].reshape(E, C, H)
        g = jnp.einsum('ech,ehf->ecf', buf, w_gate)
        u = jnp.einsum('ech,ehf->ecf', buf, w_up)
        y = jnp.einsum('ecf,efh->ech', jax.nn.silu(g) * u, w_down)
        out_tok = y.reshape(E * C, H)[jnp.clip(slot, 0, E * C - 1)]
        out_tok = jnp.where(accepted[:, None], out_tok * gate[:, None], 0.0)
        return (xt + out_tok).reshape(B, S, H)

    def _L2_attn_ref(enc_input, la_wqs, la_wks, la_wvs, la_pw, la_pb, la_g, la_b, lf_w1, lf_b1, lf_w2, lf_b2, lf_g, lf_b, sa_wqs, sa_wks, sa_wvs, sa_pw, sa_pb, sa_g, sa_b, pf_w1, pf_b1, pf_w2, pf_b2, pf_g, pf_b):
        import jax, jax.numpy as jnp
        import numpy as np
        B, L, D, H, DK, DV, DI, NL = (8, 256, 128, 16, 64, 64, 512, 32)
        EPS = 1e-05

        def _layernorm(x, g, b):
            mu = jnp.mean(x, axis=-1, keepdims=True)
            var = jnp.mean(jnp.square(x - mu), axis=-1, keepdims=True)
            return (x - mu) * jax.lax.rsqrt(var + EPS) * g + b

        def _mha(x, wqs, wks, wvs, pw, pb, g, b):
            dk = wqs.shape[-1]
            q = jnp.einsum('mld,hdk->mhlk', x, wqs)
            k = jnp.einsum('mld,hdk->mhlk', x, wks)
            v = jnp.einsum('mld,hdv->mhlv', x, wvs)
            scores = jnp.einsum('mhqk,mhsk->mhqs', q, k) / jnp.sqrt(jnp.asarray(dk, x.dtype))
            attn = jax.nn.softmax(scores, axis=-1)
            out = jnp.einsum('mhqs,mhsv->mhqv', attn, v) - v
            m, h, l, dv = out.shape
            out = out.transpose(0, 2, 1, 3).reshape(m, l, h * dv)
            out = out @ pw + pb
            return _layernorm(out + x, g, b)

        def _ffn(x, w1, b1, w2, b2, g, b):
            h = jax.nn.relu(x @ w1 + b1)
            return _layernorm(h @ w2 + b2 + x, g, b)
        b, l, d = enc_input.shape
        nl = NL
        x = enc_input.reshape(-1, nl, d)
        x = _mha(x, la_wqs, la_wks, la_wvs, la_pw, la_pb, la_g, la_b)
        x = _ffn(x, lf_w1, lf_b1, lf_w2, lf_b2, lf_g, lf_b)
        x = x.reshape(b, l // nl, nl, d).transpose(0, 2, 1, 3).reshape(-1, l // nl, d)
        x = _mha(x, sa_wqs, sa_wks, sa_wvs, sa_pw, sa_pb, sa_g, sa_b)
        x = _ffn(x, pf_w1, pf_b1, pf_w2, pf_b2, pf_g, pf_b)
        out = x.reshape(b, nl, l // nl, d).transpose(0, 2, 1, 3).reshape(b, l, d)
        return out

    def _L2_ffn_ref(x, router_w, rg, ru, rd, sg, su, sd):
        import jax, jax.numpy as jnp
        import numpy as np
        B, S, H = (4, 256, 128)
        E, K = (8, 2)
        I_R, I_S = (4 * H, 8 * H)
        CAP_FACTOR = 1.25
        SCALE = 1.0
        b, s, h = x.shape
        T = b * s
        capacity = max(int(CAP_FACTOR * T / E), 1)
        xf = x.reshape(T, h)
        eps = jnp.finfo(x.dtype).eps
        xn = xf * jax.lax.rsqrt(jnp.mean(xf * xf, axis=-1, keepdims=True) + eps)
        logits = xn @ router_w.T
        probs = jax.nn.softmax(logits, axis=-1)
        topk_p, topk_i = jax.lax.top_k(probs, K)
        rw = topk_p / jnp.sum(topk_p, axis=-1, keepdims=True)
        one_hot = jax.nn.one_hot(topk_i, E, dtype=x.dtype)
        mask = one_hot.sum(1)
        wdense = (one_hot * rw[..., None]).sum(1)
        sel = mask.T.astype(bool)
        order = jnp.argsort(~sel, axis=1, stable=True)
        dispatch = order[:, :capacity]
        count = sel.sum(axis=1)
        valid = (jnp.arange(capacity)[None, :] < count[:, None]).astype(x.dtype)
        xg = xf[dispatch]
        gate = jax.nn.silu(jnp.einsum('ech,ehi->eci', xg, rg))
        up = jnp.einsum('ech,ehi->eci', xg, ru)
        eout = jnp.einsum('eci,eih->ech', gate * up, rd)
        w = jnp.take_along_axis(wdense.T, dispatch, axis=1)
        contrib = eout * (w * valid)[..., None]
        routed = jnp.zeros_like(xf).at[dispatch.reshape(-1)].add(contrib.reshape(-1, h))
        shared = jax.nn.silu(x @ sg) * (x @ su) @ sd
        return shared + SCALE * routed.reshape(b, s, h)

    def _L3_attn_ref(x, w_qkv, w_o, log_xi):
        import jax, jax.numpy as jnp
        import numpy as np
        import math
        D_MODEL = 128
        N_HEADS = 16
        D_HEAD = D_MODEL // N_HEADS
        BLOCK = 256
        ROPE_BASE = 10000.0
        B, N = (2, 256)
        HEAD_TYPES = np.arange(N_HEADS) % 4
        PI_BITS = (HEAD_TYPES >> 1 & 1).astype(np.float32)
        E_BITS = (HEAD_TYPES & 1).astype(np.float32)

        def _rotate(t, cos, sin):
            t1 = t[..., 0::2]
            t2 = t[..., 1::2]
            r1 = t1 * cos - t2 * sin
            r2 = t1 * sin + t2 * cos
            return jnp.stack([r1, r2], axis=-1).reshape(t.shape)
        b, n, _ = x.shape
        H, dh = (N_HEADS, D_HEAD)
        qkv = (x @ w_qkv).reshape(b, n, 3, H, dh)
        q = jnp.transpose(qkv[:, :, 0], (0, 2, 1, 3))
        k = jnp.transpose(qkv[:, :, 1], (0, 2, 1, 3))
        v = jnp.transpose(qkv[:, :, 2], (0, 2, 1, 3))
        pos = jnp.arange(n, dtype=jnp.float32)
        inv_freq = ROPE_BASE ** (-(jnp.arange(0, dh, 2, dtype=jnp.float32) / dh))
        theta = pos[:, None] * inv_freq[None, :]
        cos, sin = (jnp.cos(theta), jnp.sin(theta))
        pi = jnp.asarray(PI_BITS)[None, :, None, None]
        q = pi * _rotate(q, cos, sin) + (1.0 - pi) * q
        k = pi * _rotate(k, cos, sin) + (1.0 - pi) * k
        d_mat = jnp.abs(pos[:, None] - pos[None, :])
        xi = jnp.exp(log_xi)
        e = jnp.asarray(E_BITS)[:, None, None]
        decay = -e * d_mat[None, :, :] / xi[:, None, None]
        causal = jnp.where(pos[:, None] >= pos[None, :], 0.0, -jnp.inf)
        bias = decay + causal[None, :, :]
        scores = jnp.einsum('bhqd,bhkd->bhqk', q, k) * dh ** (-0.5) + bias[None]
        attn = jax.nn.softmax(scores, axis=-1)
        out = jnp.einsum('bhqk,bhkd->bhqd', attn, v)
        out = jnp.transpose(out, (0, 2, 1, 3)).reshape(b, n, H * dh)
        return out @ w_o

    def _L3_ffn_ref(input, weight, alpha, bias):
        import jax, jax.numpy as jnp
        import numpy as np
        THRESH_FACTOR = 0.7

        def ternary_quantize(w):
            delta = THRESH_FACTOR * jnp.mean(jnp.abs(w))
            return jnp.where(w > delta, 1.0, jnp.where(w < -delta, -1.0, 0.0)).astype(w.dtype)
        w_ternary = ternary_quantize(weight)
        w_eff = w_ternary * alpha
        out = jnp.einsum('bsd,od->bso', input, w_eff) + bias
        return out
    x = L0_attn_x
    x = _layernorm(x + _L0_attn_ref(x, L0_attn_ig_w, L0_attn_ig_b, L0_attn_ag_w, L0_attn_ag_b, L0_attn_a_param), axis=-1)
    x = _layernorm(x + _L0_ffn_ref(x, L0_ffn_wqkv, L0_ffn_q_scale, L0_ffn_k_scale, L0_ffn_wo, L0_ffn_ln_g, L0_ffn_ln_b, L0_ffn_w1, L0_ffn_b1, L0_ffn_w2, L0_ffn_b2), axis=-1)
    x = _layernorm(x + _L1_attn_ref(x, L1_attn_W_in, L1_attn_conv_w, L1_attn_conv_b, L1_attn_W_xproj, L1_attn_w_dt, L1_attn_b_dt, L1_attn_A_log, L1_attn_D_param, L1_attn_W_out), axis=-1)
    x = _layernorm(x + _L1_ffn_ref(x, L1_ffn_w_router, L1_ffn_w_gate, L1_ffn_w_up, L1_ffn_w_down), axis=-1)
    x = _layernorm(x + _L2_attn_ref(x, L2_attn_la_wqs, L2_attn_la_wks, L2_attn_la_wvs, L2_attn_la_pw, L2_attn_la_pb, L2_attn_la_g, L2_attn_la_b, L2_attn_lf_w1, L2_attn_lf_b1, L2_attn_lf_w2, L2_attn_lf_b2, L2_attn_lf_g, L2_attn_lf_b, L2_attn_sa_wqs, L2_attn_sa_wks, L2_attn_sa_wvs, L2_attn_sa_pw, L2_attn_sa_pb, L2_attn_sa_g, L2_attn_sa_b, L2_attn_pf_w1, L2_attn_pf_b1, L2_attn_pf_w2, L2_attn_pf_b2, L2_attn_pf_g, L2_attn_pf_b), axis=-1)
    x = _layernorm(x + _L2_ffn_ref(x, L2_ffn_router_w, L2_ffn_rg, L2_ffn_ru, L2_ffn_rd, L2_ffn_sg, L2_ffn_su, L2_ffn_sd), axis=-1)
    x = _layernorm(x + _L3_attn_ref(x, L3_attn_w_qkv, L3_attn_w_o, L3_attn_log_xi), axis=-1)
    x = _layernorm(x + _L3_ffn_ref(x, L3_ffn_weight, L3_ffn_alpha, L3_ffn_bias), axis=-1)
    return x

_drawn_inputs = setup_inputs


def setup_inputs(seed=0):
    import zlib

    import numpy as np

    out = dict(_drawn_inputs(seed))
    spreads = {'L0_attn_ig_b': (0.0, 0.1),
     'L0_attn_ag_b': (0.0, 0.1),
     'L0_ffn_q_scale': (1.0, 0.6),
     'L0_ffn_k_scale': (1.0, 0.6),
     'L0_ffn_ln_g': (1.0, 0.6),
     'L0_ffn_ln_b': (0.0, 0.8),
     'L0_ffn_b1': (0.0, 0.8),
     'L0_ffn_b2': (0.0, 0.1),
     'L1_attn_conv_b': (0.0, 0.1),
     'L1_attn_b_dt': (0.0, 0.311),
     'L1_attn_D_param': (1.0, 0.2),
     'L2_attn_la_pb': (0.0, 0.1),
     'L2_attn_la_g': (1.0, 0.2),
     'L2_attn_la_b': (0.0, 0.1),
     'L2_attn_lf_b1': (0.0, 0.502),
     'L2_attn_lf_b2': (0.0, 0.1),
     'L2_attn_lf_g': (1.0, 0.2),
     'L2_attn_lf_b': (0.0, 0.1),
     'L2_attn_sa_pb': (0.0, 0.1),
     'L2_attn_sa_g': (1.0, 0.2),
     'L2_attn_sa_b': (0.0, 0.1),
     'L2_attn_pf_b1': (0.0, 0.388),
     'L2_attn_pf_b2': (0.0, 0.1),
     'L2_attn_pf_g': (1.0, 0.2),
     'L2_attn_pf_b': (0.0, 0.1),
     'L3_attn_log_xi': (3.465735912322998, 0.2)}
    factors = {'L0_ffn_w1': 4.401,
     'L0_ffn_w2': 4.372,
     'L2_attn_la_wqs': 8.0,
     'L2_attn_la_wks': 8.0,
     'L2_attn_sa_wqs': 8.0,
     'L2_attn_sa_wks': 8.0,
     'L2_ffn_router_w': 8.0,
     'L2_ffn_rg': 8.0,
     'L2_ffn_ru': 8.0,
     'L2_ffn_rd': 8.0,
     'L2_ffn_sg': 3.408,
     'L2_ffn_su': 3.242,
     'L2_ffn_sd': 3.469,
     'L3_ffn_bias': 5.461}
    for name, (base, spread) in spreads.items():
        noise = np.random.default_rng([zlib.crc32(name.encode()), seed]).standard_normal(out[name].shape)
        drawn = base * np.exp(spread * noise) if base else spread * noise
        out[name] = jnp.asarray(drawn.astype(out[name].dtype))
    for name, factor in factors.items():
        out[name] = (out[name] * factor).astype(out[name].dtype)
    return out
```

```python
from collections import namedtuple
from contextlib import ExitStack

import numpy as np
import concourse.bass as bass
from concourse import mybir

F32 = mybir.dt.float32
I32 = mybir.dt.int32
U32 = mybir.dt.uint32
ALU = mybir.AluOpType
ACT = mybir.ActivationFunctionType
AX = mybir.AxisListType

P = 128
B, L, D = 8, 256, 128
T = B * L
NT = T // P
TPB = L // P
EPS = 1e-5
NEG = -1e30

WIN, LH, LDH = 64, 8, 64
INNER = LH * LDH
DEPTH = 2
HID = int(D * 4 * 2 / 3)
HCH = [(0, 128), (128, 128), (256, HID - 256)]
QK_SCALE = 8.0
DIN, NS, NCONV = 2 * D, 16, 4
XP = 2 * NS + 1
E1, C1 = 32, (5 * T + 4 * 32 - 1) // (4 * 32)
E2, C2, IR, IS = 8, 5 * T // (4 * 8), 4 * D, 8 * D
SLOTS = E1 * C1
AH, ADK, NL, DI = 16, 64, 32, 512
RH, RDH = 16, 8


def group(**named):
    return namedtuple("Group", named)(**named)


class Signal:
    def __init__(self, sem, per):
        self.sem, self.per = sem, per

    def at(self, i, c):
        return i * self.per + c + 1


def settle(eng, s):
    eng.sem_inc(s.settled.sem, 1)


class Shared:
    pass


def open_stage(nc, pool, spec):
    signals = {}
    for sem, word in zip(pool, spec.split(), strict=False):
        name, per = word.split(":")
        nc.sync.sem_inc(sem, 1)
        signals[name] = Signal(sem, int(per))
    assert len(signals) == len(spec.split())
    nc.all_engine_barrier()
    return group(**signals)


def close_stage(nc, pool):
    nc.all_engine_barrier(sems_to_clear=range(pool[0].num, pool[0].num + len(pool)))


def tables():
    f = np.float32
    out = {"ident": np.eye(P, dtype=f), "ones": np.ones((P, P), f)}
    half = np.arange(0, LDH, 2).astype(f)
    inv = (f(1.0) / f(10000.0) ** (half / f(LDH))).astype(f)
    t = np.arange(L).astype(f)
    fr = np.concatenate([t[:, None] * inv[None]] * 2, -1).astype(f)
    base = ((half + f(0.4 * LDH)) / f(1.4 * LDH)).astype(f)
    power = ((t - L // 2) / f(WIN // 2)).astype(f)
    sc = np.concatenate([base[None] ** power[:, None]] * 2, -1).astype(f)
    sign = np.where(np.arange(LDH) < LDH // 2, f(-1), f(1))
    rope = np.stack([np.cos(fr) * sc, np.sin(fr) * sc * sign, np.cos(fr) / sc, np.sin(fr) / sc * sign], 1)
    out["rope"] = rope.reshape(TPB, P, 4, LDH).transpose(1, 0, 2, 3).astype(f)
    q, k = np.arange(L)[:, None], np.arange(L)[None]
    ok = (k <= q) & (k >= q - WIN) & (k // WIN >= q // WIN - 1)
    out["lmask"] = np.where(ok, f(0), f(NEG)).reshape(TPB, P, L).transpose(1, 0, 2)
    p = np.arange(P)
    out["blk32"] = np.where(p[:, None] // NL == p[None] // NL, f(0), f(NEG))
    out["blk8"] = np.where(p[:, None] // 8 == p[None] // 8, f(0), f(NEG))
    out["causal"] = np.where(k <= q, f(0), f(NEG)).reshape(TPB, P, L).transpose(1, 0, 2)
    out["mdist"] = (-np.abs(q - k)).astype(f).reshape(TPB, P, L).transpose(1, 0, 2)
    iv = (f(10000.0) ** (-(np.arange(0, RDH, 2).astype(f) / f(RDH)))).astype(f)
    th = (t[:, None] * iv[None]).astype(f)
    out["rcos"] = np.cos(th).reshape(TPB, P, RDH // 2).transpose(1, 0, 2)
    out["rsin"] = np.sin(th).reshape(TPB, P, RDH // 2).transpose(1, 0, 2)
    out["tri"] = (p[:, None] <= p[None]).astype(f)
    out["iota32"] = np.broadcast_to(np.arange(E1) - 64, (P, E1))
    out["trash"] = SLOTS + p[:, None] + P * np.arange(2 * NT)[None]
    return {n: np.ascontiguousarray(a.reshape(P, -1), dtype=f) for n, a in out.items()}


def table_layout():
    at, off = {}, 0
    for n, a in tables().items():
        at[n] = (off, a.shape[1])
        off += a.shape[1]
    return at, off


NORM = "settled:0 y_ready:1 stats:1 agg:1 var_eps:1 rstd:1 xn_ready:1 xnT_ready:1 x_updated:1 kept:1"


def norm_dve(dve, s, n, i, y, turned=True):
    if n.in_psum:
        dve.wait_ge(s.y_ready.sem, s.y_ready.at(i, 1))
    for t in range(TPB):
        last = dve.bn_stats(n.st[:, t, :], y[:, t, :])
    last.then_inc(s.stats.sem, 1)
    dve.wait_ge(s.stats.sem, s.stats.at(i, 1))
    dve.wait_ge(s.rstd.sem, s.rstd.at(i, 0))
    settle(dve, s)
    for t in range(TPB):
        last = dve.bn_aggr(n.mv[:, t, :], n.st[:, t, :])
    last.then_inc(s.agg.sem, 1)
    dve.wait_ge(s.rstd.sem, s.rstd.at(i, 1))
    if turned:
        dve.wait_ge(s.xnT_ready.sem, s.xnT_ready.at(i, 0))
    if n.keep:
        dve.wait_ge(s.kept.sem, s.kept.at(i, 0))
    for t in range(TPB):
        last = dve.tensor_scalar(n.xn[:, t, :], y[:, t, :], n.mv[:, t, 0:1], n.rstd[:, t:t + 1],
                                 ALU.subtract, ALU.mult)
    last.then_inc(s.xn_ready.sem, 1)


def norm_pool(pool, s, n, i):
    pool.wait_ge(s.agg.sem, s.agg.at(i, 1))
    pool.tensor_tensor(n.ve[:, :], n.mv[:, :, 1], n.eps[:, 0:TPB], ALU.add).then_inc(s.var_eps.sem, 1)
    pool.wait_ge(s.var_eps.sem, s.var_eps.at(i, 1))
    pool.wait_ge(s.xn_ready.sem, s.xn_ready.at(i, 0))
    pool.tensor_tensor(n.rstd[:, :], n.ve[:, :], n.neghalf[:, 0:TPB], ALU.pow).then_inc(s.rstd.sem, 1)
    if n.keep:
        pool.wait_ge(s.xn_ready.sem, s.xn_ready.at(i, 1))
        settle(pool, s)
        pool.tensor_copy(n.x_tok[:, bass.ds(i * L, L)], n.xn[:, :, :].rearrange("p t d -> p (t d)"))\
            .then_inc(s.kept.sem, 1)


def norm_pe(pe, s, n, i, psT):
    pe.wait_ge(s.xn_ready.sem, s.xn_ready.at(i, 1))
    for t in range(TPB):
        last = pe.transpose(psT[:, t * P:(t + 1) * P], n.xn[:, t, :], n.ident)
    last.then_inc(s.xnT_ready.sem, 1)


def norm_act(act, s, i, psT, dst, scale=1.0, bias=0.0):
    act.wait_ge(s.xnT_ready.sem, s.xnT_ready.at(i, 1))
    settle(act, s)
    act.activation(dst, psT, ACT.Identity, scale=scale, bias=bias).then_inc(s.x_updated.sem, 1)


def norm_buffers(ctx, nc, net, keep=False, in_psum=True):
    sb = lambda name, shape: ctx.enter_context(nc.sbuf_tensor(net.name(name), shape, F32))
    return group(st=sb("n_st", [P, TPB, 6]), mv=sb("n_mv", [P, TPB, 2]), ve=sb("n_ve", [P, TPB]),
                           rstd=sb("n_rstd", [P, TPB]), xn=sb("n_xn", [P, TPB, D]), neghalf=net.neghalf, eps=net.eps,
                           ident=net.tab("ident"), x_tok=net.x_tok, keep=keep, in_psum=in_psum)


def stage_load(nc, net, io):
    s = open_stage(nc, net.pool, "xT_ps:4 xT_done:4 zero:1 const:1")
    with nc.Block() as block:
        @block.sync
        def _(sp):
            sp.dma_start(net.x_tok[:, :].rearrange("p (t d) -> p t d", d=D),
                         io["L0_attn_x"].rearrange("b (t p) d -> p (b t) d", p=P)).then_inc(net.ld_x, 16)
            sp.dma_start(net.tabs[:, :], io["tables"]).then_inc(net.ld_x, 16)
            with nc.allow_non_contiguous_dma(reason="a few hundred biases, one to a partition"):
                for dst, src in net.loads_sp:
                    sp.dma_start(dst, src).then_inc(net.ld_w, 16)

        @block.gpsimd
        def _(pool):
            pool.memset(net.zero[:, :], 0.0).then_inc(s.zero.sem, 1)
            pool.wait_ge(s.zero.sem, s.zero.at(0, 1))
            for buf in net.slots:
                for k in range(SLOTS // 512):
                    pool.dma_start(buf[k * 512:(k + 1) * 512, :].rearrange("(p r) d -> p (r d)", p=P), net.zero[:, :]).then_inc(net.zeroed, 16)
            pool.memset(net.neghalf[:, :], -0.5)
            pool.memset(net.eps[:, :], EPS)
            pool.memset(net.half[:, :], 0.5).then_inc(s.const.sem, 1)

        @block.scalar
        def _(act):
            for dst, src in net.loads_act:
                act.dma_start(dst, src).then_inc(net.ld_moe, 16)
            for g in range(4):
                act.wait_ge(s.xT_ps.sem, s.xT_ps.at(0, g + 1))
                act.activation(net.xT[:, g * 512:(g + 1) * 512], net.bank[g][:, :], ACT.Copy).then_inc(s.xT_done.sem, 1)

        @block.tensor
        def _(pe):
            pe.wait_ge(net.ld_x, 32)
            for g in range(4):
                for t in range(4):
                    k = 4 * g + t
                    last = pe.transpose(net.bank[g][:, t * P:(t + 1) * P], net.x_tok[:, k * P:(k + 1) * P], net.tab("ident"))
                last.then_inc(s.xT_ps.sem, 1)
    close_stage(nc, net.pool)


def stage_recurrence(nc, net, io):
    with ExitStack() as ctx:
        sb = lambda name, shape: ctx.enter_context(nc.sbuf_tensor(net.name(name), shape, F32))
        gx, ga, a, m, p = (sb(n, [P, T]) for n in ("gx", "ga", "a_shift", "mult", "prefix"))
        first, later = sb("first", [P, T]), sb("later", [P, T])
        wi, wa = sb("ig_blocks", [P, P]), sb("ag_blocks", [P, P])
        bi, ba, ap_, t1, t2, c8, c16 = (sb(n, [P, 1]) for n in ("ig_b", "ag_b", "a_par", "t1", "t2", "c8", "c16"))
        z = sb("z", [P, L])
        n = norm_buffers(ctx, nc, net)
        ld = net.ld_a
        s = open_stage(nc, net.pool, "blocks0:1 masks0:1 masks:1 gates_ps:8 gate_x:4 gate_a:4 soft:3 decay:1 decay2:1 "
                       "v:16 root:1 h_ready:1 z_ready:1 z_used:1 " + NORM)
        x3 = lambda ap: ap[:, :].rearrange("p (b t) -> p b t", t=L)
        H, W = io["L0_attn_ig_w"].shape[0:2]
        with nc.Block() as block:
            @block.sync
            def _(sp):
                for dst, name in ((bi, "L0_attn_ig_b"), (ba, "L0_attn_ag_b")):
                    sp.dma_start(dst[:, :], io[name].rearrange("h (w o) -> (h w) o", o=1)).then_inc(ld, 16)
                sp.dma_start(ap_[:, :], io["L0_attn_a_param"].rearrange("(w o) -> w o", o=1)).then_inc(ld, 16)
                sp.wait_ge(s.blocks0.sem, s.blocks0.at(0, 1))
                for dst, name in ((wi, "L0_attn_ig_w"), (wa, "L0_attn_ag_w")):
                    for h in range(H):
                        sp.dma_start(dst[h * W:(h + 1) * W, h * W:(h + 1) * W], io[name][h]).then_inc(ld, 16)

            @block.gpsimd
            def _(pool):
                pool.memset(wi[:, :], 0.0)
                pool.memset(wa[:, :], 0.0).then_inc(s.blocks0.sem, 1)
                pool.memset(first[:, :], 0.0)
                pool.memset(later[:, :], 1.0).then_inc(s.masks0.sem, 1)
                pool.wait_ge(s.masks0.sem, s.masks0.at(0, 1))
                pool.memset(x3(first)[:, :, 0:1], 1.0)
                pool.memset(x3(later)[:, :, 0:1], 0.0)
                pool.memset(x3(a)[:, :, 0:1], 0.0).then_inc(s.masks.sem, 1)
                pool.wait_ge(s.h_ready.sem, s.h_ready.at(0, 1))
                with pool.Fori(0, B) as i:
                    pool.wait_ge(s.z_used.sem, s.z_used.at(i, 0))
                    pool.tensor_copy(z[:, :], gx[:, bass.ds(i * L, L)]).then_inc(s.z_ready.sem, 1)
                    norm_pool(pool, s, n, i)

            @block.tensor
            def _(pe):
                pe.wait_ge(ld, 16 * (3 + 2 * H))
                for j, w in enumerate((wi, wa)):
                    for g in range(4):
                        pe.matmul(net.bank[4 * j + g][:, :], w[:, :], net.xT[:, g * 512:(g + 1) * 512],
                                  start=True, stop=True).then_inc(s.gates_ps.sem, 1)
                pe.wait_ge(s.gate_a.sem, s.gate_a.at(0, 4))
                with pe.Fori(0, B) as i:
                    pe.wait_ge(s.z_ready.sem, s.z_ready.at(i, 1))
                    pe.wait_ge(s.xn_ready.sem, s.xn_ready.at(i, 0))
                    for t in range(TPB):
                        last = pe.transpose(net.bank[0][:, t * P:(t + 1) * P], z[:, t * P:(t + 1) * P], net.tab("ident"))
                    last.then_inc(s.y_ready.sem, 1)
                    pe.wait_ge(s.x_updated.sem, s.x_updated.at(i, 0))
                    norm_pe(pe, s, n, i, net.bank[1][:, 0:L])

            @block.scalar
            def _(act):
                act.wait_ge(ld, 16 * (3 + 2 * H))
                act.activation(t1[:, :], ap_[:, :], ACT.Abs).then_inc(s.soft.sem, 1)
                act.wait_ge(s.soft.sem, s.soft.at(0, 1))
                act.activation(t2[:, :], t1[:, :], ACT.Exp, scale=-1.0).then_inc(s.soft.sem, 1)
                act.wait_ge(s.soft.sem, s.soft.at(0, 2))
                act.activation(t1[:, :], t2[:, :], ACT.Ln, bias=1.0).then_inc(s.soft.sem, 1)
                for j, (dst, bias, done) in enumerate(((ga, ba, s.gate_a), (gx, bi, s.gate_x))):
                    for g in range(4):
                        act.wait_ge(s.gates_ps.sem, s.gates_ps.at(0, 8 if j == 0 else 8))
                        act.activation(dst[:, g * 512:(g + 1) * 512], net.bank[4 * (1 - j) + g][:, :], ACT.Sigmoid,
                                       bias=bias[:, :]).then_inc(done.sem, 1)
                act.wait_ge(s.gate_a.sem, s.gate_a.at(0, 4))
                act.wait_ge(s.v.sem, s.v.at(0, 3))
                act.wait_ge(s.masks.sem, s.masks.at(0, 1))
                act.activation(x3(a)[:, :, 1:L], x3(ga)[:, :, 0:L - 1], ACT.Exp, scale=c8[:, :]).then_inc(s.decay.sem, 1)
                act.activation(m[:, :], ga[:, :], ACT.Exp, scale=c16[:, :]).then_inc(s.decay2.sem, 1)
                act.wait_ge(s.v.sem, s.v.at(0, 6))
                act.activation(m[:, :], m[:, :], ACT.Sqrt).then_inc(s.root.sem, 1)
                with act.Fori(0, B) as i:
                    norm_act(act, s, i, net.bank[1][:, 0:L], net.xT[:, bass.ds(i * L, L)])

            @block.vector
            def _(dve):
                v = s.v
                dve.wait_ge(s.soft.sem, s.soft.at(0, 3))
                dve.scalar_tensor_tensor(t2[:, :], ap_[:, :], 0.0, t1[:, :], ALU.max, ALU.add).then_inc(v.sem, 1)
                dve.wait_ge(v.sem, v.at(0, 1))
                dve.tensor_scalar(c8[:, :], t2[:, :], -8.0, None, ALU.mult).then_inc(v.sem, 1)
                dve.tensor_scalar(c16[:, :], t2[:, :], -16.0, None, ALU.mult).then_inc(v.sem, 1)
                dve.wait_ge(s.gate_x.sem, s.gate_x.at(0, 4))
                dve.tensor_tensor(gx[:, :], gx[:, :], net.xT[:, :], ALU.mult).then_inc(v.sem, 1)
                dve.wait_ge(s.decay2.sem, s.decay2.at(0, 1))
                dve.tensor_scalar(m[:, :], m[:, :], -1.0, 1.0, ALU.mult, ALU.add).then_inc(v.sem, 1)
                dve.wait_ge(v.sem, v.at(0, 5))
                dve.tensor_scalar(m[:, :], m[:, :], 1e-7, None, ALU.max).then_inc(v.sem, 1)
                dve.wait_ge(s.decay.sem, s.decay.at(0, 1))
                dve.tensor_tensor_scan(p[:, :], a[:, :], first[:, :], 0.0, ALU.mult, ALU.add).then_inc(v.sem, 1)
                dve.wait_ge(v.sem, v.at(0, 7))
                dve.tensor_scalar(p[:, :], p[:, :], 1e-7, None, ALU.max).then_inc(v.sem, 1)
                dve.wait_ge(s.root.sem, s.root.at(0, 1))
                dve.tensor_tensor(gx[:, :], gx[:, :], m[:, :], ALU.mult).then_inc(v.sem, 1)
                dve.wait_ge(v.sem, v.at(0, 9))
                dve.reciprocal(m[:, :], p[:, :]).then_inc(v.sem, 1)
                dve.wait_ge(v.sem, v.at(0, 10))
                dve.tensor_tensor(gx[:, :], gx[:, :], m[:, :], ALU.mult).then_inc(v.sem, 1)
                dve.wait_ge(v.sem, v.at(0, 11))
                dve.tensor_tensor_scan(ga[:, :], later[:, :], gx[:, :], 0.0, ALU.mult, ALU.add).then_inc(v.sem, 1)
                dve.wait_ge(v.sem, v.at(0, 12))
                dve.tensor_tensor(gx[:, :], p[:, :], ga[:, :], ALU.mult).then_inc(v.sem, 1)
                dve.wait_ge(v.sem, v.at(0, 13))
                dve.tensor_tensor(gx[:, :], gx[:, :], net.xT[:, :], ALU.add).then_inc(s.h_ready.sem, 1)
                with dve.Fori(0, B) as i:
                    norm_dve(dve, s, n, i, net.bank[0][:, 0:L].rearrange("p (t d) -> p t d", d=D))
                    dve.nop().then_inc(s.z_used.sem, 1)
    close_stage(nc, net.pool)


def plan(units, ends):
    steps = [units[k:k + 4] for k in range(0, len(units), 4)]
    per_step = [us[0][3] for us in steps]
    return group(units=units, steps=steps, groups=per_step, ends=ends, n=len(units), ns=len(steps),
                           ng=sum(per_step), first=[sum(per_step[:j]) for j in range(len(steps))],
                           span=lambda o: (0 if o == 0 else ends[o - 1] + 1, ends[o]),
                           spec=f"settled:0 scored:{len(units)} masked:{len(units)} exped:{len(units)} neg_max:{len(steps)} "
                                f"turned:{sum(per_step)} probs:{sum(per_step)} mixed:{len(steps)} "
                                f"row_scale:{len(ends)} o_ready:{len(ends)} oT_ps:{len(ends)} oT_ready:{len(ends)} ")


RING = 8


def attend_buffers(ctx, nc, net, pl, scale_by):
    sb = lambda name, shape: ctx.enter_context(nc.sbuf_tensor(net.name(name), shape, F32))
    return group(pl=pl, scale_by=scale_by, prob=sb("prob", [P, RING, L]), top=sb("top", [P, pl.n]), nm=sb("neg_max", [P, pl.n]),
                           total=sb("total", [P, pl.n]), scale=sb("row_scale", [P, pl.n]), probT=sb("probT", [P, 2, 512]))


def attend_pe(pe, s, a, net, i, q_at, k_at, v_at, o_at, first_scores, out):
    pl = a.pl
    for j in range(pl.ns + 3):
        if j < pl.ns:
            first_scores(j)
            for c, (t, h, kb, nkb) in enumerate(pl.steps[j]):
                u = 4 * j + c
                if j > 0:
                    pe.wait_ge(s.masked.sem, s.masked.at(i, u - 3))
                pe.matmul(net.bank[c][:, 0:nkb * P], q_at(t, h), k_at(h, kb, nkb), start=True, stop=True)\
                    .then_inc(s.scored.sem, 1)
        if 0 < j <= pl.ns:
            us = pl.steps[j - 1]
            per = 4 // us[0][3]
            for g in range(us[0][3]):
                n = pl.first[j - 1] + g
                pe.wait_ge(s.exped.sem, s.exped.at(i, 4 * (j - 1) + per * (g + 1)))
                if n >= 2:
                    pe.wait_ge(s.probs.sem, s.probs.at(i, n - 1))
                for c in range(per * g, per * (g + 1)):
                    for k in range(us[c][3]):
                        slot = (c - per * g) * us[c][3] + k
                        last = pe.transpose(net.bank[4 + n % 2][:, slot * P:(slot + 1) * P],
                                            a.prob[:, (4 * (j - 1) + c) % RING, k * P:(k + 1) * P], net.tab("ident"))
                last.then_inc(s.turned.sem, 1)
        if 2 <= j < pl.ns + 2:
            us = pl.steps[j - 2]
            per = 4 // us[0][3]
            for o in range(len(pl.ends)):
                if o and j - 2 == pl.span(o)[0]:
                    pe.wait_ge(s.o_ready.sem, s.o_ready.at(i, o))
            for c, (t, h, kb, nkb) in enumerate(us):
                n = pl.first[j - 2] + c // per
                if c % per == 0:
                    pe.wait_ge(s.probs.sem, s.probs.at(i, n + 1))
                for k in range(nkb):
                    slot = (c % per) * nkb + k
                    last = pe.matmul(o_at(h), a.probT[:, n % 2, slot * P:(slot + 1) * P], v_at(kb + k, h),
                                     start=(k == 0), stop=(k == nkb - 1))
                if c % per == per - 1 and c < 3:
                    last.then_inc(s.probs_used.sem, 1)
            last.then_inc(s.mixed.sem, 1)
        for o, end in enumerate(pl.ends):
            if end == j - 3:
                out(o)


def attend_dve(dve, s, a, net, i, mask_at, normalise):
    pl = a.pl
    for j in range(pl.ns + 3):
        if j < pl.ns:
            if j == 0:
                dve.wait_ge(s.turned.sem, s.turned.at(i, 0))
                dve.wait_ge(s.exped.sem, s.exped.at(i, 0))
            if 4 * j >= RING:
                jj = j - RING // 4
                dve.wait_ge(s.turned.sem, s.turned.at(i, pl.first[jj] + pl.groups[jj]))
            dve.wait_ge(s.scored.sem, s.scored.at(i, 4 * j + 4))
            settle(dve, s)
            for c, (t, h, kb, nkb) in enumerate(pl.steps[j]):
                u = 4 * j + c
                dve.tensor_tensor_reduce(a.prob[:, u % RING, 0:nkb * P], net.bank[c][:, 0:nkb * P], mask_at(t, h, nkb),
                                         1.0, -3e38, ALU.add, ALU.max, a.top[:, u:u + 1]).then_inc(s.masked.sem, 1)
            dve.wait_ge(s.masked.sem, s.masked.at(i, 4 * j + 4))
            dve.tensor_scalar(a.nm[:, 4 * j:4 * j + 4], a.top[:, 4 * j:4 * j + 4], -a.scale_by, None, ALU.mult)\
                .then_inc(s.neg_max.sem, 1)
        for o, end in enumerate(pl.ends):
            if end == j - 2:
                lo, hi = 4 * pl.span(o)[0], 4 * end + 4
                dve.wait_ge(s.exped.sem, s.exped.at(i, hi))
                dve.reciprocal(a.scale[:, lo:hi], a.total[:, lo:hi]).then_inc(s.row_scale.sem, 1)
                dve.wait_ge(s.mixed.sem, s.mixed.at(i, end + 1))
                dve.wait_ge(s.row_scale.sem, s.row_scale.at(i, o + 1))
                normalise(o, a.scale[:, lo:hi])


def attend_act(act, s, a, net, i, out):
    pl = a.pl
    for j in range(pl.ns + 4):
        if j < pl.ns:
            act.wait_ge(s.neg_max.sem, s.neg_max.at(i, j + 1))
            for c, (t, h, kb, nkb) in enumerate(pl.steps[j]):
                u = 4 * j + c
                row = a.prob[:, u % RING, 0:nkb * P]
                act.activation(row, row, ACT.Exp, bias=a.nm[:, u:u + 1], scale=a.scale_by,
                               accum_out=a.total[:, u:u + 1]).then_inc(s.exped.sem, 1)
        if 0 < j <= pl.ns:
            for g in range(pl.groups[j - 1]):
                n = pl.first[j - 1] + g
                act.wait_ge(s.turned.sem, s.turned.at(i, n + 1))
                if n >= 2:
                    jj = max(k for k in range(pl.ns) if pl.first[k] <= n - 2)
                    if pl.first[jj] + pl.groups[jj] - 1 == n - 2:
                        act.wait_ge(s.mixed.sem, s.mixed.at(i, jj + 1))
                    else:
                        act.wait_ge(s.probs_used.sem, s.probs_used.at(i, sum(x - 1 for x in pl.groups[:jj]) + 1))
                act.activation(a.probT[:, n % 2, :], net.bank[4 + n % 2][:, :], ACT.Copy).then_inc(s.probs.sem, 1)
        for o, end in enumerate(pl.ends):
            if end == j - 3:
                out(o)


def stage_local_attention(nc, net, io, l, src, dst):
    with ExitStack() as ctx:
        sb = lambda name, shape: ctx.enter_context(nc.sbuf_tensor(net.name(name), shape, F32))
        pl = plan([(t, h, 0, t + 1) for t in range(TPB) for h in range(LH)], [1, 3])
        a = attend_buffers(ctx, nc, net, pl, QK_SCALE)
        hT = sb("hT", [P, L])
        qsb = sb("scales", [P, 2, LDH])
        rope = sb("rope", [P, TPB, 4, LDH])
        NQ = 2 * TPB
        sq, qn, r1, r2 = (sb(n, [P, 2, INNER]) for n in ("squares", "qk_unit", "rot_cos", "rot_sin"))
        ss, rn = sb("sum_sq", [P, NQ, LH]), sb("inv_norm", [P, NQ, LH])
        qT, kT, oT = (sb(n, [P, INNER // P, L]) for n in ("qT", "kT", "oT"))
        v, o = sb("v", [P, TPB, INNER]), sb("o", [P, TPB, INNER])
        s = open_stage(nc, net.pool, "h_clear:1 rope_ready:1 h_built:1 qkv:6 squared:4 sums:4 clipped:4 inv:4 unit:4 cosd:4 sind:4 roped:4 "
                       "qkT_ps:4 qkT:4 v_ready:2 y_ready:1 x_updated:1 probs_used:2 " + pl.spec)
        ident = net.tab("ident")
        tab4 = net.tab("rope").rearrange("p (t c d) -> p t c d", t=TPB, c=4)
        masks = net.tab("lmask").rearrange("p (t k) -> p t k", t=TPB)
        heads = lambda ap: ap.rearrange("p (h d) -> p h d", d=LDH)
        over_heads = lambda ap: ap.unsqueeze(1).to_broadcast([P, LH, ap.shape[1]])
        HF = LDH // 2
        with nc.Block() as block:
            @block.sync
            def _(sp):
                for j, nm in enumerate(("L0_ffn_q_scale", "L0_ffn_k_scale")):
                    sp.dma_start(qsb[:, j, :], io[nm][l].partition_broadcast(P)).then_inc(net.ld_s, 16)
                net.ld_s_count += 32

            @block.gpsimd
            def _(pool):
                pool.memset(hT[:, :], 0.0).then_inc(s.h_clear.sem, 1)
                pool.wait_ge(net.ld_s, net.ld_s_count)
                for j in range(2):
                    qb = lambda x: x.unsqueeze(1).to_broadcast([P, TPB, x.shape[1]])
                    pool.tensor_tensor(rope[:, :, 2 * j, :], tab4[:, :, 2 * j, :], qb(qsb[:, j, :]), ALU.mult)
                    pool.tensor_tensor(rope[:, :, 2 * j + 1, 0:HF], tab4[:, :, 2 * j + 1, 0:HF], qb(qsb[:, j, HF:LDH]), ALU.mult)
                    last = pool.tensor_tensor(rope[:, :, 2 * j + 1, HF:LDH], tab4[:, :, 2 * j + 1, HF:LDH], qb(qsb[:, j, 0:HF]), ALU.mult)
                last.then_inc(s.rope_ready.sem, 1)
                pool.wait_ge(s.rope_ready.sem, s.rope_ready.at(0, 1))
                with pool.Fori(0, B) as i:
                    for m in range(NQ):
                        t, j = m // 2, m % 2
                        pool.wait_ge(s.clipped.sem, s.clipped.at(i, m + 1))
                        pool.tensor_tensor(rn[:, m, :], ss[:, m, :], net.neghalf[:, 0:LH], ALU.pow).then_inc(s.inv.sem, 1)
                        pool.wait_ge(s.unit.sem, s.unit.at(i, m + 1))
                        if m >= 2:
                            pool.wait_ge(s.roped.sem, s.roped.at(i, m - 1))
                        src_, dst_ = heads(qn[:, m % 2, :]), heads(r2[:, m % 2, :])
                        pool.tensor_tensor(dst_[:, :, 0:HF], src_[:, :, HF:LDH], over_heads(rope[:, t, 2 * j + 1, 0:HF]), ALU.mult)
                        pool.tensor_tensor(dst_[:, :, HF:LDH], src_[:, :, 0:HF], over_heads(rope[:, t, 2 * j + 1, HF:LDH]), ALU.mult)\
                            .then_inc(s.sind.sem, 1)

            @block.tensor
            def _(pe):
                pe.wait_ge(net.ld_w, net.w_ready)
                w = net.wqkv[l]
                with pe.Fori(0, B) as i:
                    pe.wait_ge(s.h_built.sem, s.h_built.at(i, 1))
                    pe.wait_ge(s.masked.sem, s.masked.at(i, 0))
                    pe.wait_ge(s.probs.sem, s.probs.at(i, 0))
                    for t in range(TPB):
                        for part in range(3):
                            pe.matmul(net.bank[3 * t + part][:, :], hT[:, t * P:(t + 1) * P], w[:, part * INNER:(part + 1) * INNER],
                                      start=True, stop=True).then_inc(s.qkv.sem, 1)
                    pe.wait_ge(s.x_updated.sem, s.x_updated.at(i, 0))
                    for m in range(NQ):
                        pe.wait_ge(s.roped.sem, s.roped.at(i, m + 1))
                        if m >= 2:
                            pe.wait_ge(s.qkT.sem, s.qkT.at(i, m - 1))
                        for c in range(INNER // P):
                            last = pe.transpose(net.bank[6 + m % 2][:, c * P:(c + 1) * P], r1[:, m % 2, c * P:(c + 1) * P], ident)
                        last.then_inc(s.qkT_ps.sem, 1)

                    def first_scores(j):
                        if j == 0:
                            pe.wait_ge(s.qkT.sem, s.qkT.at(i, 4))
                            pe.wait_ge(s.v_ready.sem, s.v_ready.at(i, 2))

                    def out(o_):
                        pe.wait_ge(s.o_ready.sem, s.o_ready.at(i, o_ + 1))
                        if o_:
                            pe.wait_ge(s.oT_ready.sem, s.oT_ready.at(i, o_))
                        for c in range(INNER // P):
                            last = pe.transpose(net.bank[6][:, c * P:(c + 1) * P], o[:, o_, c * P:(c + 1) * P], ident)
                        last.then_inc(s.oT_ps.sem, 1)

                    row = lambda h: slice(LDH * (h % 2), LDH * (h % 2) + LDH)
                    attend_pe(pe, s, a, net, i,
                              lambda t, h: qT[row(h), h // 2, t * P:(t + 1) * P],
                              lambda h, kb, nkb: kT[row(h), h // 2, kb * P:(kb + nkb) * P],
                              lambda kb, h: v[:, kb, h * LDH:(h + 1) * LDH],
                              lambda h: net.bank[7][:, h * LDH:(h + 1) * LDH], first_scores, out)
                    pe.wait_ge(s.oT_ready.sem, s.oT_ready.at(i, 2))
                    for c in range(INNER // P):
                        last = pe.matmul(net.bank[6][:, 0:L], net.wo[l][:, c, :], oT[:, c, :], start=(c == 0), stop=(c == INNER // P - 1))
                    last.then_inc(s.y_ready.sem, 1)

            @block.scalar
            def _(act):
                act.wait_ge(s.h_clear.sem, s.h_clear.at(0, 1))
                with act.Fori(0, B) as i:
                    act.wait_ge(s.qkv.sem, s.qkv.at(i, 0))
                    act.activation(hT[0:D // 2, :], src[0:D // 2, bass.ds(i * L, L)], ACT.Copy)
                    act.activation(hT[D // 2:D, 1:L], src[D // 2:D, bass.ds(i * L, L - 1)], ACT.Copy).then_inc(s.h_built.sem, 1)
                    for m in range(NQ):
                        t, j = m // 2, m % 2
                        act.wait_ge(s.qkv.sem, s.qkv.at(i, 3 * t + j + 1))
                        if m >= 2:
                            act.wait_ge(s.sums.sem, s.sums.at(i, m - 1))
                        act.activation(sq[:, m % 2, :], net.bank[3 * t + j][:, :], ACT.Square).then_inc(s.squared.sem, 1)
                        if j == 1:
                            act.wait_ge(s.qkv.sem, s.qkv.at(i, 3 * t + 3))
                            act.activation(v[:, t, :], net.bank[3 * t + 2][:, :], ACT.Copy).then_inc(s.v_ready.sem, 1)
                    for m in range(NQ):
                        t, j = m // 2, m % 2
                        act.wait_ge(s.qkT_ps.sem, s.qkT_ps.at(i, m + 1))
                        act.activation((qT, kT)[j][:, :, t * P:(t + 1) * P],
                                       net.bank[6 + m % 2][:, :].rearrange("p (c t) -> p c t", t=P), ACT.Copy).then_inc(s.qkT.sem, 1)

                    def out(o_):
                        act.wait_ge(s.oT_ps.sem, s.oT_ps.at(i, o_ + 1))
                        act.activation(oT[:, :, o_ * P:(o_ + 1) * P], net.bank[6][:, :].rearrange("p (c t) -> p c t", t=P), ACT.Copy)\
                            .then_inc(s.oT_ready.sem, 1)
                    attend_act(act, s, a, net, i, out)

            @block.vector
            def _(dve):
                dve.wait_ge(s.rope_ready.sem, s.rope_ready.at(0, 1))
                with dve.Fori(0, B) as i:
                    for m in range(NQ):
                        t, j = m // 2, m % 2
                        dve.wait_ge(s.squared.sem, s.squared.at(i, m + 1))
                        dve.tensor_reduce(ss[:, m, :], heads(sq[:, m % 2, :]), AX.X, ALU.add).then_inc(s.sums.sem, 1)
                        dve.wait_ge(s.sums.sem, s.sums.at(i, m + 1))
                        dve.tensor_scalar(ss[:, m, :], ss[:, m, :], 1e-24, None, ALU.max).then_inc(s.clipped.sem, 1)
                        dve.wait_ge(s.inv.sem, s.inv.at(i, m + 1))
                        if m >= 2:
                            dve.wait_ge(s.sind.sem, s.sind.at(i, m - 1))
                        else:
                            dve.wait_ge(s.sind.sem, s.sind.at(i, 0))
                        dve.tensor_tensor(heads(qn[:, m % 2, :]), heads(net.bank[3 * t + j][:, :]),
                                          rn[:, m, :].unsqueeze(2).to_broadcast([P, LH, LDH]), ALU.mult).then_inc(s.unit.sem, 1)
                        dve.wait_ge(s.unit.sem, s.unit.at(i, m + 1))
                        if m >= 2:
                            dve.wait_ge(s.qkT_ps.sem, s.qkT_ps.at(i, m - 1))
                        else:
                            dve.wait_ge(s.qkT_ps.sem, s.qkT_ps.at(i, 0))
                        dve.tensor_tensor(heads(r1[:, m % 2, :]), heads(qn[:, m % 2, :]), over_heads(rope[:, t, 2 * j, :]), ALU.mult)\
                            .then_inc(s.cosd.sem, 1)
                        dve.wait_ge(s.cosd.sem, s.cosd.at(i, m + 1))
                        dve.wait_ge(s.sind.sem, s.sind.at(i, m + 1))
                        dve.tensor_tensor(r1[:, m % 2, :], r1[:, m % 2, :], r2[:, m % 2, :], ALU.add).then_inc(s.roped.sem, 1)

                    def normalise(o_, rs):
                        dve.tensor_tensor(heads(o[:, o_, :]), heads(net.bank[7][:, :]),
                                          rs.unsqueeze(2).to_broadcast([P, LH, LDH]), ALU.mult).then_inc(s.o_ready.sem, 1)
                    attend_dve(dve, s, a, net, i, lambda t, h, nkb: masks[:, t, 0:nkb * P], normalise)
                    dve.wait_ge(s.y_ready.sem, s.y_ready.at(i, 1))
                    dve.tensor_tensor(dst[:, bass.ds(i * L, L)], net.bank[6][:, 0:L], src[:, bass.ds(i * L, L)], ALU.add)\
                        .then_inc(s.x_updated.sem, 1)
    close_stage(nc, net.pool)


def part(s, prefix):
    return group(**{k[len(prefix):]: v for k, v in s._asdict().items() if k.startswith(prefix)})


def prefixed(prefix, spec):
    return " ".join(prefix + w for w in spec.split()) + " "


def stage_gated_mlp(nc, net, io, l, x, final):
    with ExitStack() as ctx:
        sb = lambda name, shape: ctx.enter_context(nc.sbuf_tensor(net.name(name), shape, F32))
        n = norm_buffers(ctx, nc, net)
        nf = norm_buffers(ctx, nc, net)
        hT, hn, z, z1 = sb("hT", [P, L]), sb("hn", [P, L]), sb("z", [P, L]), sb("z1", [P, L])
        gate, u = sb("gate", [P, len(HCH), L]), sb("u", [P, len(HCH), L])
        s = open_stage(nc, net.pool, "h_clear:1 h_built:1 ag_ps:6 gelu:3 u_ready:3 mlp_ps:1 sum1:1 sum2:1 "
                       + NORM + " " + prefixed("f_", NORM))
        f = part(s, "f_")
        bank = net.bank
        sm = net.small
        with nc.Block() as block:
            @block.gpsimd
            def _(pool):
                pool.memset(hT[:, :], 0.0).then_inc(s.h_clear.sem, 1)
                with pool.Fori(0, B) as i:
                    norm_pool(pool, s, n, i)
                    if final:
                        norm_pool(pool, f, nf, i)

            @block.scalar
            def _(act):
                act.wait_ge(net.ld_w, net.w_ready)
                act.wait_ge(s.h_clear.sem, s.h_clear.at(0, 1))
                with act.Fori(0, B) as i:
                    act.wait_ge(s.y_ready.sem, s.y_ready.at(i, 0))
                    act.activation(hT[0:D // 2, :], x[0:D // 2, bass.ds(i * L, L)], ACT.Copy)
                    act.activation(hT[D // 2:D, 1:L], x[D // 2:D, bass.ds(i * L, L - 1)], ACT.Copy).then_inc(s.h_built.sem, 1)
                    norm_act(act, s, i, bank[1][:, 0:L], hn[:, :], sm("ln_g", l), sm("ln_b", l))
                    for c, (at, w) in enumerate(HCH):
                        act.wait_ge(s.ag_ps.sem, s.ag_ps.at(i, 2 * c + 2))
                        act.wait_ge(s.u_ready.sem, s.u_ready.at(i, 0))
                        act.activation(gate[0:w, c, :], bank[5 + c][0:w, 0:L], ACT.Gelu, bias=sm("b1g", l)[0:w, c:c + 1])\
                            .then_inc(s.gelu.sem, 1)
                    if final:
                        norm_act(act, f, i, bank[1][:, 0:L], net.xT[:, bass.ds(i * L, L)])

            @block.tensor
            def _(pe):
                pe.wait_ge(net.ld_w, net.w_ready)
                with pe.Fori(0, B) as i:
                    pe.wait_ge(s.h_built.sem, s.h_built.at(i, 1))
                    if final:
                        pe.wait_ge(f.xn_ready.sem, f.xn_ready.at(i, 0))
                        pe.wait_ge(f.x_updated.sem, f.x_updated.at(i, 0))
                    for t in range(TPB):
                        last = pe.transpose(bank[0][:, t * P:(t + 1) * P], hT[:, t * P:(t + 1) * P], net.tab("ident"))
                    last.then_inc(s.y_ready.sem, 1)
                    norm_pe(pe, s, n, i, bank[1][:, 0:L])
                    pe.wait_ge(s.x_updated.sem, s.x_updated.at(i, 1))
                    pe.wait_ge(s.sum1.sem, s.sum1.at(i, 0))
                    for c, (at, w) in enumerate(HCH):
                        pe.matmul(bank[2 + c][0:w, 0:L], net.w1[l][:, at:at + w], hn[:, :], start=True, stop=True).then_inc(s.ag_ps.sem, 1)
                        pe.matmul(bank[5 + c][0:w, 0:L], net.w1[l][:, HID + at:HID + at + w], hn[:, :], start=True, stop=True)\
                            .then_inc(s.ag_ps.sem, 1)
                    for c, (at, w) in enumerate(HCH):
                        pe.wait_ge(s.u_ready.sem, s.u_ready.at(i, 3))
                        last = pe.matmul(bank[2][:, 0:L], net.w2[l][0:w, c, :], u[0:w, c, :], start=(c == 0), stop=(c == len(HCH) - 1))
                    last.then_inc(s.mlp_ps.sem, 1)
                    if final:
                        pe.wait_ge(s.sum2.sem, s.sum2.at(i, 1))
                        for t in range(TPB):
                            last = pe.transpose(bank[0][:, t * P:(t + 1) * P], z[:, t * P:(t + 1) * P], net.tab("ident"))
                        last.then_inc(f.y_ready.sem, 1)
                        norm_pe(pe, f, nf, i, bank[1][:, 0:L])

            @block.vector
            def _(dve):
                dve.wait_ge(net.ld_w, net.w_ready)
                y = bank[0][:, 0:L].rearrange("p (t d) -> p t d", d=D)
                with dve.Fori(0, B) as i:
                    norm_dve(dve, s, n, i, y)
                    for c, (at, w) in enumerate(HCH):
                        dve.wait_ge(s.gelu.sem, s.gelu.at(i, c + 1))
                        dve.wait_ge(s.mlp_ps.sem, s.mlp_ps.at(i, 0))
                        dve.scalar_tensor_tensor(u[0:w, c, :], bank[2 + c][0:w, 0:L], sm("b1a", l)[0:w, c:c + 1], gate[0:w, c, :],
                                                 ALU.add, ALU.mult).then_inc(s.u_ready.sem, 1)
                    dve.wait_ge(s.mlp_ps.sem, s.mlp_ps.at(i, 1))
                    dst = z1[:, :] if final else x[:, bass.ds(i * L, L)]
                    dve.scalar_tensor_tensor(dst, bank[2][:, 0:L], sm("b2", l), x[:, bass.ds(i * L, L)], ALU.add, ALU.add)\
                        .then_inc(s.sum1.sem, 1)
                    if final:
                        dve.wait_ge(s.sum1.sem, s.sum1.at(i, 1))
                        dve.wait_ge(f.y_ready.sem, f.y_ready.at(i, 0))
                        dve.tensor_tensor(z[:, :], z1[:, :], net.xT[:, bass.ds(i * L, L)], ALU.add).then_inc(s.sum2.sem, 1)
                        norm_dve(dve, f, nf, i, y)
    close_stage(nc, net.pool)


def stage_scan_inputs(nc, net, io, xc, sz):
    with ExitStack() as ctx:
        sb = lambda name, shape: ctx.enter_context(nc.sbuf_tensor(net.name(name), shape, F32))
        PAD = NCONV - 1
        xp, acc = sb("x_padded", [P, 2, PAD + L]), sb("conv", [P, 2, L])
        s = open_stage(nc, net.pool, "clear:1 xz:4 xp_ready:2 sz_ready:2 taps:8 xc_ready:2")
        with nc.Block() as block:
            @block.gpsimd
            def _(pool):
                pool.memset(xp[:, :, :], 0.0).then_inc(s.clear.sem, 1)

            @block.tensor
            def _(pe):
                pe.wait_ge(net.ld_w, net.w_ready)
                with pe.Fori(0, B) as i:
                    for m in range(4):
                        read = s.xp_ready if m < 2 else s.sz_ready
                        pe.wait_ge(read.sem, read.at(i, 0))
                        pe.matmul(net.bank[m][:, 0:L], net.w_in[:, m * P:(m + 1) * P], net.xT[:, bass.ds(i * L, L)],
                                  start=True, stop=True).then_inc(s.xz.sem, 1)

            @block.scalar
            def _(act):
                act.wait_ge(s.clear.sem, s.clear.at(0, 1))
                with act.Fori(0, B) as i:
                    for c in range(2):
                        act.wait_ge(s.xz.sem, s.xz.at(i, c + 1))
                        act.wait_ge(s.taps.sem, s.taps.at(i, 0))
                        act.activation(xp[:, c, PAD:PAD + L], net.bank[c][:, 0:L], ACT.Copy).then_inc(s.xp_ready.sem, 1)
                    for c in range(2):
                        act.wait_ge(s.xz.sem, s.xz.at(i, c + 3))
                        act.activation(sz[:, c, bass.ds(i * L, L)], net.bank[2 + c][:, 0:L], ACT.Silu).then_inc(s.sz_ready.sem, 1)
                    for c in range(2):
                        act.wait_ge(s.taps.sem, s.taps.at(i, 4 * c + 4))
                        act.activation(xc[:, c, bass.ds(i * L, L)], acc[:, c, :], ACT.Silu).then_inc(s.xc_ready.sem, 1)

            @block.vector
            def _(dve):
                dve.wait_ge(net.ld_w, net.w_ready)
                with dve.Fori(0, B) as i:
                    dve.wait_ge(s.xc_ready.sem, s.xc_ready.at(i, 0))
                    for c in range(2):
                        dve.wait_ge(s.xp_ready.sem, s.xp_ready.at(i, c + 1))
                        for j in range(NCONV):
                            tap = net.conv_w[:, c, j:j + 1]
                            if j == 0:
                                dve.tensor_scalar(acc[:, c, :], xp[:, c, 0:L], tap, net.conv_b[:, c:c + 1], ALU.mult, ALU.add)\
                                    .then_inc(s.taps.sem, 1)
                            else:
                                dve.wait_ge(s.taps.sem, s.taps.at(i, 4 * c + j))
                                dve.scalar_tensor_tensor(acc[:, c, :], xp[:, c, j:j + L], tap, acc[:, c, :], ALU.mult, ALU.add)\
                                    .then_inc(s.taps.sem, 1)
    close_stage(nc, net.pool)


def stage_scan(nc, net, io, xc, sz):
    with ExitStack() as ctx:
        sb = lambda name, shape: ctx.enter_context(nc.sbuf_tensor(net.name(name), shape, F32))
        R = 4
        n = norm_buffers(ctx, nc, net, keep=True)
        xs, x33 = sb("xs", [P, L]), sb("x_ssm", [XP, L])
        e1, r1, delta, dx, y1, y2 = (sb(k, [P, 2, L]) for k in ("soft_tail", "step_in", "delta", "delta_x", "y1", "y2"))
        dA, dB, h, hc = (sb(k, [P, R, 2, L]) for k in ("decay", "inject", "state", "readout"))
        a_neg, a_exp = sb("a_neg", [P, 2, NS]), sb("a_exp", [P, 2, NS])
        s = open_stage(nc, net.pool, "clear:1 a_ready:1 a_exp:1 xs_ready:1 ssm_ps:1 x33:1 dt_ps:2 tail:6 top:2 delta_ready:2 dx_ready:1 "
                       f"bc_ps:{NS} decay:{2 * NS} inject:{NS} state:{NS} readout:{NS} summed:{NS} y1_ready:2 y2_ready:1 " + NORM)
        bank = net.bank
        pick = lambda k: net.tab("ident")[0:XP, 1 + k:2 + k].to_broadcast([XP, P])
        flat = lambda ap: ap.rearrange("p c t -> p (c t)")
        both = lambda ap: ap.unsqueeze(1).to_broadcast([P, 2, L])
        with nc.Block() as block:
            @block.gpsimd
            def _(pool):
                pool.memset(dA[:, :, :, :], 0.0).then_inc(s.clear.sem, 1)
                with pool.Fori(0, B) as i:
                    pool.wait_ge(s.y_ready.sem, s.y_ready.at(i, 0))
                    settle(pool, s)
                    pool.tensor_copy(xs[:, :], net.xT[:, bass.ds(i * L, L)]).then_inc(s.xs_ready.sem, 1)
                    norm_pool(pool, s, n, i)

            @block.tensor
            def _(pe):
                pe.wait_ge(net.ld_w, net.w_ready)
                with pe.Fori(0, B) as i:
                    pe.wait_ge(s.x33.sem, s.x33.at(i, 0))
                    for c in range(2):
                        last = pe.matmul(bank[0][0:XP, 0:L], net.w_xproj[:, c, :], xc[:, c, bass.ds(i * L, L)], start=(c == 0), stop=(c == 1))
                    last.then_inc(s.ssm_ps.sem, 1)
                    pe.wait_ge(s.x33.sem, s.x33.at(i, 1))
                    pe.wait_ge(s.top.sem, s.top.at(i, 0))
                    for c in range(2):
                        pe.matmul(bank[1][:, c * L:(c + 1) * L], net.w_dt[:, c * P:(c + 1) * P], x33[0:1, :], start=True, stop=True)\
                            .then_inc(s.dt_ps.sem, 1)
                    for k in range(NS + 3):
                        if k < NS:
                            if k >= R:
                                pe.wait_ge(s.readout.sem, s.readout.at(i, k - R + 1))
                            elif k == 0:
                                pe.wait_ge(s.readout.sem, s.readout.at(i, 0))
                            pe.matmul(bank[2 + k % R][:, 0:L], pick(k), x33[:, :], start=True, stop=True)
                            pe.matmul(bank[2 + k % R][:, L:2 * L], pick(NS + k), x33[:, :], start=True, stop=True).then_inc(s.bc_ps.sem, 1)
                        if k >= 3:
                            m = k - 3
                            if m == 0:
                                pe.wait_ge(s.y1_ready.sem, s.y1_ready.at(i, 0))
                            pe.wait_ge(s.readout.sem, s.readout.at(i, m + 1))
                            pe.matmul(bank[6][:, :], net.tab("ident"), flat(hc[:, m % R, :, :]), start=(m == 0), stop=(m == NS - 1))\
                                .then_inc(s.summed.sem, 1)
                    pe.wait_ge(s.y2_ready.sem, s.y2_ready.at(i, 1))
                    pe.wait_ge(s.xs_ready.sem, s.xs_ready.at(i, 1))
                    pe.wait_ge(s.x_updated.sem, s.x_updated.at(i, 0))
                    for t in range(TPB):
                        tok = slice(t * P, (t + 1) * P)
                        for c in range(2):
                            pe.matmul(bank[7][:, tok], y2[:, c, tok], net.w_out[:, c, :], start=(c == 0), stop=False)
                        last = pe.matmul(bank[7][:, tok], xs[:, tok], net.tab("ident"), start=False, stop=True)
                    last.then_inc(s.y_ready.sem, 1)
                    norm_pe(pe, s, n, i, bank[7][:, L:2 * L])

            @block.scalar
            def _(act):
                act.wait_ge(net.ld_w, net.w_ready)
                act.wait_ge(s.clear.sem, s.clear.at(0, 1))
                act.activation(a_exp[:, :, :], net.a_log[:, :, :], ACT.Exp).then_inc(s.a_exp.sem, 1)
                act.wait_ge(s.a_ready.sem, s.a_ready.at(0, 1))
                with act.Fori(0, B) as i:
                    act.wait_ge(s.ssm_ps.sem, s.ssm_ps.at(i, 1))
                    act.wait_ge(s.bc_ps.sem, s.bc_ps.at(i, 0))
                    act.activation(x33[:, :], bank[0][0:XP, 0:L], ACT.Copy).then_inc(s.x33.sem, 1)
                    act.wait_ge(s.delta_ready.sem, s.delta_ready.at(i, 0))
                    for c in range(2):
                        act.wait_ge(s.top.sem, s.top.at(i, c + 1))
                        act.activation(e1[:, c, :], r1[:, c, :], ACT.Abs).then_inc(s.tail.sem, 1)
                    for c in range(2):
                        act.wait_ge(s.tail.sem, s.tail.at(i, c + 1))
                        act.activation(e1[:, c, :], e1[:, c, :], ACT.Exp, scale=-1.0).then_inc(s.tail.sem, 1)
                    for c in range(2):
                        act.wait_ge(s.tail.sem, s.tail.at(i, c + 3))
                        act.activation(e1[:, c, :], e1[:, c, :], ACT.Ln, bias=1.0).then_inc(s.tail.sem, 1)
                    act.wait_ge(s.delta_ready.sem, s.delta_ready.at(i, 2))
                    for k in range(NS):
                        if k >= R:
                            act.wait_ge(s.state.sem, s.state.at(i, k - R + 1))
                        for c in range(2):
                            act.activation(dA[:, k % R, c, 1:L], delta[:, c, 1:L], ACT.Exp, scale=a_neg[:, c, k:k + 1]).then_inc(s.decay.sem, 1)
                    norm_act(act, s, i, bank[7][:, L:2 * L], net.xT[:, bass.ds(i * L, L)])

            @block.vector
            def _(dve):
                dve.wait_ge(net.ld_w, net.w_ready)
                dve.wait_ge(s.a_exp.sem, s.a_exp.at(0, 1))
                dve.tensor_scalar(a_neg[:, :, :], a_exp[:, :, :], -1.0, None, ALU.mult).then_inc(s.a_ready.sem, 1)
                with dve.Fori(0, B) as i:
                    xcb = xc[:, :, bass.ds(i * L, L)]
                    dve.wait_ge(s.decay.sem, s.decay.at(i, 0))
                    dve.wait_ge(s.dt_ps.sem, s.dt_ps.at(i, 2))
                    for c in range(2):
                        dve.tensor_scalar(r1[:, c, :], bank[1][:, c * L:(c + 1) * L], net.b_dt[:, c:c + 1], None, ALU.add)\
                            .then_inc(s.top.sem, 1)
                    for c in range(2):
                        dve.wait_ge(s.tail.sem, s.tail.at(i, c + 5))
                        dve.scalar_tensor_tensor(delta[:, c, :], r1[:, c, :], 0.0, e1[:, c, :], ALU.max, ALU.add).then_inc(s.delta_ready.sem, 1)
                    dve.wait_ge(s.delta_ready.sem, s.delta_ready.at(i, 2))
                    dve.tensor_tensor(dx[:, :, :], delta[:, :, :], xcb, ALU.mult).then_inc(s.dx_ready.sem, 1)
                    dve.wait_ge(s.dx_ready.sem, s.dx_ready.at(i, 1))
                    for k in range(NS + 2):
                        if k < NS:
                            dve.wait_ge(s.bc_ps.sem, s.bc_ps.at(i, k + 1))
                            dve.tensor_tensor(dB[:, k % R, :, :], dx[:, :, :], both(bank[2 + k % R][:, 0:L]), ALU.mult).then_inc(s.inject.sem, 1)
                        if 1 <= k <= NS:
                            m = k - 1
                            dve.wait_ge(s.inject.sem, s.inject.at(i, m + 1))
                            dve.wait_ge(s.decay.sem, s.decay.at(i, 2 * m + 2))
                            dve.tensor_tensor_scan(flat(h[:, m % R, :, :]), flat(dA[:, m % R, :, :]), flat(dB[:, m % R, :, :]), 0.0,
                                                   ALU.mult, ALU.add).then_inc(s.state.sem, 1)
                        if k >= 2:
                            m = k - 2
                            dve.wait_ge(s.state.sem, s.state.at(i, m + 1))
                            if m >= R:
                                dve.wait_ge(s.summed.sem, s.summed.at(i, m - R + 1))
                            else:
                                dve.wait_ge(s.summed.sem, s.summed.at(i, 0))
                            dve.tensor_tensor(hc[:, m % R, :, :], h[:, m % R, :, :], both(bank[2 + m % R][:, L:2 * L]), ALU.mult)\
                                .then_inc(s.readout.sem, 1)
                    dve.wait_ge(s.summed.sem, s.summed.at(i, NS))
                    for c in range(2):
                        dve.scalar_tensor_tensor(y1[:, c, :], xc[:, c, bass.ds(i * L, L)], net.d_par[:, c:c + 1], bank[6][:, c * L:(c + 1) * L],
                                                 ALU.mult, ALU.add).then_inc(s.y1_ready.sem, 1)
                    dve.wait_ge(s.y1_ready.sem, s.y1_ready.at(i, 2))
                    dve.wait_ge(s.y_ready.sem, s.y_ready.at(i, 0))
                    dve.tensor_tensor(y2[:, :, :], y1[:, :, :], sz[:, :, bass.ds(i * L, L)], ALU.mult).then_inc(s.y2_ready.sem, 1)
                    norm_dve(dve, s, n, i, bank[7][:, 0:L].rearrange("p (t d) -> p t d", d=D))
    close_stage(nc, net.pool)


def choose_first(dve, link, probs, iota, best, eq, index, hot, n):
    wide = lambda ap: ap.unsqueeze(2).to_broadcast([P, NT, n])
    link(dve.tensor_reduce(best, probs, AX.X, ALU.max))
    link(dve.tensor_tensor(eq, probs, wide(best), ALU.is_ge))
    link(dve.tensor_tensor(eq, eq, iota, ALU.mult))
    link(dve.tensor_reduce(index, eq, AX.X, ALU.min))
    link(dve.tensor_tensor(hot, iota, wide(index), ALU.is_equal))


def running_count(dve, link, net, pre, within, totals, n):
    link(dve.memset(pre[:, 0, :], 0.0))
    for t in range(1, NT):
        link(dve.tensor_tensor(pre[:, t, :], pre[:, t - 1, :], totals[:, t - 1, :], ALU.add))
    link(dve.tensor_tensor(pre[:, :, :], pre[:, :, :], within, ALU.add))


def slots_of(dve, link, b, pre, hot, index, trash, capacity, scatter, gather, accepted):
    link(dve.tensor_tensor(b.tmp, pre, hot, ALU.mult))
    link(dve.tensor_reduce(b.pos, b.tmp, AX.X, ALU.add))
    link(dve.tensor_scalar(accepted, b.pos, float(capacity), None, ALU.is_le))
    link(dve.scalar_tensor_tensor(b.slot, index, float(capacity), b.pos, ALU.mult, ALU.add))
    link(dve.tensor_scalar(b.slot, b.slot, float(64 * capacity - 1), None, ALU.add))
    link(dve.tensor_tensor(b.kept, b.slot, accepted, ALU.mult))
    link(dve.tensor_copy(gather, b.kept))
    link(dve.tensor_tensor(b.slot, b.slot, trash, ALU.subtract))
    link(dve.tensor_tensor(b.slot, b.slot, accepted, ALU.mult))
    link(dve.tensor_tensor(b.slot, b.slot, trash, ALU.add))
    link(dve.tensor_copy(scatter, b.slot))


def stage_switch_experts(nc, net, io):
    with ExitStack() as ctx:
        sb = lambda name, shape, dt=F32: ctx.enter_context(nc.sbuf_tensor(net.name(name), shape, dt))
        n = norm_buffers(ctx, nc, net, in_psum=False)
        prob, eq, hot, pre = (sb(k, [P, NT, E1]) for k in ("prob", "equal", "hot", "pre"))
        top, tot, inv, gate, index, acc, pos, slot, kept = (sb(k, [P, NT]) for k in (
            "top", "total", "inv", "gate", "index", "accepted", "pos", "slot", "kept"))
        scatter, gather = sb("scatter", [P, NT], I32), sb("gather", [P, NT], I32)
        KT = SLOTS // P
        rows, rowsT = sb("rows", [P, KT, D]), sb("rowsT", [P, SLOTS])
        act_g, hid = sb("act_g", [P, 2, 4 * C1]), sb("hid", [P, 2, 4 * C1])
        y, yg = sb("y", [P, E1, D]), sb("y_token", [P, NT, D])
        STEPS = E1 // 4
        s = open_stage(nc, net.pool, f"v:80 logits:1 shifted:1 exp:1 hot:1 counts:1 slots:1 rowsT_ps:5 rowsT:5 g_ps:{STEPS} u_ps:{STEPS} "
                       f"silu:{STEPS} hid:{STEPS} y_ps:{STEPS} y_sb:{STEPS} combined:{NT + 1} " + NORM)
        bank = net.bank
        b3 = lambda k: bank[k][:, :].rearrange("p (t e) -> p t e", e=E1)
        wide = lambda ap: ap.unsqueeze(2).to_broadcast([P, NT, E1])
        iota = net.tab("iota32").unsqueeze(1).to_broadcast([P, NT, E1])
        moved, stored, fetched = net.moved, net.stored, net.fetched
        with nc.Block() as block:
            def down(pe, j):
                pe.wait_ge(s.hid.sem, s.hid.at(0, j + 1))
                if j >= 2:
                    pe.wait_ge(s.y_sb.sem, s.y_sb.at(0, j - 1))
                for k in range(4):
                    e = 4 * j + k
                    last = pe.matmul(bank[4 + j % 2][0:C1, k * P:(k + 1) * P], hid[:, j % 2, k * C1:(k + 1) * C1], net.moe_w[2][:, e, :], start=True, stop=True)
                last.then_inc(s.y_ps.sem, 1)

            @block.tensor
            def _(pe):
                pe.wait_ge(net.ld_w, net.w_ready)
                for t in range(NT):
                    last = pe.matmul(bank[0][:, t * E1:(t + 1) * E1], net.xT[:, t * P:(t + 1) * P], net.w_router[:, :], start=True, stop=True)
                last.then_inc(s.logits.sem, 1)
                pe.wait_ge(s.hot.sem, s.hot.at(0, 1))
                flat = hot[:, :, :].rearrange("p t e -> p (t e)")
                pe.matmul(bank[1][:, :], net.tab("tri"), flat, start=True, stop=True)
                pe.matmul(bank[2][:, :], net.tab("ones"), flat, start=True, stop=True).then_inc(s.counts.sem, 1)
                pe.wait_ge(net.rows_in, 16)
                for g in range(KT // 4):
                    if g == 1:
                        pe.wait_ge(s.slots.sem, s.slots.at(0, 1))
                    for k in range(4):
                        last = pe.transpose(bank[g][:, k * P:(k + 1) * P], rows[:, 4 * g + k, :], net.tab("ident"))
                    last.then_inc(s.rowsT_ps.sem, 1)
                pe.wait_ge(net.ld_moe, 16 * 3)
                for j in range(STEPS):
                    for w, ps, done in ((net.moe_w[0], 0, s.g_ps), (net.moe_w[1], 2, s.u_ps)):
                        if j == 0:
                            pe.wait_ge(s.rowsT.sem, s.rowsT.at(0, 5))
                        if j >= 2:
                            pe.wait_ge(s.hid.sem, s.hid.at(0, j - 1))
                        for k in range(4):
                            e = 4 * j + k
                            last = pe.matmul(bank[ps + j % 2][:, k * C1:(k + 1) * C1], w[:, e, :], rowsT[:, e * C1:(e + 1) * C1], start=True, stop=True)
                        last.then_inc(done.sem, 1)
                    if j >= 1:
                        down(pe, j - 1)
                down(pe, STEPS - 1)
                with pe.Fori(0, B) as i:
                    pe.wait_ge(s.x_updated.sem, s.x_updated.at(i, 0))
                    norm_pe(pe, s, n, i, bank[6][:, 0:L])

            def copy_y(act, j):
                act.wait_ge(s.y_ps.sem, s.y_ps.at(0, j + 1))
                act.activation(y[0:C1, 4 * j:4 * j + 4, :], bank[4 + j % 2][0:C1, :].rearrange("p (k d) -> p k d", d=D), ACT.Copy).then_inc(s.y_sb.sem, 1)

            @block.scalar
            def _(act):
                act.wait_ge(s.shifted.sem, s.shifted.at(0, 1))
                act.activation(prob[:, :, :], prob[:, :, :], ACT.Exp).then_inc(s.exp.sem, 1)
                for g in range(KT // 4):
                    act.wait_ge(s.rowsT_ps.sem, s.rowsT_ps.at(0, g + 1))
                    act.activation(rowsT[:, g * 512:(g + 1) * 512], bank[g][:, :], ACT.Copy).then_inc(s.rowsT.sem, 1)
                for j in range(STEPS):
                    act.wait_ge(s.g_ps.sem, s.g_ps.at(0, j + 1))
                    if j >= 2:
                        act.wait_ge(s.hid.sem, s.hid.at(0, j - 1))
                    act.activation(act_g[:, j % 2, :], bank[j % 2][:, 0:4 * C1], ACT.Silu).then_inc(s.silu.sem, 1)
                    if j >= 1:
                        copy_y(act, j - 1)
                copy_y(act, STEPS - 1)
                with act.Fori(0, B) as i:
                    norm_act(act, s, i, bank[6][:, 0:L], net.xT[:, bass.ds(i * L, L)])

            @block.vector
            def _(dve):
                count = [0]

                def link(ins):
                    count[0] += 1
                    ins.then_inc(s.v.sem, 1)
                    dve.wait_ge(s.v.sem, s.v.at(0, count[0]))

                dve.wait_ge(s.logits.sem, s.logits.at(0, 1))
                link(dve.tensor_reduce(top[:, :], b3(0), AX.X, ALU.max))
                dve.tensor_tensor(prob[:, :, :], b3(0), wide(top[:, :]), ALU.subtract).then_inc(s.shifted.sem, 1)
                dve.wait_ge(s.exp.sem, s.exp.at(0, 1))
                link(dve.tensor_reduce(tot[:, :], prob[:, :, :], AX.X, ALU.add))
                link(dve.reciprocal(inv[:, :], tot[:, :]))
                link(dve.tensor_tensor(prob[:, :, :], prob[:, :, :], wide(inv[:, :]), ALU.mult))
                choose_first(dve, link, prob[:, :, :], iota, gate[:, :], eq[:, :, :], index[:, :], hot[:, :, :], E1)
                dve.nop().then_inc(s.hot.sem, 1)
                dve.wait_ge(s.counts.sem, s.counts.at(0, 1))
                running_count(dve, link, net, pre, b3(1), b3(2), E1)
                b = group(tmp=eq[:, :, :], pos=pos[:, :], slot=slot[:, :], kept=kept[:, :])
                slots_of(dve, link, b, pre[:, :, :], hot[:, :, :], index[:, :], net.tab("trash")[:, 0:NT], C1,
                         scatter[:, :], gather[:, :], acc[:, :])
                link(dve.tensor_tensor(gate[:, :], gate[:, :], acc[:, :], ALU.mult))
                dve.nop().then_inc(s.slots.sem, 1)
                for j in range(STEPS):
                    dve.wait_ge(s.silu.sem, s.silu.at(0, j + 1))
                    dve.wait_ge(s.u_ps.sem, s.u_ps.at(0, j + 1))
                    if j >= 2:
                        dve.wait_ge(s.y_ps.sem, s.y_ps.at(0, j - 1))
                    dve.tensor_tensor(hid[:, j % 2, :], act_g[:, j % 2, :], bank[2 + j % 2][:, 0:4 * C1], ALU.mult).then_inc(s.hid.sem, 1)
                dve.wait_ge(fetched, 16 * NT)
                for t in range(NT):
                    dve.tensor_scalar(yg[:, t, :], yg[:, t, :], gate[:, t:t + 1], None, ALU.mult).then_inc(s.combined.sem, 1)
                dve.wait_ge(s.combined.sem, s.combined.at(0, NT))
                flat = yg[:, :, :].rearrange("p t d -> p (t d)")
                dve.scalar_tensor_tensor(flat, net.x_tok[:, :], 2.0, flat, ALU.mult, ALU.add).then_inc(s.combined.sem, 1)
                dve.wait_ge(s.combined.sem, s.combined.at(0, NT + 1))
                with dve.Fori(0, B) as i:
                    norm_dve(dve, s, n, i, yg[:, bass.ds(TPB * i, TPB), :])

            @block.gpsimd
            def _(pool):
                pool.wait_ge(s.slots.sem, s.slots.at(0, 1))
                pool.wait_ge(net.zeroed, net.zero_ready)
                for t in range(NT):
                    pool.indirect_dma_start(net.slots[0], bass.IndirectOffsetOnAxis(ap=scatter[:, t:t + 1], axis=0),
                                            net.x_tok[:, t * P:(t + 1) * P], None).then_inc(moved, 16)
                pool.wait_ge(stored, 16)
                for t in range(NT):
                    pool.indirect_dma_start(yg[:, t, :], None, net.slots_out[0],
                                            bass.IndirectOffsetOnAxis(ap=gather[:, t:t + 1], axis=0)).then_inc(fetched, 16)
                with pool.Fori(0, B) as i:
                    norm_pool(pool, s, n, i)

            @block.sync
            def _(sp):
                sp.wait_ge(moved, 16 * NT)
                sp.dma_start(rows[:, :, :], net.slots[0][0:SLOTS, :].rearrange("(k p) d -> p k d", p=P)).then_inc(net.rows_in, 16)
                sp.wait_ge(s.y_sb.sem, s.y_sb.at(0, STEPS))
                sp.dma_start(net.slots_out[0].rearrange("(e c) d -> c e d", c=C1), y[0:C1, :, :]).then_inc(stored, 16)
    close_stage(nc, net.pool)


def stage_mha(nc, net, w, mask, src, dst, load=()):
    with ExitStack() as ctx:
        sb = lambda name, shape: ctx.enter_context(nc.sbuf_tensor(net.name(name), shape, F32))
        OG = AH // 8
        pl = plan([(t, h, t, 1) for t in range(TPB) for h in range(AH)], [2 * k + 1 for k in range(TPB * OG)])
        a = attend_buffers(ctx, nc, net, pl, ADK ** -0.5)
        n = norm_buffers(ctx, nc, net)
        HC = AH * ADK // P
        xs = sb("xs", [P, L])
        qT, kT, oT = (sb(k, [P, HC, L]) for k in ("qT", "kT", "oT"))
        v, o = sb("v", [P, TPB, AH * ADK]), sb("o", [P, 2, 512])
        s = open_stage(nc, net.pool, "xs_ready:1 qk_ps:8 qk:8 v_ps:4 v_ready:4 weighted:4 probs_used:0 " + pl.spec
                       + NORM.replace("settled:0 ", ""))
        bank = net.bank
        ident = net.tab("ident")
        with nc.Block() as block:
            @block.sync
            def _(sp):
                with nc.allow_non_contiguous_dma(reason="biases, one to a partition, and a small router"):
                    for to, of, done in load:
                        sp.dma_start(to, of).then_inc(done, 16)

            @block.gpsimd
            def _(pool):
                with pool.Fori(0, B) as i:
                    norm_pool(pool, s, n, i)

            @block.tensor
            def _(pe):
                pe.wait_ge(net.ld_w2, net.w2_ready)
                with pe.Fori(0, B) as i:
                    pe.wait_ge(s.xs_ready.sem, s.xs_ready.at(i, 1))
                    pe.wait_ge(s.masked.sem, s.masked.at(i, 0))
                    pe.wait_ge(s.probs.sem, s.probs.at(i, 0))
                    pe.wait_ge(s.x_updated.sem, s.x_updated.at(i, 0))
                    for j, wt in enumerate((w.q, w.k)):
                        for b in range(4):
                            if j == 1:
                                pe.wait_ge(s.qk.sem, s.qk.at(i, b + 1))
                            for k in range(2):
                                c = 2 * b + k
                                last = pe.matmul(bank[b][:, k * L:(k + 1) * L], wt[:, c * P:(c + 1) * P], xs[:, :], start=True, stop=True)
                            last.then_inc(s.qk_ps.sem, 1)
                        if j == 0:
                            for t in range(TPB):
                                for k in range(2):
                                    pe.matmul(bank[4 + 2 * t + k][:, :], xs[:, t * P:(t + 1) * P], w.v[:, k * 512:(k + 1) * 512],
                                              start=True, stop=True).then_inc(s.v_ps.sem, 1)

                    def first_scores(j):
                        if j == 0:
                            pe.wait_ge(s.qk.sem, s.qk.at(i, 8))
                            pe.wait_ge(s.v_ready.sem, s.v_ready.at(i, 4))

                    def out(g):
                        pe.wait_ge(s.o_ready.sem, s.o_ready.at(i, g + 1))
                        if g:
                            pe.wait_ge(s.oT_ready.sem, s.oT_ready.at(i, g))
                        for c in range(4):
                            last = pe.transpose(bank[6][:, c * P:(c + 1) * P], o[:, g % 2, c * P:(c + 1) * P], ident)
                        last.then_inc(s.oT_ps.sem, 1)

                    row = lambda h: slice(ADK * (h % 2), ADK * (h % 2) + ADK)
                    attend_pe(pe, s, a, net, i,
                              lambda t, h: qT[row(h), h // 2, t * P:(t + 1) * P],
                              lambda h, kb, nkb: kT[row(h), h // 2, kb * P:(kb + nkb) * P],
                              lambda kb, h: v[:, kb, h * ADK:(h + 1) * ADK],
                              lambda h: bank[7][:, (h % 8) * ADK:(h % 8 + 1) * ADK], first_scores, out)
                    pe.wait_ge(s.oT_ready.sem, s.oT_ready.at(i, 4))
                    for t in range(TPB):
                        tok = slice(t * P, (t + 1) * P)
                        for c in range(HC):
                            pe.matmul(bank[6][:, tok], oT[:, c, tok], w.p[:, c, :], start=(c == 0), stop=False)
                        pe.matmul(bank[6][:, tok], net.tab("ones")[0:1, :], w.pb[:, :], start=False, stop=False)
                        last = pe.matmul(bank[6][:, tok], xs[:, tok], ident, start=False, stop=True)
                    last.then_inc(s.y_ready.sem, 1)
                    norm_pe(pe, s, n, i, bank[7][:, 0:L])

            @block.scalar
            def _(act):
                act.wait_ge(net.ld_w2, net.w2_ready)
                with act.Fori(0, B) as i:
                    act.wait_ge(s.y_ready.sem, s.y_ready.at(i, 0))
                    act.activation(xs[:, :], src[:, bass.ds(i * L, L)], ACT.Copy).then_inc(s.xs_ready.sem, 1)
                    for j, to in enumerate((qT, kT)):
                        for b in range(4):
                            act.wait_ge(s.qk_ps.sem, s.qk_ps.at(i, 4 * j + b + 1))
                            act.activation(to[:, 2 * b:2 * b + 2, :], bank[b][:, :].rearrange("p (c t) -> p c t", t=L), ACT.Copy)\
                                .then_inc(s.qk.sem, 1)

                    def out(g):
                        t, half = g // OG, g % OG
                        act.wait_ge(s.oT_ps.sem, s.oT_ps.at(i, g + 1))
                        act.activation(oT[:, 4 * half:4 * half + 4, t * P:(t + 1) * P], bank[6][:, :].rearrange("p (c t) -> p c t", t=P), ACT.Copy)\
                            .then_inc(s.oT_ready.sem, 1)
                    attend_act(act, s, a, net, i, out)
                    norm_act(act, s, i, bank[7][:, 0:L], dst[:, bass.ds(i * L, L)], w.g[:, :], w.b[:, :])

            @block.vector
            def _(dve):
                heads = lambda ap: ap.rearrange("p (h d) -> p h d", d=ADK)
                with dve.Fori(0, B) as i:
                    for k in range(4):
                        dve.wait_ge(s.v_ps.sem, s.v_ps.at(i, k + 1))
                        dve.tensor_copy(v[:, k // 2, (k % 2) * 512:(k % 2 + 1) * 512], bank[4 + k][:, :]).then_inc(s.v_ready.sem, 1)

                    def normalise(g, rs):
                        t, half = g // OG, g % OG
                        if g >= 2:
                            dve.wait_ge(s.oT_ps.sem, s.oT_ps.at(i, g - 1))
                        else:
                            dve.wait_ge(s.oT_ps.sem, s.oT_ps.at(i, 0))
                        dve.tensor_tensor(heads(o[:, g % 2, :]), heads(bank[7][:, :]), rs.unsqueeze(2).to_broadcast([P, 8, ADK]), ALU.mult)\
                            .then_inc(s.weighted.sem, 1)
                        dve.wait_ge(s.weighted.sem, s.weighted.at(i, g + 1))
                        dve.tensor_tensor(o[:, g % 2, :], o[:, g % 2, :], v[:, t, half * 512:(half + 1) * 512], ALU.subtract)\
                            .then_inc(s.o_ready.sem, 1)
                    attend_dve(dve, s, a, net, i, lambda t, h, nkb: mask, normalise)
                    norm_dve(dve, s, n, i, bank[6][:, 0:L].rearrange("p (t d) -> p t d", d=D))
    close_stage(nc, net.pool)


def stage_relu_mlp(nc, net, w, x, final, order, order_to):
    with ExitStack() as ctx:
        sb = lambda name, shape: ctx.enter_context(nc.sbuf_tensor(net.name(name), shape, F32))
        n, nf = norm_buffers(ctx, nc, net), norm_buffers(ctx, nc, net, keep=True)
        C = DI // P
        xs, x0, z, hid = sb("xs", [P, L]), sb("x0", [P, L]), sb("z", [P, L]), sb("hid", [P, C, L])
        s = open_stage(nc, net.pool, f"xs_ready:1 x0_ready:1 h_ps:{C} hid:{C} " + NORM + " " + prefixed("f_", NORM))
        f = part(s, "f_")
        bank, ident = net.bank, net.tab("ident")
        with nc.Block() as block:
            @block.gpsimd
            def _(pool):
                with pool.Fori(0, B) as i:
                    norm_pool(pool, s, n, i)
                    if final:
                        norm_pool(pool, f, nf, i)

            @block.tensor
            def _(pe):
                pe.wait_ge(net.ld_w2, net.w2_ready)
                with pe.Fori(0, B) as i:
                    pe.wait_ge(s.xs_ready.sem, s.xs_ready.at(i, 1))
                    for c in range(C):
                        pe.wait_ge(s.hid.sem, s.hid.at(i, 0))
                        pe.matmul(bank[c][:, 0:L], w.w1[:, c * P:(c + 1) * P], xs[:, :], start=True, stop=True).then_inc(s.h_ps.sem, 1)
                    pe.wait_ge(s.xn_ready.sem, s.xn_ready.at(i, 0))
                    pe.wait_ge(s.hid.sem, s.hid.at(i, C))
                    for t in range(TPB):
                        tok = slice(t * P, (t + 1) * P)
                        for c in range(C):
                            pe.matmul(bank[4][:, tok], hid[:, c, tok], w.w2[:, c, :], start=(c == 0), stop=False)
                        pe.matmul(bank[4][:, tok], net.tab("ones")[0:1, :], w.b2[:, :], start=False, stop=False)
                        last = pe.matmul(bank[4][:, tok], xs[:, tok], ident, start=False, stop=True)
                    last.then_inc(s.y_ready.sem, 1)
                    pe.wait_ge(s.x_updated.sem, s.x_updated.at(i, 0))
                    norm_pe(pe, s, n, i, bank[5][:, 0:L])
                    if final:
                        pe.wait_ge(s.x_updated.sem, s.x_updated.at(i, 1))
                        pe.wait_ge(s.x0_ready.sem, s.x0_ready.at(i, 1))
                        pe.wait_ge(f.xn_ready.sem, f.xn_ready.at(i, 0))
                        for t in range(TPB):
                            tok = slice(t * P, (t + 1) * P)
                            pe.matmul(bank[6][:, tok], z[:, tok], ident, start=True, stop=False)
                            last = pe.matmul(bank[6][:, tok], x0[:, tok], ident, start=False, stop=True)
                        last.then_inc(f.y_ready.sem, 1)
                        pe.wait_ge(f.x_updated.sem, f.x_updated.at(i, 0))
                        norm_pe(pe, f, nf, i, bank[7][:, 0:L])

            @block.scalar
            def _(act):
                act.wait_ge(net.ld_w2, net.w2_ready)
                with act.Fori(0, B) as i:
                    act.wait_ge(s.y_ready.sem, s.y_ready.at(i, 0))
                    act.activation(xs[:, :], x[:, bass.ds(i * L, L)], ACT.Copy).then_inc(s.xs_ready.sem, 1)
                    if final:
                        act.wait_ge(f.y_ready.sem, f.y_ready.at(i, 0))
                        act.activation(x0[:, :], net.xT[:, bass.ds(i * L, L)], ACT.Copy).then_inc(s.x0_ready.sem, 1)
                    for c in range(C):
                        act.wait_ge(s.h_ps.sem, s.h_ps.at(i, c + 1))
                        act.activation(hid[:, c, :], bank[c][:, 0:L], ACT.Relu, bias=w.b1[:, c:c + 1]).then_inc(s.hid.sem, 1)
                    dst = z[:, :] if final else x[:, bass.ds(i * L, L)]
                    if final:
                        act.wait_ge(f.y_ready.sem, f.y_ready.at(i, 0))
                    norm_act(act, s, i, order(bank[5][:, 0:L]), order_to(dst), w.g[:, :], w.b[:, :])
                    if final:
                        norm_act(act, f, i, bank[7][:, 0:L], net.xT[:, bass.ds(i * L, L)])

            @block.vector
            def _(dve):
                y = lambda k: bank[k][:, 0:L].rearrange("p (t d) -> p t d", d=D)
                with dve.Fori(0, B) as i:
                    norm_dve(dve, s, n, i, y(4))
                    if final:
                        norm_dve(dve, f, nf, i, y(6))
    close_stage(nc, net.pool)


def stage_top2_experts(nc, net, io):
    with ExitStack() as ctx:
        sb = lambda name, shape, dt=F32: ctx.enter_context(nc.sbuf_tensor(net.name(name), shape, dt))
        n = norm_buffers(ctx, nc, net, in_psum=False)
        prob, rest, eq, hot1, hot2, pre = (sb(k, [P, NT, E2]) for k in ("prob", "rest", "equal", "hot1", "hot2", "pre"))
        (top, tot, inv, p1, p2, i1, i2, acc1, acc2, pos, slot, kept, ms, rms) = (sb(k, [P, NT]) for k in (
            "top", "total", "inv", "p1", "p2", "index1", "index2", "acc1", "acc2", "pos", "slot", "kept", "mean_sq", "rms"))
        scatter, gather = sb("scatter", [P, 2, NT], I32), sb("gather", [P, 2, NT], I32)
        sq = sb("square", [P, D])
        KT = SLOTS // P
        rows, rowsT = sb("rows", [P, KT, D]), sb("rowsT", [P, SLOTS])
        FC = IR // P
        act_g, hid = sb("act_g", [P, 2, C2]), sb("hid", [P, FC, C2])
        yg1, yg2 = sb("y_first", [P, NT, D]), sb("y_second", [P, NT, D])
        y = sb("y", [P, 2, 3, D])
        SC = IS // P
        sgate, shid = sb("shared_gate", [P, 2, L]), sb("shared_hid", [P, SC, L])
        xs, z = sb("xs", [P, L]), sb("z", [P, TPB, D])
        MS = [(0, P), (P, P), (2 * P, C2 - 2 * P)]
        s = open_stage(nc, net.pool, f"v:120 logits:1 squares:{NT} mean:1 rms:1 shifted:1 exp:1 hot:1 counts:1 slots:1 rowsT_ps:5 rowsT:5 "
                       f"g_ps:{E2 * FC} u_ps:{E2 * FC} silu:{E2 * FC} hid:{E2 * FC} y_ps:{E2} y_sb:{E2} "
                       f"xs_ready:1 sg_ps:{SC} su_ps:{SC} s_silu:{SC} s_hid:{SC} z_ready:1 " + NORM)
        bank = net.bank
        b3 = lambda k: bank[k][:, 0:NT * E2].rearrange("p (t e) -> p t e", e=E2)
        wide = lambda ap: ap.unsqueeze(2).to_broadcast([P, NT, E2])
        iota = net.tab("iota32")[:, 0:E2].unsqueeze(1).to_broadcast([P, NT, E2])
        rg, ru = (net.moe_w[k][:, :, :].rearrange("p e f -> p (e f)").rearrange("p (e i) -> p e i", e=E2) for k in range(2))
        rd = net.moe_w[2][:, :, :].rearrange("p (e c) d -> p e c d", e=E2)
        moved, stored, fetched = net.moved2, net.stored2, net.fetched2
        with nc.Block() as block:
            def down(pe, e):
                pe.wait_ge(s.hid.sem, s.hid.at(0, FC * (e + 1)))
                if e >= 1:
                    pe.wait_ge(s.y_sb.sem, s.y_sb.at(0, e))
                for m, (at, w) in enumerate(MS):
                    for c in range(FC):
                        last = pe.matmul(bank[4][0:w, m * P:(m + 1) * P], hid[:, c, at:at + w], rd[:, e, c, :], start=(c == 0), stop=(c == FC - 1))
                last.then_inc(s.y_ps.sem, 1)

            @block.tensor
            def _(pe):
                pe.wait_ge(net.ld_w3, net.w3_ready)
                for t in range(NT):
                    last = pe.matmul(bank[0][:, t * E2:(t + 1) * E2], net.xT[:, t * P:(t + 1) * P], net.router2[:, :], start=True, stop=True)
                last.then_inc(s.logits.sem, 1)
                pe.wait_ge(s.hot.sem, s.hot.at(0, 1))
                flat = eq[:, :, :].rearrange("p t e -> p (t e)")
                pe.matmul(bank[1][:, 0:NT * E2], net.tab("tri"), flat, start=True, stop=True)
                pe.matmul(bank[2][:, 0:NT * E2], net.tab("ones"), flat, start=True, stop=True).then_inc(s.counts.sem, 1)
                pe.wait_ge(net.rows_in, 32)
                pe.wait_ge(s.slots.sem, s.slots.at(0, 1))
                for g in range(KT // 4):
                    for k in range(4):
                        last = pe.transpose(bank[g][:, k * P:(k + 1) * P], rows[:, 4 * g + k, :], net.tab("ident"))
                    last.then_inc(s.rowsT_ps.sem, 1)
                pe.wait_ge(s.rowsT.sem, s.rowsT.at(0, 5))
                for e in range(E2):
                    x = rowsT[:, e * C2:(e + 1) * C2]
                    for c in range(FC):
                        j = FC * e + c
                        for w, ps, done in ((rg, 0, s.g_ps), (ru, 2, s.u_ps)):
                            if j >= 2:
                                pe.wait_ge(s.hid.sem, s.hid.at(0, j - 1))
                            pe.matmul(bank[ps + j % 2][:, 0:C2], w[:, e, c * P:(c + 1) * P], x, start=True, stop=True).then_inc(done.sem, 1)
                    down(pe, e)
                with pe.Fori(0, B) as i:
                    pe.wait_ge(s.xs_ready.sem, s.xs_ready.at(i, 1))
                    for c in range(SC):
                        for w, ps, done in ((net.sg, 0, s.sg_ps), (net.su, 2, s.su_ps)):
                            pe.wait_ge(s.s_hid.sem, s.s_hid.at(i, max(0, c - 1)))
                            pe.matmul(bank[ps + c % 2][:, 0:L], w[:, c * P:(c + 1) * P], xs[:, :], start=True, stop=True).then_inc(done.sem, 1)
                    pe.wait_ge(s.s_hid.sem, s.s_hid.at(i, SC))
                    pe.wait_ge(s.z_ready.sem, s.z_ready.at(i, 0))
                    for t in range(TPB):
                        tok = slice(t * P, (t + 1) * P)
                        for c in range(SC):
                            pe.matmul(bank[5][:, tok], shid[:, c, tok], net.sd[:, c, :], start=(c == 0), stop=False)
                        last = pe.matmul(bank[5][:, tok], xs[:, tok], net.tab("ident"), start=False, stop=True)
                    last.then_inc(s.y_ready.sem, 1)
                    pe.wait_ge(s.x_updated.sem, s.x_updated.at(i, 0))
                    norm_pe(pe, s, n, i, bank[6][:, 0:L])

            def copy_y(act, e):
                act.wait_ge(s.y_ps.sem, s.y_ps.at(0, e + 1))
                if e >= 2:
                    act.wait_ge(stored[e % 2], 16 * 2 * (e // 2))
                act.activation(y[:, e % 2, 0:2, :], bank[4][:, 0:2 * P].rearrange("p (k d) -> p k d", d=D), ACT.Copy)
                act.activation(y[0:C2 - 2 * P, e % 2, 2, :], bank[4][0:C2 - 2 * P, 2 * P:3 * P], ACT.Copy).then_inc(s.y_sb.sem, 1)

            @block.scalar
            def _(act):
                for t in range(NT):
                    act.activation(sq[:, :], net.x_tok[:, t * P:(t + 1) * P], ACT.Square, accum_out=ms[:, t:t + 1]).then_inc(s.squares.sem, 1)
                    act.wait_ge(s.squares.sem, s.squares.at(0, t + 1))
                act.wait_ge(s.shifted.sem, s.shifted.at(0, 1))
                act.activation(prob[:, :, :], prob[:, :, :], ACT.Exp).then_inc(s.exp.sem, 1)
                for g in range(KT // 4):
                    act.wait_ge(s.rowsT_ps.sem, s.rowsT_ps.at(0, g + 1))
                    act.activation(rowsT[:, g * 512:(g + 1) * 512], bank[g][:, :], ACT.Copy).then_inc(s.rowsT.sem, 1)
                for e in range(E2):
                    for c in range(FC):
                        j = FC * e + c
                        act.wait_ge(s.g_ps.sem, s.g_ps.at(0, j + 1))
                        if j >= 2:
                            act.wait_ge(s.hid.sem, s.hid.at(0, j - 1))
                        act.activation(act_g[:, j % 2, :], bank[j % 2][:, 0:C2], ACT.Silu).then_inc(s.silu.sem, 1)
                    copy_y(act, e)
                with act.Fori(0, B) as i:
                    act.wait_ge(s.y_ready.sem, s.y_ready.at(i, 0))
                    act.activation(xs[:, :], net.xT[:, bass.ds(i * L, L)], ACT.Copy).then_inc(s.xs_ready.sem, 1)
                    for c in range(SC):
                        act.wait_ge(s.sg_ps.sem, s.sg_ps.at(i, c + 1))
                        act.wait_ge(s.s_hid.sem, s.s_hid.at(i, max(0, c - 1)))
                        act.activation(sgate[:, c % 2, :], bank[c % 2][:, 0:L], ACT.Silu).then_inc(s.s_silu.sem, 1)
                    norm_act(act, s, i, bank[6][:, 0:L], net.xT[:, bass.ds(i * L, L)])

            @block.vector
            def _(dve):
                count = [0]

                def link(ins):
                    count[0] += 1
                    ins.then_inc(s.v.sem, 1)
                    dve.wait_ge(s.v.sem, s.v.at(0, count[0]))

                dve.wait_ge(s.squares.sem, s.squares.at(0, NT))
                dve.tensor_scalar(ms[:, :], ms[:, :], 1.0 / D, float(np.finfo(np.float32).eps), ALU.mult, ALU.add).then_inc(s.mean.sem, 1)
                dve.wait_ge(s.logits.sem, s.logits.at(0, 1))
                dve.wait_ge(s.rms.sem, s.rms.at(0, 1))
                link(dve.tensor_tensor(prob[:, :, :], b3(0), wide(rms[:, :]), ALU.mult))
                link(dve.tensor_reduce(top[:, :], prob[:, :, :], AX.X, ALU.max))
                dve.tensor_tensor(prob[:, :, :], prob[:, :, :], wide(top[:, :]), ALU.subtract).then_inc(s.shifted.sem, 1)
                dve.wait_ge(s.exp.sem, s.exp.at(0, 1))
                link(dve.tensor_reduce(tot[:, :], prob[:, :, :], AX.X, ALU.add))
                link(dve.reciprocal(inv[:, :], tot[:, :]))
                link(dve.tensor_tensor(prob[:, :, :], prob[:, :, :], wide(inv[:, :]), ALU.mult))
                choose_first(dve, link, prob[:, :, :], iota, p1[:, :], eq[:, :, :], i1[:, :], hot1[:, :, :], E2)
                link(dve.scalar_tensor_tensor(rest[:, :, :], hot1[:, :, :], -2.0, prob[:, :, :], ALU.mult, ALU.add))
                choose_first(dve, link, rest[:, :, :], iota, p2[:, :], eq[:, :, :], i2[:, :], hot2[:, :, :], E2)
                link(dve.tensor_tensor(eq[:, :, :], hot1[:, :, :], hot2[:, :, :], ALU.add))
                dve.nop().then_inc(s.hot.sem, 1)
                link(dve.tensor_tensor(tot[:, :], p1[:, :], p2[:, :], ALU.add))
                link(dve.reciprocal(inv[:, :], tot[:, :]))
                dve.wait_ge(s.counts.sem, s.counts.at(0, 1))
                running_count(dve, link, net, pre, b3(1), b3(2), E2)
                b = group(tmp=eq[:, :, :], pos=pos[:, :], slot=slot[:, :], kept=kept[:, :])
                for k, (hot, index, acc, p) in enumerate(((hot1, i1, acc1, p1), (hot2, i2, acc2, p2))):
                    slots_of(dve, link, b, pre[:, :, :], hot[:, :, :], index[:, :], net.tab("trash")[:, k * NT:(k + 1) * NT], C2,
                             scatter[:, k, :], gather[:, k, :], acc[:, :])
                    link(dve.tensor_tensor(p[:, :], p[:, :], inv[:, :], ALU.mult))
                    link(dve.tensor_tensor(p[:, :], p[:, :], acc[:, :], ALU.mult))
                dve.nop().then_inc(s.slots.sem, 1)
                for e in range(E2):
                    for c in range(FC):
                        j = FC * e + c
                        dve.wait_ge(s.silu.sem, s.silu.at(0, j + 1))
                        dve.wait_ge(s.u_ps.sem, s.u_ps.at(0, j + 1))
                        if e >= 1:
                            dve.wait_ge(s.y_ps.sem, s.y_ps.at(0, e))
                        dve.tensor_tensor(hid[:, c, :], act_g[:, j % 2, :], bank[2 + j % 2][:, 0:C2], ALU.mult).then_inc(s.hid.sem, 1)
                dve.wait_ge(fetched, 16 * 2 * NT)
                wide_d = lambda ap: ap.unsqueeze(2).to_broadcast([P, NT, D])
                link(dve.tensor_tensor(yg1[:, :, :], yg1[:, :, :], wide_d(p1[:, :]), ALU.mult))
                link(dve.tensor_tensor(yg2[:, :, :], yg2[:, :, :], wide_d(p2[:, :]), ALU.mult))
                link(dve.tensor_tensor(yg1[:, :, :], yg1[:, :, :], yg2[:, :, :], ALU.add))
                with dve.Fori(0, B) as i:
                    for c in range(SC):
                        dve.wait_ge(s.s_silu.sem, s.s_silu.at(i, c + 1))
                        dve.wait_ge(s.su_ps.sem, s.su_ps.at(i, c + 1))
                        dve.wait_ge(s.y_ready.sem, s.y_ready.at(i, 0))
                        dve.tensor_tensor(shid[:, c, :], sgate[:, c % 2, :], bank[2 + c % 2][:, 0:L], ALU.mult).then_inc(s.s_hid.sem, 1)
                    dve.wait_ge(s.y_ready.sem, s.y_ready.at(i, 1))
                    dve.tensor_tensor(z[:, :, :], bank[5][:, 0:L].rearrange("p (t d) -> p t d", d=D), yg1[:, bass.ds(TPB * i, TPB), :], ALU.add)\
                        .then_inc(s.z_ready.sem, 1)
                    dve.wait_ge(s.z_ready.sem, s.z_ready.at(i, 1))
                    settle(dve, s)
                    norm_dve(dve, s, n, i, z[:, :, :])

            @block.gpsimd
            def _(pool):
                pool.wait_ge(s.mean.sem, s.mean.at(0, 1))
                pool.tensor_tensor(rms[:, :], ms[:, :], net.neghalf[:, 0:NT], ALU.pow).then_inc(s.rms.sem, 1)
                pool.wait_ge(s.slots.sem, s.slots.at(0, 1))
                pool.wait_ge(net.zeroed, net.zero_ready)
                for k in range(2):
                    for t in range(NT):
                        pool.indirect_dma_start(net.slots[1], bass.IndirectOffsetOnAxis(ap=scatter[:, k, t:t + 1], axis=0),
                                                net.x_tok[:, t * P:(t + 1) * P], None).then_inc(moved, 16)
                for half in stored:
                    pool.wait_ge(half, 16 * 2 * E2 // 2)
                for k, to in enumerate((yg1, yg2)):
                    for t in range(NT):
                        pool.indirect_dma_start(to[:, t, :], None, net.slots_out[1],
                                                bass.IndirectOffsetOnAxis(ap=gather[:, k, t:t + 1], axis=0)).then_inc(fetched, 16)
                with pool.Fori(0, B) as i:
                    norm_pool(pool, s, n, i)

            @block.sync
            def _(sp):
                sp.wait_ge(moved, 16 * 2 * NT)
                sp.dma_start(rows[:, :, :], net.slots[1][0:SLOTS, :].rearrange("(k p) d -> p k d", p=P)).then_inc(net.rows_in, 16)
                for e in range(E2):
                    sp.wait_ge(s.y_sb.sem, s.y_sb.at(0, e + 1))
                    at = e * C2
                    sp.dma_start(net.slots_out[1][at:at + 2 * P, :].rearrange("(k p) d -> p k d", p=P), y[:, e % 2, 0:2, :]).then_inc(stored[e % 2], 16)
                    sp.dma_start(net.slots_out[1][at + 2 * P:at + C2, :], y[0:C2 - 2 * P, e % 2, 2, :]).then_inc(stored[e % 2], 16)
    close_stage(nc, net.pool)


def stage_decayed_attention(nc, net, io):
    with ExitStack() as ctx:
        sb = lambda name, shape: ctx.enter_context(nc.sbuf_tensor(net.name(name), shape, F32))
        pl = plan([(t, h, 0, t + 1) for t in range(TPB) for h in range(RH)], [3, 7])
        a = attend_buffers(ctx, nc, net, pl, RDH ** -0.5)
        n = norm_buffers(ctx, nc, net)
        xs = sb("xs", [P, L])
        bias = sb("bias", [P, TPB, RH // 2, L])
        xi, rate = sb("xi", [P, RH]), sb("rate", [P, RH])
        W = 32
        qk = sb("qk_wide", [P, TPB, 2, RH, W])
        prod = sb("prod", [P, 4, 8, 2, RDH // 2])
        qT, kT = sb("qT", [P, 4, L]), sb("kT", [P, 4, L])
        v, o, oT = sb("v", [P, TPB, D]), sb("o", [P, TPB, D]), sb("oT", [P, L])
        s = open_stage(nc, net.pool, "clear:1 rate0:1 rate:1 bias:16 xs_ready:1 qkv:2 plain:2 v_ready:2 cosd:2 turn:2 "
                       "wide:2 qkT_ps:4 qkT:4 probs_used:4 " + pl.spec + NORM.replace("settled:0 ", ""))
        bank, ident = net.bank, net.tab("ident")
        tiles = lambda k: net.tab(k).rearrange("p (t k) -> p t k", t=TPB)
        causal, mdist, rcos, rsin = tiles("causal"), tiles("mdist"), tiles("rcos"), tiles("rsin")
        with nc.Block() as block:
            @block.sync
            def _(sp):
                sp.dma_start(xi[:, :], io["L3_attn_log_xi"].partition_broadcast(P)).then_inc(net.ld_xi, 16)

            @block.gpsimd
            def _(pool):
                pool.memset(qk[:, :, :, :, :], 0.0).then_inc(s.clear.sem, 1)
                with pool.Fori(0, B) as i:
                    norm_pool(pool, s, n, i)

            @block.tensor
            def _(pe):
                pe.wait_ge(net.ld_w3, net.w3_ready)
                with pe.Fori(0, B) as i:
                    pe.wait_ge(s.xs_ready.sem, s.xs_ready.at(i, 1))
                    pe.wait_ge(s.masked.sem, s.masked.at(i, 0))
                    pe.wait_ge(s.probs.sem, s.probs.at(i, 0))
                    pe.wait_ge(s.x_updated.sem, s.x_updated.at(i, 0))
                    for t in range(TPB):
                        pe.matmul(bank[t][:, 0:3 * D], xs[:, t * P:(t + 1) * P], net.w_qkv3[:, :], start=True, stop=True).then_inc(s.qkv.sem, 1)
                    for t in range(TPB):
                        pe.wait_ge(s.wide.sem, s.wide.at(i, t + 1))
                        pe.wait_ge(s.plain.sem, s.plain.at(i, t + 1))
                        for j in range(2):
                            for c in range(4):
                                last = pe.transpose(bank[4 + 2 * t + j][:, c * P:(c + 1) * P],
                                                    qk[:, t, j, 4 * c:4 * c + 4, :].rearrange("p h w -> p (h w)"), ident)
                            last.then_inc(s.qkT_ps.sem, 1)

                    def first_scores(j):
                        if j == 0:
                            pe.wait_ge(s.qkT.sem, s.qkT.at(i, 4))
                            pe.wait_ge(s.v_ready.sem, s.v_ready.at(i, 2))

                    def out(g):
                        pe.wait_ge(s.o_ready.sem, s.o_ready.at(i, g + 1))
                        if g:
                            pe.wait_ge(s.oT_ready.sem, s.oT_ready.at(i, g))
                        pe.transpose(bank[6][:, 0:P], o[:, g, :], ident).then_inc(s.oT_ps.sem, 1)

                    row = lambda h: slice(W * (h % 4), W * (h % 4) + W)
                    attend_pe(pe, s, a, net, i,
                              lambda t, h: qT[row(h), h // 4, t * P:(t + 1) * P],
                              lambda h, kb, nkb: kT[row(h), h // 4, kb * P:(kb + nkb) * P],
                              lambda kb, h: v[:, kb, h * RDH:(h + 1) * RDH],
                              lambda h: bank[7][:, h * RDH:(h + 1) * RDH], first_scores, out)
                    pe.wait_ge(s.oT_ready.sem, s.oT_ready.at(i, 2))
                    for t in range(TPB):
                        tok = slice(t * P, (t + 1) * P)
                        pe.matmul(bank[6][:, tok], oT[:, tok], net.w_o3[:, :], start=True, stop=False)
                        last = pe.matmul(bank[6][:, tok], xs[:, tok], ident, start=False, stop=True)
                    last.then_inc(s.y_ready.sem, 1)
                    norm_pe(pe, s, n, i, bank[7][:, 0:L])

            @block.scalar
            def _(act):
                act.wait_ge(net.ld_xi, 16)
                act.activation(rate[:, :], xi[:, :], ACT.Exp, scale=-1.0).then_inc(s.rate0.sem, 1)
                act.wait_ge(s.clear.sem, s.clear.at(0, 1))
                with act.Fori(0, B) as i:
                    act.wait_ge(s.y_ready.sem, s.y_ready.at(i, 0))
                    act.activation(xs[:, :], net.xT[:, bass.ds(i * L, L)], ACT.Copy).then_inc(s.xs_ready.sem, 1)
                    act.wait_ge(s.qkT_ps.sem, s.qkT_ps.at(i, 0))
                    for t in range(TPB):
                        act.wait_ge(s.wide.sem, s.wide.at(i, t + 1))
                        src = bank[t][:, 0:2 * D].rearrange("p (j g y d) -> p j g y d", j=2, g=4, y=4)
                        for y in range(2):
                            for j in range(2):
                                dst = qk[:, t, j, :, 0:RDH].rearrange("p (g y) d -> p g y d", y=4)[:, :, y, :]
                                last = act.activation(dst, src[:, j, :, y, :], ACT.Copy)
                        last.then_inc(s.plain.sem, 1)
                        act.activation(v[:, t, :], bank[t][:, 2 * D:3 * D], ACT.Copy).then_inc(s.v_ready.sem, 1)
                    for t in range(TPB):
                        for j, to in enumerate((qT, kT)):
                            act.wait_ge(s.qkT_ps.sem, s.qkT_ps.at(i, 2 * t + j + 1))
                            act.activation(to[:, :, t * P:(t + 1) * P], bank[4 + 2 * t + j][:, :].rearrange("p (c t) -> p c t", t=P), ACT.Copy)\
                                .then_inc(s.qkT.sem, 1)

                    def out(g):
                        act.wait_ge(s.oT_ps.sem, s.oT_ps.at(i, g + 1))
                        act.activation(oT[:, g * P:(g + 1) * P], bank[6][:, 0:P], ACT.Copy).then_inc(s.oT_ready.sem, 1)
                    attend_act(act, s, a, net, i, out)
                    norm_act(act, s, i, bank[7][:, 0:L], net.xT[:, bass.ds(i * L, L)])

            @block.vector
            def _(dve):
                dve.wait_ge(s.rate0.sem, s.rate0.at(0, 1))
                dve.tensor_scalar(rate[:, :], rate[:, :], RDH ** 0.5, None, ALU.mult).then_inc(s.rate.sem, 1)
                dve.wait_ge(s.rate.sem, s.rate.at(0, 1))
                for t in range(TPB):
                    for h in range(RH // 2):
                        dve.scalar_tensor_tensor(bias[:, t, h, :], mdist[:, t, :], rate[:, 2 * h + 1:2 * h + 2], causal[:, t, :],
                                                 ALU.mult, ALU.add).then_inc(s.bias.sem, 1)
                dve.wait_ge(s.bias.sem, s.bias.at(0, 16))
                dve.wait_ge(s.clear.sem, s.clear.at(0, 1))
                HR = RDH // 2
                with dve.Fori(0, B) as i:
                    dve.wait_ge(s.qkT_ps.sem, s.qkT_ps.at(i, 0))
                    for t in range(TPB):
                        dve.wait_ge(s.qkv.sem, s.qkv.at(i, 2))
                        src = bank[t][:, 0:2 * D].rearrange("p (g y e x) -> p g y e x", g=8, y=4, x=2)
                        ev, od = src[:, :, 2:4, :, 0], src[:, :, 2:4, :, 1]
                        cos, sin = (x[:, t, :].unsqueeze(1).unsqueeze(1).to_broadcast([P, 8, 2, HR]) for x in (rcos, rsin))
                        if t:
                            dve.wait_ge(s.wide.sem, s.wide.at(i, t))
                        dve.tensor_tensor(prod[:, 0, :, :, :], ev, cos, ALU.mult)
                        dve.tensor_tensor(prod[:, 1, :, :, :], od, sin, ALU.mult)
                        dve.tensor_tensor(prod[:, 2, :, :, :], ev, sin, ALU.mult)
                        dve.tensor_tensor(prod[:, 3, :, :, :], od, cos, ALU.mult).then_inc(s.cosd.sem, 1)
                        dve.wait_ge(s.cosd.sem, s.cosd.at(i, t + 1))
                        dst = qk[:, t, :, :, 0:RDH].rearrange("p j h (e x) -> p (j h) e x", x=2).rearrange("p (g y) e x -> p g y e x", y=4)
                        dve.tensor_tensor(dst[:, :, 2:4, :, 0], prod[:, 0, :, :, :], prod[:, 1, :, :, :], ALU.subtract)
                        dve.tensor_tensor(dst[:, :, 2:4, :, 1], prod[:, 2, :, :, :], prod[:, 3, :, :, :], ALU.add).then_inc(s.wide.sem, 1)

                    def normalise(g, rs):
                        heads = lambda ap: ap.rearrange("p (h d) -> p h d", d=RDH)
                        dve.wait_ge(s.oT_ps.sem, s.oT_ps.at(i, 0))
                        dve.tensor_tensor(heads(o[:, g, :]), heads(bank[7][:, 0:D]), rs.unsqueeze(2).to_broadcast([P, RH, RDH]), ALU.mult)\
                            .then_inc(s.o_ready.sem, 1)
                    attend_dve(dve, s, a, net, i, lambda t, h, nkb: (bias[:, t, h // 2, 0:nkb * P] if h % 2 else causal[:, t, 0:nkb * P]), normalise)
                    norm_dve(dve, s, n, i, bank[6][:, 0:L].rearrange("p (t d) -> p t d", d=D))
    close_stage(nc, net.pool)


def stage_ternary(nc, net, io, out):
    with ExitStack() as ctx:
        sb = lambda name, shape: ctx.enter_context(nc.sbuf_tensor(net.name(name), shape, F32))
        n = norm_buffers(ctx, nc, net, keep=True)
        w, pos, neg, mag, wT = (sb(k, [P, P]) for k in ("weight", "above", "below", "magnitude", "ternaryT"))
        xs = sb("xs", [P, L])
        part_sum, delta, mdelta, alpha, bias = sb("abs_sum", [P, 1]), sb("delta", [P, 1]), sb("minus_delta", [P, 1]), sb("alpha", [P, 1]), sb("bias", [1, D])
        s = open_stage(nc, net.pool, "mag:1 v:8 mean_ps:1 tern:1 wT_ps:1 wT:1 xs_ready:1 " + NORM)
        bank, ident = net.bank, net.tab("ident")
        with nc.Block() as block:
            @block.sync
            def _(sp):
                sp.dma_start(w[:, :], io["L3_ffn_weight"]).then_inc(net.ld_t, 16)
                sp.dma_start(alpha[:, :], io["L3_ffn_alpha"].partition_broadcast(P)).then_inc(net.ld_t, 16)
                sp.dma_start(bias[:, :], io["L3_ffn_bias"].rearrange("(o d) -> o d", o=1)).then_inc(net.ld_t, 16)
                sp.wait_ge(s.kept.sem, s.kept.at(B - 1, 1))
                sp.dma_start(out.rearrange("b (t p) d -> p (b t) d", p=P), net.x_tok[:, :].rearrange("p (t d) -> p t d", d=D)).then_inc(net.out_done, 16)
                sp.wait_ge(net.out_done, 16)

            @block.gpsimd
            def _(pool):
                with pool.Fori(0, B) as i:
                    norm_pool(pool, s, n, i)

            @block.scalar
            def _(act):
                act.wait_ge(net.ld_t, 48)
                act.activation(mag[:, :], w[:, :], ACT.Abs, accum_out=part_sum[:, :]).then_inc(s.mag.sem, 1)
                act.wait_ge(s.wT_ps.sem, s.wT_ps.at(0, 1))
                act.activation(wT[:, :], bank[1][:, 0:P], ACT.Copy).then_inc(s.wT.sem, 1)
                with act.Fori(0, B) as i:
                    act.wait_ge(s.y_ready.sem, s.y_ready.at(i, 0))
                    act.activation(xs[:, :], net.xT[:, bass.ds(i * L, L)], ACT.Copy).then_inc(s.xs_ready.sem, 1)

            @block.tensor
            def _(pe):
                pe.wait_ge(s.mag.sem, s.mag.at(0, 1))
                pe.matmul(bank[0][:, 0:1], net.tab("ones"), part_sum[:, :], start=True, stop=True).then_inc(s.mean_ps.sem, 1)
                pe.wait_ge(s.tern.sem, s.tern.at(0, 1))
                pe.transpose(bank[1][:, 0:P], pos[:, :], ident).then_inc(s.wT_ps.sem, 1)
                pe.wait_ge(s.wT.sem, s.wT.at(0, 1))
                with pe.Fori(0, B) as i:
                    pe.wait_ge(s.xs_ready.sem, s.xs_ready.at(i, 1))
                    pe.wait_ge(s.xn_ready.sem, s.xn_ready.at(i, 0))
                    for t in range(TPB):
                        tok = slice(t * P, (t + 1) * P)
                        pe.matmul(bank[2][:, tok], xs[:, tok], wT[:, :], start=True, stop=False)
                        pe.matmul(bank[2][:, tok], net.tab("ones")[0:1, :], bias[:, :], start=False, stop=False)
                        last = pe.matmul(bank[2][:, tok], xs[:, tok], ident, start=False, stop=True)
                    last.then_inc(s.y_ready.sem, 1)

            @block.vector
            def _(dve):
                dve.wait_ge(s.mean_ps.sem, s.mean_ps.at(0, 1))
                v = s.v
                dve.tensor_scalar(delta[:, :], bank[0][:, 0:1], 1.0 / (D * D), 0.7, ALU.mult, ALU.mult)
                dve.tensor_scalar(mdelta[:, :], bank[0][:, 0:1], 1.0 / (D * D), -0.7, ALU.mult, ALU.mult).then_inc(v.sem, 1)
                dve.wait_ge(v.sem, v.at(0, 1))
                dve.tensor_scalar(pos[:, :], w[:, :], delta[:, :], None, ALU.is_gt)
                dve.tensor_scalar(neg[:, :], w[:, :], mdelta[:, :], None, ALU.is_lt).then_inc(v.sem, 1)
                dve.wait_ge(v.sem, v.at(0, 2))
                dve.tensor_tensor(pos[:, :], pos[:, :], neg[:, :], ALU.subtract).then_inc(v.sem, 1)
                dve.wait_ge(v.sem, v.at(0, 3))
                dve.tensor_scalar(pos[:, :], pos[:, :], alpha[:, :], None, ALU.mult).then_inc(s.tern.sem, 1)
                with dve.Fori(0, B) as i:
                    norm_dve(dve, s, n, i, bank[2][:, 0:L].rearrange("p (t d) -> p t d", d=D), turned=False)
    close_stage(nc, net.pool)


def network(nc, io, out):
    at, width = table_layout()
    with ExitStack() as ctx:
        sb = lambda name, shape: ctx.enter_context(nc.sbuf_tensor(name, shape, F32))
        net = Shared()
        net.count = 0

        def name(base):
            net.count += 1
            return f"{base}_{net.count}"
        net.name = name
        net.tabs = sb("tabs", [P, width])
        net.tab = lambda n: net.tabs[:, at[n][0]:at[n][0] + at[n][1]]
        net.xT, net.x_tok = sb("xT", [P, T]), sb("x_tok", [P, T])
        net.neghalf, net.half, net.eps = sb("neghalf", [P, 64]), sb("half", [P, 64]), sb("eps", [P, 64])
        net.bank = [ctx.enter_context(nc.psum_tensor(f"bank{k}", [P, 512], F32)) for k in range(8)]
        sem = lambda name: ctx.enter_context(nc.semaphore(name))
        net.ld_x, net.ld_w, net.ld_moe, net.ld_a, net.out_done = (sem(n) for n in ("ld_x", "ld_w", "ld_moe", "ld_a", "out_done"))
        net.pool = [sem(f"stage_signal_{k}") for k in range(60)]
        net.loads_sp, net.loads_act = [], []
        net.ld_s, net.ld_s_count = sem("ld_s"), 0
        net.xw = sb("x_work", [P, T])
        col = lambda ap: ap.rearrange("(c p) -> p c", p=P)
        small = {}
        for l in range(DEPTH):
            for key, width_ in (("ln_g", 1), ("ln_b", 1), ("b1a", 3), ("b1g", 3), ("b2", 1)):
                small[key, l] = sb(f"{key}_{l}", [P, width_])
            for key, nm in (("ln_g", "L0_ffn_ln_g"), ("ln_b", "L0_ffn_ln_b"), ("b2", "L0_ffn_b2")):
                net.loads_sp.append((small[key, l][:, :], col(io[nm][l])))
            for c, (a0, w) in enumerate(HCH):
                for key, off in (("b1a", 0), ("b1g", HID)):
                    net.loads_sp.append((small[key, l][0:w, c:c + 1], io["L0_ffn_b1"][l, off + a0:off + a0 + w].rearrange("(w o) -> w o", o=1)))
        net.small = lambda key, l: small[key, l][:, :]
        net.w_in, net.w_out, net.w_xproj = sb("w_in", [P, 2 * DIN]), sb("w_out", [P, 2, D]), sb("w_xproj", [P, 2, XP])
        net.conv_w, net.conv_b, net.w_dt = sb("conv_w", [P, 2, NCONV]), sb("conv_b", [P, 2]), sb("w_dt", [1, DIN])
        net.b_dt, net.a_log, net.d_par = sb("b_dt", [P, 2]), sb("a_log", [P, 2, NS]), sb("d_par", [P, 2])
        halves = lambda ap: ap.rearrange("(c p) n -> p c n", p=P)
        net.loads_sp += [(net.w_in[:, :], io["L1_attn_W_in"]), (net.w_out[:, :, :], halves(io["L1_attn_W_out"])),
                         (net.w_xproj[:, :, :], halves(io["L1_attn_W_xproj"])),
                         (net.conv_w[:, :, :], halves(io["L1_attn_conv_w"].rearrange("d o k -> d (o k)"))),
                         (net.conv_b[:, :], col(io["L1_attn_conv_b"])), (net.b_dt[:, :], col(io["L1_attn_b_dt"])),
                         (net.d_par[:, :], col(io["L1_attn_D_param"])), (net.a_log[:, :, :], halves(io["L1_attn_A_log"])),
                         (net.w_dt[:, :], io["L1_attn_w_dt"].rearrange("(o d) -> o d", o=1))]
        net.w_router = sb("w_router", [P, E1])
        net.loads_sp.append((net.w_router[:, :], io["L1_ffn_w_router"]))
        net.moe_w = [sb(f"moe_w{k}", [P, E1, P]) for k in range(3)]
        net.loads_act = [(net.moe_w[k][:, :, :], io[nm].rearrange("e h f -> h e f"))
                         for k, nm in enumerate(("L1_ffn_w_gate", "L1_ffn_w_up", "L1_ffn_w_down"))]
        net.moved, net.stored, net.fetched, net.rows_in, net.zeroed = (sem(k) for k in ("moved", "stored", "fetched", "rows_in", "zeroed"))
        net.slots = [nc.dram_tensor(f"slots{k}", [SLOTS + (k + 1) * T, D], F32, kind="Internal").ap() for k in range(2)]
        net.slots_out = [nc.dram_tensor(f"slots_out{k}", [SLOTS, D], F32, kind="Internal").ap() for k in range(2)]
        net.zero = sb("zero", [P, 512])
        net.loads2, net.loads3 = [], []
        net.ld_w2, net.ld_w3, net.moved2, net.fetched2, net.ld_xi, net.ld_t = (
            sem(k) for k in ("ld_w2", "ld_w3", "moved2", "fetched2", "ld_xi", "ld_t"))
        net.stored2 = [sem(f"stored2_{k}") for k in range(2)]
        net.router2, net.sg, net.su, net.sd = sb("router2", [P, E2]), sb("sg", [P, IS]), sb("su", [P, IS]), sb("sd", [P, IS // P, D])
        net.w_qkv3, net.w_o3 = sb("w_qkv3", [P, 3 * D]), sb("w_o3", [P, D])
        net.zero_ready = 16 * 2 * (SLOTS // 512)
        first_layer = ExitStack()
        fb = lambda name, shape: first_layer.enter_context(nc.sbuf_tensor(name, shape, F32))
        net.wqkv = [fb(f"wqkv{l}", [P, 3 * INNER]) for l in range(DEPTH)]
        net.wo = [fb(f"wo{l}", [P, INNER // P, D]) for l in range(DEPTH)]
        for l in range(DEPTH):
            net.loads_sp += [(net.wqkv[l][:, :], io["L0_ffn_wqkv"][l]),
                             (net.wo[l][:, :, :], io["L0_ffn_wo"][l].rearrange("(c p) d -> p c d", p=P))]
        net.w1 = [fb(f"w1_{l}", [P, 2 * HID]) for l in range(DEPTH)]
        net.w2 = [fb(f"w2_{l}", [P, len(HCH), D]) for l in range(DEPTH)]
        for l in range(DEPTH):
            net.loads_sp.append((net.w1[l][:, :], io["L0_ffn_w1"][l]))
            for c, (a0, w) in enumerate(HCH):
                net.loads_sp.append((net.w2[l][0:w, c, :], io["L0_ffn_w2"][l, a0:a0 + w, :]))
        net.w_ready = 16 * len(net.loads_sp)
        stage_load(nc, net, io)
        stage_recurrence(nc, net, io)
        stage_local_attention(nc, net, io, 0, net.xT, net.xw)
        stage_gated_mlp(nc, net, io, 0, net.xw, False)
        stage_local_attention(nc, net, io, 1, net.xw, net.xw)
        stage_gated_mlp(nc, net, io, 1, net.xw, True)
        first_layer.close()
        with ExitStack() as scope:
            xc, sz = (scope.enter_context(nc.sbuf_tensor(k, [P, 2, T], F32)) for k in ("xc", "silu_z"))
            stage_scan_inputs(nc, net, io, xc, sz)
            stage_scan(nc, net, io, xc, sz)
        stage_switch_experts(nc, net, io)
        second = ExitStack()
        w = second_weights(nc, net, io, second)
        split = lambda ap: ap.rearrange("p (s j) -> p j s", j=NL)
        joined = lambda ap: ap.rearrange("p (j s) -> p j s", j=NL)
        back = lambda ap: ap.rearrange("p (j s) -> p s j", j=NL)
        rows = lambda ap: ap.rearrange("p (s j) -> p s j", j=NL)
        stage_mha(nc, net, w["la"], net.tab("blk32"), net.xT, net.xw, net.loads2 + net.loads3)
        stage_relu_mlp(nc, net, w["lf"], net.xw, False, split, joined)
        stage_mha(nc, net, w["sa"], net.tab("blk8"), net.xw, net.xw)
        stage_relu_mlp(nc, net, w["pf"], net.xw, True, back, rows)
        second.close()
        stage_top2_experts(nc, net, io)
        stage_decayed_attention(nc, net, io)
        stage_ternary(nc, net, io, out)


def second_weights(nc, net, io, scope):
    sb = lambda name, shape: scope.enter_context(nc.sbuf_tensor(name, shape, F32))
    col = lambda ap: ap.rearrange("(c p) -> p c", p=P)
    row = lambda ap: ap.rearrange("(o d) -> o d", o=1)
    pre = "L2_attn_"
    w = {}
    for k in ("la", "sa"):
        w[k] = m = group(q=sb(k + "_q", [P, AH * ADK]), k=sb(k + "_k", [P, AH * ADK]), v=sb(k + "_v", [P, AH * ADK]),
                                   p=sb(k + "_p", [P, AH * ADK // P, D]), pb=sb(k + "_pb", [1, D]), g=sb(k + "_g", [P, 1]), b=sb(k + "_b", [P, 1]))
        for to, nm in ((m.q, "_wqs"), (m.k, "_wks"), (m.v, "_wvs")):
            net.loads2.append((to[:, :].rearrange("d (h k) -> d h k", h=AH), io[pre + k + nm].rearrange("h d k -> d h k")))
        net.loads2 += [(m.p[:, :, :], io[pre + k + "_pw"].rearrange("(c p) d -> p c d", p=P)), (m.pb[:, :], row(io[pre + k + "_pb"]))]
    for k in ("lf", "pf"):
        w[k] = m = group(w1=sb(k + "_w1", [P, DI]), w2=sb(k + "_w2", [P, DI // P, D]), b1=sb(k + "_b1", [P, DI // P]),
                                   b2=sb(k + "_b2", [1, D]), g=sb(k + "_g", [P, 1]), b=sb(k + "_b", [P, 1]))
        net.loads2 += [(m.w1[:, :], io[pre + k + "_w1"]), (m.w2[:, :, :], io[pre + k + "_w2"].rearrange("(c p) d -> p c d", p=P)),
                       (m.b1[:, :], col(io[pre + k + "_b1"])), (m.b2[:, :], row(io[pre + k + "_b2"]))]
    for k, m in w.items():
        net.loads2 += [(m.g[:, :], col(io[pre + k + "_g"])), (m.b[:, :], col(io[pre + k + "_b"]))]
    net.loads2 = [(a, b, net.ld_w2) for a, b in net.loads2]
    net.w2_ready = 16 * len(net.loads2)
    f = "L2_ffn_"
    flat = lambda k: net.moe_w[k][:, :, :].rearrange("p e f -> p (e f)").rearrange("p (e i) -> p e i", e=E2)
    net.loads3 = [(flat(0), io[f + "rg"].rearrange("e h i -> h e i")), (flat(1), io[f + "ru"].rearrange("e h i -> h e i")),
                  (net.moe_w[2][:, :, :], io[f + "rd"].rearrange("e (c p) d -> p (e c) d", p=P)),
                  (net.router2[:, :], io[f + "router_w"].rearrange("e h -> h e")),
                  (net.sg[:, :], io[f + "sg"]), (net.su[:, :], io[f + "su"]),
                  (net.sd[:, :, :], io[f + "sd"].rearrange("(c p) d -> p c d", p=P)),
                  (net.w_qkv3[:, :], io["L3_attn_w_qkv"]), (net.w_o3[:, :], io["L3_attn_w_o"])]
    net.loads3 = [(a, b, net.ld_w3) for a, b in net.loads3]
    net.w3_ready = 16 * len(net.loads3)
    return w


_INS = [
    "L0_attn_x", "L0_attn_ig_w", "L0_attn_ig_b", "L0_attn_ag_w", "L0_attn_ag_b", "L0_attn_a_param",
    "L0_ffn_wqkv", "L0_ffn_q_scale", "L0_ffn_k_scale", "L0_ffn_wo", "L0_ffn_ln_g", "L0_ffn_ln_b", "L0_ffn_w1", "L0_ffn_b1",
    "L0_ffn_w2", "L0_ffn_b2",
    "L1_attn_W_in", "L1_attn_conv_w", "L1_attn_conv_b", "L1_attn_W_xproj", "L1_attn_w_dt", "L1_attn_b_dt", "L1_attn_A_log",
    "L1_attn_D_param", "L1_attn_W_out",
    "L1_ffn_w_router", "L1_ffn_w_gate", "L1_ffn_w_up", "L1_ffn_w_down",
    *(f"L2_attn_{a}_{k}" for a, ks in (("la", "wqs wks wvs pw pb g b"), ("lf", "w1 b1 w2 b2 g b"),
                                      ("sa", "wqs wks wvs pw pb g b"), ("pf", "w1 b1 w2 b2 g b")) for k in ks.split()),
    "L2_ffn_router_w", "L2_ffn_rg", "L2_ffn_ru", "L2_ffn_rd", "L2_ffn_sg", "L2_ffn_su", "L2_ffn_sd",
    "L3_attn_w_qkv", "L3_attn_w_o", "L3_attn_log_xi", "L3_ffn_weight", "L3_ffn_alpha", "L3_ffn_bias",
]


def kernel(**inputs):
    import numpy as _np
    import concourse.bacc as _bacc
    from concourse import mybir as _mybir
    from concourse.bass_utils import run_bass_kernel_spmd as _run

    nc = _bacc.Bacc("TRN2", target_bir_lowering=False, num_devices=1)
    arrays, io = {}, {}
    given = {name: inputs[name] for name in _INS}
    given["tables"] = _np.concatenate(list(tables().values()), axis=1)
    for name, a in given.items():
        a = _np.ascontiguousarray(a)
        arrays[f"in_{name}_dram"] = a
        io[name] = nc.dram_tensor(f"in_{name}_dram", a.shape, _mybir.dt.from_np(a.dtype), kind="ExternalInput").ap()
    out = nc.dram_tensor("out_0_dram", (B, L, D), _mybir.dt.float32, kind="ExternalOutput").ap()
    network(nc, io, out)
    r = _run(nc, [arrays], core_ids=[0])
    return r.results[0]["out_0_dram"]
```

```python
from collections import namedtuple
from contextlib import ExitStack

import numpy as np
import concourse.bass as bass
from concourse import mybir

F32 = mybir.dt.float32
I32 = mybir.dt.int32
BF16 = mybir.dt.bfloat16
ALU = mybir.AluOpType
ACT = mybir.ActivationFunctionType
AX = mybir.AxisListType

P = 128
B, L, D = 8, 256, 128
T = B * L
NT = T // P
TPB = L // P
EPS = 1e-5
NEG = -1e30

WIN, LH, LDH = 64, 8, 64
INNER = LH * LDH
DEPTH = 2
HID = int(D * 4 * 2 / 3)
HCH = [(0, 128), (128, 128), (256, HID - 256)]
QK_SCALE = 8.0
DIN, NS, NCONV = 2 * D, 16, 4
XP = 2 * NS + 1
E1, C1 = 32, (5 * T + 4 * 32 - 1) // (4 * 32)
E2, C2, IR, IS = 8, 5 * T // (4 * 8), 4 * D, 8 * D
SLOTS = E1 * C1
AH, ADK, NL, DI = 16, 64, 32, 512
RH, RDH = 16, 8


def group(**named):
    return namedtuple("Group", named)(**named)


class Signal:
    def __init__(self, sem, per):
        self.sem, self.per = sem, per

    def at(self, i, c):
        return i * self.per + c + 1


def settle(eng, s):
    eng.sem_inc(s.settled.sem, 1)


class Shared:
    pass


def open_stage(nc, pool, spec):
    signals = {}
    for sem, word in zip(pool, spec.split(), strict=False):
        name, per = word.split(":")
        nc.sync.sem_inc(sem, 1)
        signals[name] = Signal(sem, int(per))
    assert len(signals) == len(spec.split())
    nc.all_engine_barrier()
    return group(**signals)


def close_stage(nc, pool):
    nc.all_engine_barrier(sems_to_clear=range(pool[0].num, pool[0].num + len(pool)))


def tables():
    f = np.float32
    out = {"ident": np.eye(P, dtype=f), "ones": np.ones((P, P), f)}
    half = np.arange(0, LDH, 2).astype(f)
    inv = (f(1.0) / f(10000.0) ** (half / f(LDH))).astype(f)
    t = np.arange(L).astype(f)
    fr = np.concatenate([t[:, None] * inv[None]] * 2, -1).astype(f)
    base = ((half + f(0.4 * LDH)) / f(1.4 * LDH)).astype(f)
    power = ((t - L // 2) / f(WIN // 2)).astype(f)
    sc = np.concatenate([base[None] ** power[:, None]] * 2, -1).astype(f)
    sign = np.where(np.arange(LDH) < LDH // 2, f(-1), f(1))
    rope = np.stack([np.cos(fr) * sc, np.sin(fr) * sc * sign, np.cos(fr) / sc, np.sin(fr) / sc * sign], 1)
    out["rope"] = rope.reshape(TPB, P, 4, LDH).transpose(1, 0, 2, 3).astype(f)
    q, k = np.arange(L)[:, None], np.arange(L)[None]
    ok = (k <= q) & (k >= q - WIN) & (k // WIN >= q // WIN - 1)
    by_query = lambda ok: np.where(ok, f(0), f(NEG)).reshape(TPB, P, L).transpose(1, 0, 2)
    by_key = lambda ok: np.concatenate([np.where(ok.T, f(0), f(NEG))[0:P], np.where(ok.T, f(0), f(NEG))[P:, P:]], 1)
    out["lmask"], out["lmaskT"] = by_query(ok), by_key(ok)
    p = np.arange(P)
    out["blk8"] = np.where(p[:, None] % NL // (L // NL) == np.arange(NL)[None] // (L // NL), f(0), f(NEG))
    out["causal"], out["causalT"] = by_query(k <= q), by_key(k <= q)
    out["pos"] = t.reshape(TPB, P).T
    iv = (f(10000.0) ** (-(np.arange(0, RDH, 2).astype(f) / f(RDH)))).astype(f)
    th = (t[:, None] * iv[None]).astype(f)
    out["rcos"] = np.cos(th).reshape(TPB, P, RDH // 2).transpose(1, 0, 2)
    out["rsin"] = np.sin(th).reshape(TPB, P, RDH // 2).transpose(1, 0, 2)
    out["tri"] = (p[:, None] <= p[None]).astype(f)
    out["iota32"] = np.broadcast_to(np.arange(E1) - 64, (P, E1))
    out["trash"] = SLOTS + p[:, None] + P * np.arange(2 * NT)[None]
    return {n: np.ascontiguousarray(a.reshape(P, -1), dtype=f) for n, a in out.items()}


def table_layout():
    at, off = {}, 0
    for n, a in tables().items():
        at[n] = (off, a.shape[1])
        off += a.shape[1]
    return at, off


NORM = "settled:0 y_ready:1 stats:1 agg:1 var_eps:1 rstd:1 xn_ready:1 xnT_ready:1 x_updated:1 kept:1"


def norm_dve(dve, s, n, i, y, turned=True):
    norm_stats(dve, s, n, i, y)
    norm_apply(dve, s, n, i, y, turned)


def norm_stats(dve, s, n, i, y):
    if n.in_psum:
        dve.wait_ge(s.y_ready.sem, s.y_ready.at(i, 1))
    for t in range(TPB):
        last = dve.bn_stats(n.st[:, t, :], y[:, t, :])
    last.then_inc(s.stats.sem, 1)
    dve.wait_ge(s.stats.sem, s.stats.at(i, 1))
    dve.wait_ge(s.rstd.sem, s.rstd.at(i, 0))
    settle(dve, s)
    for t in range(TPB):
        last = dve.bn_aggr(n.mv[:, t, :], n.st[:, t, :])
    last.then_inc(s.agg.sem, 1)


def norm_apply(dve, s, n, i, y, turned=True):
    dve.wait_ge(s.rstd.sem, s.rstd.at(i, 1))
    if turned:
        dve.wait_ge(s.xnT_ready.sem, s.xnT_ready.at(i, 0))
    if n.keep:
        dve.wait_ge(s.kept.sem, s.kept.at(i, 0))
    for t in range(TPB):
        last = dve.tensor_scalar(n.xn[:, t, :], y[:, t, :], n.mv[:, t, 0:1], n.rstd[:, t:t + 1],
                                 ALU.subtract, ALU.mult)
    last.then_inc(s.xn_ready.sem, 1)


def norm_pool(pool, s, n, i):
    norm_rstd(pool, s, n, i)
    if n.keep:
        pool.wait_ge(s.xn_ready.sem, s.xn_ready.at(i, 1))
        settle(pool, s)
        pool.tensor_copy(n.x_tok[:, bass.ds(i * L, L)], n.xn[:, :, :].rearrange("p t d -> p (t d)"))\
            .then_inc(s.kept.sem, 1)


def norm_rstd(pool, s, n, i):
    pool.wait_ge(s.agg.sem, s.agg.at(i, 1))
    pool.tensor_tensor(n.ve[:, :], n.mv[:, :, 1], n.eps[:, 0:TPB], ALU.add).then_inc(s.var_eps.sem, 1)
    pool.wait_ge(s.var_eps.sem, s.var_eps.at(i, 1))
    pool.wait_ge(s.xn_ready.sem, s.xn_ready.at(i, 0))
    pool.tensor_tensor(n.rstd[:, :], n.ve[:, :], n.neghalf[:, 0:TPB], ALU.pow).then_inc(s.rstd.sem, 1)


def norm_pe(pe, s, n, i, psT):
    pe.wait_ge(s.xn_ready.sem, s.xn_ready.at(i, 1))
    for t in range(TPB):
        last = pe.transpose(psT[:, t * P:(t + 1) * P], n.xn[:, t, :], n.ident)
    last.then_inc(s.xnT_ready.sem, 1)


def norm_act(act, s, i, psT, dst, scale=1.0, bias=0.0):
    act.wait_ge(s.xnT_ready.sem, s.xnT_ready.at(i, 1))
    settle(act, s)
    act.activation(dst, psT, ACT.Identity, scale=scale, bias=bias).then_inc(s.x_updated.sem, 1)


def norm_buffers(ctx, nc, net, keep=False, in_psum=True):
    sb = lambda name, shape: ctx.enter_context(nc.sbuf_tensor(net.name(name), shape, F32))
    return group(st=sb("n_st", [P, TPB, 6]), mv=sb("n_mv", [P, TPB, 2]), ve=sb("n_ve", [P, TPB]),
                           rstd=sb("n_rstd", [P, TPB]), xn=sb("n_xn", [P, TPB, D]), neghalf=net.neghalf, eps=net.eps,
                           ident=net.tab("ident"), x_tok=net.x_tok, keep=keep, in_psum=in_psum)


def skewed(eng, turn, behind):
    turn(-1, True, False, False)
    turn(0, True, True, False)
    with eng.Fori(1, B - 1) as i:
        turn(i, True, True, behind)
    turn(B - 1, False, True, behind)
    if behind:
        turn(B, False, False, True)


def stage_load(nc, net, io):
    s = open_stage(nc, net.pool, "xT_ps:4 xT_done:4 zero:1 in16:1 const:1")
    with nc.Block() as block:
        @block.sync
        def _(sp):
            sp.dma_start(net.x_tok[:, :].rearrange("p (t d) -> p t d", d=D),
                         io["L0_attn_x"].rearrange("b (t p) d -> p (b t) d", p=P)).then_inc(net.ld_x, 16)
            sp.dma_start(net.tabs[:, :], io["tables"]).then_inc(net.ld_x, 16)
            with nc.allow_non_contiguous_dma(reason="a few hundred biases, one to a partition"):
                for dst, src in net.loads_sp:
                    sp.dma_start(dst, src).then_inc(net.ld_w, 16)

        @block.gpsimd
        def _(pool):
            pool.memset(net.zero[:, :], 0.0).then_inc(s.zero.sem, 1)
            pool.wait_ge(s.zero.sem, s.zero.at(0, 1))
            for buf in net.slots:
                for k in range(SLOTS // 512):
                    pool.dma_start(buf[k * 512:(k + 1) * 512, :].rearrange("(p r) d -> p (r d)", p=P), net.zero[:, :]).then_inc(net.zeroed, 16)
            pool.wait_ge(net.ld_x, 32)
            for to, of in ((net.ident16, "ident"), (net.lmask16, "lmaskT"), (net.cmask16, "causalT")):
                last = pool.tensor_copy(to[:, :], net.tab(of))
            last.then_inc(s.in16.sem, 1)
            pool.wait_ge(s.in16.sem, s.in16.at(0, 1))
            pool.tensor_tensor(net.pick16[:, :], net.ident16[:, 0:PART], net.ident16[:, PART:2 * PART], ALU.add)
            pool.memset(net.neghalf[:, :], -0.5)
            pool.memset(net.eps[:, :], EPS)
            pool.memset(net.half[:, :], 0.5).then_inc(s.const.sem, 1)

        @block.scalar
        def _(act):
            for dst, src in net.loads_act:
                act.dma_start(dst, src).then_inc(net.ld_moe, 16)
            for g in range(4):
                act.wait_ge(s.xT_ps.sem, s.xT_ps.at(0, g + 1))
                act.activation(net.xT[:, g * 512:(g + 1) * 512], net.bank[g][:, :], ACT.Copy).then_inc(s.xT_done.sem, 1)

        @block.tensor
        def _(pe):
            pe.wait_ge(net.ld_x, 32)
            for g in range(4):
                for t in range(4):
                    k = 4 * g + t
                    last = pe.transpose(net.bank[g][:, t * P:(t + 1) * P], net.x_tok[:, k * P:(k + 1) * P], net.tab("ident"))
                last.then_inc(s.xT_ps.sem, 1)
    close_stage(nc, net.pool)


def stage_recurrence(nc, net, io):
    with ExitStack() as ctx:
        sb = lambda name, shape: ctx.enter_context(nc.sbuf_tensor(net.name(name), shape, F32))
        gx, ga, a, m, p = (sb(n, [P, T]) for n in ("gx", "ga", "a_shift", "mult", "prefix"))
        first, later = sb("first", [P, T]), sb("later", [P, T])
        wi, wa = sb("ig_blocks", [P, P]), sb("ag_blocks", [P, P])
        bi, ba, ap_, t1, t2, c8, c16 = (sb(n, [P, 1]) for n in ("ig_b", "ag_b", "a_par", "t1", "t2", "c8", "c16"))
        z = sb("z", [P, L])
        n = norm_buffers(ctx, nc, net)
        ld = net.ld_a
        s = open_stage(nc, net.pool, "blocks0:1 masks0:1 masks:1 gates_ps:8 gate_x:4 gate_a:4 soft:3 decay:1 decay2:1 "
                       "v:16 root:1 h_ready:1 z_ready:1 z_used:1 " + NORM)
        x3 = lambda ap: ap[:, :].rearrange("p (b t) -> p b t", t=L)
        H, W = io["L0_attn_ig_w"].shape[0:2]
        with nc.Block() as block:
            @block.sync
            def _(sp):
                for dst, name in ((bi, "L0_attn_ig_b"), (ba, "L0_attn_ag_b")):
                    sp.dma_start(dst[:, :], io[name].rearrange("h (w o) -> (h w) o", o=1)).then_inc(ld, 16)
                sp.dma_start(ap_[:, :], io["L0_attn_a_param"].rearrange("(w o) -> w o", o=1)).then_inc(ld, 16)
                sp.wait_ge(s.blocks0.sem, s.blocks0.at(0, 1))
                for dst, name in ((wi, "L0_attn_ig_w"), (wa, "L0_attn_ag_w")):
                    for h in range(H):
                        sp.dma_start(dst[h * W:(h + 1) * W, h * W:(h + 1) * W], io[name][h]).then_inc(ld, 16)

            @block.gpsimd
            def _(pool):
                pool.memset(wi[:, :], 0.0)
                pool.memset(wa[:, :], 0.0).then_inc(s.blocks0.sem, 1)
                pool.memset(first[:, :], 0.0)
                pool.memset(later[:, :], 1.0).then_inc(s.masks0.sem, 1)
                pool.wait_ge(s.masks0.sem, s.masks0.at(0, 1))
                pool.memset(x3(first)[:, :, 0:1], 1.0)
                pool.memset(x3(later)[:, :, 0:1], 0.0)
                pool.memset(x3(a)[:, :, 0:1], 0.0).then_inc(s.masks.sem, 1)
                pool.wait_ge(s.h_ready.sem, s.h_ready.at(0, 1))
                with pool.Fori(0, B) as i:
                    pool.wait_ge(s.z_used.sem, s.z_used.at(i, 0))
                    pool.tensor_copy(z[:, :], gx[:, bass.ds(i * L, L)]).then_inc(s.z_ready.sem, 1)
                    norm_pool(pool, s, n, i)

            @block.tensor
            def _(pe):
                pe.wait_ge(ld, 16 * (3 + 2 * H))
                for j, w in enumerate((wi, wa)):
                    for g in range(4):
                        pe.matmul(net.bank[4 * j + g][:, :], w[:, :], net.xT[:, g * 512:(g + 1) * 512],
                                  start=True, stop=True).then_inc(s.gates_ps.sem, 1)
                pe.wait_ge(s.gate_a.sem, s.gate_a.at(0, 4))
                with pe.Fori(0, B) as i:
                    pe.wait_ge(s.z_ready.sem, s.z_ready.at(i, 1))
                    pe.wait_ge(s.xn_ready.sem, s.xn_ready.at(i, 0))
                    for t in range(TPB):
                        last = pe.transpose(net.bank[0][:, t * P:(t + 1) * P], z[:, t * P:(t + 1) * P], net.tab("ident"))
                    last.then_inc(s.y_ready.sem, 1)
                    pe.wait_ge(s.x_updated.sem, s.x_updated.at(i, 0))
                    norm_pe(pe, s, n, i, net.bank[1][:, 0:L])

            @block.scalar
            def _(act):
                act.wait_ge(ld, 16 * (3 + 2 * H))
                act.activation(t1[:, :], ap_[:, :], ACT.Abs).then_inc(s.soft.sem, 1)
                act.wait_ge(s.soft.sem, s.soft.at(0, 1))
                act.activation(t2[:, :], t1[:, :], ACT.Exp, scale=-1.0).then_inc(s.soft.sem, 1)
                act.wait_ge(s.soft.sem, s.soft.at(0, 2))
                act.activation(t1[:, :], t2[:, :], ACT.Ln, bias=1.0).then_inc(s.soft.sem, 1)
                for j, (dst, bias, done) in enumerate(((ga, ba, s.gate_a), (gx, bi, s.gate_x))):
                    for g in range(4):
                        act.wait_ge(s.gates_ps.sem, s.gates_ps.at(0, 8 if j == 0 else 8))
                        act.activation(dst[:, g * 512:(g + 1) * 512], net.bank[4 * (1 - j) + g][:, :], ACT.Sigmoid,
                                       bias=bias[:, :]).then_inc(done.sem, 1)
                act.wait_ge(s.gate_a.sem, s.gate_a.at(0, 4))
                act.wait_ge(s.v.sem, s.v.at(0, 3))
                act.wait_ge(s.masks.sem, s.masks.at(0, 1))
                act.activation(x3(a)[:, :, 1:L], x3(ga)[:, :, 0:L - 1], ACT.Exp, scale=c8[:, :]).then_inc(s.decay.sem, 1)
                act.activation(m[:, :], ga[:, :], ACT.Exp, scale=c16[:, :]).then_inc(s.decay2.sem, 1)
                act.wait_ge(s.v.sem, s.v.at(0, 6))
                act.activation(m[:, :], m[:, :], ACT.Sqrt).then_inc(s.root.sem, 1)
                with act.Fori(0, B) as i:
                    norm_act(act, s, i, net.bank[1][:, 0:L], net.xT[:, bass.ds(i * L, L)])

            @block.vector
            def _(dve):
                v = s.v
                dve.wait_ge(s.soft.sem, s.soft.at(0, 3))
                dve.scalar_tensor_tensor(t2[:, :], ap_[:, :], 0.0, t1[:, :], ALU.max, ALU.add).then_inc(v.sem, 1)
                dve.wait_ge(v.sem, v.at(0, 1))
                dve.tensor_scalar(c8[:, :], t2[:, :], -8.0, None, ALU.mult).then_inc(v.sem, 1)
                dve.tensor_scalar(c16[:, :], t2[:, :], -16.0, None, ALU.mult).then_inc(v.sem, 1)
                dve.wait_ge(s.gate_x.sem, s.gate_x.at(0, 4))
                dve.tensor_tensor(gx[:, :], gx[:, :], net.xT[:, :], ALU.mult).then_inc(v.sem, 1)
                dve.wait_ge(s.decay2.sem, s.decay2.at(0, 1))
                dve.tensor_scalar(m[:, :], m[:, :], -1.0, 1.0, ALU.mult, ALU.add).then_inc(v.sem, 1)
                dve.wait_ge(v.sem, v.at(0, 5))
                dve.tensor_scalar(m[:, :], m[:, :], 1e-7, None, ALU.max).then_inc(v.sem, 1)
                dve.wait_ge(s.decay.sem, s.decay.at(0, 1))
                dve.tensor_tensor_scan(p[:, :], a[:, :], first[:, :], 0.0, ALU.mult, ALU.add).then_inc(v.sem, 1)
                dve.wait_ge(v.sem, v.at(0, 7))
                dve.tensor_scalar(p[:, :], p[:, :], 1e-7, None, ALU.max).then_inc(v.sem, 1)
                dve.wait_ge(s.root.sem, s.root.at(0, 1))
                dve.tensor_tensor(gx[:, :], gx[:, :], m[:, :], ALU.mult).then_inc(v.sem, 1)
                dve.wait_ge(v.sem, v.at(0, 9))
                dve.reciprocal(m[:, :], p[:, :]).then_inc(v.sem, 1)
                dve.wait_ge(v.sem, v.at(0, 10))
                dve.tensor_tensor(gx[:, :], gx[:, :], m[:, :], ALU.mult).then_inc(v.sem, 1)
                dve.wait_ge(v.sem, v.at(0, 11))
                dve.tensor_tensor_scan(ga[:, :], later[:, :], gx[:, :], 0.0, ALU.mult, ALU.add).then_inc(v.sem, 1)
                dve.wait_ge(v.sem, v.at(0, 12))
                dve.tensor_tensor(gx[:, :], p[:, :], ga[:, :], ALU.mult).then_inc(v.sem, 1)
                dve.wait_ge(v.sem, v.at(0, 13))
                dve.tensor_tensor(gx[:, :], gx[:, :], net.xT[:, :], ALU.add).then_inc(s.h_ready.sem, 1)
                with dve.Fori(0, B) as i:
                    norm_dve(dve, s, n, i, net.bank[0][:, 0:L].rearrange("p (t d) -> p t d", d=D))
                    dve.nop().then_inc(s.z_used.sem, 1)
    close_stage(nc, net.pool)


HPG = 4
PART = 32


def attend_spec(H):
    n = 3 * H // HPG
    return f"settled:0 scored:{H} masked:{2 * H} top16:1 top_parts:1 top_ps:1 top_row:1 shifted:{n} exped:{n} mixed:1 row_inv:1 o_ready:1 "


def attend_buffers(ctx, nc, net, H, dv, scale_by, mask_q, maskT, ring, out, tail):
    sb = lambda name, shape: ctx.enter_context(nc.sbuf_tensor(net.name(name), shape, F32))
    sb16 = lambda name, shape: ctx.enter_context(nc.sbuf_tensor(net.name(name), shape, mybir.dt.bfloat16))
    R = H // HPG
    per = 512 // (dv + 1)
    first = dict(top=H, tail=H + 1, shifted=H + 1 + tail)
    assert (H + 1 + 3 * R + tail) % len(ring) == 0
    return group(H=H, R=R, dv=dv, per=per, scale_by=scale_by, mask_q=mask_q, maskT=maskT, first=first, ring=[net.bank[k] for k in ring],
                 out=[net.bank[k] for k in out], top=sb("top", [P, TPB, H]), top16=sb16("top16", [P, TPB, H]),
                 top_parts=sb("top_parts", [P, TPB, P]), top_row=sb16("minus_top", [P, L]), pick=net.pick16, prob=sb("prob", [P, 3 * R, 512]), inv=sb("inv", [P, TPB * H]))


def scores_pe(pe, s, a, net, i, h, q_at, k_at):
    if h < len(a.ring):
        pe.wait_ge(s.exped.sem, s.exped.at(i, 0))
    else:
        pe.wait_ge(s.masked.sem, s.masked.at(i, 2 * (h - len(a.ring)) + 2))
    to = a.ring[h % len(a.ring)]
    pe.matmul(to[:, 0:P], q_at(h, 0, P), k_at(h, 0, P), start=True, stop=True)
    pe.matmul(to[:, P:P + L], q_at(h, P, P), k_at(h, 0, L), start=True, stop=True).then_inc(s.scored.sem, 1)


def top_pe(pe, s, a, net, i):
    to = a.ring[a.first["top"] % len(a.ring)]
    pe.wait_ge(s.top_parts.sem, s.top_parts.at(i, 1))
    for t in range(TPB):
        last = pe.transpose(to[:, t * P:(t + 1) * P], a.top_parts[:, t, :], net.tab("ident"))
    last.then_inc(s.top_ps.sem, 1)


def tail_bank(pe, s, a, i, m, last):
    k = a.first["tail"] + m
    if last:
        pe.wait_ge(s.exped.sem, s.exped.at(i, 3 * a.R))
    elif k - len(a.ring) < a.H:
        pe.wait_ge(s.masked.sem, s.masked.at(i + 1, 2 * a.H))
    else:
        pe.wait_ge(s.top_row.sem, s.top_row.at(i + 1, 1))
    return a.ring[k % len(a.ring)]


def scores_dve(dve, s, a, net, i):
    for h in range(a.H):
        dve.wait_ge(s.scored.sem, s.scored.at(i, h + 1))
        settle(dve, s)
        for t in range(TPB):
            n = (t + 1) * P
            scores = a.ring[h % len(a.ring)][:, t * P:t * P + n]
            dve.tensor_tensor_reduce(scores, scores, a.mask_q[:, t, 0:n], 1.0, -3e38, ALU.add, ALU.max, a.top[:, t, h:h + 1])\
                .then_inc(s.masked.sem, 1)
    dve.wait_ge(s.masked.sem, s.masked.at(i, 2 * a.H))
    dve.tensor_copy(a.top16[:, :, :], a.top[:, :, :]).then_inc(s.top16.sem, 1)
    dve.wait_ge(s.top16.sem, s.top16.at(i, 1))
    dve.wait_ge(s.top_ps.sem, s.top_ps.at(i, 0))
    dve.tensor_copy(a.top_parts[:, :, 0:a.H], a.top16[:, :, :])
    dve.tensor_tensor(a.top_parts[:, :, PART:PART + a.H], a.top[:, :, :], a.top16[:, :, :], ALU.subtract).then_inc(s.top_parts.sem, 1)


def shifted_pe(pe, s, a, net, i, n, tail, q_at, k_at):
    pick = lambda h: a.pick[:, h:h + 1].to_broadcast([P, P])
    r, part = n // 3, n % 3
    pe.wait_ge(s.top_row.sem, s.top_row.at(i, 1))
    before = a.first["shifted"] + n - len(a.ring) - a.first["tail"]
    if n >= len(a.ring):
        pe.wait_ge(s.exped.sem, s.exped.at(i, n - len(a.ring) + 1))
    elif before >= 0 and tail:
        pe.wait_ge(tail[before].sem, tail[before].at(i, 0))
    to = a.ring[(a.first["shifted"] + n) % len(a.ring)]
    heads = [r + a.R * m for m in range(HPG)]
    kt, lo, w, hs = (1, P, P, heads) if part == 2 else (0, 0, L, heads[2 * part:2 * part + 2])
    mask = a.maskT[:, 0:L] if part < 2 else a.maskT[:, L:L + P]
    pe.matmul(to[:, :], net.ident16[:, :], mask.unsqueeze(1).to_broadcast([P, len(hs), w]), start=True, stop=False)
    for m, h in enumerate(hs):
        pe.matmul(to[:, m * w:(m + 1) * w], k_at(h, kt * P, P), q_at(h, lo, w), start=False, stop=False)
        last = pe.matmul(to[:, m * w:(m + 1) * w], pick(h), a.top_row[:, lo:L], start=False, stop=(m == len(hs) - 1))
    last.then_inc(s.shifted.sem, 1)


def mix_pe(pe, s, a, i, r, v_at):
    pe.wait_ge(s.exped.sem, s.exped.at(i, 3 * r + 3))
    pe.wait_ge(s.o_ready.sem, s.o_ready.at(i, 0))
    for m in range(HPG):
        h = r + a.R * m
        first, later = a.prob[:, 3 * r + m // 2, :], a.prob[:, 3 * r + 2, :]
        for t in range(TPB):
            q = slice((m % 2) * L + t * P, (m % 2) * L + (t + 1) * P)
            u = t * a.H + h
            to = a.out[u // a.per][:, (u % a.per) * (a.dv + 1):(u % a.per + 1) * (a.dv + 1)]
            last = pe.matmul(to, first[:, q], v_at(0, h), start=True, stop=(t == 0))
            if t == 1:
                last = pe.matmul(to, later[:, m * P:(m + 1) * P], v_at(1, h), start=False, stop=True)
    if r == a.R - 1:
        last.then_inc(s.mixed.sem, 1)


def top_row_act(act, s, a, i):
    act.wait_ge(s.top_ps.sem, s.top_ps.at(i, 1))
    n = a.first["top"]
    act.activation(a.top_row[:, :], a.ring[n % len(a.ring)][:, 0:L], ACT.Copy, scale=-1.0).then_inc(s.top_row.sem, 1)


def exp_act(act, s, a, i, n):
    act.wait_ge(s.shifted.sem, s.shifted.at(i, n + 1))
    act.activation(a.prob[:, n, :], a.ring[(a.first["shifted"] + n) % len(a.ring)][:, :], ACT.Exp, scale=a.scale_by).then_inc(s.exped.sem, 1)


def normalise_dve(dve, s, a, i, o, o_read):
    dve.wait_ge(s.mixed.sem, s.mixed.at(i, 1))
    units = [(lo, min(lo + a.per, TPB * a.H)) for lo in range(0, TPB * a.H, a.per)]
    out = [a.out[k][:, 0:(hi - lo) * (a.dv + 1)].rearrange("p (u d) -> p u d", d=a.dv + 1) for k, (lo, hi) in enumerate(units)]
    for (lo, hi), of in zip(units, out, strict=True):
        last = dve.reciprocal(a.inv[:, lo:hi], of[:, :, a.dv])
    last.then_inc(s.row_inv.sem, 1)
    dve.wait_ge(s.row_inv.sem, s.row_inv.at(i, 1))
    dve.wait_ge(o_read.sem, o_read.at(i, 0))
    for (lo, hi), of in zip(units, out, strict=True):
        last = dve.tensor_tensor(o[:, lo:hi, :], of[:, :, 0:a.dv], a.inv[:, lo:hi].unsqueeze(2).to_broadcast([P, hi - lo, a.dv]), ALU.mult)
    last.then_inc(s.o_ready.sem, 1)


def stage_local_attention(nc, net, io, l, src, dst):
    with ExitStack() as ctx:
        sb = lambda name, shape: ctx.enter_context(nc.sbuf_tensor(net.name(name), shape, F32))
        CH = INNER // P
        a = attend_buffers(ctx, nc, net, LH, LDH, QK_SCALE, net.tab("lmask").rearrange("p (t k) -> p t k", t=TPB), net.lmask16,
                           ring=(2, 3, 4), out=(5, 6, 7), tail=3)
        hT = sb("hT", [P, L])
        qsb = sb("scales", [P, 2, LDH])
        rope = sb("rope", [P, TPB, 4, LDH])
        NQ = 2 * TPB
        sq, rc, rs = (sb(n, [P, 2, INNER]) for n in ("squares", "rot_cos", "rot_sin"))
        rot = sb("rotated", [P, NQ, INNER])
        ss, rn = sb("sum_sq", [P, NQ, LH]), sb("inv_norm", [P, NQ, LH])
        qT, kT, v = sb("qT", [P, CH, L]), sb("kT", [P, 2, CH, L]), sb("v", [P, 2, TPB, LH, LDH + 1])
        q16, k16 = (ctx.enter_context(nc.sbuf_tensor(net.name(n), [P, CH, L], mybir.dt.bfloat16)) for n in ("q16", "k16"))
        o, oT = sb("o", [P, TPB, INNER]), sb("oT", [P, CH, L])
        s = open_stage(nc, net.pool, "clear:1 tables:1 h_built:1 front_ps:10 squared:4 sums:4 clipped:4 inv:4 cosd:4 sind:4 added:4 roped:4 "
                       "qkT:4 v_ready:2 oT_ps:2 oT_ready:2 y_ready:1 x_updated:1 " + attend_spec(LH))
        tail = [s.oT_ready, s.oT_ready, s.x_updated]
        tail_at = [a.ring[(a.first["tail"] + k) % len(a.ring)] for k in range(3)]
        ident = net.tab("ident")
        tab4 = net.tab("rope").rearrange("p (t c d) -> p t c d", t=TPB, c=4)
        heads = lambda ap: ap.rearrange("p (h d) -> p h d", d=LDH)
        over_heads = lambda ap: ap.unsqueeze(1).to_broadcast([P, LH, ap.shape[1]])
        HF = LDH // 2
        ITEM = {("q", 0): 0, ("k", 0): 1, ("v", 0): 2, ("q", 1): 3, ("k", 1): 4, ("v", 1): 5, "turned": 6}
        qk_item = lambda m: ITEM["qk"[m % 2], m // 2]
        front_bank = lambda n: net.bank[n % 2]
        with nc.Block() as block:
            @block.sync
            def _(sp):
                for j, nm in enumerate(("L0_ffn_q_scale", "L0_ffn_k_scale")):
                    sp.dma_start(qsb[:, j, :], io[nm][l].partition_broadcast(P)).then_inc(net.ld_s, 16)
                net.ld_s_count += 32

            @block.gpsimd
            def _(pool):
                pool.memset(hT[:, :], 0.0)
                pool.memset(a.top_parts[:, :, :], 0.0)
                pool.memset(v[:, :, :, :, LDH:LDH + 1], 1.0)
                pool.memset(kT[:, :, :, :], 0.0).then_inc(s.clear.sem, 1)
                pool.wait_ge(net.ld_s, net.ld_s_count)
                for j in range(2):
                    qb = lambda x: x.unsqueeze(1).to_broadcast([P, TPB, x.shape[1]])
                    pool.tensor_tensor(rope[:, :, 2 * j, :], tab4[:, :, 2 * j, :], qb(qsb[:, j, :]), ALU.mult)
                    pool.tensor_tensor(rope[:, :, 2 * j + 1, 0:HF], tab4[:, :, 2 * j + 1, 0:HF], qb(qsb[:, j, HF:LDH]), ALU.mult)
                    last = pool.tensor_tensor(rope[:, :, 2 * j + 1, HF:LDH], tab4[:, :, 2 * j + 1, HF:LDH], qb(qsb[:, j, 0:HF]), ALU.mult)
                last.then_inc(s.tables.sem, 1)

                with pool.Fori(0, B) as i:
                    pool.wait_ge(s.front_ps.sem, s.front_ps.at(i, 0))
                    for m in range(NQ):
                        pool.wait_ge(s.sind.sem, s.sind.at(i, m + 1))
                        pool.tensor_tensor(rot[:, m, :], rc[:, m % 2, :], rs[:, m % 2, :], ALU.add).then_inc(s.added.sem, 1)
                        pool.wait_ge(s.clipped.sem, s.clipped.at(i, m + 1))
                        pool.tensor_tensor(rn[:, m, :], ss[:, m, :], net.neghalf[:, 0:LH], ALU.pow).then_inc(s.inv.sem, 1)

            @block.tensor
            def _(pe):
                pe.wait_ge(net.ld_w, net.w_ready)
                w = net.wqkv[l]

                def project(i, n):
                    t, j = n // 3, n % 3
                    if n < 2:
                        pe.wait_ge(s.qkT.sem, s.qkT.at(i, 0))
                    elif (n - 2) % 3 == 2:
                        pe.wait_ge(s.v_ready.sem, s.v_ready.at(i, (n - 2) // 3 + 1))
                    else:
                        m = 2 * ((n - 2) // 3) + (n - 2) % 3
                        pe.wait_ge(s.squared.sem, s.squared.at(i, m + 1))
                        pe.wait_ge(s.sind.sem, s.sind.at(i, m + 1))
                    pe.wait_ge(s.h_built.sem, s.h_built.at(i, 1))
                    pe.matmul(front_bank(n)[:, :], hT[:, t * P:(t + 1) * P], w[:, j * INNER:(j + 1) * INNER], start=True, stop=True)\
                        .then_inc(s.front_ps.sem, 1)

                def turn(i):
                    for m in range(NQ):
                        n = ITEM["turned"] + m
                        if m == 0:
                            pe.wait_ge(s.squared.sem, s.squared.at(i, 4))
                            pe.wait_ge(s.sind.sem, s.sind.at(i, 4))
                        elif m == 1:
                            pe.wait_ge(s.v_ready.sem, s.v_ready.at(i, 2))
                        else:
                            pe.wait_ge(s.qkT.sem, s.qkT.at(i, m - 1))
                        pe.wait_ge(s.roped.sem, s.roped.at(i, m + 1))
                        for c in range(CH):
                            last = pe.transpose(front_bank(n)[:, c * P:(c + 1) * P], rot[:, m, c * P:(c + 1) * P], ident)
                        last.then_inc(s.front_ps.sem, 1)

                row = lambda h: slice(LDH * (h % 2), LDH * (h % 2) + LDH)
                q16_at = lambda h, at, w: q16[row(h), h // 2, at:at + w]
                k16_at = lambda h, at, w: k16[row(h), h // 2, at:at + w]

                def front(i, p):
                    for n in range(6):
                        project(i, n)
                    turn(i)
                    pe.wait_ge(s.qkT.sem, s.qkT.at(i, NQ))
                    for h in range(LH):
                        scores_pe(pe, s, a, net, i, h, q16_at, k16_at)
                    project(i + 1, 0)
                    project(i + 1, 1)
                    top_pe(pe, s, a, net, i)

                def run(i, p, ahead):
                    q_at = lambda h, at, w: qT[:, h // 2, at:at + w]
                    k_at = lambda h, at, w: kT[:, h % 2, h // 2, at:at + w]
                    v_at = lambda kb, h: v[:, p, kb, h, :]
                    pe.wait_ge(s.v_ready.sem, s.v_ready.at(i, TPB))
                    for n in range(6):
                        shifted_pe(pe, s, a, net, i, n, tail, q_at, k_at)
                        if ahead and n in (1, 2, 3, 4):
                            project(i + 1, n + 1)
                    if ahead:
                        turn(i + 1)
                    mix_pe(pe, s, a, i, 0, v_at)
                    if ahead:
                        pe.wait_ge(s.qkT.sem, s.qkT.at(i + 1, NQ))
                    for h in range(LH):
                        if ahead:
                            scores_pe(pe, s, a, net, i + 1, h, q16_at, k16_at)
                        if h == 2:
                            mix_pe(pe, s, a, i, 1, v_at)
                    if ahead == 2:
                        project(i + 2, 0)
                        project(i + 2, 1)
                    if ahead:
                        top_pe(pe, s, a, net, i + 1)
                    for t in range(TPB):
                        to = tail_bank(pe, s, a, i, t, not ahead)
                        pe.wait_ge(s.o_ready.sem, s.o_ready.at(i, 1))
                        for c in range(CH):
                            last = pe.transpose(to[:, c * P:(c + 1) * P], o[:, t, c * P:(c + 1) * P], ident)
                        last.then_inc(s.oT_ps.sem, 1)
                    to = tail_bank(pe, s, a, i, 2, not ahead)
                    pe.wait_ge(s.oT_ready.sem, s.oT_ready.at(i, 2))
                    for c in range(CH):
                        last = pe.matmul(to[:, 0:L], net.wo[l][:, c, :], oT[:, c, :], start=(c == 0), stop=(c == CH - 1))
                    last.then_inc(s.y_ready.sem, 1)

                front(0, 0)
                with pe.Fori(0, B // 2 - 1) as j:
                    run(2 * j, 0, 2)
                    run(2 * j + 1, 1, 2)
                run(B - 2, 0, 1)
                run(B - 1, 1, 0)

            @block.scalar
            def _(act):
                act.wait_ge(s.clear.sem, s.clear.at(0, 1))

                def shift(i):
                    act.wait_ge(s.front_ps.sem, s.front_ps.at(i, 0))
                    act.activation(hT[0:D // 2, :], src[0:D // 2, bass.ds(i * L, L)], ACT.Copy)
                    act.activation(hT[D // 2:D, 1:L], src[D // 2:D, bass.ds(i * L, L - 1)], ACT.Copy).then_inc(s.h_built.sem, 1)

                def square(i, m):
                    n = qk_item(m)
                    act.wait_ge(s.front_ps.sem, s.front_ps.at(i, n + 1))
                    act.wait_ge(s.sums.sem, s.sums.at(i, max(0, m - 1)))
                    act.activation(sq[:, m % 2, :], front_bank(n)[:, :], ACT.Square).then_inc(s.squared.sem, 1)

                def copy_v(i, p, t):
                    n = ITEM["v", t]
                    act.wait_ge(s.front_ps.sem, s.front_ps.at(i, n + 1))
                    act.activation(v[:, p, t, :, 0:LDH], heads(front_bank(n)[:, :]), ACT.Copy).then_inc(s.v_ready.sem, 1)

                def copy_qk(i):
                    for m in range(NQ):
                        t, j = m // 2, m % 2
                        n = ITEM["turned"] + m
                        act.wait_ge(s.front_ps.sem, s.front_ps.at(i, n + 1))
                        of = front_bank(n)[:, :].rearrange("p (c t) -> p c t", t=P)
                        tok = slice(t * P, (t + 1) * P)
                        if j == 0:
                            act.activation(q16[:, :, tok], of, ACT.Copy)
                            act.activation(qT[:, :, tok], of, ACT.Copy).then_inc(s.qkT.sem, 1)
                        else:
                            act.activation(k16[:, :, tok], of, ACT.Copy)
                            act.activation(kT[0:LDH, 0, :, tok], of[0:LDH], ACT.Copy)
                            act.activation(kT[LDH:P, 1, :, tok], of[LDH:P], ACT.Copy).then_inc(s.qkT.sem, 1)

                def front(i, p):
                    shift(i)
                    square(i, 0)
                    square(i, 1)
                    copy_v(i, p, 0)
                    square(i, 2)
                    square(i, 3)
                    copy_v(i, p, 1)
                    copy_qk(i)
                    shift(i + 1)
                    top_row_act(act, s, a, i)
                    square(i + 1, 0)
                    square(i + 1, 1)

                def run(i, p, ahead):
                    for n in range(6):
                        exp_act(act, s, a, i, n)
                        if ahead and n in (1, 2, 3, 4):
                            (lambda: copy_v(i + 1, 1 - p, 0), lambda: square(i + 1, 2), lambda: square(i + 1, 3),
                             lambda: copy_v(i + 1, 1 - p, 1))[n - 1]()
                    if ahead:
                        copy_qk(i + 1)
                    if ahead == 2:
                        shift(i + 2)
                    if ahead:
                        top_row_act(act, s, a, i + 1)
                    if ahead == 2:
                        square(i + 2, 0)
                        square(i + 2, 1)
                    act.wait_ge(s.y_ready.sem, s.y_ready.at(i, 0))
                    for t in range(TPB):
                        act.wait_ge(s.oT_ps.sem, s.oT_ps.at(i, t + 1))
                        act.activation(oT[:, :, t * P:(t + 1) * P], tail_at[t][:, :].rearrange("p (c t) -> p c t", t=P), ACT.Copy)\
                            .then_inc(s.oT_ready.sem, 1)

                front(0, 0)
                with act.Fori(0, B // 2 - 1) as j:
                    run(2 * j, 0, 2)
                    run(2 * j + 1, 1, 2)
                run(B - 2, 0, 1)
                run(B - 1, 1, 0)

            @block.vector
            def _(dve):
                dve.wait_ge(s.tables.sem, s.tables.at(0, 1))

                def rotate(i, m):
                    t, j = m // 2, m % 2
                    n = qk_item(m)
                    dve.wait_ge(s.front_ps.sem, s.front_ps.at(i, n + 1))
                    dve.wait_ge(s.squared.sem, s.squared.at(i, m + 1))
                    dve.wait_ge(s.added.sem, s.added.at(i, max(0, m - 1)))
                    of = heads(front_bank(n)[:, :])
                    dve.tensor_tensor(heads(rc[:, m % 2, :]), of, over_heads(rope[:, t, 2 * j, :]), ALU.mult).then_inc(s.cosd.sem, 1)
                    sin = heads(rs[:, m % 2, :])
                    dve.tensor_tensor(sin[:, :, 0:HF], of[:, :, HF:LDH], over_heads(rope[:, t, 2 * j + 1, 0:HF]), ALU.mult)
                    dve.tensor_tensor(sin[:, :, HF:LDH], of[:, :, 0:HF], over_heads(rope[:, t, 2 * j + 1, HF:LDH]), ALU.mult)\
                        .then_inc(s.sind.sem, 1)
                    dve.tensor_reduce(ss[:, m, :], heads(sq[:, m % 2, :]), AX.X, ALU.add).then_inc(s.sums.sem, 1)
                    dve.wait_ge(s.sums.sem, s.sums.at(i, m + 1))
                    dve.tensor_scalar(ss[:, m, :], ss[:, m, :], 1e-24, None, ALU.max).then_inc(s.clipped.sem, 1)

                def finish(i):
                    for m in range(NQ):
                        dve.wait_ge(s.inv.sem, s.inv.at(i, m + 1))
                        r = heads(rot[:, m, :])
                        dve.tensor_tensor(r, r, rn[:, m, :].unsqueeze(2).to_broadcast([P, LH, LDH]), ALU.mult).then_inc(s.roped.sem, 1)
                    scores_dve(dve, s, a, net, i)

                def front(i, p):
                    for m in range(NQ):
                        rotate(i, m)
                    finish(i)
                    rotate(i + 1, 0)
                    rotate(i + 1, 1)

                def run(i, p, ahead):
                    if ahead:
                        rotate(i + 1, 2)
                        rotate(i + 1, 3)
                        finish(i + 1)
                    normalise_dve(dve, s, a, i, o[:, :, :].rearrange("p t (h d) -> p (t h) d", h=LH), s.oT_ps)
                    if ahead == 2:
                        rotate(i + 2, 0)
                        rotate(i + 2, 1)
                    dve.wait_ge(s.y_ready.sem, s.y_ready.at(i, 1))
                    dve.tensor_tensor(dst[:, bass.ds(i * L, L)], tail_at[2][:, 0:L], src[:, bass.ds(i * L, L)], ALU.add)\
                        .then_inc(s.x_updated.sem, 1)

                front(0, 0)
                with dve.Fori(0, B // 2 - 1) as j:
                    run(2 * j, 0, 2)
                    run(2 * j + 1, 1, 2)
                run(B - 2, 0, 1)
                run(B - 1, 1, 0)
    close_stage(nc, net.pool)


def part(s, prefix):
    return group(**{k[len(prefix):]: v for k, v in s._asdict().items() if k.startswith(prefix)})


def prefixed(prefix, spec):
    return " ".join(prefix + w for w in spec.split()) + " "


def stage_gated_mlp(nc, net, io, l, x, final):
    with ExitStack() as ctx:
        sb = lambda name, shape: ctx.enter_context(nc.sbuf_tensor(net.name(name), shape, F32))
        n, nf = norm_buffers(ctx, nc, net), norm_buffers(ctx, nc, net)
        hT, hn, z, z1 = sb("hT", [P, L]), sb("hn", [P, T]), sb("z", [P, L]), sb("z1", [P, L])
        gate, u = sb("gate", [P, len(HCH), L]), sb("u", [P, len(HCH), L])
        s = open_stage(nc, net.pool, "h_clear:1 h_built:1 ag_ps:3 gelu:3 u_ready:3 mlp_ps:1 sum1:1 sum2:1 "
                       + NORM + " " + prefixed("f_", NORM))
        f = part(s, "f_")
        ident, sm = net.tab("ident"), net.small
        h_bank, hnT_bank, out_bank, z_bank, zT_bank = (net.bank[k] for k in (0, 1, 5, 6, 7))
        ag_bank = lambda c: net.bank[2 + c]
        tiles = lambda bank: bank[:, 0:L].rearrange("p (t d) -> p t d", d=D)
        with nc.Block() as block:
            @block.gpsimd
            def _(pool):
                pool.memset(hT[:, :], 0.0).then_inc(s.h_clear.sem, 1)

                def turn(i, ahead, own, behind):
                    if ahead:
                        norm_pool(pool, s, n, i + 1)
                    if behind:
                        norm_pool(pool, f, nf, i - 1)
                skewed(pool, turn, final)

            @block.scalar
            def _(act):
                act.wait_ge(net.ld_w, net.w_ready)
                act.wait_ge(s.h_clear.sem, s.h_clear.at(0, 1))

                def turn(i, ahead, own, behind):
                    if ahead:
                        act.wait_ge(s.y_ready.sem, s.y_ready.at(i + 1, 0))
                        act.activation(hT[0:D // 2, :], x[0:D // 2, bass.ds((i + 1) * L, L)], ACT.Copy)
                        act.activation(hT[D // 2:D, 1:L], x[D // 2:D, bass.ds((i + 1) * L, L - 1)], ACT.Copy).then_inc(s.h_built.sem, 1)
                    if own:
                        act.wait_ge(s.u_ready.sem, s.u_ready.at(i, 0))
                        for c, (at, w) in enumerate(HCH):
                            act.wait_ge(s.ag_ps.sem, s.ag_ps.at(i, c + 1))
                            act.activation(gate[0:w, c, :], ag_bank(c)[0:w, L:2 * L], ACT.Gelu, bias=sm("b1g", l)[0:w, c:c + 1])\
                                .then_inc(s.gelu.sem, 1)
                    if ahead:
                        norm_act(act, s, i + 1, hnT_bank[:, 0:L], hn[:, bass.ds((i + 1) * L, L)], sm("ln_g", l), sm("ln_b", l))
                    if behind:
                        norm_act(act, f, i - 1, zT_bank[:, 0:L], net.xT[:, bass.ds((i - 1) * L, L)])
                skewed(act, turn, final)

            @block.tensor
            def _(pe):
                pe.wait_ge(net.ld_w, net.w_ready)

                def turn(i, ahead, own, behind):
                    if ahead:
                        pe.wait_ge(s.h_built.sem, s.h_built.at(i + 1, 1))
                        pe.wait_ge(s.xn_ready.sem, s.xn_ready.at(i + 1, 0))
                        for t in range(TPB):
                            last = pe.transpose(h_bank[:, t * P:(t + 1) * P], hT[:, t * P:(t + 1) * P], ident)
                        last.then_inc(s.y_ready.sem, 1)
                    if behind:
                        pe.wait_ge(s.sum2.sem, s.sum2.at(i - 1, 1))
                        pe.wait_ge(f.xn_ready.sem, f.xn_ready.at(i - 1, 0))
                        for t in range(TPB):
                            last = pe.transpose(z_bank[:, t * P:(t + 1) * P], z[:, t * P:(t + 1) * P], ident)
                        last.then_inc(f.y_ready.sem, 1)
                    if own:
                        pe.wait_ge(s.x_updated.sem, s.x_updated.at(i, 1))
                        pe.wait_ge(s.u_ready.sem, s.u_ready.at(i, 0))
                        for c, (at, w) in enumerate(HCH):
                            for j in range(2):
                                last = pe.matmul(ag_bank(c)[0:w, j * L:(j + 1) * L], net.w1[l][:, j * HID + at:j * HID + at + w],
                                                 hn[:, bass.ds(i * L, L)], start=True, stop=True)
                            last.then_inc(s.ag_ps.sem, 1)
                    if ahead:
                        pe.wait_ge(s.x_updated.sem, s.x_updated.at(i + 1, 0))
                        norm_pe(pe, s, n, i + 1, hnT_bank[:, 0:L])
                    if own:
                        pe.wait_ge(s.sum1.sem, s.sum1.at(i, 0))
                        pe.wait_ge(s.u_ready.sem, s.u_ready.at(i, len(HCH)))
                        for c, (at, w) in enumerate(HCH):
                            last = pe.matmul(out_bank[:, 0:L], net.w2[l][0:w, c, :], u[0:w, c, :], start=(c == 0), stop=(c == len(HCH) - 1))
                        last.then_inc(s.mlp_ps.sem, 1)
                    if behind:
                        pe.wait_ge(f.x_updated.sem, f.x_updated.at(i - 1, 0))
                        norm_pe(pe, f, nf, i - 1, zT_bank[:, 0:L])
                skewed(pe, turn, final)

            @block.vector
            def _(dve):
                dve.wait_ge(net.ld_w, net.w_ready)

                def turn(i, ahead, own, behind):
                    if ahead:
                        norm_stats(dve, s, n, i + 1, tiles(h_bank))
                    if behind:
                        norm_stats(dve, f, nf, i - 1, tiles(z_bank))
                    if own:
                        dve.wait_ge(s.mlp_ps.sem, s.mlp_ps.at(i, 0))
                    for c, (at, w) in enumerate(HCH):
                        if own:
                            dve.wait_ge(s.gelu.sem, s.gelu.at(i, c + 1))
                            dve.scalar_tensor_tensor(u[0:w, c, :], ag_bank(c)[0:w, 0:L], sm("b1a", l)[0:w, c:c + 1], gate[0:w, c, :],
                                                     ALU.add, ALU.mult).then_inc(s.u_ready.sem, 1)
                        if ahead and c == 0:
                            norm_apply(dve, s, n, i + 1, tiles(h_bank))
                    if behind:
                        norm_apply(dve, f, nf, i - 1, tiles(z_bank))
                    if own:
                        dve.wait_ge(s.mlp_ps.sem, s.mlp_ps.at(i, 1))
                        dst = z1[:, :] if final else x[:, bass.ds(i * L, L)]
                        dve.scalar_tensor_tensor(dst, out_bank[:, 0:L], sm("b2", l), x[:, bass.ds(i * L, L)], ALU.add, ALU.add)\
                            .then_inc(s.sum1.sem, 1)
                    if own and final:
                        dve.wait_ge(s.sum1.sem, s.sum1.at(i, 1))
                        dve.wait_ge(f.y_ready.sem, f.y_ready.at(i, 0))
                        dve.tensor_tensor(z[:, :], z1[:, :], net.xT[:, bass.ds(i * L, L)], ALU.add).then_inc(s.sum2.sem, 1)
                skewed(dve, turn, final)
    close_stage(nc, net.pool)


def stage_scan_inputs(nc, net, io, xc, sz):
    with ExitStack() as ctx:
        sb = lambda name, shape: ctx.enter_context(nc.sbuf_tensor(net.name(name), shape, F32))
        PAD = NCONV - 1
        xp, acc = sb("x_padded", [P, 2, PAD + L]), sb("conv", [P, 2, L])
        s = open_stage(nc, net.pool, "clear:1 xz:4 xp_ready:2 sz_ready:2 taps:8 xc_ready:2")
        with nc.Block() as block:
            @block.gpsimd
            def _(pool):
                pool.memset(xp[:, :, :], 0.0).then_inc(s.clear.sem, 1)

            @block.tensor
            def _(pe):
                pe.wait_ge(net.ld_w, net.w_ready)
                with pe.Fori(0, B) as i:
                    for m in range(4):
                        read = s.xp_ready if m < 2 else s.sz_ready
                        pe.wait_ge(read.sem, read.at(i, 0))
                        pe.matmul(net.bank[m][:, 0:L], net.w_in[:, m * P:(m + 1) * P], net.xT[:, bass.ds(i * L, L)],
                                  start=True, stop=True).then_inc(s.xz.sem, 1)

            @block.scalar
            def _(act):
                act.wait_ge(s.clear.sem, s.clear.at(0, 1))
                with act.Fori(0, B) as i:
                    for c in range(2):
                        act.wait_ge(s.xz.sem, s.xz.at(i, c + 1))
                        act.wait_ge(s.taps.sem, s.taps.at(i, 0))
                        act.activation(xp[:, c, PAD:PAD + L], net.bank[c][:, 0:L], ACT.Copy).then_inc(s.xp_ready.sem, 1)
                    for c in range(2):
                        act.wait_ge(s.xz.sem, s.xz.at(i, c + 3))
                        act.activation(sz[:, c, bass.ds(i * L, L)], net.bank[2 + c][:, 0:L], ACT.Silu).then_inc(s.sz_ready.sem, 1)
                    for c in range(2):
                        act.wait_ge(s.taps.sem, s.taps.at(i, 4 * c + 4))
                        act.activation(xc[:, c, bass.ds(i * L, L)], acc[:, c, :], ACT.Silu).then_inc(s.xc_ready.sem, 1)

            @block.vector
            def _(dve):
                dve.wait_ge(net.ld_w, net.w_ready)
                with dve.Fori(0, B) as i:
                    dve.wait_ge(s.xc_ready.sem, s.xc_ready.at(i, 0))
                    for c in range(2):
                        dve.wait_ge(s.xp_ready.sem, s.xp_ready.at(i, c + 1))
                        for j in range(NCONV):
                            tap = net.conv_w[:, c, j:j + 1]
                            if j == 0:
                                dve.tensor_scalar(acc[:, c, :], xp[:, c, 0:L], tap, net.conv_b[:, c:c + 1], ALU.mult, ALU.add)\
                                    .then_inc(s.taps.sem, 1)
                            else:
                                dve.wait_ge(s.taps.sem, s.taps.at(i, 4 * c + j))
                                dve.scalar_tensor_tensor(acc[:, c, :], xp[:, c, j:j + L], tap, acc[:, c, :], ALU.mult, ALU.add)\
                                    .then_inc(s.taps.sem, 1)
    close_stage(nc, net.pool)


def stage_scan(nc, net, io, xc, sz):
    with ExitStack() as ctx:
        sb = lambda name, shape, dt=F32: ctx.enter_context(nc.sbuf_tensor(net.name(name), shape, dt))
        R = 4
        G = 512
        PARTS = 3
        LAG = 3
        n = norm_buffers(ctx, nc, net, keep=True)
        xs, dt_row = sb("xs", [P, L]), sb("dt_row", [1, 2, G])
        w_wide = sb("w_wide", [P, 2, P])
        bc = sb("bc_parts", [P, T], BF16)
        high, mid = sb("high", [P, 2, G], BF16), sb("mid", [P, 2, G], BF16)
        sel = sb("select", [P, 2 * NS], BF16)
        delta, dx, y1, y2 = sb("delta", [P, 2, T]), sb("delta_x", [P, 2, T]), sb("y1", [P, 2, L]), sb("y2", [P, 2, L])
        dA, dB, h = (sb(k, [P, R, 2, L]) for k in ("decay", "inject", "state"))
        b_rows = sb("b_rows", [P, R, L])
        hc = net.xw[:, 0:R * 2 * L].rearrange("p (r c t) -> p r c t", r=R, c=2)
        e1, top = (dB[:, 2 * k:2 * k + 2, :, :].rearrange("p r c t -> p (r c t)").rearrange("p (c t) -> p c t", c=2) for k in range(2))
        rest1, rest2 = (h[:, 2 * k:2 * k + 2, :, :].rearrange("p r c t -> p (r c t)").rearrange("p (b t) -> p b t", b=2) for k in range(2))
        a_neg, a_exp = sb("a_neg", [P, 2, NS]), sb("a_exp", [P, 2, NS])
        groups = T // G
        s = open_stage(nc, net.pool, f"clear:1 wide0:1 wide:1 sel:2 a_ready:1 a_exp:1 ssm_ps:{groups} dt_row:{groups} high:{groups} rest1:{groups} "
                       f"mid:{groups} rest2:{groups} parts:{groups} dt_ps:{groups} tail:{3 * groups} top:{groups} delta_ready:{groups} dx_ready:{groups} "
                       f"xs_ready:1 bc_ps:{NS} b_ready:{NS} decay:{2 * NS} inject:{NS} state:{NS} readout:{NS} summed:{NS} y1_ready:2 y2_ready:1 " + NORM)
        bank, ident = net.bank, net.tab("ident")
        row = lambda k: slice(2 * NS * k, 2 * NS * (k + 1))
        pick = lambda k: sel[:, k:k + 1].to_broadcast([P, P])
        flat = lambda ap: ap.rearrange("p c t -> p (c t)")
        both = lambda ap: ap.unsqueeze(1).to_broadcast([P, 2, L])
        bc_bank = lambda k: bank[2 + k % R]
        ssm_bank = lambda g: bank[g % 2]
        dt_bank = lambda g, c: bank[2 + 2 * (g % 2) + c]
        sum_bank, y_bank = bank[6], bank[7]
        y = y_bank[:, 0:L].rearrange("p (t d) -> p t d", d=D)
        group_of = lambda g: slice(g * G, (g + 1) * G)
        with nc.Block() as block:
            @block.gpsimd
            def _(pool):
                pool.memset(w_wide[:, :, :], 0.0).then_inc(s.wide0.sem, 1)
                pool.memset(bc[:, :], 0.0)
                pool.memset(dA[:, :, :, :], 0.0).then_inc(s.clear.sem, 1)
                pool.tensor_tensor(sel[:, :], net.ident16[:, row(1)], net.ident16[:, row(2)], ALU.add).then_inc(s.sel.sem, 1)
                pool.wait_ge(s.sel.sem, s.sel.at(0, 1))
                pool.tensor_tensor(sel[:, :], sel[:, :], net.ident16[:, row(3)], ALU.add).then_inc(s.sel.sem, 1)
                pool.wait_ge(s.dx_ready.sem, s.dx_ready.at(0, groups))

                def batch(i, behind):
                    for k in range(NS):
                        if behind or k >= R:
                            pool.wait_ge(s.state.sem, s.state.at(i, k - R + 1))
                        pool.wait_ge(s.b_ready.sem, s.b_ready.at(i, k + 1))
                        settle(pool, s)
                        pool.tensor_tensor(dB[:, k % R, :, :], dx[:, :, bass.ds(i * L, L)], both(b_rows[:, k % R, :]), ALU.mult)\
                            .then_inc(s.inject.sem, 1)
                        if behind and k == 9:
                            norm_rstd(pool, s, n, i - 1)

                batch(0, False)
                with pool.Fori(1, B) as i:
                    batch(i, True)
                norm_rstd(pool, s, n, B - 1)

            @block.tensor
            def _(pe):
                pe.wait_ge(net.ld_w, net.w_ready)
                pe.wait_ge(s.wide.sem, s.wide.at(0, 1))

                def steps(g):
                    pe.wait_ge(s.dt_row.sem, s.dt_row.at(0, g + 1))
                    if g >= 2:
                        pe.wait_ge(s.top.sem, s.top.at(0, g - 1))
                        pe.wait_ge(s.tail.sem, s.tail.at(0, 3 * (g - 2) + 1))
                    for c in range(2):
                        last = pe.matmul(dt_bank(g, c)[:, :], net.w_dt[:, c * P:(c + 1) * P], dt_row[:, g % 2, :], start=True, stop=True)
                    last.then_inc(s.dt_ps.sem, 1)

                for g in range(groups):
                    if g >= 2:
                        pe.wait_ge(s.rest1.sem, s.rest1.at(0, g - 1))
                        pe.wait_ge(s.parts.sem, s.parts.at(0, g - 1))
                    for c in range(2):
                        last = pe.matmul(ssm_bank(g)[:, :], w_wide[:, c, :], xc[:, c, group_of(g)], start=(c == 0), stop=(c == 1))
                    last.then_inc(s.ssm_ps.sem, 1)
                    if g >= 1:
                        steps(g - 1)
                steps(groups - 1)
                pe.wait_ge(s.parts.sem, s.parts.at(0, groups))
                pe.wait_ge(s.sel.sem, s.sel.at(0, 2))
                pe.wait_ge(s.top.sem, s.top.at(0, groups))
                pe.wait_ge(s.tail.sem, s.tail.at(0, 3 * groups))

                def add(i, m):
                    pe.wait_ge(s.readout.sem, s.readout.at(i, m + 1))
                    if m == 0:
                        pe.wait_ge(s.y1_ready.sem, s.y1_ready.at(i, 0))
                    pe.matmul(sum_bank[:, :], ident, flat(hc[:, m % R, :, :]), start=(m == 0), stop=(m % NS == NS - 1))\
                        .then_inc(s.summed.sem, 1)

                def project(i):
                    pe.wait_ge(s.y2_ready.sem, s.y2_ready.at(i, 1))
                    pe.wait_ge(s.xs_ready.sem, s.xs_ready.at(i, 1))
                    pe.wait_ge(s.x_updated.sem, s.x_updated.at(i, 0))
                    for t in range(TPB):
                        tok = slice(t * P, (t + 1) * P)
                        for c in range(2):
                            pe.matmul(y_bank[:, tok], y2[:, c, tok], net.w_out[:, c, :], start=(c == 0), stop=False)
                        last = pe.matmul(y_bank[:, tok], xs[:, tok], ident, start=False, stop=True)
                    last.then_inc(s.y_ready.sem, 1)

                def batch(i, behind):
                    for k in range(NS):
                        if behind or k >= R:
                            pe.wait_ge(s.readout.sem, s.readout.at(i, k - R + 1))
                        tok = bass.ds(i * L, L)
                        pe.matmul(bc_bank(k)[:, 0:L], pick(k), bc[:, tok], start=True, stop=True)
                        pe.matmul(bc_bank(k)[:, L:2 * L], pick(NS + k), bc[:, tok], start=True, stop=True).then_inc(s.bc_ps.sem, 1)
                        if behind or k >= LAG:
                            add(i, k - LAG)
                        if behind and k == 7:
                            project(i - 1)
                        if behind and k == 13:
                            norm_pe(pe, s, n, i - 1, y_bank[:, L:2 * L])

                batch(0, False)
                with pe.Fori(1, B) as i:
                    batch(i, True)
                for m in range(NS - LAG, NS):
                    add(B - 1, m)
                project(B - 1)
                norm_pe(pe, s, n, B - 1, y_bank[:, L:2 * L])

            @block.scalar
            def _(act):
                act.wait_ge(net.ld_w, net.w_ready)
                act.wait_ge(s.clear.sem, s.clear.at(0, 1))
                act.activation(a_exp[:, :, :], net.a_log[:, :, :], ACT.Exp).then_inc(s.a_exp.sem, 1)

                def split(g):
                    b = g % 2
                    act.wait_ge(s.ssm_ps.sem, s.ssm_ps.at(0, g + 1))
                    if g >= 2:
                        act.wait_ge(s.dt_ps.sem, s.dt_ps.at(0, g - 1))
                        act.wait_ge(s.rest1.sem, s.rest1.at(0, g - 1))
                        act.wait_ge(s.rest2.sem, s.rest2.at(0, g - 1))
                    act.activation(dt_row[:, b, :], ssm_bank(g)[0:1, :], ACT.Copy).then_inc(s.dt_row.sem, 1)
                    act.activation(high[:, b, :], ssm_bank(g)[:, :], ACT.Copy).then_inc(s.high.sem, 1)
                    act.wait_ge(s.high.sem, s.high.at(0, g + 1))
                    act.activation(bc[row(1), group_of(g)], high[row(1), b, :], ACT.Copy)
                    act.wait_ge(s.rest1.sem, s.rest1.at(0, g + 1))
                    act.activation(mid[:, b, :], rest1[:, b, :], ACT.Copy).then_inc(s.mid.sem, 1)
                    act.activation(bc[row(2), group_of(g)], rest1[row(2), b, :], ACT.Copy)
                    act.wait_ge(s.rest2.sem, s.rest2.at(0, g + 1))
                    act.activation(bc[row(3), group_of(g)], rest2[row(3), b, :], ACT.Copy).then_inc(s.parts.sem, 1)

                def soften(g):
                    act.wait_ge(s.dt_ps.sem, s.dt_ps.at(0, g + 1))
                    if g >= 1:
                        act.wait_ge(s.delta_ready.sem, s.delta_ready.at(0, g))
                    for c in range(2):
                        last = act.activation(e1[:, c, :], dt_bank(g, c)[:, :], ACT.Abs, bias=net.b_dt[:, c:c + 1])
                    last.then_inc(s.tail.sem, 1)
                    act.wait_ge(s.tail.sem, s.tail.at(0, 3 * g + 1))
                    act.activation(e1[:, :, :], e1[:, :, :], ACT.Exp, scale=-1.0).then_inc(s.tail.sem, 1)
                    act.wait_ge(s.tail.sem, s.tail.at(0, 3 * g + 2))
                    act.activation(e1[:, :, :], e1[:, :, :], ACT.Ln, bias=1.0).then_inc(s.tail.sem, 1)

                for g in range(groups):
                    split(g)
                    if g >= 1:
                        soften(g - 1)
                soften(groups - 1)
                act.wait_ge(s.a_ready.sem, s.a_ready.at(0, 1))
                act.wait_ge(s.delta_ready.sem, s.delta_ready.at(0, groups))

                def keep(i):
                    norm_act(act, s, i, y_bank[:, L:2 * L], net.xT[:, bass.ds(i * L, L)])
                    act.activation(n.x_tok[:, bass.ds(i * L, L)], n.xn[:, :, :].rearrange("p t d -> p (t d)"), ACT.Copy).then_inc(s.kept.sem, 1)

                def batch(i, behind):
                    for k in range(NS):
                        if behind or k >= R:
                            act.wait_ge(s.state.sem, s.state.at(i, k - R + 1))
                        act.wait_ge(s.bc_ps.sem, s.bc_ps.at(i, k + 1))
                        act.activation(b_rows[:, k % R, :], bc_bank(k)[:, 0:L], ACT.Copy).then_inc(s.b_ready.sem, 1)
                        for c in range(2):
                            act.activation(dA[:, k % R, c, 1:L], delta[:, c, bass.ds(i * L + 1, L - 1)], ACT.Exp, scale=a_neg[:, c, k:k + 1])\
                                .then_inc(s.decay.sem, 1)
                        if k == 12:
                            act.wait_ge(s.y_ready.sem, s.y_ready.at(i, 0))
                            settle(act, s)
                            act.activation(xs[:, :], net.xT[:, bass.ds(i * L, L)], ACT.Copy).then_inc(s.xs_ready.sem, 1)
                        if behind and k == NS - 1:
                            keep(i - 1)

                batch(0, False)
                with act.Fori(1, B) as i:
                    batch(i, True)
                keep(B - 1)

            @block.vector
            def _(dve):
                dve.wait_ge(net.ld_w, net.w_ready)
                dve.wait_ge(s.wide0.sem, s.wide0.at(0, 1))
                dve.tensor_copy(w_wide[:, :, 0:1], net.w_xproj[:, :, 0:1])
                for k in range(PARTS):
                    last = dve.tensor_copy(w_wide[:, :, row(1 + k)], net.w_xproj[:, :, 1:XP])
                last.then_inc(s.wide.sem, 1)
                dve.wait_ge(s.a_exp.sem, s.a_exp.at(0, 1))
                dve.tensor_scalar(a_neg[:, :, :], a_exp[:, :, :], -1.0, None, ALU.mult).then_inc(s.a_ready.sem, 1)

                def split(g):
                    b = g % 2
                    dve.wait_ge(s.high.sem, s.high.at(0, g + 1))
                    if g >= 2:
                        dve.wait_ge(s.parts.sem, s.parts.at(0, g - 1))
                    dve.tensor_tensor(rest1[:, b, :], ssm_bank(g)[:, :], high[:, b, :], ALU.subtract).then_inc(s.rest1.sem, 1)
                    dve.wait_ge(s.rest1.sem, s.rest1.at(0, g + 1))
                    dve.wait_ge(s.mid.sem, s.mid.at(0, g + 1))
                    dve.tensor_tensor(rest2[:, b, :], rest1[:, b, :], mid[:, b, :], ALU.subtract).then_inc(s.rest2.sem, 1)

                def soften(g):
                    dve.wait_ge(s.tail.sem, s.tail.at(0, 3 * g + 1))
                    for c in range(2):
                        last = dve.tensor_scalar(top[:, c, :], dt_bank(g, c)[:, :], net.b_dt[:, c:c + 1], 0.0, ALU.add, ALU.max)
                    last.then_inc(s.top.sem, 1)
                    dve.wait_ge(s.top.sem, s.top.at(0, g + 1))
                    dve.wait_ge(s.tail.sem, s.tail.at(0, 3 * g + 3))
                    dve.tensor_tensor(delta[:, :, group_of(g)], top[:, :, :], e1[:, :, :], ALU.add).then_inc(s.delta_ready.sem, 1)
                    dve.wait_ge(s.delta_ready.sem, s.delta_ready.at(0, g + 1))
                    dve.tensor_tensor(dx[:, :, group_of(g)], delta[:, :, group_of(g)], xc[:, :, group_of(g)], ALU.mult).then_inc(s.dx_ready.sem, 1)

                for g in range(groups):
                    split(g)
                    if g >= 1:
                        soften(g - 1)
                soften(groups - 1)

                def scan(i, m):
                    dve.wait_ge(s.inject.sem, s.inject.at(i, m + 1))
                    dve.wait_ge(s.decay.sem, s.decay.at(i, 2 * m + 2))
                    dve.tensor_tensor_scan(flat(h[:, m % R, :, :]), flat(dA[:, m % R, :, :]), flat(dB[:, m % R, :, :]), 0.0, ALU.mult, ALU.add)\
                        .then_inc(s.state.sem, 1)

                def read(i, m, behind=True):
                    dve.wait_ge(s.state.sem, s.state.at(i, m + 1))
                    if behind or m >= R:
                        dve.wait_ge(s.summed.sem, s.summed.at(i, m - R + 1))
                    dve.tensor_tensor(hc[:, m % R, :, :], h[:, m % R, :, :], both(bc_bank(m)[:, L:2 * L]), ALU.mult).then_inc(s.readout.sem, 1)

                def skip(i):
                    dve.wait_ge(s.summed.sem, s.summed.at(i, NS))
                    for c in range(2):
                        dve.scalar_tensor_tensor(y1[:, c, :], xc[:, c, bass.ds(i * L, L)], net.d_par[:, c:c + 1], sum_bank[:, c * L:(c + 1) * L],
                                                 ALU.mult, ALU.add).then_inc(s.y1_ready.sem, 1)

                def gate(i):
                    dve.wait_ge(s.y1_ready.sem, s.y1_ready.at(i, 2))
                    dve.wait_ge(s.y_ready.sem, s.y_ready.at(i, 0))
                    dve.tensor_tensor(y2[:, :, :], y1[:, :, :], sz[:, :, bass.ds(i * L, L)], ALU.mult).then_inc(s.y2_ready.sem, 1)

                def batch(i, behind):
                    for k in range(NS):
                        if behind or k >= 1:
                            scan(i, k - 1)
                        if behind or k >= 2:
                            read(i, k - 2, behind)
                        if behind and k == 2:
                            skip(i - 1)
                        if behind and k == 3:
                            gate(i - 1)
                        if behind and k == 8:
                            norm_stats(dve, s, n, i - 1, y)
                        if behind and k == 11:
                            norm_apply(dve, s, n, i - 1, y)

                batch(0, False)
                with dve.Fori(1, B) as i:
                    batch(i, True)
                scan(B - 1, NS - 1)
                read(B - 1, NS - 2)
                read(B - 1, NS - 1)
                skip(B - 1)
                gate(B - 1)
                norm_dve(dve, s, n, B - 1, y)
    close_stage(nc, net.pool)


def choose_first(dve, link, probs, iota, best, eq, index, hot, n):
    wide = lambda ap: ap.unsqueeze(2).to_broadcast([P, NT, n])
    link(dve.tensor_reduce(best, probs, AX.X, ALU.max))
    link(dve.tensor_tensor(eq, probs, wide(best), ALU.is_ge))
    link(dve.tensor_tensor(eq, eq, iota, ALU.mult))
    link(dve.tensor_reduce(index, eq, AX.X, ALU.min))
    link(dve.tensor_tensor(hot, iota, wide(index), ALU.is_equal))


def running_count(dve, link, net, pre, within, totals, n):
    link(dve.memset(pre[:, 0, :], 0.0))
    for t in range(1, NT):
        link(dve.tensor_tensor(pre[:, t, :], pre[:, t - 1, :], totals[:, t - 1, :], ALU.add))
    link(dve.tensor_tensor(pre[:, :, :], pre[:, :, :], within, ALU.add))


def slots_of(dve, link, b, pre, hot, index, trash, capacity, scatter, gather, accepted):
    link(dve.tensor_tensor(b.tmp, pre, hot, ALU.mult))
    link(dve.tensor_reduce(b.pos, b.tmp, AX.X, ALU.add))
    link(dve.tensor_scalar(accepted, b.pos, float(capacity), None, ALU.is_le))
    link(dve.scalar_tensor_tensor(b.slot, index, float(capacity), b.pos, ALU.mult, ALU.add))
    link(dve.tensor_scalar(b.slot, b.slot, float(64 * capacity - 1), None, ALU.add))
    link(dve.tensor_tensor(b.kept, b.slot, accepted, ALU.mult))
    link(dve.tensor_copy(gather, b.kept))
    link(dve.tensor_tensor(b.slot, b.slot, trash, ALU.subtract))
    link(dve.tensor_tensor(b.slot, b.slot, accepted, ALU.mult))
    link(dve.tensor_tensor(b.slot, b.slot, trash, ALU.add))
    link(dve.tensor_copy(scatter, b.slot))


def stage_switch_experts(nc, net, io):
    with ExitStack() as ctx:
        sb = lambda name, shape, dt=F32: ctx.enter_context(nc.sbuf_tensor(net.name(name), shape, dt))
        n = norm_buffers(ctx, nc, net, in_psum=False)
        prob, eq, hot, pre = (sb(k, [P, NT, E1]) for k in ("prob", "equal", "hot", "pre"))
        top, tot, inv, gate, index, acc, pos, slot, kept = (sb(k, [P, NT]) for k in (
            "top", "total", "inv", "gate", "index", "accepted", "pos", "slot", "kept"))
        scatter, gather = sb("scatter", [P, NT], I32), sb("gather", [P, NT], I32)
        KT = SLOTS // P
        rows, rowsT = sb("rows", [P, KT, D]), sb("rowsT", [P, SLOTS])
        act_g, hid = sb("act_g", [P, 2, 4 * C1]), sb("hid", [P, 2, 4 * C1])
        y, yg = sb("y", [P, E1, D]), sb("y_token", [P, NT, D])
        STEPS = E1 // 4
        s = open_stage(nc, net.pool, f"v:80 logits:1 shifted:1 exp:1 hot:1 counts:1 slots:1 rowsT_ps:5 rowsT:5 g_ps:{STEPS} u_ps:{STEPS} "
                       f"silu:{STEPS} hid:{STEPS} y_ps:{STEPS} y_sb:{STEPS} combined:{NT + 1} " + NORM)
        bank = net.bank
        b3 = lambda k: bank[k][:, :].rearrange("p (t e) -> p t e", e=E1)
        wide = lambda ap: ap.unsqueeze(2).to_broadcast([P, NT, E1])
        iota = net.tab("iota32").unsqueeze(1).to_broadcast([P, NT, E1])
        moved, stored, fetched = net.moved, net.stored, net.fetched
        with nc.Block() as block:
            def down(pe, j):
                pe.wait_ge(s.hid.sem, s.hid.at(0, j + 1))
                if j >= 2:
                    pe.wait_ge(s.y_sb.sem, s.y_sb.at(0, j - 1))
                for k in range(4):
                    e = 4 * j + k
                    last = pe.matmul(bank[4 + j % 2][0:C1, k * P:(k + 1) * P], hid[:, j % 2, k * C1:(k + 1) * C1], net.moe_w[2][:, e, :], start=True, stop=True)
                last.then_inc(s.y_ps.sem, 1)

            @block.tensor
            def _(pe):
                pe.wait_ge(net.ld_w, net.w_ready)
                for t in range(NT):
                    last = pe.matmul(bank[0][:, t * E1:(t + 1) * E1], net.xT[:, t * P:(t + 1) * P], net.w_router[:, :], start=True, stop=True)
                last.then_inc(s.logits.sem, 1)
                pe.wait_ge(s.hot.sem, s.hot.at(0, 1))
                flat = hot[:, :, :].rearrange("p t e -> p (t e)")
                pe.matmul(bank[1][:, :], net.tab("tri"), flat, start=True, stop=True)
                pe.matmul(bank[2][:, :], net.tab("ones"), flat, start=True, stop=True).then_inc(s.counts.sem, 1)
                pe.wait_ge(net.rows_in, 16)
                for g in range(KT // 4):
                    if g == 1:
                        pe.wait_ge(s.slots.sem, s.slots.at(0, 1))
                    for k in range(4):
                        last = pe.transpose(bank[g][:, k * P:(k + 1) * P], rows[:, 4 * g + k, :], net.tab("ident"))
                    last.then_inc(s.rowsT_ps.sem, 1)
                pe.wait_ge(net.ld_moe, 16 * 3)
                for j in range(STEPS):
                    for w, ps, done in ((net.moe_w[0], 0, s.g_ps), (net.moe_w[1], 2, s.u_ps)):
                        if j == 0:
                            pe.wait_ge(s.rowsT.sem, s.rowsT.at(0, 5))
                        if j >= 2:
                            pe.wait_ge(s.hid.sem, s.hid.at(0, j - 1))
                        for k in range(4):
                            e = 4 * j + k
                            last = pe.matmul(bank[ps + j % 2][:, k * C1:(k + 1) * C1], w[:, e, :], rowsT[:, e * C1:(e + 1) * C1], start=True, stop=True)
                        last.then_inc(done.sem, 1)
                    if j >= 1:
                        down(pe, j - 1)
                down(pe, STEPS - 1)
                with pe.Fori(0, B) as i:
                    pe.wait_ge(s.x_updated.sem, s.x_updated.at(i, 0))
                    norm_pe(pe, s, n, i, bank[6][:, 0:L])

            def copy_y(act, j):
                act.wait_ge(s.y_ps.sem, s.y_ps.at(0, j + 1))
                act.activation(y[0:C1, 4 * j:4 * j + 4, :], bank[4 + j % 2][0:C1, :].rearrange("p (k d) -> p k d", d=D), ACT.Copy).then_inc(s.y_sb.sem, 1)

            @block.scalar
            def _(act):
                act.wait_ge(s.shifted.sem, s.shifted.at(0, 1))
                act.activation(prob[:, :, :], prob[:, :, :], ACT.Exp).then_inc(s.exp.sem, 1)
                for g in range(KT // 4):
                    act.wait_ge(s.rowsT_ps.sem, s.rowsT_ps.at(0, g + 1))
                    act.activation(rowsT[:, g * 512:(g + 1) * 512], bank[g][:, :], ACT.Copy).then_inc(s.rowsT.sem, 1)
                for j in range(STEPS):
                    act.wait_ge(s.g_ps.sem, s.g_ps.at(0, j + 1))
                    if j >= 2:
                        act.wait_ge(s.hid.sem, s.hid.at(0, j - 1))
                    act.activation(act_g[:, j % 2, :], bank[j % 2][:, 0:4 * C1], ACT.Silu).then_inc(s.silu.sem, 1)
                    if j >= 1:
                        copy_y(act, j - 1)
                copy_y(act, STEPS - 1)
                with act.Fori(0, B) as i:
                    norm_act(act, s, i, bank[6][:, 0:L], net.xT[:, bass.ds(i * L, L)])

            @block.vector
            def _(dve):
                count = [0]

                def link(ins):
                    count[0] += 1
                    ins.then_inc(s.v.sem, 1)
                    dve.wait_ge(s.v.sem, s.v.at(0, count[0]))

                dve.wait_ge(s.logits.sem, s.logits.at(0, 1))
                link(dve.tensor_reduce(top[:, :], b3(0), AX.X, ALU.max))
                dve.tensor_tensor(prob[:, :, :], b3(0), wide(top[:, :]), ALU.subtract).then_inc(s.shifted.sem, 1)
                dve.wait_ge(s.exp.sem, s.exp.at(0, 1))
                link(dve.tensor_reduce(tot[:, :], prob[:, :, :], AX.X, ALU.add))
                link(dve.reciprocal(inv[:, :], tot[:, :]))
                link(dve.tensor_tensor(prob[:, :, :], prob[:, :, :], wide(inv[:, :]), ALU.mult))
                choose_first(dve, link, prob[:, :, :], iota, gate[:, :], eq[:, :, :], index[:, :], hot[:, :, :], E1)
                dve.nop().then_inc(s.hot.sem, 1)
                dve.wait_ge(s.counts.sem, s.counts.at(0, 1))
                running_count(dve, link, net, pre, b3(1), b3(2), E1)
                b = group(tmp=eq[:, :, :], pos=pos[:, :], slot=slot[:, :], kept=kept[:, :])
                slots_of(dve, link, b, pre[:, :, :], hot[:, :, :], index[:, :], net.tab("trash")[:, 0:NT], C1,
                         scatter[:, :], gather[:, :], acc[:, :])
                link(dve.tensor_tensor(gate[:, :], gate[:, :], acc[:, :], ALU.mult))
                dve.nop().then_inc(s.slots.sem, 1)
                for j in range(STEPS):
                    dve.wait_ge(s.silu.sem, s.silu.at(0, j + 1))
                    dve.wait_ge(s.u_ps.sem, s.u_ps.at(0, j + 1))
                    if j >= 2:
                        dve.wait_ge(s.y_ps.sem, s.y_ps.at(0, j - 1))
                    dve.tensor_tensor(hid[:, j % 2, :], act_g[:, j % 2, :], bank[2 + j % 2][:, 0:4 * C1], ALU.mult).then_inc(s.hid.sem, 1)
                dve.wait_ge(fetched, 16 * NT)
                for t in range(NT):
                    dve.tensor_scalar(yg[:, t, :], yg[:, t, :], gate[:, t:t + 1], None, ALU.mult).then_inc(s.combined.sem, 1)
                dve.wait_ge(s.combined.sem, s.combined.at(0, NT))
                flat = yg[:, :, :].rearrange("p t d -> p (t d)")
                dve.scalar_tensor_tensor(flat, net.x_tok[:, :], 2.0, flat, ALU.mult, ALU.add).then_inc(s.combined.sem, 1)
                dve.wait_ge(s.combined.sem, s.combined.at(0, NT + 1))
                with dve.Fori(0, B) as i:
                    norm_dve(dve, s, n, i, yg[:, bass.ds(TPB * i, TPB), :])

            @block.gpsimd
            def _(pool):
                pool.wait_ge(s.slots.sem, s.slots.at(0, 1))
                pool.wait_ge(net.zeroed, net.zero_ready)
                for t in range(NT):
                    pool.indirect_dma_start(net.slots[0], bass.IndirectOffsetOnAxis(ap=scatter[:, t:t + 1], axis=0),
                                            net.x_tok[:, t * P:(t + 1) * P], None).then_inc(moved, 16)
                pool.wait_ge(stored, 16)
                for t in range(NT):
                    pool.indirect_dma_start(yg[:, t, :], None, net.slots_out[0],
                                            bass.IndirectOffsetOnAxis(ap=gather[:, t:t + 1], axis=0)).then_inc(fetched, 16)
                with pool.Fori(0, B) as i:
                    norm_pool(pool, s, n, i)

            @block.sync
            def _(sp):
                sp.wait_ge(moved, 16 * NT)
                sp.dma_start(rows[:, :, :], net.slots[0][0:SLOTS, :].rearrange("(k p) d -> p k d", p=P)).then_inc(net.rows_in, 16)
                sp.wait_ge(s.y_sb.sem, s.y_sb.at(0, STEPS))
                sp.dma_start(net.slots_out[0].rearrange("(e c) d -> c e d", c=C1), y[0:C1, :, :]).then_inc(stored, 16)
    close_stage(nc, net.pool)


def stage_mha(nc, net, w, mask, src, dst, load=()):
    with ExitStack() as ctx:
        sb = lambda name, shape: ctx.enter_context(nc.sbuf_tensor(net.name(name), shape, F32))
        K = 4
        BL = P // NL
        HW = AH * NL
        RING = 6 * K
        qk_w, vp_w = sb("wk_wq", [P, AH, D]), sb("wv_wp", [P, AH, D])
        w_res = sb("residual", [P, D])
        U, Z = sb("U", [P, 2, AH, P]), sb("Z", [P, AH, P])
        turned = U[:, :, :, :].rearrange("p a h t -> p (a h t)")
        xs, x_tok = sb("xs", [P, K, P]), sb("x_rows", [P, 2, D])
        S, A = sb("prob", [P, AH, NL]), sb("probT", [P, 2, HW])
        top, tot, inv = sb("top", [P, AH]), sb("total", [P, AH]), sb("inv", [P, AH])
        st, mv, ve, rstd, xn = sb("st", [P, 6]), sb("mv", [P, 2, 2]), sb("ve", [P, 2]), sb("rstd", [P, 2]), sb("xn", [P, 2, D])
        s = open_stage(nc, net.pool, f"settled:0 w_ps:6 w_act:6 m_ps:8 m_act:4 m_dve:4 sum_ps:1 w_res:1 xs_ready:1 ring_ps:{RING} ring:{RING} "
                       f"scored:{K} masked:{K} top:{K} shifted:{K} exped:{K} total:{K} inv:{K} prob:{K} probT:{K} "
                       f"z_ps:{BL * K} z_act:{2 * K} z_dve:{2 * K} y_ready:{K} stats:{K} agg:{K} var_eps:{K} rstd:{K} xn_ready:{K}")
        bank, ident = net.bank, net.tab("ident")
        items, at_step = [], []
        for k in range(-1, K + 2):
            here = [("u", k + 1, g) for g in range(5) if k + 1 < K] + [("n", k - 2, 0) for _ in range(1) if 0 <= k - 2]
            at_step.append((len(items), here))
            items += here
        assert len(items) == RING and RING % 2 == 0
        per_head = lambda ap: ap.unsqueeze(2).to_broadcast([P, AH, NL])
        with nc.Block() as block:
            @block.sync
            def _(sp):
                with nc.allow_non_contiguous_dma(reason="biases, one to a partition, and a small router"):
                    for to, of, done in load:
                        sp.dma_start(to, of).then_inc(done, 16)

            @block.gpsimd
            def _(pool):
                with pool.Fori(0, T // (K * P)) as i:
                    for k in range(K):
                        pool.wait_ge(s.agg.sem, s.agg.at(i, k + 1))
                        pool.tensor_tensor(ve[:, k % 2:k % 2 + 1], mv[:, k % 2, 1:2], net.eps[:, 0:1], ALU.add).then_inc(s.var_eps.sem, 1)
                        pool.wait_ge(s.var_eps.sem, s.var_eps.at(i, k + 1))
                        pool.tensor_tensor(rstd[:, k % 2:k % 2 + 1], ve[:, k % 2:k % 2 + 1], net.neghalf[:, 0:1], ALU.pow).then_inc(s.rstd.sem, 1)

            @block.tensor
            def _(pe):
                pe.wait_ge(net.ld_w2, net.w2_ready)
                for j, wt in enumerate((w.q, w.k, w.v)):
                    for b in range(2):
                        for c in range(4):
                            last = pe.transpose(bank[2 * j + b][:, c * P:(c + 1) * P], wt[:, (4 * b + c) * P:(4 * b + c + 1) * P], ident)
                        last.then_inc(s.w_ps.sem, 1)
                pe.wait_ge(s.w_act.sem, s.w_act.at(0, 6))
                row = lambda h: slice(ADK * (h % 2), ADK * (h % 2) + ADK)
                part = lambda j, h: turned[row(h), (8 * j + h // 2) * P:(8 * j + h // 2 + 1) * P]
                for q in range(8):
                    for m in range(4):
                        h = 2 * (4 * (q % 2) + m) + (q // 2) % 2
                        if q < 4:
                            last = pe.matmul(bank[q][:, m * P:(m + 1) * P], part(1, h), part(0, h), start=True, stop=True)
                        else:
                            last = pe.matmul(bank[q][:, m * P:(m + 1) * P], part(2, h), w.p[row(h), h // 2, :], start=True, stop=True)
                    last.then_inc(s.m_ps.sem, 1)
                pe.wait_ge(s.m_act.sem, s.m_act.at(0, 4))
                for c in range(AH // 2):
                    last = pe.matmul(bank[0][:, 0:D], turned[:, (16 + c) * P:(17 + c) * P], w.p[:, c, :], start=(c == 0), stop=(c == AH // 2 - 1))
                last.then_inc(s.sum_ps.sem, 1)
                pe.wait_ge(s.w_res.sem, s.w_res.at(0, 1))
                with pe.Fori(0, T // (K * P)) as i:
                    pe.wait_ge(s.xs_ready.sem, s.xs_ready.at(i, 1))

                    def ring(step):
                        n0, here = at_step[step + 1]
                        for d, (what, k, g) in enumerate(here):
                            n = n0 + d
                            to = bank[n % 2]
                            pe.wait_ge(s.ring.sem, s.ring.at(i, max(0, n - 1)))
                            if what == "n":
                                pe.wait_ge(s.xn_ready.sem, s.xn_ready.at(i, k + 1))
                                last = pe.transpose(to[:, 0:P], xn[:, k % 2, :], ident)
                            elif g == 0:
                                last = pe.transpose(to[:, 0:P], xs[:, k, :], ident)
                            else:
                                for m in range(4):
                                    last = pe.matmul(to[:, m * P:(m + 1) * P], qk_w[:, 4 * (g - 1) + m, :], xs[:, k, :], start=True, stop=True)
                            last.then_inc(s.ring_ps.sem, 1)

                    ring(-1)
                    for k in range(K + 2):
                        if k < K:
                            pe.wait_ge(s.ring.sem, s.ring.at(i, at_step[k][0] + 5))
                            pe.wait_ge(s.shifted.sem, s.shifted.at(i, k))
                            for b in range(BL):
                                blk = slice(NL * b, NL * (b + 1))
                                last = pe.matmul(bank[2][blk, :], xs[:, k, blk], U[:, k % 2, :, blk], start=True, stop=True)
                            last.then_inc(s.scored.sem, 1)
                        ring(k)
                        if 1 <= k <= K:
                            j = k - 1
                            pe.wait_ge(s.z_act.sem, s.z_act.at(i, 2 * j + 2))
                            pe.wait_ge(s.z_dve.sem, s.z_dve.at(i, 2 * j + 2))
                            pe.wait_ge(s.xn_ready.sem, s.xn_ready.at(i, j))
                            for h in range(AH):
                                pe.matmul(bank[3][:, 0:D], Z[:, h, :], vp_w[:, h, :], start=(h == 0), stop=False)
                            pe.matmul(bank[3][:, 0:D], net.tab("ones")[0:1, :], w.pb[:, :], start=False, stop=False)
                            pe.matmul(bank[3][:, 0:D], xs[:, j, :], w_res[:, :], start=False, stop=True).then_inc(s.y_ready.sem, 1)
                        if k < K:
                            pe.wait_ge(s.probT.sem, s.probT.at(i, k + 1))
                            pe.wait_ge(s.z_act.sem, s.z_act.at(i, 2 * k))
                            pe.wait_ge(s.z_dve.sem, s.z_dve.at(i, 2 * k))
                            for b in range(BL):
                                blk = slice(NL * b, NL * (b + 1))
                                pe.matmul(bank[4 + b][:, :], x_tok[blk, k % 2, :], A[blk, k % 2, :], start=True, stop=True).then_inc(s.z_ps.sem, 1)

            @block.scalar
            def _(act):
                for n in range(6):
                    act.wait_ge(s.w_ps.sem, s.w_ps.at(0, n + 1))
                    act.activation(turned[:, n * 512:(n + 1) * 512], bank[n][:, :], ACT.Copy).then_inc(s.w_act.sem, 1)
                for q in range(4):
                    act.wait_ge(s.m_ps.sem, s.m_ps.at(0, q + 1))
                    h = 8 * (q % 2) + q // 2
                    act.activation(qk_w[:, h:h + 7:2, :], bank[q][:, :].rearrange("p (m d) -> p m d", m=4), ACT.Copy).then_inc(s.m_act.sem, 1)
                with act.Fori(0, T // (K * P)) as i:
                    act.wait_ge(s.y_ready.sem, s.y_ready.at(i, 0))
                    act.activation(xs[:, :, :], src[:, bass.ds(i * K * P, K * P)].rearrange("p (k t) -> p k t", k=K), ACT.Copy)\
                        .then_inc(s.xs_ready.sem, 1)

                    def ring(step, lo, hi):
                        n0, here = at_step[step + 1]
                        for d, (what, k, g) in enumerate(here):
                            if not lo <= d < hi:
                                continue
                            n = n0 + d
                            act.wait_ge(s.ring_ps.sem, s.ring_ps.at(i, n + 1))
                            if what == "n":
                                settle(act, s)
                                act.activation(dst[:, bass.ds(i * K * P + k * P, P)], bank[n % 2][:, 0:P], ACT.Identity,
                                               scale=w.g[:, :], bias=w.b[:, :]).then_inc(s.ring.sem, 1)
                            elif g == 0:
                                act.activation(x_tok[:, k % 2, :], bank[n % 2][:, 0:P], ACT.Copy).then_inc(s.ring.sem, 1)
                            else:
                                act.activation(U[:, k % 2, 4 * (g - 1):4 * g, :], bank[n % 2][:, :].rearrange("p (m t) -> p m t", m=4), ACT.Copy)\
                                    .then_inc(s.ring.sem, 1)

                    ring(-1, 0, 6)
                    for k in range(K + 2):
                        ring(k, 0, 2)
                        if k < K:
                            act.wait_ge(s.shifted.sem, s.shifted.at(i, k + 1))
                            act.activation(S[:, :, :], S[:, :, :], ACT.Exp, scale=ADK ** -0.5).then_inc(s.exped.sem, 1)
                        ring(k, 2, 6)
                        if k < K:
                            for b in range(2):
                                act.wait_ge(s.z_ps.sem, s.z_ps.at(i, BL * k + b + 1))
                                act.activation(Z[:, :, NL * b:NL * (b + 1)], bank[4 + b][:, :].rearrange("p (h q) -> p h q", h=AH), ACT.Copy)\
                                    .then_inc(s.z_act.sem, 1)

            @block.vector
            def _(dve):
                for q in range(4):
                    dve.wait_ge(s.m_ps.sem, s.m_ps.at(0, q + 5))
                    h = 8 * (q % 2) + q // 2
                    dve.tensor_copy(vp_w[:, h:h + 7:2, :], bank[4 + q][:, :].rearrange("p (m d) -> p m d", m=4)).then_inc(s.m_dve.sem, 1)
                dve.wait_ge(s.sum_ps.sem, s.sum_ps.at(0, 1))
                dve.tensor_tensor(w_res[:, :], ident, bank[0][:, 0:D], ALU.subtract).then_inc(s.w_res.sem, 1)
                with dve.Fori(0, T // (K * P)) as i:
                    for k in range(K + 1):
                        if k < K:
                            scores = bank[2][:, :].rearrange("p (h q) -> p h q", h=AH)
                            dve.wait_ge(s.scored.sem, s.scored.at(i, k + 1))
                            if mask is not None:
                                dve.tensor_tensor(S[:, :, :], scores, mask.unsqueeze(1).to_broadcast([P, AH, NL]), ALU.add).then_inc(s.masked.sem, 1)
                                dve.wait_ge(s.masked.sem, s.masked.at(i, k + 1))
                                scores = S[:, :, :]
                            dve.tensor_reduce(top[:, :], scores, AX.X, ALU.max).then_inc(s.top.sem, 1)
                            dve.wait_ge(s.top.sem, s.top.at(i, k + 1))
                            dve.tensor_tensor(S[:, :, :], scores, per_head(top[:, :]), ALU.subtract).then_inc(s.shifted.sem, 1)
                            dve.wait_ge(s.exped.sem, s.exped.at(i, k + 1))
                            dve.tensor_reduce(tot[:, :], S[:, :, :], AX.X, ALU.add).then_inc(s.total.sem, 1)
                            dve.wait_ge(s.total.sem, s.total.at(i, k + 1))
                            dve.reciprocal(inv[:, :], tot[:, :]).then_inc(s.inv.sem, 1)
                            dve.wait_ge(s.inv.sem, s.inv.at(i, k + 1))
                            dve.tensor_tensor(S[:, :, :], S[:, :, :], per_head(inv[:, :]), ALU.mult).then_inc(s.prob.sem, 1)
                            dve.wait_ge(s.prob.sem, s.prob.at(i, k + 1))
                            dve.transpose(A[:, k % 2, :], S[:, :, :].rearrange("p h q -> p (h q)")).then_inc(s.probT.sem, 1)
                        if k >= 1:
                            j = k - 1
                            dve.wait_ge(s.y_ready.sem, s.y_ready.at(i, j + 1))
                            dve.bn_stats(st[:, :], bank[3][:, 0:D]).then_inc(s.stats.sem, 1)
                            dve.wait_ge(s.stats.sem, s.stats.at(i, j + 1))
                            settle(dve, s)
                            dve.bn_aggr(mv[:, j % 2, :], st[:, :]).then_inc(s.agg.sem, 1)
                        if k < K:
                            for b in range(2, BL):
                                dve.wait_ge(s.z_ps.sem, s.z_ps.at(i, BL * k + b + 1))
                                dve.tensor_copy(Z[:, :, NL * b:NL * (b + 1)], bank[4 + b][:, :].rearrange("p (h q) -> p h q", h=AH)).then_inc(s.z_dve.sem, 1)
                        if k >= 1:
                            dve.wait_ge(s.rstd.sem, s.rstd.at(i, j + 1))
                            dve.tensor_scalar(xn[:, j % 2, :], bank[3][:, 0:D], mv[:, j % 2, 0:1], rstd[:, j % 2:j % 2 + 1], ALU.subtract, ALU.mult)\
                                .then_inc(s.xn_ready.sem, 1)
    close_stage(nc, net.pool)


def stage_relu_mlp(nc, net, w, x, final, order, order_to):
    with ExitStack() as ctx:
        sb = lambda name, shape: ctx.enter_context(nc.sbuf_tensor(net.name(name), shape, F32))
        n, nf = norm_buffers(ctx, nc, net), norm_buffers(ctx, nc, net, keep=True)
        C = DI // P
        xs, x0, z, hid = sb("xs", [P, L]), sb("x0", [P, L]), sb("z", [P, L]), sb("hid", [P, C, L])
        s = open_stage(nc, net.pool, f"xs_ready:1 x0_ready:1 h_ps:{C} hid:{C} " + NORM + " " + prefixed("f_", NORM))
        f = part(s, "f_")
        bank, ident = net.bank, net.tab("ident")
        y_bank, yT_bank, z_bank, zT_bank = bank[4:8]
        tiles = lambda bank: bank[:, 0:L].rearrange("p (t d) -> p t d", d=D)
        with nc.Block() as block:
            @block.gpsimd
            def _(pool):
                def turn(i, ahead, own, behind):
                    if own:
                        norm_pool(pool, s, n, i)
                    if behind:
                        norm_pool(pool, f, nf, i - 1)
                skewed(pool, turn, final)

            @block.tensor
            def _(pe):
                pe.wait_ge(net.ld_w2, net.w2_ready)

                def turn(i, ahead, own, behind):
                    if ahead:
                        pe.wait_ge(s.xs_ready.sem, s.xs_ready.at(i + 1, 1))
                        pe.wait_ge(s.hid.sem, s.hid.at(i + 1, 0))
                        for c in range(C):
                            pe.matmul(bank[c][:, 0:L], w.w1[:, c * P:(c + 1) * P], xs[:, :], start=True, stop=True).then_inc(s.h_ps.sem, 1)
                    if behind:
                        pe.wait_ge(s.x_updated.sem, s.x_updated.at(i - 1, 1))
                        pe.wait_ge(s.x0_ready.sem, s.x0_ready.at(i - 1, 1))
                        pe.wait_ge(f.xn_ready.sem, f.xn_ready.at(i - 1, 0))
                        for t in range(TPB):
                            tok = slice(t * P, (t + 1) * P)
                            pe.matmul(z_bank[:, tok], z[:, tok], ident, start=True, stop=False)
                            last = pe.matmul(z_bank[:, tok], x0[:, tok], ident, start=False, stop=True)
                        last.then_inc(f.y_ready.sem, 1)
                    if own:
                        pe.wait_ge(s.x_updated.sem, s.x_updated.at(i, 0))
                        norm_pe(pe, s, n, i, yT_bank[:, 0:L])
                    if ahead:
                        pe.wait_ge(s.xn_ready.sem, s.xn_ready.at(i + 1, 0))
                        pe.wait_ge(s.hid.sem, s.hid.at(i + 1, C))
                        for t in range(TPB):
                            tok = slice(t * P, (t + 1) * P)
                            for c in range(C):
                                pe.matmul(y_bank[:, tok], hid[:, c, tok], w.w2[:, c, :], start=(c == 0), stop=False)
                            pe.matmul(y_bank[:, tok], net.tab("ones")[0:1, :], w.b2[:, :], start=False, stop=False)
                            last = pe.matmul(y_bank[:, tok], xs[:, tok], ident, start=False, stop=True)
                        last.then_inc(s.y_ready.sem, 1)
                    if behind:
                        pe.wait_ge(f.x_updated.sem, f.x_updated.at(i - 1, 0))
                        norm_pe(pe, f, nf, i - 1, zT_bank[:, 0:L])
                skewed(pe, turn, final)

            @block.scalar
            def _(act):
                act.wait_ge(net.ld_w2, net.w2_ready)

                def turn(i, ahead, own, behind):
                    if ahead:
                        act.wait_ge(s.y_ready.sem, s.y_ready.at(i + 1, 0))
                        settle(act, s)
                        act.activation(xs[:, :], x[:, bass.ds((i + 1) * L, L)], ACT.Copy).then_inc(s.xs_ready.sem, 1)
                        for c in range(C):
                            act.wait_ge(s.h_ps.sem, s.h_ps.at(i + 1, c + 1))
                            act.activation(hid[:, c, :], bank[c][:, 0:L], ACT.Relu, bias=w.b1[:, c:c + 1]).then_inc(s.hid.sem, 1)
                    if own and final:
                        act.wait_ge(f.y_ready.sem, f.y_ready.at(i, 0))
                        settle(act, s)
                        act.activation(x0[:, :], net.xT[:, bass.ds(i * L, L)], ACT.Copy).then_inc(s.x0_ready.sem, 1)
                    if own:
                        dst = z[:, :] if final else x[:, bass.ds(i * L, L)]
                        norm_act(act, s, i, order(yT_bank[:, 0:L]), order_to(dst), w.g[:, :], w.b[:, :])
                    if behind:
                        norm_act(act, f, i - 1, zT_bank[:, 0:L], net.xT[:, bass.ds((i - 1) * L, L)])
                skewed(act, turn, final)

            @block.vector
            def _(dve):
                def turn(i, ahead, own, behind):
                    if own:
                        norm_stats(dve, s, n, i, tiles(y_bank))
                    if behind:
                        norm_stats(dve, f, nf, i - 1, tiles(z_bank))
                    if own:
                        norm_apply(dve, s, n, i, tiles(y_bank))
                    if behind:
                        norm_apply(dve, f, nf, i - 1, tiles(z_bank))
                skewed(dve, turn, final)
    close_stage(nc, net.pool)


def stage_top2_experts(nc, net, io):
    with ExitStack() as ctx:
        sb = lambda name, shape, dt=F32: ctx.enter_context(nc.sbuf_tensor(net.name(name), shape, dt))
        n = norm_buffers(ctx, nc, net, in_psum=False)
        prob, rest, eq, hot1, hot2, pre = (sb(k, [P, NT, E2]) for k in ("prob", "rest", "equal", "hot1", "hot2", "pre"))
        (top, tot, inv, p1, p2, i1, i2, acc1, acc2, pos, slot, kept, ms, rms) = (sb(k, [P, NT]) for k in (
            "top", "total", "inv", "p1", "p2", "index1", "index2", "acc1", "acc2", "pos", "slot", "kept", "mean_sq", "rms"))
        scatter, gather = sb("scatter", [P, 2, NT], I32), sb("gather", [P, 2, NT], I32)
        sq = sb("square", [P, D])
        KT = SLOTS // P
        rows, rowsT = sb("rows", [P, KT, D]), sb("rowsT", [P, SLOTS])
        FC = IR // P
        act_g, hid = sb("act_g", [P, 2, C2]), sb("hid", [P, 2, FC, C2])
        yg1, yg2 = sb("y_first", [P, NT, D]), sb("y_second", [P, NT, D])
        y = sb("y", [P, 2, 3, D])
        SC = IS // P
        sgate, shid = sb("shared_gate", [P, 2, L]), sb("shared_hid", [P, SC, L])
        xs, z = sb("xs", [P, L]), sb("z", [P, TPB, D])
        shared = sb("shared", [P, NT, D])
        parts = ((0, B // 2), (B // 2, B))
        MS = [(0, P), (P, P), (2 * P, C2 - 2 * P)]
        s = open_stage(nc, net.pool, f"v:120 logits:1 squares:{NT} mean:1 rms:1 shifted:1 exp:1 hot:1 counts:1 slots:1 rowsT_ps:5 rowsT:5 "
                       f"g_ps:{E2 * FC} u_ps:{E2 * FC} silu:{E2 * FC} hid:{E2 * FC} y_ps:{E2} y_sb:{E2} "
                       f"xs_ready:1 sg_ps:{SC} su_ps:{SC} s_silu:{SC} s_hid:{SC} shared_ps:1 shared:1 z_ready:1 " + NORM)
        bank = net.bank
        b3 = lambda k: bank[k][:, 0:NT * E2].rearrange("p (t e) -> p t e", e=E2)
        wide = lambda ap: ap.unsqueeze(2).to_broadcast([P, NT, E2])
        iota = net.tab("iota32")[:, 0:E2].unsqueeze(1).to_broadcast([P, NT, E2])
        rg, ru = (net.moe_w[k][:, :, :].rearrange("p e f -> p (e f)").rearrange("p (e i) -> p e i", e=E2) for k in range(2))
        rd = net.moe_w[2][:, :, :].rearrange("p (e c) d -> p e c d", e=E2)
        moved, stored, fetched = net.moved2, net.stored2, net.fetched2
        with nc.Block() as block:
            gate_bank, up_bank = (lambda c: bank[3 + c % 2]), (lambda c: bank[5 + c % 2])

            def down(pe, e):
                pe.wait_ge(s.hid.sem, s.hid.at(0, FC * (e + 1)))
                if e >= 1:
                    pe.wait_ge(s.y_sb.sem, s.y_sb.at(0, e))
                for m, (at, w) in enumerate(MS):
                    for c in range(FC):
                        last = pe.matmul(bank[4][0:w, m * P:(m + 1) * P], hid[:, e % 2, c, at:at + w], rd[:, e, c, :], start=(c == 0), stop=(c == FC - 1))
                last.then_inc(s.y_ps.sem, 1)

            @block.tensor
            def _(pe):
                pe.wait_ge(net.ld_w3, net.w3_ready)
                for t in range(NT):
                    last = pe.matmul(bank[0][:, t * E2:(t + 1) * E2], net.xT[:, t * P:(t + 1) * P], net.router2[:, :], start=True, stop=True)
                last.then_inc(s.logits.sem, 1)
                pe.wait_ge(s.hot.sem, s.hot.at(0, 1))
                flat = eq[:, :, :].rearrange("p t e -> p (t e)")
                pe.matmul(bank[1][:, 0:NT * E2], net.tab("tri"), flat, start=True, stop=True)
                pe.matmul(bank[2][:, 0:NT * E2], net.tab("ones"), flat, start=True, stop=True).then_inc(s.counts.sem, 1)

                def shared_expert(part):
                    with pe.Fori(*parts[part]) as i:
                        pe.wait_ge(s.xs_ready.sem, s.xs_ready.at(i, 1))
                        for c in range(SC):
                            pe.wait_ge(s.s_hid.sem, s.s_hid.at(i, max(0, c - 1)))
                            for w, to, done in ((net.sg, gate_bank(c), s.sg_ps), (net.su, up_bank(c), s.su_ps)):
                                pe.matmul(to[:, 0:L], w[:, c * P:(c + 1) * P], xs[:, :], start=True, stop=True).then_inc(done.sem, 1)
                        pe.wait_ge(s.s_hid.sem, s.s_hid.at(i, SC))
                        pe.wait_ge(s.shared.sem, s.shared.at(i, 0))
                        for t in range(TPB):
                            tok = slice(t * P, (t + 1) * P)
                            for c in range(SC):
                                pe.matmul(bank[7][:, tok], shid[:, c, tok], net.sd[:, c, :], start=(c == 0), stop=False)
                            last = pe.matmul(bank[7][:, tok], xs[:, tok], net.tab("ident"), start=False, stop=True)
                        last.then_inc(s.shared_ps.sem, 1)

                shared_expert(0)
                pe.wait_ge(net.rows_in, 32)
                pe.wait_ge(s.slots.sem, s.slots.at(0, 1))
                for g in range(KT // 4):
                    for k in range(4):
                        last = pe.transpose(bank[g][:, k * P:(k + 1) * P], rows[:, 4 * g + k, :], net.tab("ident"))
                    last.then_inc(s.rowsT_ps.sem, 1)
                pe.wait_ge(s.rowsT.sem, s.rowsT.at(0, 5))
                for e in range(E2):
                    x = rowsT[:, e * C2:(e + 1) * C2]
                    for c in range(FC):
                        j = FC * e + c
                        for w, ps, done in ((rg, 0, s.g_ps), (ru, 2, s.u_ps)):
                            if j >= 2:
                                pe.wait_ge(s.hid.sem, s.hid.at(0, j - 1))
                            pe.matmul(bank[ps + j % 2][:, 0:C2], w[:, e, c * P:(c + 1) * P], x, start=True, stop=True).then_inc(done.sem, 1)
                    if e >= 1:
                        down(pe, e - 1)
                down(pe, E2 - 1)
                pe.wait_ge(s.y_sb.sem, s.y_sb.at(0, E2))
                shared_expert(1)
                with pe.Fori(0, B) as i:
                    pe.wait_ge(s.x_updated.sem, s.x_updated.at(i, 0))
                    norm_pe(pe, s, n, i, bank[1][:, 0:L])

            def copy_y(act, e):
                act.wait_ge(s.y_ps.sem, s.y_ps.at(0, e + 1))
                if e >= 2:
                    act.wait_ge(stored[e % 2], 16 * 2 * (e // 2))
                act.activation(y[:, e % 2, 0:2, :], bank[4][:, 0:2 * P].rearrange("p (k d) -> p k d", d=D), ACT.Copy)
                act.activation(y[0:C2 - 2 * P, e % 2, 2, :], bank[4][0:C2 - 2 * P, 2 * P:3 * P], ACT.Copy).then_inc(s.y_sb.sem, 1)

            @block.scalar
            def _(act):
                for t in range(NT):
                    act.activation(sq[:, :], net.x_tok[:, t * P:(t + 1) * P], ACT.Square, accum_out=ms[:, t:t + 1]).then_inc(s.squares.sem, 1)
                    act.wait_ge(s.squares.sem, s.squares.at(0, t + 1))
                act.wait_ge(s.shifted.sem, s.shifted.at(0, 1))
                act.activation(prob[:, :, :], prob[:, :, :], ACT.Exp).then_inc(s.exp.sem, 1)

                def shared_expert(part):
                    with act.Fori(*parts[part]) as i:
                        act.wait_ge(s.shared_ps.sem, s.shared_ps.at(i, 0))
                        settle(act, s)
                        act.activation(xs[:, :], net.xT[:, bass.ds(i * L, L)], ACT.Copy).then_inc(s.xs_ready.sem, 1)
                        for c in range(SC):
                            act.wait_ge(s.sg_ps.sem, s.sg_ps.at(i, c + 1))
                            act.wait_ge(s.s_hid.sem, s.s_hid.at(i, max(0, c - 1)))
                            act.activation(sgate[:, c % 2, :], gate_bank(c)[:, 0:L], ACT.Silu).then_inc(s.s_silu.sem, 1)
                        act.wait_ge(s.shared_ps.sem, s.shared_ps.at(i, 1))
                        settle(act, s)
                        act.activation(shared[:, bass.ds(TPB * i, TPB), :], bank[7][:, 0:L].rearrange("p (t d) -> p t d", d=D), ACT.Copy)\
                            .then_inc(s.shared.sem, 1)

                shared_expert(0)
                for g in range(KT // 4):
                    act.wait_ge(s.rowsT_ps.sem, s.rowsT_ps.at(0, g + 1))
                    act.activation(rowsT[:, g * 512:(g + 1) * 512], bank[g][:, :], ACT.Copy).then_inc(s.rowsT.sem, 1)
                for e in range(E2):
                    for c in range(FC):
                        j = FC * e + c
                        act.wait_ge(s.g_ps.sem, s.g_ps.at(0, j + 1))
                        if j >= 2:
                            act.wait_ge(s.hid.sem, s.hid.at(0, j - 1))
                        act.activation(act_g[:, j % 2, :], bank[j % 2][:, 0:C2], ACT.Silu).then_inc(s.silu.sem, 1)
                    if e >= 1:
                        copy_y(act, e - 1)
                copy_y(act, E2 - 1)
                shared_expert(1)
                with act.Fori(0, B) as i:
                    norm_act(act, s, i, bank[1][:, 0:L], net.xT[:, bass.ds(i * L, L)])

            @block.vector
            def _(dve):
                count = [0]

                def link(ins):
                    count[0] += 1
                    ins.then_inc(s.v.sem, 1)
                    dve.wait_ge(s.v.sem, s.v.at(0, count[0]))

                dve.wait_ge(s.squares.sem, s.squares.at(0, NT))
                dve.tensor_scalar(ms[:, :], ms[:, :], 1.0 / D, float(np.finfo(np.float32).eps), ALU.mult, ALU.add).then_inc(s.mean.sem, 1)
                dve.wait_ge(s.logits.sem, s.logits.at(0, 1))
                dve.wait_ge(s.rms.sem, s.rms.at(0, 1))
                link(dve.tensor_tensor(prob[:, :, :], b3(0), wide(rms[:, :]), ALU.mult))
                link(dve.tensor_reduce(top[:, :], prob[:, :, :], AX.X, ALU.max))
                dve.tensor_tensor(prob[:, :, :], prob[:, :, :], wide(top[:, :]), ALU.subtract).then_inc(s.shifted.sem, 1)
                dve.wait_ge(s.exp.sem, s.exp.at(0, 1))
                link(dve.tensor_reduce(tot[:, :], prob[:, :, :], AX.X, ALU.add))
                link(dve.reciprocal(inv[:, :], tot[:, :]))
                link(dve.tensor_tensor(prob[:, :, :], prob[:, :, :], wide(inv[:, :]), ALU.mult))
                choose_first(dve, link, prob[:, :, :], iota, p1[:, :], eq[:, :, :], i1[:, :], hot1[:, :, :], E2)
                link(dve.scalar_tensor_tensor(rest[:, :, :], hot1[:, :, :], -2.0, prob[:, :, :], ALU.mult, ALU.add))
                choose_first(dve, link, rest[:, :, :], iota, p2[:, :], eq[:, :, :], i2[:, :], hot2[:, :, :], E2)
                link(dve.tensor_tensor(eq[:, :, :], hot1[:, :, :], hot2[:, :, :], ALU.add))
                dve.nop().then_inc(s.hot.sem, 1)
                link(dve.tensor_tensor(tot[:, :], p1[:, :], p2[:, :], ALU.add))
                link(dve.reciprocal(inv[:, :], tot[:, :]))
                dve.wait_ge(s.counts.sem, s.counts.at(0, 1))
                running_count(dve, link, net, pre, b3(1), b3(2), E2)
                b = group(tmp=eq[:, :, :], pos=pos[:, :], slot=slot[:, :], kept=kept[:, :])
                for k, (hot, index, acc, p) in enumerate(((hot1, i1, acc1, p1), (hot2, i2, acc2, p2))):
                    slots_of(dve, link, b, pre[:, :, :], hot[:, :, :], index[:, :], net.tab("trash")[:, k * NT:(k + 1) * NT], C2,
                             scatter[:, k, :], gather[:, k, :], acc[:, :])
                    link(dve.tensor_tensor(p[:, :], p[:, :], inv[:, :], ALU.mult))
                    link(dve.tensor_tensor(p[:, :], p[:, :], acc[:, :], ALU.mult))
                dve.nop().then_inc(s.slots.sem, 1)

                def shared_expert(part):
                    with dve.Fori(*parts[part]) as i:
                        for c in range(SC):
                            dve.wait_ge(s.s_silu.sem, s.s_silu.at(i, c + 1))
                            dve.wait_ge(s.su_ps.sem, s.su_ps.at(i, c + 1))
                            dve.wait_ge(s.shared_ps.sem, s.shared_ps.at(i, 0))
                            dve.tensor_tensor(shid[:, c, :], sgate[:, c % 2, :], up_bank(c)[:, 0:L], ALU.mult).then_inc(s.s_hid.sem, 1)

                shared_expert(0)
                for e in range(E2):
                    for c in range(FC):
                        j = FC * e + c
                        dve.wait_ge(s.silu.sem, s.silu.at(0, j + 1))
                        dve.wait_ge(s.u_ps.sem, s.u_ps.at(0, j + 1))
                        if e >= 2:
                            dve.wait_ge(s.y_ps.sem, s.y_ps.at(0, e - 1))
                        dve.tensor_tensor(hid[:, e % 2, c, :], act_g[:, j % 2, :], bank[2 + j % 2][:, 0:C2], ALU.mult).then_inc(s.hid.sem, 1)
                shared_expert(1)
                dve.wait_ge(s.shared.sem, s.shared.at(B - 1, 1))
                dve.wait_ge(fetched, 16 * 2 * NT)
                wide_d = lambda ap: ap.unsqueeze(2).to_broadcast([P, NT, D])
                link(dve.tensor_tensor(yg1[:, :, :], yg1[:, :, :], wide_d(p1[:, :]), ALU.mult))
                link(dve.tensor_tensor(yg2[:, :, :], yg2[:, :, :], wide_d(p2[:, :]), ALU.mult))
                link(dve.tensor_tensor(yg1[:, :, :], yg1[:, :, :], yg2[:, :, :], ALU.add))
                with dve.Fori(0, B) as i:
                    dve.wait_ge(s.xn_ready.sem, s.xn_ready.at(i, 0))
                    dve.tensor_tensor(z[:, :, :], shared[:, bass.ds(TPB * i, TPB), :], yg1[:, bass.ds(TPB * i, TPB), :], ALU.add)\
                        .then_inc(s.z_ready.sem, 1)
                    dve.wait_ge(s.z_ready.sem, s.z_ready.at(i, 1))
                    settle(dve, s)
                    norm_dve(dve, s, n, i, z[:, :, :])

            @block.gpsimd
            def _(pool):
                pool.wait_ge(s.mean.sem, s.mean.at(0, 1))
                pool.tensor_tensor(rms[:, :], ms[:, :], net.neghalf[:, 0:NT], ALU.pow).then_inc(s.rms.sem, 1)
                pool.wait_ge(s.slots.sem, s.slots.at(0, 1))
                pool.wait_ge(net.zeroed, net.zero_ready)
                for k in range(2):
                    for t in range(NT):
                        pool.indirect_dma_start(net.slots[1], bass.IndirectOffsetOnAxis(ap=scatter[:, k, t:t + 1], axis=0),
                                                net.x_tok[:, t * P:(t + 1) * P], None).then_inc(moved, 16)
                for half in stored:
                    pool.wait_ge(half, 16 * 2 * E2 // 2)
                for k, to in enumerate((yg1, yg2)):
                    for t in range(NT):
                        pool.indirect_dma_start(to[:, t, :], None, net.slots_out[1],
                                                bass.IndirectOffsetOnAxis(ap=gather[:, k, t:t + 1], axis=0)).then_inc(fetched, 16)
                with pool.Fori(0, B) as i:
                    norm_pool(pool, s, n, i)

            @block.sync
            def _(sp):
                sp.wait_ge(moved, 16 * 2 * NT)
                sp.dma_start(rows[:, :, :], net.slots[1][0:SLOTS, :].rearrange("(k p) d -> p k d", p=P)).then_inc(net.rows_in, 16)
                for e in range(E2):
                    sp.wait_ge(s.y_sb.sem, s.y_sb.at(0, e + 1))
                    at = e * C2
                    sp.dma_start(net.slots_out[1][at:at + 2 * P, :].rearrange("(k p) d -> p k d", p=P), y[:, e % 2, 0:2, :]).then_inc(stored[e % 2], 16)
                    sp.dma_start(net.slots_out[1][at + 2 * P:at + C2, :], y[0:C2 - 2 * P, e % 2, 2, :]).then_inc(stored[e % 2], 16)
    close_stage(nc, net.pool)


def stage_decayed_attention(nc, net, io):
    with ExitStack() as ctx:
        sb = lambda name, shape: ctx.enter_context(nc.sbuf_tensor(net.name(name), shape, F32))
        a = attend_buffers(ctx, nc, net, RH, RDH, RDH ** -0.5, net.tab("causal").rearrange("p (t k) -> p t k", t=TPB), net.cmask16,
                           ring=(2, 3, 4), out=(6,), tail=1)
        n = norm_buffers(ctx, nc, net)
        xs, x_old = sb("xs", [P, L]), sb("x_old", [P, L])
        xi, rate = sb("xi", [P, RH]), sb("rate", [P, RH // 2])
        W, CH = 32, RH // HPG
        qk = sb("qk_wide", [P, TPB, 2, RH, W])
        prod = sb("prod", [P, 4, 8, 2, RDH // 2])
        q16, k16 = (ctx.enter_context(nc.sbuf_tensor(net.name(k), [P, CH, L], BF16)) for k in ("q16", "k16"))
        v = sb("v", [P, 2, TPB, RH, RDH + 1])
        free = [w[:, :, :].rearrange("p e f -> p (e f)") for w in net.moe_w]
        kT = [free[p][:, 0:HPG * CH * L].rearrange("p (y c t) -> p y c t", y=HPG, c=CH) for p in range(2)]
        qT = [free[2][:, p * CH * L:(p + 1) * CH * L].rearrange("p (c t) -> p c t", c=CH) for p in range(2)]
        o, oT = sb("o", [P, TPB, D]), sb("oT", [P, L])
        s = open_stage(nc, net.pool, "clear:1 rate0:1 rate:1 decay:1 xs_ready:1 x_old:1 front_ps:6 plain:2 v_ready:2 products:2 wide:2 "
                       "qkT:4 oT_ps:1 oT_ready:1 " + attend_spec(RH) + NORM.replace("settled:0 ", ""))
        bank, ident = net.bank, net.tab("ident")
        front_bank = lambda k: bank[(0, 1, 5)[k % 3]]
        oT_bank, y_bank = bank[5], bank[7]
        tiles = lambda k: net.tab(k).rearrange("p (t k) -> p t k", t=TPB)
        rcos, rsin = tiles("rcos"), tiles("rsin")
        with nc.Block() as block:
            @block.sync
            def _(sp):
                sp.dma_start(xi[:, :], io["L3_attn_log_xi"].partition_broadcast(P)).then_inc(net.ld_xi, 16)

            @block.gpsimd
            def _(pool):
                pool.memset(qk[:, :, :, :, :], 0.0).then_inc(s.clear.sem, 1)
                pool.memset(v[:, :, :, :, RDH:RDH + 1], 1.0)
                pool.memset(a.top_parts[:, :, :], 0.0)
                pool.memset(kT[0][:, :, :, :], 0.0)
                pool.memset(kT[1][:, :, :, :], 0.0).then_inc(s.clear.sem, 1)
                with pool.Fori(0, B) as i:
                    norm_pool(pool, s, n, i)

            @block.tensor
            def _(pe):
                pe.wait_ge(net.ld_w3, net.w3_ready)

                def project(i):
                    pe.wait_ge(s.qkT.sem, s.qkT.at(i, 0))
                    pe.wait_ge(s.xs_ready.sem, s.xs_ready.at(i, 1))
                    for t in range(TPB):
                        pe.matmul(front_bank(t)[:, 0:3 * D], xs[:, t * P:(t + 1) * P], net.w_qkv3[:, :], start=True, stop=True)\
                            .then_inc(s.front_ps.sem, 1)

                def turn(i, t):
                    pe.wait_ge(s.wide.sem, s.wide.at(i, t + 1))
                    pe.wait_ge(s.v_ready.sem, s.v_ready.at(i, TPB))
                    pe.wait_ge(s.products.sem, s.products.at(i, TPB))
                    for j in range(2):
                        if t == 1 and j == 1:
                            pe.wait_ge(s.qkT.sem, s.qkT.at(i, 1))
                        to = front_bank(2 + 2 * t + j)
                        for c in range(CH):
                            last = pe.transpose(to[:, c * P:(c + 1) * P], qk[:, t, j, HPG * c:HPG * (c + 1), :].rearrange("p h w -> p (h w)"), ident)
                        last.then_inc(s.front_ps.sem, 1)

                row = lambda h: slice(W * (h % HPG), W * (h % HPG) + W)
                q16_at = lambda h, at, w: q16[row(h), h // HPG, at:at + w]
                k16_at = lambda h, at, w: k16[row(h), h // HPG, at:at + w]

                def front(i):
                    project(i)
                    for t in range(TPB):
                        turn(i, t)
                    pe.wait_ge(s.qkT.sem, s.qkT.at(i, 4))
                    for h in range(RH):
                        scores_pe(pe, s, a, net, i, h, q16_at, k16_at)
                    top_pe(pe, s, a, net, i)

                def turn_output(i):
                    pe.wait_ge(s.o_ready.sem, s.o_ready.at(i, 1))
                    for t in range(TPB):
                        last = pe.transpose(oT_bank[:, t * P:(t + 1) * P], o[:, t, :], ident)
                    last.then_inc(s.oT_ps.sem, 1)

                def output(i):
                    pe.wait_ge(s.oT_ready.sem, s.oT_ready.at(i, 1))
                    pe.wait_ge(s.x_old.sem, s.x_old.at(i, 1))
                    pe.wait_ge(s.x_updated.sem, s.x_updated.at(i, 0))
                    for t in range(TPB):
                        tok = slice(t * P, (t + 1) * P)
                        pe.matmul(y_bank[:, tok], oT[:, tok], net.w_o3[:, :], start=True, stop=False)
                        last = pe.matmul(y_bank[:, tok], x_old[:, tok], ident, start=False, stop=True)
                    last.then_inc(s.y_ready.sem, 1)

                def run(i, p, ahead, behind):
                    q_at = lambda h, at, w: qT[p][:, h // HPG, at:at + w]
                    k_at = lambda h, at, w: kT[p][:, h % HPG, h // HPG, at:at + w]
                    v_at = lambda kb, h: v[:, p, kb, h, :]
                    if ahead:
                        project(i + 1)
                    pe.wait_ge(s.v_ready.sem, s.v_ready.at(i, TPB))
                    for k in range(3 * a.R):
                        shifted_pe(pe, s, a, net, i, k, (), q_at, k_at)
                        if behind and k == 1:
                            turn_output(i - 1)
                        if behind and k == 3:
                            output(i - 1)
                        if ahead and k in (5, 7):
                            turn(i + 1, (k - 5) // 2)
                        if k in (5, 8, 11):
                            mix_pe(pe, s, a, i, (k - 5) // 3, v_at)
                        if behind and k == 9:
                            norm_pe(pe, s, n, i - 1, y_bank[:, L:2 * L])
                    if ahead:
                        pe.wait_ge(s.qkT.sem, s.qkT.at(i + 1, 4))
                    for h in range(RH):
                        if ahead:
                            scores_pe(pe, s, a, net, i + 1, h, q16_at, k16_at)
                        if h == 0:
                            mix_pe(pe, s, a, i, a.R - 1, v_at)
                    if ahead:
                        top_pe(pe, s, a, net, i + 1)

                front(0)
                run(0, 0, True, False)
                with pe.Fori(0, B // 2 - 1) as j:
                    run(2 * j + 1, 1, True, True)
                    run(2 * j + 2, 0, True, True)
                run(B - 1, 1, False, True)
                turn_output(B - 1)
                output(B - 1)
                norm_pe(pe, s, n, B - 1, y_bank[:, L:2 * L])

            @block.scalar
            def _(act):
                act.wait_ge(net.ld_xi, 16)
                act.activation(xi[:, :], xi[:, :], ACT.Exp, scale=-1.0).then_inc(s.rate0.sem, 1)
                act.wait_ge(s.clear.sem, s.clear.at(0, 2))

                def take(i, p):
                    act.activation(xs[:, :], net.xT[:, bass.ds(i * L, L)], ACT.Copy).then_inc(s.xs_ready.sem, 1)
                    act.wait_ge(s.front_ps.sem, s.front_ps.at(i, 0))
                    for t in range(TPB):
                        act.wait_ge(s.front_ps.sem, s.front_ps.at(i, t + 1))
                        src = front_bank(t)[:, 0:2 * D].rearrange("p (g y d) -> p g y d", y=HPG, d=RDH)
                        dst = qk[:, t, :, :, 0:RDH].rearrange("p j (g y) d -> p (j g) y d", y=HPG)
                        for y in range(2):
                            last = act.activation(dst[:, :, y, :], src[:, :, y, :], ACT.Copy)
                        last.then_inc(s.plain.sem, 1)
                        act.activation(v[:, p, t, :, 0:RDH], front_bank(t)[:, 2 * D:3 * D].rearrange("p (h d) -> p h d", d=RDH), ACT.Copy)\
                            .then_inc(s.v_ready.sem, 1)

                def copy_qk(i, p, t, j):
                    tok = slice(t * P, (t + 1) * P)
                    act.wait_ge(s.front_ps.sem, s.front_ps.at(i, 3 + 2 * t + j))
                    of = front_bank(2 + 2 * t + j)[:, :].rearrange("p (c t) -> p c t", t=P)
                    if j == 0:
                        act.activation(q16[:, :, tok], of, ACT.Copy)
                        last = act.activation(qT[p][:, :, tok], of, ACT.Copy)
                    else:
                        act.activation(k16[:, :, tok], of, ACT.Copy)
                        for y in range(HPG):
                            row = slice(W * y, W * (y + 1))
                            last = act.activation(kT[p][row, y, :, tok], of[row], ACT.Copy)
                    last.then_inc(s.qkT.sem, 1)

                def front(i, p):
                    take(i, p)
                    for t in range(TPB):
                        for j in range(2):
                            copy_qk(i, p, t, j)
                    top_row_act(act, s, a, i)

                def keep_old(i):
                    act.wait_ge(s.y_ready.sem, s.y_ready.at(i, 0))
                    settle(act, s)
                    act.activation(x_old[:, :], net.xT[:, bass.ds(i * L, L)], ACT.Copy).then_inc(s.x_old.sem, 1)

                def copy_output(i):
                    act.wait_ge(s.oT_ps.sem, s.oT_ps.at(i, 1))
                    act.activation(oT[:, :], oT_bank[:, 0:L], ACT.Copy).then_inc(s.oT_ready.sem, 1)

                def run(i, p, ahead, behind):
                    if ahead:
                        take(i + 1, 1 - p)
                    if behind:
                        keep_old(i - 1)
                    for k in range(3 * a.R):
                        exp_act(act, s, a, i, k)
                        if behind and k == 1:
                            copy_output(i - 1)
                        if ahead and k in (5, 6, 7, 8):
                            copy_qk(i + 1, 1 - p, (k - 5) // 2, (k - 5) % 2)
                        if behind and k == 10:
                            norm_act(act, s, i - 1, y_bank[:, L:2 * L], net.xT[:, bass.ds((i - 1) * L, L)])
                    if ahead:
                        top_row_act(act, s, a, i + 1)

                front(0, 0)
                run(0, 0, True, False)
                with act.Fori(0, B // 2 - 1) as j:
                    run(2 * j + 1, 1, True, True)
                    run(2 * j + 2, 0, True, True)
                run(B - 1, 1, False, True)
                keep_old(B - 1)
                copy_output(B - 1)
                norm_act(act, s, B - 1, y_bank[:, L:2 * L], net.xT[:, (B - 1) * L:B * L])

            @block.vector
            def _(dve):
                dve.wait_ge(s.rate0.sem, s.rate0.at(0, 1))
                dve.tensor_scalar(rate[:, :], xi[:, 1:RH:2], RDH ** 0.5, None, ALU.mult).then_inc(s.rate.sem, 1)
                dve.wait_ge(s.rate.sem, s.rate.at(0, 1))
                dve.wait_ge(s.clear.sem, s.clear.at(0, 1))
                for t in range(TPB):
                    pos = net.tab("pos")[:, t:t + 1]
                    dve.tensor_scalar(qk[:, t, 0, 1:RH:2, RDH + 1], rate[:, :], pos, -1.0, ALU.mult, ALU.mult)
                    dve.tensor_scalar(qk[:, t, 1, 1:RH:2, RDH], rate[:, :], pos, None, ALU.mult)
                    dve.memset(qk[:, t, 0, 1:RH:2, RDH], 1.0)
                    last = dve.memset(qk[:, t, 1, 1:RH:2, RDH + 1], 1.0)
                last.then_inc(s.decay.sem, 1)
                dve.wait_ge(s.decay.sem, s.decay.at(0, 1))
                HR = RDH // 2
                y = y_bank[:, 0:L].rearrange("p (t d) -> p t d", d=D)

                def rotate(i):
                    dve.wait_ge(s.front_ps.sem, s.front_ps.at(i, 0))
                    for t in range(TPB):
                        dve.wait_ge(s.v_ready.sem, s.v_ready.at(i, t + 1))
                        src = front_bank(t)[:, 0:2 * D].rearrange("p (g y e x) -> p g y e x", g=8, y=HPG, x=2)
                        ev, od = src[:, :, 2:4, :, 0], src[:, :, 2:4, :, 1]
                        cos, sin = (x[:, t, :].unsqueeze(1).unsqueeze(1).to_broadcast([P, 8, 2, HR]) for x in (rcos, rsin))
                        dve.wait_ge(s.wide.sem, s.wide.at(i, t))
                        dve.tensor_tensor(prod[:, 0, :, :, :], ev, cos, ALU.mult)
                        dve.tensor_tensor(prod[:, 1, :, :, :], od, sin, ALU.mult)
                        dve.tensor_tensor(prod[:, 2, :, :, :], ev, sin, ALU.mult)
                        dve.tensor_tensor(prod[:, 3, :, :, :], od, cos, ALU.mult).then_inc(s.products.sem, 1)
                        dve.wait_ge(s.products.sem, s.products.at(i, t + 1))
                        dst = qk[:, t, :, :, 0:RDH].rearrange("p j h (e x) -> p (j h) e x", x=2).rearrange("p (g y) e x -> p g y e x", y=HPG)
                        dve.tensor_tensor(dst[:, :, 2:4, :, 0], prod[:, 0, :, :, :], prod[:, 1, :, :, :], ALU.subtract)
                        dve.tensor_tensor(dst[:, :, 2:4, :, 1], prod[:, 2, :, :, :], prod[:, 3, :, :, :], ALU.add).then_inc(s.wide.sem, 1)

                def run(i, p, ahead, behind):
                    if ahead:
                        rotate(i + 1)
                    if behind:
                        norm_dve(dve, s, n, i - 1, y)
                    if ahead:
                        scores_dve(dve, s, a, net, i + 1)
                    normalise_dve(dve, s, a, i, o[:, :, :].rearrange("p t (h d) -> p (t h) d", h=RH), s.oT_ps)

                rotate(0)
                scores_dve(dve, s, a, net, 0)
                run(0, 0, True, False)
                with dve.Fori(0, B // 2 - 1) as j:
                    run(2 * j + 1, 1, True, True)
                    run(2 * j + 2, 0, True, True)
                run(B - 1, 1, False, True)
                norm_dve(dve, s, n, B - 1, y)
    close_stage(nc, net.pool)


def stage_ternary(nc, net, io, out):
    with ExitStack() as ctx:
        sb = lambda name, shape: ctx.enter_context(nc.sbuf_tensor(net.name(name), shape, F32))
        n = norm_buffers(ctx, nc, net, keep=True)
        w, pos, neg, mag, wT = (sb(k, [P, P]) for k in ("weight", "above", "below", "magnitude", "ternaryT"))
        xs = sb("xs", [P, L])
        part_sum, delta, mdelta, alpha, bias = sb("abs_sum", [P, 1]), sb("delta", [P, 1]), sb("minus_delta", [P, 1]), sb("alpha", [P, 1]), sb("bias", [1, D])
        s = open_stage(nc, net.pool, "mag:1 v:8 mean_ps:1 tern:1 wT_ps:1 wT:1 xs_ready:1 " + NORM)
        bank, ident = net.bank, net.tab("ident")
        with nc.Block() as block:
            @block.sync
            def _(sp):
                sp.dma_start(w[:, :], io["L3_ffn_weight"]).then_inc(net.ld_t, 16)
                sp.dma_start(alpha[:, :], io["L3_ffn_alpha"].partition_broadcast(P)).then_inc(net.ld_t, 16)
                sp.dma_start(bias[:, :], io["L3_ffn_bias"].rearrange("(o d) -> o d", o=1)).then_inc(net.ld_t, 16)
                sp.wait_ge(s.kept.sem, s.kept.at(B - 1, 1))
                sp.dma_start(out.rearrange("b (t p) d -> p (b t) d", p=P), net.x_tok[:, :].rearrange("p (t d) -> p t d", d=D)).then_inc(net.out_done, 16)
                sp.wait_ge(net.out_done, 16)

            @block.gpsimd
            def _(pool):
                with pool.Fori(0, B) as i:
                    norm_pool(pool, s, n, i)

            @block.scalar
            def _(act):
                act.wait_ge(net.ld_t, 48)
                act.activation(mag[:, :], w[:, :], ACT.Abs, accum_out=part_sum[:, :]).then_inc(s.mag.sem, 1)
                act.wait_ge(s.wT_ps.sem, s.wT_ps.at(0, 1))
                act.activation(wT[:, :], bank[1][:, 0:P], ACT.Copy).then_inc(s.wT.sem, 1)
                with act.Fori(0, B) as i:
                    act.wait_ge(s.y_ready.sem, s.y_ready.at(i, 0))
                    act.activation(xs[:, :], net.xT[:, bass.ds(i * L, L)], ACT.Copy).then_inc(s.xs_ready.sem, 1)

            @block.tensor
            def _(pe):
                pe.wait_ge(s.mag.sem, s.mag.at(0, 1))
                pe.matmul(bank[0][:, 0:1], net.tab("ones"), part_sum[:, :], start=True, stop=True).then_inc(s.mean_ps.sem, 1)
                pe.wait_ge(s.tern.sem, s.tern.at(0, 1))
                pe.transpose(bank[1][:, 0:P], pos[:, :], ident).then_inc(s.wT_ps.sem, 1)
                pe.wait_ge(s.wT.sem, s.wT.at(0, 1))
                with pe.Fori(0, B) as i:
                    pe.wait_ge(s.xs_ready.sem, s.xs_ready.at(i, 1))
                    pe.wait_ge(s.xn_ready.sem, s.xn_ready.at(i, 0))
                    for t in range(TPB):
                        tok = slice(t * P, (t + 1) * P)
                        pe.matmul(bank[2][:, tok], xs[:, tok], wT[:, :], start=True, stop=False)
                        pe.matmul(bank[2][:, tok], net.tab("ones")[0:1, :], bias[:, :], start=False, stop=False)
                        last = pe.matmul(bank[2][:, tok], xs[:, tok], ident, start=False, stop=True)
                    last.then_inc(s.y_ready.sem, 1)

            @block.vector
            def _(dve):
                dve.wait_ge(s.mean_ps.sem, s.mean_ps.at(0, 1))
                v = s.v
                dve.tensor_scalar(delta[:, :], bank[0][:, 0:1], 1.0 / (D * D), 0.7, ALU.mult, ALU.mult)
                dve.tensor_scalar(mdelta[:, :], bank[0][:, 0:1], 1.0 / (D * D), -0.7, ALU.mult, ALU.mult).then_inc(v.sem, 1)
                dve.wait_ge(v.sem, v.at(0, 1))
                dve.tensor_scalar(pos[:, :], w[:, :], delta[:, :], None, ALU.is_gt)
                dve.tensor_scalar(neg[:, :], w[:, :], mdelta[:, :], None, ALU.is_lt).then_inc(v.sem, 1)
                dve.wait_ge(v.sem, v.at(0, 2))
                dve.tensor_tensor(pos[:, :], pos[:, :], neg[:, :], ALU.subtract).then_inc(v.sem, 1)
                dve.wait_ge(v.sem, v.at(0, 3))
                dve.tensor_scalar(pos[:, :], pos[:, :], alpha[:, :], None, ALU.mult).then_inc(s.tern.sem, 1)
                with dve.Fori(0, B) as i:
                    norm_dve(dve, s, n, i, bank[2][:, 0:L].rearrange("p (t d) -> p t d", d=D), turned=False)
    close_stage(nc, net.pool)


def network(nc, io, out):
    at, width = table_layout()
    with ExitStack() as ctx:
        sb = lambda name, shape: ctx.enter_context(nc.sbuf_tensor(name, shape, F32))
        net = Shared()
        net.count = 0

        def name(base):
            net.count += 1
            return f"{base}_{net.count}"
        net.name = name
        net.tabs = sb("tabs", [P, width])
        net.tab = lambda n: net.tabs[:, at[n][0]:at[n][0] + at[n][1]]
        net.xT, net.x_tok = sb("xT", [P, T]), sb("x_tok", [P, T])
        net.neghalf, net.half, net.eps = sb("neghalf", [P, 64]), sb("half", [P, 64]), sb("eps", [P, 64])
        net.ident16, net.lmask16, net.cmask16 = (ctx.enter_context(nc.sbuf_tensor(k, [P, w], mybir.dt.bfloat16)) for k, w in (
            ("ident16", P), ("lmask16", L + P), ("cmask16", L + P)))
        net.pick16 = ctx.enter_context(nc.sbuf_tensor("pick16", [P, PART], mybir.dt.bfloat16))
        net.bank = [ctx.enter_context(nc.psum_tensor(f"bank{k}", [P, 512], F32)) for k in range(8)]
        sem = lambda name: ctx.enter_context(nc.semaphore(name))
        net.ld_x, net.ld_w, net.ld_moe, net.ld_a, net.out_done = (sem(n) for n in ("ld_x", "ld_w", "ld_moe", "ld_a", "out_done"))
        net.pool = [sem(f"stage_signal_{k}") for k in range(60)]
        net.loads_sp, net.loads_act = [], []
        net.ld_s, net.ld_s_count = sem("ld_s"), 0
        net.xw = sb("x_work", [P, T])
        col = lambda ap: ap.rearrange("(c p) -> p c", p=P)
        small = {}
        for l in range(DEPTH):
            for key, width_ in (("ln_g", 1), ("ln_b", 1), ("b1a", 3), ("b1g", 3), ("b2", 1)):
                small[key, l] = sb(f"{key}_{l}", [P, width_])
            for key, nm in (("ln_g", "L0_ffn_ln_g"), ("ln_b", "L0_ffn_ln_b"), ("b2", "L0_ffn_b2")):
                net.loads_sp.append((small[key, l][:, :], col(io[nm][l])))
            for c, (a0, w) in enumerate(HCH):
                for key, off in (("b1a", 0), ("b1g", HID)):
                    net.loads_sp.append((small[key, l][0:w, c:c + 1], io["L0_ffn_b1"][l, off + a0:off + a0 + w].rearrange("(w o) -> w o", o=1)))
        net.small = lambda key, l: small[key, l][:, :]
        net.w_in, net.w_out, net.w_xproj = sb("w_in", [P, 2 * DIN]), sb("w_out", [P, 2, D]), sb("w_xproj", [P, 2, XP])
        net.conv_w, net.conv_b, net.w_dt = sb("conv_w", [P, 2, NCONV]), sb("conv_b", [P, 2]), sb("w_dt", [1, DIN])
        net.b_dt, net.a_log, net.d_par = sb("b_dt", [P, 2]), sb("a_log", [P, 2, NS]), sb("d_par", [P, 2])
        halves = lambda ap: ap.rearrange("(c p) n -> p c n", p=P)
        net.loads_sp += [(net.w_in[:, :], io["L1_attn_W_in"]), (net.w_out[:, :, :], halves(io["L1_attn_W_out"])),
                         (net.w_xproj[:, :, :], halves(io["L1_attn_W_xproj"])),
                         (net.conv_w[:, :, :], halves(io["L1_attn_conv_w"].rearrange("d o k -> d (o k)"))),
                         (net.conv_b[:, :], col(io["L1_attn_conv_b"])), (net.b_dt[:, :], col(io["L1_attn_b_dt"])),
                         (net.d_par[:, :], col(io["L1_attn_D_param"])), (net.a_log[:, :, :], halves(io["L1_attn_A_log"])),
                         (net.w_dt[:, :], io["L1_attn_w_dt"].rearrange("(o d) -> o d", o=1))]
        net.w_router = sb("w_router", [P, E1])
        net.loads_sp.append((net.w_router[:, :], io["L1_ffn_w_router"]))
        net.moe_w = [sb(f"moe_w{k}", [P, E1, P]) for k in range(3)]
        net.loads_act = [(net.moe_w[k][:, :, :], io[nm].rearrange("e h f -> h e f"))
                         for k, nm in enumerate(("L1_ffn_w_gate", "L1_ffn_w_up", "L1_ffn_w_down"))]
        net.moved, net.stored, net.fetched, net.rows_in, net.zeroed = (sem(k) for k in ("moved", "stored", "fetched", "rows_in", "zeroed"))
        net.slots = [nc.dram_tensor(f"slots{k}", [SLOTS + (k + 1) * T, D], F32, kind="Internal").ap() for k in range(2)]
        net.slots_out = [nc.dram_tensor(f"slots_out{k}", [SLOTS, D], F32, kind="Internal").ap() for k in range(2)]
        net.zero = sb("zero", [P, 512])
        net.loads2, net.loads3 = [], []
        net.ld_w2, net.ld_w3, net.moved2, net.fetched2, net.ld_xi, net.ld_t = (
            sem(k) for k in ("ld_w2", "ld_w3", "moved2", "fetched2", "ld_xi", "ld_t"))
        net.stored2 = [sem(f"stored2_{k}") for k in range(2)]
        net.zero_ready = 16 * 2 * (SLOTS // 512)
        first_layer = ExitStack()
        fb = lambda name, shape: first_layer.enter_context(nc.sbuf_tensor(name, shape, F32))
        net.wqkv = [fb(f"wqkv{l}", [P, 3 * INNER]) for l in range(DEPTH)]
        net.wo = [fb(f"wo{l}", [P, INNER // P, D]) for l in range(DEPTH)]
        for l in range(DEPTH):
            net.loads_sp += [(net.wqkv[l][:, :], io["L0_ffn_wqkv"][l]),
                             (net.wo[l][:, :, :], io["L0_ffn_wo"][l].rearrange("(c p) d -> p c d", p=P))]
        net.w1 = [fb(f"w1_{l}", [P, 2 * HID]) for l in range(DEPTH)]
        net.w2 = [fb(f"w2_{l}", [P, len(HCH), D]) for l in range(DEPTH)]
        for l in range(DEPTH):
            net.loads_sp.append((net.w1[l][:, :], io["L0_ffn_w1"][l]))
            for c, (a0, w) in enumerate(HCH):
                net.loads_sp.append((net.w2[l][0:w, c, :], io["L0_ffn_w2"][l, a0:a0 + w, :]))
        net.w_ready = 16 * len(net.loads_sp)
        stage_load(nc, net, io)
        stage_recurrence(nc, net, io)
        stage_local_attention(nc, net, io, 0, net.xT, net.xw)
        stage_gated_mlp(nc, net, io, 0, net.xw, False)
        stage_local_attention(nc, net, io, 1, net.xw, net.xw)
        stage_gated_mlp(nc, net, io, 1, net.xw, True)
        first_layer.close()
        with ExitStack() as scope:
            xc, sz = (scope.enter_context(nc.sbuf_tensor(k, [P, 2, T], F32)) for k in ("xc", "silu_z"))
            stage_scan_inputs(nc, net, io, xc, sz)
            stage_scan(nc, net, io, xc, sz)
        net.router2, net.sg, net.su, net.sd = sb("router2", [P, E2]), sb("sg", [P, IS]), sb("su", [P, IS]), sb("sd", [P, IS // P, D])
        net.w_qkv3, net.w_o3 = sb("w_qkv3", [P, 3 * D]), sb("w_o3", [P, D])
        stage_switch_experts(nc, net, io)
        second = ExitStack()
        w = second_weights(nc, net, io, second)
        split = lambda ap: ap.rearrange("p (s j) -> p j s", j=NL)
        joined = lambda ap: ap.rearrange("p (j s) -> p j s", j=NL)
        back = lambda ap: ap.rearrange("p (j s) -> p s j", j=NL)
        rows = lambda ap: ap.rearrange("p (s j) -> p s j", j=NL)
        stage_mha(nc, net, w["la"], None, net.xT, net.xw, net.loads2 + net.loads3)
        stage_relu_mlp(nc, net, w["lf"], net.xw, False, split, joined)
        stage_mha(nc, net, w["sa"], net.tab("blk8"), net.xw, net.xw)
        stage_relu_mlp(nc, net, w["pf"], net.xw, True, back, rows)
        second.close()
        stage_top2_experts(nc, net, io)
        stage_decayed_attention(nc, net, io)
        stage_ternary(nc, net, io, out)


def second_weights(nc, net, io, scope):
    sb = lambda name, shape: scope.enter_context(nc.sbuf_tensor(name, shape, F32))
    col = lambda ap: ap.rearrange("(c p) -> p c", p=P)
    row = lambda ap: ap.rearrange("(o d) -> o d", o=1)
    pre = "L2_attn_"
    w = {}
    for k in ("la", "sa"):
        w[k] = m = group(q=sb(k + "_q", [P, AH * ADK]), k=sb(k + "_k", [P, AH * ADK]), v=sb(k + "_v", [P, AH * ADK]),
                                   p=sb(k + "_p", [P, AH * ADK // P, D]), pb=sb(k + "_pb", [1, D]), g=sb(k + "_g", [P, 1]), b=sb(k + "_b", [P, 1]))
        for to, nm in ((m.q, "_wqs"), (m.k, "_wks"), (m.v, "_wvs")):
            net.loads2.append((to[:, :].rearrange("d (h k) -> d h k", h=AH), io[pre + k + nm].rearrange("h d k -> d h k")))
        net.loads2 += [(m.p[:, :, :], io[pre + k + "_pw"].rearrange("(c p) d -> p c d", p=P)), (m.pb[:, :], row(io[pre + k + "_pb"]))]
    for k in ("lf", "pf"):
        w[k] = m = group(w1=sb(k + "_w1", [P, DI]), w2=sb(k + "_w2", [P, DI // P, D]), b1=sb(k + "_b1", [P, DI // P]),
                                   b2=sb(k + "_b2", [1, D]), g=sb(k + "_g", [P, 1]), b=sb(k + "_b", [P, 1]))
        net.loads2 += [(m.w1[:, :], io[pre + k + "_w1"]), (m.w2[:, :, :], io[pre + k + "_w2"].rearrange("(c p) d -> p c d", p=P)),
                       (m.b1[:, :], col(io[pre + k + "_b1"])), (m.b2[:, :], row(io[pre + k + "_b2"]))]
    for k, m in w.items():
        net.loads2 += [(m.g[:, :], col(io[pre + k + "_g"])), (m.b[:, :], col(io[pre + k + "_b"]))]
    net.loads2 = [(a, b, net.ld_w2) for a, b in net.loads2]
    net.w2_ready = 16 * len(net.loads2)
    f = "L2_ffn_"
    flat = lambda k: net.moe_w[k][:, :, :].rearrange("p e f -> p (e f)").rearrange("p (e i) -> p e i", e=E2)
    net.loads3 = [(flat(0), io[f + "rg"].rearrange("e h i -> h e i")), (flat(1), io[f + "ru"].rearrange("e h i -> h e i")),
                  (net.moe_w[2][:, :, :], io[f + "rd"].rearrange("e (c p) d -> p (e c) d", p=P)),
                  (net.router2[:, :], io[f + "router_w"].rearrange("e h -> h e")),
                  (net.sg[:, :], io[f + "sg"]), (net.su[:, :], io[f + "su"]),
                  (net.sd[:, :, :], io[f + "sd"].rearrange("(c p) d -> p c d", p=P)),
                  (net.w_qkv3[:, :], io["L3_attn_w_qkv"]), (net.w_o3[:, :], io["L3_attn_w_o"])]
    net.loads3 = [(a, b, net.ld_w3) for a, b in net.loads3]
    net.w3_ready = 16 * len(net.loads3)
    return w


_INS = [
    "L0_attn_x", "L0_attn_ig_w", "L0_attn_ig_b", "L0_attn_ag_w", "L0_attn_ag_b", "L0_attn_a_param",
    "L0_ffn_wqkv", "L0_ffn_q_scale", "L0_ffn_k_scale", "L0_ffn_wo", "L0_ffn_ln_g", "L0_ffn_ln_b", "L0_ffn_w1", "L0_ffn_b1",
    "L0_ffn_w2", "L0_ffn_b2",
    "L1_attn_W_in", "L1_attn_conv_w", "L1_attn_conv_b", "L1_attn_W_xproj", "L1_attn_w_dt", "L1_attn_b_dt", "L1_attn_A_log",
    "L1_attn_D_param", "L1_attn_W_out",
    "L1_ffn_w_router", "L1_ffn_w_gate", "L1_ffn_w_up", "L1_ffn_w_down",
    *(f"L2_attn_{a}_{k}" for a, ks in (("la", "wqs wks wvs pw pb g b"), ("lf", "w1 b1 w2 b2 g b"),
                                      ("sa", "wqs wks wvs pw pb g b"), ("pf", "w1 b1 w2 b2 g b")) for k in ks.split()),
    "L2_ffn_router_w", "L2_ffn_rg", "L2_ffn_ru", "L2_ffn_rd", "L2_ffn_sg", "L2_ffn_su", "L2_ffn_sd",
    "L3_attn_w_qkv", "L3_attn_w_o", "L3_attn_log_xi", "L3_ffn_weight", "L3_ffn_alpha", "L3_ffn_bias",
]


def kernel(**inputs):
    import numpy as _np
    import concourse.bacc as _bacc
    from concourse import mybir as _mybir
    from concourse.bass_utils import run_bass_kernel_spmd as _run

    nc = _bacc.Bacc("TRN2", target_bir_lowering=False, num_devices=1)
    arrays, io = {}, {}
    given = {name: inputs[name] for name in _INS}
    given["tables"] = _np.concatenate(list(tables().values()), axis=1)
    for name, a in given.items():
        a = _np.ascontiguousarray(a)
        arrays[f"in_{name}_dram"] = a
        io[name] = nc.dram_tensor(f"in_{name}_dram", a.shape, _mybir.dt.from_np(a.dtype), kind="ExternalInput").ap()
    out = nc.dram_tensor("out_0_dram", (B, L, D), _mybir.dt.float32, kind="ExternalOutput").ap()
    network(nc, io, out)
    r = _run(nc, [arrays], core_ids=[0])
    return r.results[0]["out_0_dram"]
```

```python
from collections import namedtuple
from contextlib import ExitStack

import numpy as np
import concourse.bass as bass
from concourse import mybir

F32 = mybir.dt.float32
I32 = mybir.dt.int32
BF16 = mybir.dt.bfloat16
ALU = mybir.AluOpType
ACT = mybir.ActivationFunctionType
AX = mybir.AxisListType

P = 128
B, L, D = 8, 256, 128
T = B * L
NT = T // P
TPB = L // P
EPS = 1e-5
NEG = -1e30

WIN, LH, LDH = 64, 8, 64
INNER = LH * LDH
DEPTH = 2
HID = int(D * 4 * 2 / 3)
HCH = [(0, 128), (128, 128), (256, HID - 256)]
QK_SCALE = 8.0
DIN, NS, NCONV = 2 * D, 16, 4
XP = 2 * NS + 1
E1, C1 = 32, (5 * T + 4 * 32 - 1) // (4 * 32)
E2, C2, IR, IS = 8, 5 * T // (4 * 8), 4 * D, 8 * D
SLOTS = E1 * C1
AH, ADK, NL, DI = 16, 64, 32, 512
RH, RDH = 16, 8


def group(**named):
    return namedtuple("Group", named)(**named)


class Signal:
    def __init__(self, sem, per):
        self.sem, self.per = sem, per

    def at(self, i, c):
        return i * self.per + c + 1


def settle(eng, s):
    eng.sem_inc(s.settled.sem, 1)


class Shared:
    pass


def open_stage(nc, pool, spec):
    signals = {}
    engines = (nc.sync, nc.scalar, nc.vector, nc.gpsimd)
    for k, (sem, word) in enumerate(zip(pool, spec.split(), strict=False)):
        name, per = word.split(":")
        engines[k % len(engines)].sem_inc(sem, 1)
        signals[name] = Signal(sem, int(per))
    assert len(signals) == len(spec.split())
    nc.all_engine_barrier()
    return group(**signals)


def close_stage(nc, pool):
    nc.all_engine_barrier(sems_to_clear=range(pool[0].num, pool[0].num + len(pool)))


def tables():
    f = np.float32
    out = {"ident": np.eye(P, dtype=f), "ones": np.ones((P, P), f)}
    half = np.arange(0, LDH, 2).astype(f)
    inv = (f(1.0) / f(10000.0) ** (half / f(LDH))).astype(f)
    t = np.arange(L).astype(f)
    fr = np.concatenate([t[:, None] * inv[None]] * 2, -1).astype(f)
    base = ((half + f(0.4 * LDH)) / f(1.4 * LDH)).astype(f)
    power = ((t - L // 2) / f(WIN // 2)).astype(f)
    sc = np.concatenate([base[None] ** power[:, None]] * 2, -1).astype(f)
    sign = np.where(np.arange(LDH) < LDH // 2, f(-1), f(1))
    rope = np.stack([np.cos(fr) * sc, np.sin(fr) * sc * sign, np.cos(fr) / sc, np.sin(fr) / sc * sign], 1)
    out["rope"] = rope.reshape(TPB, P, 4, LDH).transpose(1, 0, 2, 3).astype(f)
    q, k = np.arange(L)[:, None], np.arange(L)[None]
    ok = (k <= q) & (k >= q - WIN) & (k // WIN >= q // WIN - 1)
    by_query = lambda ok: np.where(ok, f(0), f(NEG)).reshape(TPB, P, L).transpose(1, 0, 2)
    by_key = lambda ok: np.concatenate([np.where(ok.T, f(0), f(NEG))[0:P], np.where(ok.T, f(0), f(NEG))[P:, P:]], 1)
    out["lmask"], out["lmaskT"] = by_query(ok), by_key(ok)
    p = np.arange(P)
    out["blk8"] = np.where(p[:, None] % NL // (L // NL) == np.arange(NL)[None] // (L // NL), f(0), f(NEG))
    out["causal"], out["causalT"] = by_query(k <= q), by_key(k <= q)
    out["pos"] = t.reshape(TPB, P).T
    iv = (f(10000.0) ** (-(np.arange(0, RDH, 2).astype(f) / f(RDH)))).astype(f)
    th = (t[:, None] * iv[None]).astype(f)
    out["rcos"] = np.cos(th).reshape(TPB, P, RDH // 2).transpose(1, 0, 2)
    out["rsin"] = np.sin(th).reshape(TPB, P, RDH // 2).transpose(1, 0, 2)
    out["tri"] = (p[:, None] <= p[None]).astype(f)
    out["iota32"] = np.broadcast_to(np.arange(E1) - 64, (P, E1))
    out["trash"] = SLOTS + p[:, None] + P * np.arange(2 * NT)[None]
    return {n: np.ascontiguousarray(a.reshape(P, -1), dtype=f) for n, a in out.items()}


def table_layout():
    at, off = {}, 0
    for n, a in tables().items():
        at[n] = (off, a.shape[1])
        off += a.shape[1]
    return at, off


NORM = "settled:0 y_ready:1 stats:1 agg:1 var_eps:1 rstd:1 xn_ready:1 xnT_ready:1 x_updated:1 kept:1"


def norm_dve(dve, s, n, i, y, turned=True):
    norm_stats(dve, s, n, i, y)
    norm_apply(dve, s, n, i, y, turned)


def norm_stats(dve, s, n, i, y):
    if n.in_psum:
        dve.wait_ge(s.y_ready.sem, s.y_ready.at(i, 1))
    for t in range(TPB):
        last = dve.bn_stats(n.st[:, t, :], y[:, t, :])
    last.then_inc(s.stats.sem, 1)
    dve.wait_ge(s.stats.sem, s.stats.at(i, 1))
    dve.wait_ge(s.rstd.sem, s.rstd.at(i, 0))
    settle(dve, s)
    for t in range(TPB):
        last = dve.bn_aggr(n.mv[:, t, :], n.st[:, t, :])
    last.then_inc(s.agg.sem, 1)


def norm_apply(dve, s, n, i, y, turned=True):
    dve.wait_ge(s.rstd.sem, s.rstd.at(i, 1))
    if turned:
        dve.wait_ge(s.xnT_ready.sem, s.xnT_ready.at(i, 0))
    if n.keep:
        dve.wait_ge(s.kept.sem, s.kept.at(i, 0))
    for t in range(TPB):
        last = dve.tensor_scalar(n.xn[:, t, :], y[:, t, :], n.mv[:, t, 0:1], n.rstd[:, t:t + 1],
                                 ALU.subtract, ALU.mult)
    last.then_inc(s.xn_ready.sem, 1)


def norm_pool(pool, s, n, i):
    norm_rstd(pool, s, n, i)
    if n.keep:
        pool.wait_ge(s.xn_ready.sem, s.xn_ready.at(i, 1))
        settle(pool, s)
        pool.tensor_copy(n.x_tok[:, bass.ds(i * L, L)], n.xn[:, :, :].rearrange("p t d -> p (t d)"))\
            .then_inc(s.kept.sem, 1)


def norm_rstd(pool, s, n, i):
    pool.wait_ge(s.agg.sem, s.agg.at(i, 1))
    pool.tensor_tensor(n.ve[:, :], n.mv[:, :, 1], n.eps[:, 0:TPB], ALU.add).then_inc(s.var_eps.sem, 1)
    pool.wait_ge(s.var_eps.sem, s.var_eps.at(i, 1))
    pool.wait_ge(s.xn_ready.sem, s.xn_ready.at(i, 0))
    pool.tensor_tensor(n.rstd[:, :], n.ve[:, :], n.neghalf[:, 0:TPB], ALU.pow).then_inc(s.rstd.sem, 1)


def norm_pe(pe, s, n, i, psT):
    pe.wait_ge(s.xn_ready.sem, s.xn_ready.at(i, 1))
    for t in range(TPB):
        last = pe.transpose(psT[:, t * P:(t + 1) * P], n.xn[:, t, :], n.ident)
    last.then_inc(s.xnT_ready.sem, 1)


def norm_act(act, s, i, psT, dst, scale=1.0, bias=0.0):
    act.wait_ge(s.xnT_ready.sem, s.xnT_ready.at(i, 1))
    settle(act, s)
    act.activation(dst, psT, ACT.Identity, scale=scale, bias=bias).then_inc(s.x_updated.sem, 1)


def norm_buffers(ctx, nc, net, keep=False, in_psum=True):
    sb = lambda name, shape: ctx.enter_context(nc.sbuf_tensor(net.name(name), shape, F32))
    return group(st=sb("n_st", [P, TPB, 6]), mv=sb("n_mv", [P, TPB, 2]), ve=sb("n_ve", [P, TPB]),
                           rstd=sb("n_rstd", [P, TPB]), xn=sb("n_xn", [P, TPB, D]), neghalf=net.neghalf, eps=net.eps,
                           ident=net.tab("ident"), x_tok=net.x_tok, keep=keep, in_psum=in_psum)


def skewed(eng, turn, behind):
    turn(-1, True, False, False)
    turn(0, True, True, False)
    with eng.Fori(1, B - 1) as i:
        turn(i, True, True, behind)
    turn(B - 1, False, True, behind)
    if behind:
        turn(B, False, False, True)


def stage_load(nc, net, io):
    s = open_stage(nc, net.pool, "xT_ps:4 xT_done:4 zero:1 in16:1 const:1 blocks0:1")
    with nc.Block() as block:
        @block.sync
        def _(sp):
            sp.dma_start(net.x_tok[:, :].rearrange("p (t d) -> p t d", d=D),
                         io["L0_attn_x"].rearrange("b (t p) d -> p (b t) d", p=P)).then_inc(net.ld_x, 16)
            sp.dma_start(net.tabs[:, :], io["tables"]).then_inc(net.ld_x, 16)
            wi, wa, bi, ba, ap_ = net.gates
            for dst, name in ((bi, "L0_attn_ig_b"), (ba, "L0_attn_ag_b")):
                sp.dma_start(dst[:, :], io[name].rearrange("h (w o) -> (h w) o", o=1)).then_inc(net.ld_a, 16)
            sp.dma_start(ap_[:, :], io["L0_attn_a_param"].rearrange("(w o) -> w o", o=1)).then_inc(net.ld_a, 16)
            sp.wait_ge(s.blocks0.sem, s.blocks0.at(0, 1))
            H, W = io["L0_attn_ig_w"].shape[0:2]
            for dst, name in ((wi, "L0_attn_ig_w"), (wa, "L0_attn_ag_w")):
                for h in range(H):
                    sp.dma_start(dst[h * W:(h + 1) * W, h * W:(h + 1) * W], io[name][h]).then_inc(net.ld_a, 16)

        @block.gpsimd
        def _(pool):
            pool.memset(net.zero[:, :], 0.0).then_inc(s.zero.sem, 1)
            for w in net.gates[0:2]:
                last = pool.memset(w[:, :], 0.0)
            last.then_inc(s.blocks0.sem, 1)
            pool.wait_ge(net.ld_x, 32)
            for to, of in ((net.ident16, "ident"), (net.lmask16, "lmaskT"), (net.cmask16, "causalT")):
                last = pool.tensor_copy(to[:, :], net.tab(of))
            last.then_inc(s.in16.sem, 1)
            pool.wait_ge(s.in16.sem, s.in16.at(0, 1))
            pool.tensor_tensor(net.pick16[:, :], net.ident16[:, 0:PART], net.ident16[:, PART:2 * PART], ALU.add)
            pool.memset(net.neghalf[:, :], -0.5)
            pool.memset(net.eps[:, :], EPS).then_inc(s.const.sem, 1)

        @block.scalar
        def _(act):
            for g in range(4):
                act.wait_ge(s.xT_ps.sem, s.xT_ps.at(0, g + 1))
                act.activation(net.xT[:, g * 512:(g + 1) * 512], net.bank[g][:, :], ACT.Copy).then_inc(s.xT_done.sem, 1)

        @block.tensor
        def _(pe):
            pe.wait_ge(net.ld_x, 32)
            for g in range(4):
                for t in range(4):
                    k = 4 * g + t
                    last = pe.transpose(net.bank[g][:, t * P:(t + 1) * P], net.x_tok[:, k * P:(k + 1) * P], net.tab("ident"))
                last.then_inc(s.xT_ps.sem, 1)
    close_stage(nc, net.pool)


def stage_recurrence(nc, net, io):
    with ExitStack() as ctx:
        sb = lambda name, shape: ctx.enter_context(nc.sbuf_tensor(net.name(name), shape, F32))
        gx, ga, a, m, p = (sb(n, [P, T]) for n in ("gx", "ga", "a_shift", "mult", "prefix"))
        first, later = sb("first", [P, T]), sb("later", [P, T])
        wi, wa, bi, ba, ap_ = net.gates
        t1, t2, c8, c16 = (sb(n, [P, 1]) for n in ("t1", "t2", "c8", "c16"))
        z = sb("z", [P, 2, L])
        n = norm_buffers(ctx, nc, net)
        ld = net.ld_a
        s = open_stage(nc, net.pool, "masks0:1 masks:1 gates_ps:8 gate_x:4 gate_a:4 soft:3 decay:1 decay2:1 "
                       "v:16 root:1 h_ready:1 z_ready:1 " + NORM)
        x3 = lambda ap: ap[:, :].rearrange("p (b t) -> p b t", t=L)
        H, W = io["L0_attn_ig_w"].shape[0:2]
        with nc.Block() as block:
            @block.sync
            def _(sp):
                with nc.allow_non_contiguous_dma(reason="a few hundred biases, one to a partition"):
                    for dst, src in net.loads_sp:
                        sp.dma_start(dst, src).then_inc(net.ld_w, 16)
                for dst, src in net.loads_moe:
                    sp.dma_start(dst, src).then_inc(net.ld_moe, 16)
                for buf in net.slots:
                    for k in range(SLOTS // 512):
                        sp.dma_start(buf[k * 512:(k + 1) * 512, :].rearrange("(p r) d -> p (r d)", p=P), net.zero[:, :]).then_inc(net.zeroed, 16)

            @block.gpsimd
            def _(pool):
                pool.memset(first[:, :], 0.0)
                pool.memset(later[:, :], 1.0).then_inc(s.masks0.sem, 1)
                pool.wait_ge(s.masks0.sem, s.masks0.at(0, 1))
                pool.memset(x3(first)[:, :, 0:1], 1.0)
                pool.memset(x3(later)[:, :, 0:1], 0.0)
                pool.memset(x3(a)[:, :, 0:1], 0.0).then_inc(s.masks.sem, 1)
                pool.wait_ge(s.h_ready.sem, s.h_ready.at(0, 1))
                with pool.Fori(0, B) as i:
                    norm_pool(pool, s, n, i)

            @block.tensor
            def _(pe):
                pe.wait_ge(ld, 16 * (3 + 2 * H))
                for j, w in enumerate((wi, wa)):
                    for g in range(4):
                        pe.matmul(net.bank[4 * j + g][:, :], w[:, :], net.xT[:, g * 512:(g + 1) * 512],
                                  start=True, stop=True).then_inc(s.gates_ps.sem, 1)
                pe.wait_ge(s.gate_a.sem, s.gate_a.at(0, 4))

                def turn_h(i, p):
                    pe.wait_ge(s.z_ready.sem, s.z_ready.at(i, 1))
                    for t in range(TPB):
                        last = pe.transpose(net.bank[p][:, t * P:(t + 1) * P], z[:, p, t * P:(t + 1) * P], net.tab("ident"))
                    last.then_inc(s.y_ready.sem, 1)

                turn_h(0, 0)
                turn_h(1, 1)
                with pe.Fori(0, B // 2 - 1) as j:
                    for p in range(2):
                        i = 2 * j + p
                        pe.wait_ge(s.x_updated.sem, s.x_updated.at(i, 0))
                        norm_pe(pe, s, n, i, net.bank[2][:, 0:L])
                        turn_h(i + 2, p)
                for i in (B - 2, B - 1):
                    pe.wait_ge(s.x_updated.sem, s.x_updated.at(i, 0))
                    norm_pe(pe, s, n, i, net.bank[2][:, 0:L])

            @block.scalar
            def _(act):
                act.wait_ge(ld, 16 * (3 + 2 * H))
                act.activation(t1[:, :], ap_[:, :], ACT.Abs).then_inc(s.soft.sem, 1)
                act.wait_ge(s.soft.sem, s.soft.at(0, 1))
                act.activation(t2[:, :], t1[:, :], ACT.Exp, scale=-1.0).then_inc(s.soft.sem, 1)
                act.wait_ge(s.soft.sem, s.soft.at(0, 2))
                act.activation(t1[:, :], t2[:, :], ACT.Ln, bias=1.0).then_inc(s.soft.sem, 1)
                for j, (dst, bias, done) in enumerate(((ga, ba, s.gate_a), (gx, bi, s.gate_x))):
                    for g in range(4):
                        act.wait_ge(s.gates_ps.sem, s.gates_ps.at(0, 8 if j == 0 else 8))
                        act.activation(dst[:, g * 512:(g + 1) * 512], net.bank[4 * (1 - j) + g][:, :], ACT.Sigmoid,
                                       bias=bias[:, :]).then_inc(done.sem, 1)
                act.wait_ge(s.gate_a.sem, s.gate_a.at(0, 4))
                act.wait_ge(s.v.sem, s.v.at(0, 3))
                act.wait_ge(s.masks.sem, s.masks.at(0, 1))
                act.activation(x3(a)[:, :, 1:L], x3(ga)[:, :, 0:L - 1], ACT.Exp, scale=c8[:, :]).then_inc(s.decay.sem, 1)
                act.activation(m[:, :], ga[:, :], ACT.Exp, scale=c16[:, :]).then_inc(s.decay2.sem, 1)
                act.wait_ge(s.v.sem, s.v.at(0, 6))
                act.activation(m[:, :], m[:, :], ACT.Sqrt).then_inc(s.root.sem, 1)

                def copy_h(i, p):
                    settle(act, s)
                    act.activation(z[:, p, :], gx[:, bass.ds(i * L, L)], ACT.Copy).then_inc(s.z_ready.sem, 1)

                act.wait_ge(s.h_ready.sem, s.h_ready.at(0, 1))
                copy_h(0, 0)
                copy_h(1, 1)
                with act.Fori(0, B // 2 - 1) as j:
                    for p in range(2):
                        i = 2 * j + p
                        act.wait_ge(s.y_ready.sem, s.y_ready.at(i, 1))
                        copy_h(i + 2, p)
                        norm_act(act, s, i, net.bank[2][:, 0:L], net.xT[:, bass.ds(i * L, L)])
                for i in (B - 2, B - 1):
                    norm_act(act, s, i, net.bank[2][:, 0:L], net.xT[:, bass.ds(i * L, L)])

            @block.vector
            def _(dve):
                v = s.v
                dve.wait_ge(s.soft.sem, s.soft.at(0, 3))
                dve.scalar_tensor_tensor(t2[:, :], ap_[:, :], 0.0, t1[:, :], ALU.max, ALU.add).then_inc(v.sem, 1)
                dve.wait_ge(v.sem, v.at(0, 1))
                dve.tensor_scalar(c8[:, :], t2[:, :], -8.0, None, ALU.mult).then_inc(v.sem, 1)
                dve.tensor_scalar(c16[:, :], t2[:, :], -16.0, None, ALU.mult).then_inc(v.sem, 1)
                dve.wait_ge(s.gate_x.sem, s.gate_x.at(0, 4))
                dve.tensor_tensor(gx[:, :], gx[:, :], net.xT[:, :], ALU.mult).then_inc(v.sem, 1)
                dve.wait_ge(s.decay2.sem, s.decay2.at(0, 1))
                dve.tensor_scalar(m[:, :], m[:, :], -1.0, 1.0, ALU.mult, ALU.add).then_inc(v.sem, 1)
                dve.wait_ge(v.sem, v.at(0, 5))
                dve.tensor_scalar(m[:, :], m[:, :], 1e-7, None, ALU.max).then_inc(v.sem, 1)
                dve.wait_ge(s.decay.sem, s.decay.at(0, 1))
                dve.tensor_tensor_scan(p[:, :], a[:, :], first[:, :], 0.0, ALU.mult, ALU.add).then_inc(v.sem, 1)
                dve.wait_ge(v.sem, v.at(0, 7))
                dve.tensor_scalar(p[:, :], p[:, :], 1e-7, None, ALU.max).then_inc(v.sem, 1)
                dve.wait_ge(s.root.sem, s.root.at(0, 1))
                dve.tensor_tensor(gx[:, :], gx[:, :], m[:, :], ALU.mult).then_inc(v.sem, 1)
                dve.wait_ge(v.sem, v.at(0, 9))
                dve.reciprocal(m[:, :], p[:, :]).then_inc(v.sem, 1)
                dve.wait_ge(v.sem, v.at(0, 10))
                dve.tensor_tensor(gx[:, :], gx[:, :], m[:, :], ALU.mult).then_inc(v.sem, 1)
                dve.wait_ge(v.sem, v.at(0, 11))
                dve.tensor_tensor_scan(ga[:, :], later[:, :], gx[:, :], 0.0, ALU.mult, ALU.add).then_inc(v.sem, 1)
                dve.wait_ge(v.sem, v.at(0, 12))
                dve.tensor_tensor(gx[:, :], p[:, :], ga[:, :], ALU.mult).then_inc(v.sem, 1)
                dve.wait_ge(v.sem, v.at(0, 13))
                dve.tensor_tensor(gx[:, :], gx[:, :], net.xT[:, :], ALU.add).then_inc(s.h_ready.sem, 1)
                with dve.Fori(0, B // 2) as j:
                    for b in range(2):
                        norm_dve(dve, s, n, 2 * j + b, net.bank[b][:, 0:L].rearrange("p (t d) -> p t d", d=D))
    close_stage(nc, net.pool)


HPG = 4
PART = 32


def attend_spec(H):
    n = 3 * H // HPG
    return f"settled:0 scored:{H} masked:{2 * H} top16:1 top_parts:1 top_ps:1 top_row:1 shifted:{n} exped:{n} mixed:1 row_inv:1 o_ready:1 "


def attend_buffers(ctx, nc, net, H, dv, scale_by, mask_q, maskT, ring, out, tail, scores=None, causal=False):
    sb = lambda name, shape: ctx.enter_context(nc.sbuf_tensor(net.name(name), shape, F32))
    sb16 = lambda name, shape: ctx.enter_context(nc.sbuf_tensor(net.name(name), shape, BF16))
    R = H // HPG
    per = 512 // (dv + 1)
    first = dict(top=H, tail=H + 1, shifted=H + 1 + tail)
    assert (H + 1 + 3 * R + tail) % len(ring) == 0
    ring_banks = [net.bank[k] for k in ring]
    score_banks = ring_banks if scores is None else [net.bank[k] for k in scores]
    top_bank = ring_banks[H % len(ring)] if scores is None else score_banks[-1]
    return group(causal=causal, scores=score_banks, own=scores is not None, top_bank=top_bank, H=H, R=R, dv=dv, per=per, scale_by=scale_by, mask_q=mask_q, maskT=maskT, first=first, ring=ring_banks,
                 out=[net.bank[k] for k in out], top=sb("top", [P, TPB, H]), top16=sb16("top16", [P, TPB, H]),
                 top_parts=sb("top_parts", [P, TPB, P]), top_row=sb16("minus_top", [P, L]), pick=net.pick16, prob=sb("prob", [P, 3 * R, 512]), inv=sb("inv", [P, TPB * H]))


def scores_pe(pe, s, a, net, i, h, q_at, k_at):
    if h >= len(a.scores):
        pe.wait_ge(s.masked.sem, s.masked.at(i, 2 * (h - len(a.scores)) + 2))
    elif not a.own:
        pe.wait_ge(s.exped.sem, s.exped.at(i, 0))
    to = a.scores[h % len(a.scores)]
    pe.matmul(to[:, 0:P], q_at(h, 0, P), k_at(h, 0, P), start=True, stop=True)
    pe.matmul(to[:, P:P + L], q_at(h, P, P), k_at(h, 0, L), start=True, stop=True).then_inc(s.scored.sem, 1)


def top_pe(pe, s, a, net, i):
    to = a.top_bank
    pe.wait_ge(s.top_parts.sem, s.top_parts.at(i, 1))
    for t in range(TPB):
        last = pe.transpose(to[:, t * P:(t + 1) * P], a.top_parts[:, t, :], net.tab("ident"))
    last.then_inc(s.top_ps.sem, 1)


def tail_bank(pe, s, a, i, m, last):
    k = a.first["tail"] + m
    if last:
        pe.wait_ge(s.exped.sem, s.exped.at(i, 3 * a.R))
    elif k - len(a.ring) < a.H:
        pe.wait_ge(s.masked.sem, s.masked.at(i + 1, 2 * a.H))
    else:
        pe.wait_ge(s.top_row.sem, s.top_row.at(i + 1, 1))
    return a.ring[k % len(a.ring)]


def scores_dve(dve, s, a, net, i):
    for h in range(a.H):
        dve.wait_ge(s.scored.sem, s.scored.at(i, h + 1))
        settle(dve, s)
        for t in range(TPB):
            n = (t + 1) * P
            scores = a.scores[h % len(a.scores)][:, t * P:t * P + n]
            dve.tensor_tensor_reduce(scores, scores, a.mask_q[:, t, 0:n], 1.0, -3e38, ALU.add, ALU.max, a.top[:, t, h:h + 1])\
                .then_inc(s.masked.sem, 1)
    dve.wait_ge(s.masked.sem, s.masked.at(i, 2 * a.H))
    dve.tensor_copy(a.top16[:, :, :], a.top[:, :, :]).then_inc(s.top16.sem, 1)
    dve.wait_ge(s.top16.sem, s.top16.at(i, 1))
    dve.wait_ge(s.top_ps.sem, s.top_ps.at(i, 0))
    dve.tensor_copy(a.top_parts[:, :, 0:a.H], a.top16[:, :, :])
    dve.tensor_tensor(a.top_parts[:, :, PART:PART + a.H], a.top[:, :, :], a.top16[:, :, :], ALU.subtract).then_inc(s.top_parts.sem, 1)


def shifted_pe(pe, s, a, net, i, n, tail, q_at, k_at):
    pick = lambda h: a.pick[:, h:h + 1].to_broadcast([P, P])
    r, part = n // 3, n % 3
    pe.wait_ge(s.top_row.sem, s.top_row.at(i, 1))
    before = a.first["shifted"] + n - len(a.ring) - a.first["tail"]
    if n >= len(a.ring):
        pe.wait_ge(s.exped.sem, s.exped.at(i, n - len(a.ring) + 1))
    elif a.own:
        pe.wait_ge(s.exped.sem, s.exped.at(i, 0))
    elif before >= 0:
        pe.wait_ge(tail[before].sem, tail[before].at(i, 0))
    to = a.ring[(a.first["shifted"] + n) % len(a.ring)]
    heads = [r + a.R * m for m in range(HPG)]
    kt, lo, w, hs = (1, P, P, heads) if part == 2 else (0, 0, L, heads[2 * part:2 * part + 2])
    diagonal = a.maskT[:, 0:P] if part < 2 else a.maskT[:, L:L + P]
    if not a.causal:
        mask = a.maskT[:, 0:L] if part < 2 else diagonal
        pe.matmul(to[:, :], net.ident16[:, :], mask.unsqueeze(1).to_broadcast([P, len(hs), w]), start=True, stop=False)
    for m, h in enumerate(hs):
        pe.matmul(to[:, m * w:(m + 1) * w], k_at(h, kt * P, P), q_at(h, lo, w), start=a.causal, stop=False)
        if a.causal:
            pe.matmul(to[:, m * w:m * w + P], net.ident16[:, :], diagonal, start=False, stop=False)
        last = pe.matmul(to[:, m * w:(m + 1) * w], pick(h), a.top_row[:, lo:L], start=False, stop=(a.causal or m == len(hs) - 1))
    last.then_inc(s.shifted.sem, 1)


def mix_pe(pe, s, a, i, r, v_at):
    pe.wait_ge(s.exped.sem, s.exped.at(i, 3 * r + 3))
    pe.wait_ge(s.o_ready.sem, s.o_ready.at(i, 0))
    for m in range(HPG):
        h = r + a.R * m
        first, later = a.prob[:, 3 * r + m // 2, :], a.prob[:, 3 * r + 2, :]
        for t in range(TPB):
            q = slice((m % 2) * L + t * P, (m % 2) * L + (t + 1) * P)
            u = t * a.H + h
            to = a.out[u // a.per][:, (u % a.per) * (a.dv + 1):(u % a.per + 1) * (a.dv + 1)]
            last = pe.matmul(to, first[:, q], v_at(0, h), start=True, stop=(t == 0))
            if t == 1:
                last = pe.matmul(to, later[:, m * P:(m + 1) * P], v_at(1, h), start=False, stop=True)
    if r == a.R - 1:
        last.then_inc(s.mixed.sem, 1)


def top_row_act(act, s, a, i):
    act.wait_ge(s.top_ps.sem, s.top_ps.at(i, 1))
    act.activation(a.top_row[:, :], a.top_bank[:, 0:L], ACT.Copy, scale=-1.0).then_inc(s.top_row.sem, 1)


def exp_act(act, s, a, i, n):
    act.wait_ge(s.shifted.sem, s.shifted.at(i, n + 1))
    act.activation(a.prob[:, n, :], a.ring[(a.first["shifted"] + n) % len(a.ring)][:, :], ACT.Exp, scale=a.scale_by).then_inc(s.exped.sem, 1)


def normalise_dve(dve, s, a, i, o, o_read):
    dve.wait_ge(s.mixed.sem, s.mixed.at(i, 1))
    units = [(lo, min(lo + a.per, TPB * a.H)) for lo in range(0, TPB * a.H, a.per)]
    out = [a.out[k][:, 0:(hi - lo) * (a.dv + 1)].rearrange("p (u d) -> p u d", d=a.dv + 1) for k, (lo, hi) in enumerate(units)]
    for (lo, hi), of in zip(units, out, strict=True):
        last = dve.reciprocal(a.inv[:, lo:hi], of[:, :, a.dv])
    last.then_inc(s.row_inv.sem, 1)
    dve.wait_ge(s.row_inv.sem, s.row_inv.at(i, 1))
    dve.wait_ge(o_read.sem, o_read.at(i, 0))
    for (lo, hi), of in zip(units, out, strict=True):
        last = dve.tensor_tensor(o[:, lo:hi, :], of[:, :, 0:a.dv], a.inv[:, lo:hi].unsqueeze(2).to_broadcast([P, hi - lo, a.dv]), ALU.mult)
    last.then_inc(s.o_ready.sem, 1)


def stage_local_attention(nc, net, io, l, src, dst):
    with ExitStack() as ctx:
        sb = lambda name, shape: ctx.enter_context(nc.sbuf_tensor(net.name(name), shape, F32))
        CH = INNER // P
        a = attend_buffers(ctx, nc, net, LH, LDH, QK_SCALE, net.tab("lmask").rearrange("p (t k) -> p t k", t=TPB), net.lmask16,
                           ring=(2, 3, 4), out=(5, 6, 7), tail=3)
        hT = sb("hT", [P, L])
        qsb = sb("scales", [P, 2, LDH])
        rope = sb("rope", [P, TPB, 4, LDH])
        NQ = 2 * TPB
        sq, rc, rs = (sb(n, [P, 2, INNER]) for n in ("squares", "rot_cos", "rot_sin"))
        rot = sb("rotated", [P, NQ, INNER])
        ss, rn = sb("sum_sq", [P, NQ, LH]), sb("inv_norm", [P, NQ, LH])
        qT, kT, v = sb("qT", [P, CH, L]), sb("kT", [P, 2, CH, L]), sb("v", [P, 2, TPB, LH, LDH + 1])
        q16, k16 = (ctx.enter_context(nc.sbuf_tensor(net.name(n), [P, CH, L], BF16)) for n in ("q16", "k16"))
        o, oT = sb("o", [P, TPB, INNER]), sb("oT", [P, CH, L])
        s = open_stage(nc, net.pool, "clear:1 tables:1 h_built:1 front_ps:10 squared:4 sums:4 clipped:4 inv:4 cosd:4 sind:4 added:4 roped:4 "
                       "qkT:4 v_ready:2 oT_ps:2 oT_ready:2 y_ready:1 x_updated:1 " + attend_spec(LH))
        tail = [s.oT_ready, s.oT_ready, s.x_updated]
        tail_at = [a.ring[(a.first["tail"] + k) % len(a.ring)] for k in range(3)]
        ident = net.tab("ident")
        tab4 = net.tab("rope").rearrange("p (t c d) -> p t c d", t=TPB, c=4)
        heads = lambda ap: ap.rearrange("p (h d) -> p h d", d=LDH)
        over_heads = lambda ap: ap.unsqueeze(1).to_broadcast([P, LH, ap.shape[1]])
        HF = LDH // 2
        ITEM = {("q", 0): 0, ("k", 0): 1, ("v", 0): 2, ("q", 1): 3, ("k", 1): 4, ("v", 1): 5, "turned": 6}
        qk_item = lambda m: ITEM["qk"[m % 2], m // 2]
        front_bank = lambda n: net.bank[n % 2]
        with nc.Block() as block:
            @block.sync
            def _(sp):
                for j, nm in enumerate(("L0_ffn_q_scale", "L0_ffn_k_scale")):
                    sp.dma_start(qsb[:, j, :], io[nm][l].partition_broadcast(P)).then_inc(net.ld_s, 16)
                net.ld_s_count += 32

            @block.gpsimd
            def _(pool):
                pool.memset(hT[:, :], 0.0)
                pool.memset(a.top_parts[:, :, :], 0.0)
                pool.memset(v[:, :, :, :, LDH:LDH + 1], 1.0)
                pool.memset(kT[:, :, :, :], 0.0).then_inc(s.clear.sem, 1)
                pool.wait_ge(net.ld_s, net.ld_s_count)
                for j in range(2):
                    qb = lambda x: x.unsqueeze(1).to_broadcast([P, TPB, x.shape[1]])
                    pool.tensor_tensor(rope[:, :, 2 * j, :], tab4[:, :, 2 * j, :], qb(qsb[:, j, :]), ALU.mult)
                    pool.tensor_tensor(rope[:, :, 2 * j + 1, 0:HF], tab4[:, :, 2 * j + 1, 0:HF], qb(qsb[:, j, HF:LDH]), ALU.mult)
                    last = pool.tensor_tensor(rope[:, :, 2 * j + 1, HF:LDH], tab4[:, :, 2 * j + 1, HF:LDH], qb(qsb[:, j, 0:HF]), ALU.mult)
                last.then_inc(s.tables.sem, 1)

                with pool.Fori(0, B) as i:
                    pool.wait_ge(s.front_ps.sem, s.front_ps.at(i, 0))
                    for m in range(NQ):
                        pool.wait_ge(s.sind.sem, s.sind.at(i, m + 1))
                        pool.tensor_tensor(rot[:, m, :], rc[:, m % 2, :], rs[:, m % 2, :], ALU.add).then_inc(s.added.sem, 1)
                        pool.wait_ge(s.clipped.sem, s.clipped.at(i, m + 1))
                        pool.tensor_tensor(rn[:, m, :], ss[:, m, :], net.neghalf[:, 0:LH], ALU.pow).then_inc(s.inv.sem, 1)

            @block.tensor
            def _(pe):
                pe.wait_ge(net.ld_w, net.w_ready)
                w = net.wqkv[l]

                def project(i, n):
                    t, j = n // 3, n % 3
                    if n < 2:
                        pe.wait_ge(s.qkT.sem, s.qkT.at(i, 0))
                    elif (n - 2) % 3 == 2:
                        pe.wait_ge(s.v_ready.sem, s.v_ready.at(i, (n - 2) // 3 + 1))
                    else:
                        m = 2 * ((n - 2) // 3) + (n - 2) % 3
                        pe.wait_ge(s.squared.sem, s.squared.at(i, m + 1))
                        pe.wait_ge(s.sind.sem, s.sind.at(i, m + 1))
                    pe.wait_ge(s.h_built.sem, s.h_built.at(i, 1))
                    pe.matmul(front_bank(n)[:, :], hT[:, t * P:(t + 1) * P], w[:, j * INNER:(j + 1) * INNER], start=True, stop=True)\
                        .then_inc(s.front_ps.sem, 1)

                def turn(i):
                    for m in range(NQ):
                        n = ITEM["turned"] + m
                        if m == 0:
                            pe.wait_ge(s.squared.sem, s.squared.at(i, 4))
                            pe.wait_ge(s.sind.sem, s.sind.at(i, 4))
                        elif m == 1:
                            pe.wait_ge(s.v_ready.sem, s.v_ready.at(i, 2))
                        else:
                            pe.wait_ge(s.qkT.sem, s.qkT.at(i, m - 1))
                        pe.wait_ge(s.roped.sem, s.roped.at(i, m + 1))
                        for c in range(CH):
                            last = pe.transpose(front_bank(n)[:, c * P:(c + 1) * P], rot[:, m, c * P:(c + 1) * P], ident)
                        last.then_inc(s.front_ps.sem, 1)

                row = lambda h: slice(LDH * (h % 2), LDH * (h % 2) + LDH)
                q16_at = lambda h, at, w: q16[row(h), h // 2, at:at + w]
                k16_at = lambda h, at, w: k16[row(h), h // 2, at:at + w]

                def front(i, p):
                    for n in range(6):
                        project(i, n)
                    turn(i)
                    pe.wait_ge(s.qkT.sem, s.qkT.at(i, NQ))
                    for h in range(LH):
                        scores_pe(pe, s, a, net, i, h, q16_at, k16_at)
                    project(i + 1, 0)
                    project(i + 1, 1)
                    top_pe(pe, s, a, net, i)

                def run(i, p, ahead):
                    q_at = lambda h, at, w: qT[:, h // 2, at:at + w]
                    k_at = lambda h, at, w: kT[:, h % 2, h // 2, at:at + w]
                    v_at = lambda kb, h: v[:, p, kb, h, :]
                    pe.wait_ge(s.v_ready.sem, s.v_ready.at(i, TPB))
                    for n in range(6):
                        shifted_pe(pe, s, a, net, i, n, tail, q_at, k_at)
                        if ahead and n in (1, 2, 3, 4):
                            project(i + 1, n + 1)
                    if ahead:
                        turn(i + 1)
                    mix_pe(pe, s, a, i, 0, v_at)
                    if ahead:
                        pe.wait_ge(s.qkT.sem, s.qkT.at(i + 1, NQ))
                    for h in range(LH):
                        if ahead:
                            scores_pe(pe, s, a, net, i + 1, h, q16_at, k16_at)
                        if h == 2:
                            mix_pe(pe, s, a, i, 1, v_at)
                    if ahead == 2:
                        project(i + 2, 0)
                        project(i + 2, 1)
                    if ahead:
                        top_pe(pe, s, a, net, i + 1)
                    for t in range(TPB):
                        to = tail_bank(pe, s, a, i, t, not ahead)
                        pe.wait_ge(s.o_ready.sem, s.o_ready.at(i, 1))
                        for c in range(CH):
                            last = pe.transpose(to[:, c * P:(c + 1) * P], o[:, t, c * P:(c + 1) * P], ident)
                        last.then_inc(s.oT_ps.sem, 1)
                    to = tail_bank(pe, s, a, i, 2, not ahead)
                    pe.wait_ge(s.oT_ready.sem, s.oT_ready.at(i, 2))
                    for c in range(CH):
                        last = pe.matmul(to[:, 0:L], net.wo[l][:, c, :], oT[:, c, :], start=(c == 0), stop=(c == CH - 1))
                    last.then_inc(s.y_ready.sem, 1)

                front(0, 0)
                with pe.Fori(0, B // 2 - 1) as j:
                    run(2 * j, 0, 2)
                    run(2 * j + 1, 1, 2)
                run(B - 2, 0, 1)
                run(B - 1, 1, 0)

            @block.scalar
            def _(act):
                act.wait_ge(s.clear.sem, s.clear.at(0, 1))

                def shift(i):
                    act.wait_ge(s.front_ps.sem, s.front_ps.at(i, 0))
                    act.activation(hT[0:D // 2, :], src[0:D // 2, bass.ds(i * L, L)], ACT.Copy)
                    act.activation(hT[D // 2:D, 1:L], src[D // 2:D, bass.ds(i * L, L - 1)], ACT.Copy).then_inc(s.h_built.sem, 1)

                def square(i, m):
                    n = qk_item(m)
                    act.wait_ge(s.front_ps.sem, s.front_ps.at(i, n + 1))
                    act.wait_ge(s.sums.sem, s.sums.at(i, max(0, m - 1)))
                    act.activation(sq[:, m % 2, :], front_bank(n)[:, :], ACT.Square).then_inc(s.squared.sem, 1)

                def copy_v(i, p, t):
                    n = ITEM["v", t]
                    act.wait_ge(s.front_ps.sem, s.front_ps.at(i, n + 1))
                    act.activation(v[:, p, t, :, 0:LDH], heads(front_bank(n)[:, :]), ACT.Copy).then_inc(s.v_ready.sem, 1)

                def copy_qk(i):
                    for m in range(NQ):
                        t, j = m // 2, m % 2
                        n = ITEM["turned"] + m
                        act.wait_ge(s.front_ps.sem, s.front_ps.at(i, n + 1))
                        of = front_bank(n)[:, :].rearrange("p (c t) -> p c t", t=P)
                        tok = slice(t * P, (t + 1) * P)
                        if j == 0:
                            act.activation(q16[:, :, tok], of, ACT.Copy)
                            act.activation(qT[:, :, tok], of, ACT.Copy).then_inc(s.qkT.sem, 1)
                        else:
                            act.activation(k16[:, :, tok], of, ACT.Copy)
                            act.activation(kT[0:LDH, 0, :, tok], of[0:LDH], ACT.Copy)
                            act.activation(kT[LDH:P, 1, :, tok], of[LDH:P], ACT.Copy).then_inc(s.qkT.sem, 1)

                def front(i, p):
                    shift(i)
                    square(i, 0)
                    square(i, 1)
                    copy_v(i, p, 0)
                    square(i, 2)
                    square(i, 3)
                    copy_v(i, p, 1)
                    copy_qk(i)
                    shift(i + 1)
                    top_row_act(act, s, a, i)
                    square(i + 1, 0)
                    square(i + 1, 1)

                def run(i, p, ahead):
                    for n in range(6):
                        exp_act(act, s, a, i, n)
                        if ahead and n in (1, 2, 3, 4):
                            (lambda: copy_v(i + 1, 1 - p, 0), lambda: square(i + 1, 2), lambda: square(i + 1, 3),
                             lambda: copy_v(i + 1, 1 - p, 1))[n - 1]()
                    if ahead:
                        copy_qk(i + 1)
                    if ahead == 2:
                        shift(i + 2)
                    if ahead:
                        top_row_act(act, s, a, i + 1)
                    if ahead == 2:
                        square(i + 2, 0)
                        square(i + 2, 1)
                    act.wait_ge(s.y_ready.sem, s.y_ready.at(i, 0))
                    for t in range(TPB):
                        act.wait_ge(s.oT_ps.sem, s.oT_ps.at(i, t + 1))
                        act.activation(oT[:, :, t * P:(t + 1) * P], tail_at[t][:, :].rearrange("p (c t) -> p c t", t=P), ACT.Copy)\
                            .then_inc(s.oT_ready.sem, 1)

                front(0, 0)
                with act.Fori(0, B // 2 - 1) as j:
                    run(2 * j, 0, 2)
                    run(2 * j + 1, 1, 2)
                run(B - 2, 0, 1)
                run(B - 1, 1, 0)

            @block.vector
            def _(dve):
                dve.wait_ge(s.tables.sem, s.tables.at(0, 1))

                def rotate(i, m):
                    t, j = m // 2, m % 2
                    n = qk_item(m)
                    dve.wait_ge(s.front_ps.sem, s.front_ps.at(i, n + 1))
                    dve.wait_ge(s.squared.sem, s.squared.at(i, m + 1))
                    dve.wait_ge(s.added.sem, s.added.at(i, max(0, m - 1)))
                    of = heads(front_bank(n)[:, :])
                    dve.tensor_tensor(heads(rc[:, m % 2, :]), of, over_heads(rope[:, t, 2 * j, :]), ALU.mult).then_inc(s.cosd.sem, 1)
                    sin = heads(rs[:, m % 2, :])
                    dve.tensor_tensor(sin[:, :, 0:HF], of[:, :, HF:LDH], over_heads(rope[:, t, 2 * j + 1, 0:HF]), ALU.mult)
                    dve.tensor_tensor(sin[:, :, HF:LDH], of[:, :, 0:HF], over_heads(rope[:, t, 2 * j + 1, HF:LDH]), ALU.mult)\
                        .then_inc(s.sind.sem, 1)
                    dve.tensor_reduce(ss[:, m, :], heads(sq[:, m % 2, :]), AX.X, ALU.add).then_inc(s.sums.sem, 1)
                    dve.wait_ge(s.sums.sem, s.sums.at(i, m + 1))
                    dve.tensor_scalar(ss[:, m, :], ss[:, m, :], 1e-24, None, ALU.max).then_inc(s.clipped.sem, 1)

                def finish(i):
                    for m in range(NQ):
                        dve.wait_ge(s.inv.sem, s.inv.at(i, m + 1))
                        r = heads(rot[:, m, :])
                        dve.tensor_tensor(r, r, rn[:, m, :].unsqueeze(2).to_broadcast([P, LH, LDH]), ALU.mult).then_inc(s.roped.sem, 1)
                    scores_dve(dve, s, a, net, i)

                def front(i, p):
                    for m in range(NQ):
                        rotate(i, m)
                    finish(i)
                    rotate(i + 1, 0)
                    rotate(i + 1, 1)

                def run(i, p, ahead):
                    if ahead:
                        rotate(i + 1, 2)
                        rotate(i + 1, 3)
                        finish(i + 1)
                    normalise_dve(dve, s, a, i, o[:, :, :].rearrange("p t (h d) -> p (t h) d", h=LH), s.oT_ps)
                    if ahead == 2:
                        rotate(i + 2, 0)
                        rotate(i + 2, 1)
                    dve.wait_ge(s.y_ready.sem, s.y_ready.at(i, 1))
                    dve.tensor_tensor(dst[:, bass.ds(i * L, L)], tail_at[2][:, 0:L], src[:, bass.ds(i * L, L)], ALU.add)\
                        .then_inc(s.x_updated.sem, 1)

                front(0, 0)
                with dve.Fori(0, B // 2 - 1) as j:
                    run(2 * j, 0, 2)
                    run(2 * j + 1, 1, 2)
                run(B - 2, 0, 1)
                run(B - 1, 1, 0)
    close_stage(nc, net.pool)


def part(s, prefix):
    return group(**{k[len(prefix):]: v for k, v in s._asdict().items() if k.startswith(prefix)})


def prefixed(prefix, spec):
    return " ".join(prefix + w for w in spec.split()) + " "


def stage_gated_mlp(nc, net, io, l, x, final):
    with ExitStack() as ctx:
        sb = lambda name, shape: ctx.enter_context(nc.sbuf_tensor(net.name(name), shape, F32))
        n, nf = norm_buffers(ctx, nc, net), norm_buffers(ctx, nc, net)
        hT, hn, z, z1 = sb("hT", [P, L]), sb("hn", [P, T]), sb("z", [P, L]), sb("z1", [P, L])
        gate, u = sb("gate", [P, len(HCH), L]), sb("u", [P, len(HCH), L])
        s = open_stage(nc, net.pool, "h_clear:1 h_built:1 ag_ps:3 gelu:3 u_ready:3 mlp_ps:1 sum1:1 sum2:1 "
                       + NORM + " " + prefixed("f_", NORM))
        f = part(s, "f_")
        ident, sm = net.tab("ident"), net.small
        h_bank, hnT_bank, out_bank, z_bank, zT_bank = (net.bank[k] for k in (0, 1, 5, 6, 7))
        ag_bank = lambda c: net.bank[2 + c]
        tiles = lambda bank: bank[:, 0:L].rearrange("p (t d) -> p t d", d=D)
        with nc.Block() as block:
            @block.gpsimd
            def _(pool):
                pool.memset(hT[:, :], 0.0).then_inc(s.h_clear.sem, 1)

                def turn(i, ahead, own, behind):
                    if ahead:
                        norm_pool(pool, s, n, i + 1)
                    if behind:
                        norm_pool(pool, f, nf, i - 1)
                skewed(pool, turn, final)

            @block.scalar
            def _(act):
                act.wait_ge(net.ld_w, net.w_ready)
                act.wait_ge(s.h_clear.sem, s.h_clear.at(0, 1))

                def turn(i, ahead, own, behind):
                    if ahead:
                        act.wait_ge(s.y_ready.sem, s.y_ready.at(i + 1, 0))
                        act.activation(hT[0:D // 2, :], x[0:D // 2, bass.ds((i + 1) * L, L)], ACT.Copy)
                        act.activation(hT[D // 2:D, 1:L], x[D // 2:D, bass.ds((i + 1) * L, L - 1)], ACT.Copy).then_inc(s.h_built.sem, 1)
                    if own:
                        act.wait_ge(s.u_ready.sem, s.u_ready.at(i, 0))
                        for c, (at, w) in enumerate(HCH):
                            act.wait_ge(s.ag_ps.sem, s.ag_ps.at(i, c + 1))
                            act.activation(gate[0:w, c, :], ag_bank(c)[0:w, L:2 * L], ACT.Gelu, bias=sm("b1g", l)[0:w, c:c + 1])\
                                .then_inc(s.gelu.sem, 1)
                    if ahead:
                        norm_act(act, s, i + 1, hnT_bank[:, 0:L], hn[:, bass.ds((i + 1) * L, L)], sm("ln_g", l), sm("ln_b", l))
                    if behind:
                        norm_act(act, f, i - 1, zT_bank[:, 0:L], net.xT[:, bass.ds((i - 1) * L, L)])
                skewed(act, turn, final)

            @block.tensor
            def _(pe):
                pe.wait_ge(net.ld_w, net.w_ready)

                def turn(i, ahead, own, behind):
                    if ahead:
                        pe.wait_ge(s.h_built.sem, s.h_built.at(i + 1, 1))
                        pe.wait_ge(s.xn_ready.sem, s.xn_ready.at(i + 1, 0))
                        for t in range(TPB):
                            last = pe.transpose(h_bank[:, t * P:(t + 1) * P], hT[:, t * P:(t + 1) * P], ident)
                        last.then_inc(s.y_ready.sem, 1)
                    if behind:
                        pe.wait_ge(s.sum2.sem, s.sum2.at(i - 1, 1))
                        pe.wait_ge(f.xn_ready.sem, f.xn_ready.at(i - 1, 0))
                        for t in range(TPB):
                            last = pe.transpose(z_bank[:, t * P:(t + 1) * P], z[:, t * P:(t + 1) * P], ident)
                        last.then_inc(f.y_ready.sem, 1)
                    if own:
                        pe.wait_ge(s.x_updated.sem, s.x_updated.at(i, 1))
                        pe.wait_ge(s.u_ready.sem, s.u_ready.at(i, 0))
                        for c, (at, w) in enumerate(HCH):
                            for j in range(2):
                                last = pe.matmul(ag_bank(c)[0:w, j * L:(j + 1) * L], net.w1[l][:, j * HID + at:j * HID + at + w],
                                                 hn[:, bass.ds(i * L, L)], start=True, stop=True)
                            last.then_inc(s.ag_ps.sem, 1)
                    if ahead:
                        pe.wait_ge(s.x_updated.sem, s.x_updated.at(i + 1, 0))
                        norm_pe(pe, s, n, i + 1, hnT_bank[:, 0:L])
                    if own:
                        pe.wait_ge(s.sum1.sem, s.sum1.at(i, 0))
                        pe.wait_ge(s.u_ready.sem, s.u_ready.at(i, len(HCH)))
                        for c, (at, w) in enumerate(HCH):
                            last = pe.matmul(out_bank[:, 0:L], net.w2[l][0:w, c, :], u[0:w, c, :], start=(c == 0), stop=(c == len(HCH) - 1))
                        last.then_inc(s.mlp_ps.sem, 1)
                    if behind:
                        pe.wait_ge(f.x_updated.sem, f.x_updated.at(i - 1, 0))
                        norm_pe(pe, f, nf, i - 1, zT_bank[:, 0:L])
                skewed(pe, turn, final)

            @block.vector
            def _(dve):
                dve.wait_ge(net.ld_w, net.w_ready)

                def turn(i, ahead, own, behind):
                    if ahead:
                        norm_stats(dve, s, n, i + 1, tiles(h_bank))
                    if behind:
                        norm_stats(dve, f, nf, i - 1, tiles(z_bank))
                    if own:
                        dve.wait_ge(s.mlp_ps.sem, s.mlp_ps.at(i, 0))
                    for c, (at, w) in enumerate(HCH):
                        if own:
                            dve.wait_ge(s.gelu.sem, s.gelu.at(i, c + 1))
                            dve.scalar_tensor_tensor(u[0:w, c, :], ag_bank(c)[0:w, 0:L], sm("b1a", l)[0:w, c:c + 1], gate[0:w, c, :],
                                                     ALU.add, ALU.mult).then_inc(s.u_ready.sem, 1)
                        if ahead and c == 0:
                            norm_apply(dve, s, n, i + 1, tiles(h_bank))
                    if behind:
                        norm_apply(dve, f, nf, i - 1, tiles(z_bank))
                    if own:
                        dve.wait_ge(s.mlp_ps.sem, s.mlp_ps.at(i, 1))
                        dst = z1[:, :] if final else x[:, bass.ds(i * L, L)]
                        dve.scalar_tensor_tensor(dst, out_bank[:, 0:L], sm("b2", l), x[:, bass.ds(i * L, L)], ALU.add, ALU.add)\
                            .then_inc(s.sum1.sem, 1)
                    if own and final:
                        dve.wait_ge(s.sum1.sem, s.sum1.at(i, 1))
                        dve.wait_ge(f.y_ready.sem, f.y_ready.at(i, 0))
                        dve.tensor_tensor(z[:, :], z1[:, :], net.xT[:, bass.ds(i * L, L)], ALU.add).then_inc(s.sum2.sem, 1)
                skewed(dve, turn, final)
    close_stage(nc, net.pool)


def stage_scan_inputs(nc, net, io, xc, sz):
    with ExitStack() as ctx:
        sb = lambda name, shape: ctx.enter_context(nc.sbuf_tensor(net.name(name), shape, F32))
        PAD = NCONV - 1
        xp, acc = sb("x_padded", [P, 2, PAD + L]), sb("conv", [P, 2, L])
        s = open_stage(nc, net.pool, "clear:1 xz:4 xp_ready:2 sz_ready:2 taps:8 xc_ready:2")
        with nc.Block() as block:
            @block.gpsimd
            def _(pool):
                pool.memset(xp[:, :, :], 0.0).then_inc(s.clear.sem, 1)

            @block.tensor
            def _(pe):
                pe.wait_ge(net.ld_w, net.w_ready)
                with pe.Fori(0, B) as i:
                    for m in range(4):
                        read = s.xp_ready if m < 2 else s.sz_ready
                        pe.wait_ge(read.sem, read.at(i, 0))
                        pe.matmul(net.bank[m][:, 0:L], net.w_in[:, m * P:(m + 1) * P], net.xT[:, bass.ds(i * L, L)],
                                  start=True, stop=True).then_inc(s.xz.sem, 1)

            @block.scalar
            def _(act):
                with act.Fori(0, B) as i:
                    for c in range(2):
                        act.wait_ge(s.xz.sem, s.xz.at(i, c + 3))
                        act.activation(sz[:, c, bass.ds(i * L, L)], net.bank[2 + c][:, 0:L], ACT.Silu).then_inc(s.sz_ready.sem, 1)
                    for c in range(2):
                        act.wait_ge(s.taps.sem, s.taps.at(i, 2 * (NCONV - 1) + c + 1))
                        act.activation(xc[:, c, bass.ds(i * L, L)], acc[:, c, :], ACT.Silu).then_inc(s.xc_ready.sem, 1)

            @block.vector
            def _(dve):
                dve.wait_ge(net.ld_w, net.w_ready)
                dve.wait_ge(s.clear.sem, s.clear.at(0, 1))
                with dve.Fori(0, B) as i:
                    dve.wait_ge(s.taps.sem, s.taps.at(i, 0))
                    for c in range(2):
                        dve.wait_ge(s.xz.sem, s.xz.at(i, c + 1))
                        dve.tensor_copy(xp[:, c, PAD:PAD + L], net.bank[c][:, 0:L]).then_inc(s.xp_ready.sem, 1)
                    dve.wait_ge(s.xc_ready.sem, s.xc_ready.at(i, 0))
                    for j in range(NCONV):
                        for c in range(2):
                            tap = net.conv_w[:, c, j:j + 1]
                            if j == 0:
                                dve.wait_ge(s.xp_ready.sem, s.xp_ready.at(i, c + 1))
                                dve.tensor_scalar(acc[:, c, :], xp[:, c, 0:L], tap, net.conv_b[:, c:c + 1], ALU.mult, ALU.add)\
                                    .then_inc(s.taps.sem, 1)
                            else:
                                dve.wait_ge(s.taps.sem, s.taps.at(i, 2 * (j - 1) + c + 1))
                                dve.scalar_tensor_tensor(acc[:, c, :], xp[:, c, j:j + L], tap, acc[:, c, :], ALU.mult, ALU.add)\
                                    .then_inc(s.taps.sem, 1)
    close_stage(nc, net.pool)


def stage_scan(nc, net, io, xc, sz):
    with ExitStack() as ctx:
        sb = lambda name, shape, dt=F32: ctx.enter_context(nc.sbuf_tensor(net.name(name), shape, dt))
        R = 4
        G = 512
        PARTS = 3
        LAG = 4
        n = norm_buffers(ctx, nc, net, keep=True)
        xs, dt_row = sb("xs", [P, L]), sb("dt_row", [1, 2, G])
        w_wide = sb("w_wide", [P, 2, P])
        bc = sb("bc_parts", [P, T], BF16)
        high, mid = sb("high", [P, 2, G], BF16), sb("mid", [P, 2, G], BF16)
        sel = sb("select", [P, 2 * NS], BF16)
        delta, dx, y1, y2 = sb("delta", [P, 2, T]), sb("delta_x", [P, 2, T]), sb("y1", [P, 2, L]), sb("y2", [P, 2, L])
        dA, dB, h = (sb(k, [P, R, 2, L]) for k in ("decay", "inject", "state"))
        b_rows = sb("b_rows", [P, R, L])
        hc = net.xw[:, 0:R * 2 * L].rearrange("p (r c t) -> p r c t", r=R, c=2)
        rest1, rest2 = (h[:, 2 * k:2 * k + 2, :, :].rearrange("p r c t -> p (r c t)").rearrange("p (b t) -> p b t", b=2) for k in range(2))
        a_neg, a_exp = sb("a_neg", [P, 2, NS]), sb("a_exp", [P, 2, NS])
        groups = T // G
        s = open_stage(nc, net.pool, f"clear:1 wide0:1 wide:1 sel:2 a_ready:1 a_exp:1 ssm_ps:{groups} dt_row:{groups} high:{groups} rest1:{groups} "
                       f"mid:{groups} rest2:{groups} parts:{groups} dt_ps:{groups} tail:{3 * groups} part1:{groups} part2:{groups} top:{groups} delta_ready:{groups} dx_ready:{groups} "
                       f"xs_ready:1 bc_ps:{NS} b_ready:{NS} decay:{2 * NS} inject:{NS} state:{NS} readout:{NS} summed:{NS} y1_ready:2 y2_ready:1 " + NORM)
        bank, ident = net.bank, net.tab("ident")
        row = lambda k: slice(2 * NS * k, 2 * NS * (k + 1))
        pick = lambda k: sel[:, k:k + 1].to_broadcast([P, P])
        flat = lambda ap: ap.rearrange("p c t -> p (c t)")
        both = lambda ap: ap.unsqueeze(1).to_broadcast([P, 2, L])
        bc_bank = lambda k: bank[2 + k % R]
        ssm_bank = lambda g: bank[g % 2]
        dt_bank = lambda g, c: bank[2 + 2 * (g % 2) + c]
        sum_bank, y_bank = bank[6], bank[7]
        y = y_bank[:, 0:L].rearrange("p (t d) -> p t d", d=D)
        group_of = lambda g: slice(g * G, (g + 1) * G)
        with nc.Block() as block:
            @block.gpsimd
            def _(pool):
                pool.memset(w_wide[:, :, :], 0.0).then_inc(s.wide0.sem, 1)
                pool.memset(bc[:, :], 0.0)
                pool.memset(dA[:, :, :, :], 0.0).then_inc(s.clear.sem, 1)
                pool.tensor_tensor(sel[:, :], net.ident16[:, row(1)], net.ident16[:, row(2)], ALU.add).then_inc(s.sel.sem, 1)
                pool.wait_ge(s.sel.sem, s.sel.at(0, 1))
                pool.tensor_tensor(sel[:, :], sel[:, :], net.ident16[:, row(3)], ALU.add).then_inc(s.sel.sem, 1)
                pool.wait_ge(s.sel.sem, s.sel.at(0, 2))
                for g in range(groups):
                    b = g % 2
                    if g >= 1:
                        pool.wait_ge(s.parts.sem, s.parts.at(0, g))
                    pool.wait_ge(s.high.sem, s.high.at(0, g + 1))
                    pool.tensor_copy(bc[row(1), group_of(g)], high[row(1), b, :]).then_inc(s.part1.sem, 1)
                    pool.wait_ge(s.part1.sem, s.part1.at(0, g + 1))
                    pool.wait_ge(s.rest1.sem, s.rest1.at(0, g + 1))
                    pool.tensor_copy(bc[row(2), group_of(g)], rest1[row(2), b, :]).then_inc(s.part2.sem, 1)
                    pool.wait_ge(s.part2.sem, s.part2.at(0, g + 1))
                    pool.wait_ge(s.rest2.sem, s.rest2.at(0, g + 1))
                    pool.tensor_copy(bc[row(3), group_of(g)], rest2[row(3), b, :]).then_inc(s.parts.sem, 1)
                pool.wait_ge(s.parts.sem, s.parts.at(0, groups))
                pool.wait_ge(s.dx_ready.sem, s.dx_ready.at(0, groups))

                def batch(i, behind):
                    for k in range(NS):
                        if behind or k >= R:
                            pool.wait_ge(s.state.sem, s.state.at(i, k - R + 1))
                        pool.wait_ge(s.b_ready.sem, s.b_ready.at(i, k + 1))
                        settle(pool, s)
                        pool.tensor_tensor(dB[:, k % R, :, :], dx[:, :, bass.ds(i * L, L)], both(b_rows[:, k % R, :]), ALU.mult)\
                            .then_inc(s.inject.sem, 1)
                        if behind and k == 10:
                            norm_rstd(pool, s, n, i - 1)

                batch(0, False)
                with pool.Fori(1, B) as i:
                    batch(i, True)
                norm_rstd(pool, s, n, B - 1)

            @block.tensor
            def _(pe):
                pe.wait_ge(net.ld_w, net.w_ready)
                pe.wait_ge(s.wide.sem, s.wide.at(0, 1))

                def steps(g):
                    pe.wait_ge(s.dt_row.sem, s.dt_row.at(0, g + 1))
                    if g >= 2:
                        pe.wait_ge(s.top.sem, s.top.at(0, g - 1))
                        pe.wait_ge(s.tail.sem, s.tail.at(0, g - 1))
                    for c in range(2):
                        last = pe.matmul(dt_bank(g, c)[:, :], net.w_dt[:, c * P:(c + 1) * P], dt_row[:, g % 2, :], start=True, stop=True)
                    last.then_inc(s.dt_ps.sem, 1)

                for g in range(groups):
                    if g >= 2:
                        pe.wait_ge(s.rest1.sem, s.rest1.at(0, g - 1))
                    for c in range(2):
                        last = pe.matmul(ssm_bank(g)[:, :], w_wide[:, c, :], xc[:, c, group_of(g)], start=(c == 0), stop=(c == 1))
                    last.then_inc(s.ssm_ps.sem, 1)
                    if g >= 1:
                        steps(g - 1)
                steps(groups - 1)
                pe.wait_ge(s.parts.sem, s.parts.at(0, groups))
                pe.wait_ge(s.sel.sem, s.sel.at(0, 2))
                pe.wait_ge(s.top.sem, s.top.at(0, groups))
                pe.wait_ge(s.tail.sem, s.tail.at(0, groups))

                def add(i, m):
                    pe.wait_ge(s.readout.sem, s.readout.at(i, m + 1))
                    if m == 0:
                        pe.wait_ge(s.y1_ready.sem, s.y1_ready.at(i, 0))
                    pe.matmul(sum_bank[:, :], ident, flat(hc[:, m % R, :, :]), start=(m == 0), stop=(m % NS == NS - 1))\
                        .then_inc(s.summed.sem, 1)

                def project(i):
                    pe.wait_ge(s.y2_ready.sem, s.y2_ready.at(i, 1))
                    pe.wait_ge(s.xs_ready.sem, s.xs_ready.at(i, 1))
                    pe.wait_ge(s.x_updated.sem, s.x_updated.at(i, 0))
                    for t in range(TPB):
                        tok = slice(t * P, (t + 1) * P)
                        for c in range(2):
                            pe.matmul(y_bank[:, tok], y2[:, c, tok], net.w_out[:, c, :], start=(c == 0), stop=False)
                        last = pe.matmul(y_bank[:, tok], xs[:, tok], ident, start=False, stop=True)
                    last.then_inc(s.y_ready.sem, 1)

                def batch(i, behind):
                    for k in range(NS):
                        if behind or k >= R:
                            pe.wait_ge(s.readout.sem, s.readout.at(i, k - R + 1))
                        tok = bass.ds(i * L, L)
                        pe.matmul(bc_bank(k)[:, 0:L], pick(k), bc[:, tok], start=True, stop=True)
                        pe.matmul(bc_bank(k)[:, L:2 * L], pick(NS + k), bc[:, tok], start=True, stop=True).then_inc(s.bc_ps.sem, 1)
                        if behind or k >= LAG:
                            add(i, k - LAG)
                        if behind and k == 8:
                            project(i - 1)
                        if behind and k == 13:
                            norm_pe(pe, s, n, i - 1, y_bank[:, L:2 * L])

                batch(0, False)
                with pe.Fori(1, B) as i:
                    batch(i, True)
                for m in range(NS - LAG, NS):
                    add(B - 1, m)
                project(B - 1)
                norm_pe(pe, s, n, B - 1, y_bank[:, L:2 * L])

            @block.scalar
            def _(act):
                act.wait_ge(net.ld_w, net.w_ready)
                act.wait_ge(s.clear.sem, s.clear.at(0, 1))
                act.activation(a_exp[:, :, :], net.a_log[:, :, :], ACT.Exp).then_inc(s.a_exp.sem, 1)

                def split(g):
                    b = g % 2
                    act.wait_ge(s.ssm_ps.sem, s.ssm_ps.at(0, g + 1))
                    if g >= 2:
                        act.wait_ge(s.dt_ps.sem, s.dt_ps.at(0, g - 1))
                        act.wait_ge(s.rest1.sem, s.rest1.at(0, g - 1))
                        act.wait_ge(s.part1.sem, s.part1.at(0, g - 1))
                    act.activation(dt_row[:, b, :], ssm_bank(g)[0:1, :], ACT.Copy).then_inc(s.dt_row.sem, 1)
                    act.activation(high[:, b, :], ssm_bank(g)[:, :], ACT.Copy).then_inc(s.high.sem, 1)

                def split_rest(g):
                    act.wait_ge(s.rest1.sem, s.rest1.at(0, g + 1))
                    if g >= 2:
                        act.wait_ge(s.rest2.sem, s.rest2.at(0, g - 1))
                    act.activation(mid[:, g % 2, :], rest1[:, g % 2, :], ACT.Copy).then_inc(s.mid.sem, 1)

                def magnitude(g):
                    act.wait_ge(s.dt_ps.sem, s.dt_ps.at(0, g + 1))
                    for c in range(2):
                        last = act.activation(delta[:, c, group_of(g)], dt_bank(g, c)[:, :], ACT.Abs, bias=net.b_dt[:, c:c + 1])
                    last.then_inc(s.tail.sem, 1)

                for g in range(groups + 1):
                    if g < groups:
                        split(g)
                    if g >= 1:
                        magnitude(g - 1)
                        split_rest(g - 1)
                for n_done, func, scale, bias in ((0, ACT.Exp, -1.0, 0.0), (groups, ACT.Ln, 1.0, 1.0)):
                    for g in range(groups):
                        of = delta[:, :, group_of(g)]
                        act.wait_ge(s.tail.sem, s.tail.at(0, n_done + g + 1))
                        act.activation(of, of, func, scale=scale, bias=bias).then_inc(s.tail.sem, 1)
                act.wait_ge(s.a_ready.sem, s.a_ready.at(0, 1))
                act.wait_ge(s.delta_ready.sem, s.delta_ready.at(0, groups))

                def keep(i):
                    norm_act(act, s, i, y_bank[:, L:2 * L], net.xT[:, bass.ds(i * L, L)])
                    act.activation(n.x_tok[:, bass.ds(i * L, L)], n.xn[:, :, :].rearrange("p t d -> p (t d)"), ACT.Copy).then_inc(s.kept.sem, 1)

                def batch(i, behind):
                    for k in range(NS):
                        if behind or k >= R:
                            act.wait_ge(s.state.sem, s.state.at(i, k - R + 1))
                        act.wait_ge(s.bc_ps.sem, s.bc_ps.at(i, k + 1))
                        act.activation(b_rows[:, k % R, :], bc_bank(k)[:, 0:L], ACT.Copy).then_inc(s.b_ready.sem, 1)
                        for c in range(2):
                            act.activation(dA[:, k % R, c, 1:L], delta[:, c, bass.ds(i * L + 1, L - 1)], ACT.Exp, scale=a_neg[:, c, k:k + 1])\
                                .then_inc(s.decay.sem, 1)
                        if k == 12:
                            act.wait_ge(s.y_ready.sem, s.y_ready.at(i, 0))
                            settle(act, s)
                            act.activation(xs[:, :], net.xT[:, bass.ds(i * L, L)], ACT.Copy).then_inc(s.xs_ready.sem, 1)
                        if behind and k == NS - 1:
                            keep(i - 1)

                batch(0, False)
                with act.Fori(1, B) as i:
                    batch(i, True)
                keep(B - 1)

            @block.vector
            def _(dve):
                dve.wait_ge(net.ld_w, net.w_ready)
                dve.wait_ge(s.wide0.sem, s.wide0.at(0, 1))
                dve.tensor_copy(w_wide[:, :, 0:1], net.w_xproj[:, :, 0:1])
                for k in range(PARTS):
                    last = dve.tensor_copy(w_wide[:, :, row(1 + k)], net.w_xproj[:, :, 1:XP])
                last.then_inc(s.wide.sem, 1)
                dve.wait_ge(s.a_exp.sem, s.a_exp.at(0, 1))
                dve.tensor_scalar(a_neg[:, :, :], a_exp[:, :, :], -1.0, None, ALU.mult).then_inc(s.a_ready.sem, 1)

                def split_first(g):
                    b = g % 2
                    dve.wait_ge(s.high.sem, s.high.at(0, g + 1))
                    if g >= 2:
                        dve.wait_ge(s.mid.sem, s.mid.at(0, g - 1))
                        dve.wait_ge(s.parts.sem, s.parts.at(0, g - 1))
                    dve.tensor_tensor(rest1[:, b, :], ssm_bank(g)[:, :], high[:, b, :], ALU.subtract).then_inc(s.rest1.sem, 1)

                def split_second(g):
                    b = g % 2
                    dve.wait_ge(s.rest1.sem, s.rest1.at(0, g + 1))
                    dve.wait_ge(s.mid.sem, s.mid.at(0, g + 1))
                    dve.tensor_tensor(rest2[:, b, :], rest1[:, b, :], mid[:, b, :], ALU.subtract).then_inc(s.rest2.sem, 1)

                def top(g):
                    dve.wait_ge(s.tail.sem, s.tail.at(0, g + 1))
                    for c in range(2):
                        last = dve.tensor_scalar(dx[:, c, group_of(g)], dt_bank(g, c)[:, :], net.b_dt[:, c:c + 1], 0.0, ALU.add, ALU.max)
                    last.then_inc(s.top.sem, 1)

                def step(g):
                    dve.wait_ge(s.top.sem, s.top.at(0, g + 1))
                    dve.wait_ge(s.tail.sem, s.tail.at(0, 2 * groups + g + 1))
                    dve.tensor_tensor(delta[:, :, group_of(g)], dx[:, :, group_of(g)], delta[:, :, group_of(g)], ALU.add).then_inc(s.delta_ready.sem, 1)
                    dve.wait_ge(s.delta_ready.sem, s.delta_ready.at(0, g + 1))
                    dve.tensor_tensor(dx[:, :, group_of(g)], delta[:, :, group_of(g)], xc[:, :, group_of(g)], ALU.mult).then_inc(s.dx_ready.sem, 1)

                for g in range(groups + 1):
                    if g < groups:
                        split_first(g)
                    if g >= 1:
                        top(g - 1)
                        split_second(g - 1)
                for g in range(groups):
                    step(g)

                def scan(i, m):
                    dve.wait_ge(s.inject.sem, s.inject.at(i, m + 1))
                    dve.wait_ge(s.decay.sem, s.decay.at(i, 2 * m + 2))
                    dve.tensor_tensor_scan(flat(h[:, m % R, :, :]), flat(dA[:, m % R, :, :]), flat(dB[:, m % R, :, :]), 0.0, ALU.mult, ALU.add)\
                        .then_inc(s.state.sem, 1)

                def read(i, m, behind=True):
                    dve.wait_ge(s.state.sem, s.state.at(i, m + 1))
                    if behind or m >= R:
                        dve.wait_ge(s.summed.sem, s.summed.at(i, m - R + 1))
                    dve.tensor_tensor(hc[:, m % R, :, :], h[:, m % R, :, :], both(bc_bank(m)[:, L:2 * L]), ALU.mult).then_inc(s.readout.sem, 1)

                def skip(i):
                    dve.wait_ge(s.summed.sem, s.summed.at(i, NS))
                    for c in range(2):
                        dve.scalar_tensor_tensor(y1[:, c, :], xc[:, c, bass.ds(i * L, L)], net.d_par[:, c:c + 1], sum_bank[:, c * L:(c + 1) * L],
                                                 ALU.mult, ALU.add).then_inc(s.y1_ready.sem, 1)

                def gate(i):
                    dve.wait_ge(s.y1_ready.sem, s.y1_ready.at(i, 2))
                    dve.wait_ge(s.y_ready.sem, s.y_ready.at(i, 0))
                    dve.tensor_tensor(y2[:, :, :], y1[:, :, :], sz[:, :, bass.ds(i * L, L)], ALU.mult).then_inc(s.y2_ready.sem, 1)

                def batch(i, behind):
                    for k in range(NS):
                        if behind or k >= 1:
                            scan(i, k - 1)
                        if behind or k >= 2:
                            read(i, k - 2, behind)
                        if behind and k == 3:
                            skip(i - 1)
                        if behind and k == 4:
                            gate(i - 1)
                        if behind and k == 9:
                            norm_stats(dve, s, n, i - 1, y)
                        if behind and k == 12:
                            norm_apply(dve, s, n, i - 1, y)

                batch(0, False)
                with dve.Fori(1, B) as i:
                    batch(i, True)
                scan(B - 1, NS - 1)
                read(B - 1, NS - 2)
                read(B - 1, NS - 1)
                skip(B - 1)
                gate(B - 1)
                norm_dve(dve, s, n, B - 1, y)
    close_stage(nc, net.pool)


def choose_first(dve, link, probs, iota, best, eq, index, hot, n):
    wide = lambda ap: ap.unsqueeze(2).to_broadcast([P, NT, n])
    link(dve.tensor_reduce(best, probs, AX.X, ALU.max))
    link(dve.tensor_tensor(eq, probs, wide(best), ALU.is_ge))
    link(dve.tensor_tensor(eq, eq, iota, ALU.mult))
    link(dve.tensor_reduce(index, eq, AX.X, ALU.min))
    link(dve.tensor_tensor(hot, iota, wide(index), ALU.is_equal))


def running_count(dve, link, net, pre, within, totals, n):
    link(dve.memset(pre[:, 0, :], 0.0))
    for t in range(1, NT):
        link(dve.tensor_tensor(pre[:, t, :], pre[:, t - 1, :], totals[:, t - 1, :], ALU.add))
    link(dve.tensor_tensor(pre[:, :, :], pre[:, :, :], within, ALU.add))


def slots_of(dve, link, b, pre, hot, index, trash, capacity, scatter, gather, accepted):
    link(dve.tensor_tensor(b.tmp, pre, hot, ALU.mult))
    link(dve.tensor_reduce(b.pos, b.tmp, AX.X, ALU.add))
    link(dve.tensor_scalar(accepted, b.pos, float(capacity), None, ALU.is_le))
    link(dve.scalar_tensor_tensor(b.slot, index, float(capacity), b.pos, ALU.mult, ALU.add))
    link(dve.tensor_scalar(b.slot, b.slot, float(64 * capacity - 1), None, ALU.add))
    link(dve.tensor_tensor(b.kept, b.slot, accepted, ALU.mult))
    link(dve.tensor_copy(gather, b.kept))
    link(dve.tensor_tensor(b.slot, b.slot, trash, ALU.subtract))
    link(dve.tensor_tensor(b.slot, b.slot, accepted, ALU.mult))
    link(dve.tensor_tensor(b.slot, b.slot, trash, ALU.add))
    link(dve.tensor_copy(scatter, b.slot))


def stage_switch_experts(nc, net, io):
    with ExitStack() as ctx:
        sb = lambda name, shape, dt=F32: ctx.enter_context(nc.sbuf_tensor(net.name(name), shape, dt))
        n = norm_buffers(ctx, nc, net, in_psum=False)
        prob, eq, hot, pre = (sb(k, [P, NT, E1]) for k in ("prob", "equal", "hot", "pre"))
        top, tot, inv, gate, index, acc, pos, slot, kept = (sb(k, [P, NT]) for k in (
            "top", "total", "inv", "gate", "index", "accepted", "pos", "slot", "kept"))
        scatter, gather = sb("scatter", [P, NT], I32), sb("gather", [P, NT], I32)
        KT = SLOTS // P
        rows, rowsT = sb("rows", [P, KT, D]), sb("rowsT", [P, SLOTS])
        act_g, hid = sb("act_g", [P, 2, 4 * C1]), sb("hid", [P, 2, 4 * C1])
        y, yg = sb("y", [P, E1, D]), sb("y_token", [P, NT, D])
        STEPS = E1 // 4
        s = open_stage(nc, net.pool, f"v:80 logits:1 shifted:1 exp:1 hot:1 counts:1 slots:1 rowsT_ps:5 rowsT:5 g_ps:{STEPS} u_ps:{STEPS} "
                       f"silu:{STEPS} hid:{STEPS} y_ps:{STEPS} y_sb:{STEPS} combined:{NT + 1} " + NORM)
        bank = net.bank
        b3 = lambda k: bank[k][:, :].rearrange("p (t e) -> p t e", e=E1)
        wide = lambda ap: ap.unsqueeze(2).to_broadcast([P, NT, E1])
        iota = net.tab("iota32").unsqueeze(1).to_broadcast([P, NT, E1])
        moved, stored, fetched = net.moved, net.stored, net.fetched
        with nc.Block() as block:
            def down(pe, j):
                pe.wait_ge(s.hid.sem, s.hid.at(0, j + 1))
                if j >= 2:
                    pe.wait_ge(s.y_sb.sem, s.y_sb.at(0, j - 1))
                for k in range(4):
                    e = 4 * j + k
                    last = pe.matmul(bank[4 + j % 2][0:C1, k * P:(k + 1) * P], hid[:, j % 2, k * C1:(k + 1) * C1], net.moe_w[2][:, e, :], start=True, stop=True)
                last.then_inc(s.y_ps.sem, 1)

            @block.tensor
            def _(pe):
                pe.wait_ge(net.ld_w, net.w_ready)
                for t in range(NT):
                    last = pe.matmul(bank[0][:, t * E1:(t + 1) * E1], net.xT[:, t * P:(t + 1) * P], net.w_router[:, :], start=True, stop=True)
                last.then_inc(s.logits.sem, 1)
                pe.wait_ge(s.hot.sem, s.hot.at(0, 1))
                flat = hot[:, :, :].rearrange("p t e -> p (t e)")
                pe.matmul(bank[1][:, :], net.tab("tri"), flat, start=True, stop=True)
                pe.matmul(bank[2][:, :], net.tab("ones"), flat, start=True, stop=True).then_inc(s.counts.sem, 1)
                pe.wait_ge(net.rows_in, 16)
                for g in range(KT // 4):
                    if g == 1:
                        pe.wait_ge(s.slots.sem, s.slots.at(0, 1))
                    for k in range(4):
                        last = pe.transpose(bank[g][:, k * P:(k + 1) * P], rows[:, 4 * g + k, :], net.tab("ident"))
                    last.then_inc(s.rowsT_ps.sem, 1)
                pe.wait_ge(net.ld_moe, 16 * 3)
                for j in range(STEPS):
                    for w, ps, done in ((net.moe_w[0], 0, s.g_ps), (net.moe_w[1], 2, s.u_ps)):
                        if j == 0:
                            pe.wait_ge(s.rowsT.sem, s.rowsT.at(0, 5))
                        if j >= 2:
                            pe.wait_ge(s.hid.sem, s.hid.at(0, j - 1))
                        for k in range(4):
                            e = 4 * j + k
                            last = pe.matmul(bank[ps + j % 2][:, k * C1:(k + 1) * C1], w[:, e, :], rowsT[:, e * C1:(e + 1) * C1], start=True, stop=True)
                        last.then_inc(done.sem, 1)
                    if j >= 1:
                        down(pe, j - 1)
                down(pe, STEPS - 1)
                with pe.Fori(0, B) as i:
                    pe.wait_ge(s.x_updated.sem, s.x_updated.at(i, 0))
                    norm_pe(pe, s, n, i, bank[6][:, 0:L])

            def copy_y(act, j):
                act.wait_ge(s.y_ps.sem, s.y_ps.at(0, j + 1))
                act.activation(y[0:C1, 4 * j:4 * j + 4, :], bank[4 + j % 2][0:C1, :].rearrange("p (k d) -> p k d", d=D), ACT.Copy).then_inc(s.y_sb.sem, 1)

            @block.scalar
            def _(act):
                act.wait_ge(s.shifted.sem, s.shifted.at(0, 1))
                act.activation(prob[:, :, :], prob[:, :, :], ACT.Exp).then_inc(s.exp.sem, 1)
                for g in range(KT // 4):
                    act.wait_ge(s.rowsT_ps.sem, s.rowsT_ps.at(0, g + 1))
                    act.activation(rowsT[:, g * 512:(g + 1) * 512], bank[g][:, :], ACT.Copy).then_inc(s.rowsT.sem, 1)
                for j in range(STEPS):
                    act.wait_ge(s.g_ps.sem, s.g_ps.at(0, j + 1))
                    if j >= 2:
                        act.wait_ge(s.hid.sem, s.hid.at(0, j - 1))
                    act.activation(act_g[:, j % 2, :], bank[j % 2][:, 0:4 * C1], ACT.Silu).then_inc(s.silu.sem, 1)
                    if j >= 1:
                        copy_y(act, j - 1)
                copy_y(act, STEPS - 1)
                with act.Fori(0, B) as i:
                    norm_act(act, s, i, bank[6][:, 0:L], net.xT[:, bass.ds(i * L, L)])

            @block.vector
            def _(dve):
                count = [0]

                def link(ins):
                    count[0] += 1
                    ins.then_inc(s.v.sem, 1)
                    dve.wait_ge(s.v.sem, s.v.at(0, count[0]))

                dve.wait_ge(s.logits.sem, s.logits.at(0, 1))
                link(dve.tensor_reduce(top[:, :], b3(0), AX.X, ALU.max))
                dve.tensor_tensor(prob[:, :, :], b3(0), wide(top[:, :]), ALU.subtract).then_inc(s.shifted.sem, 1)
                dve.wait_ge(s.exp.sem, s.exp.at(0, 1))
                link(dve.tensor_reduce(tot[:, :], prob[:, :, :], AX.X, ALU.add))
                link(dve.reciprocal(inv[:, :], tot[:, :]))
                link(dve.tensor_tensor(prob[:, :, :], prob[:, :, :], wide(inv[:, :]), ALU.mult))
                choose_first(dve, link, prob[:, :, :], iota, gate[:, :], eq[:, :, :], index[:, :], hot[:, :, :], E1)
                dve.nop().then_inc(s.hot.sem, 1)
                dve.wait_ge(s.counts.sem, s.counts.at(0, 1))
                running_count(dve, link, net, pre, b3(1), b3(2), E1)
                b = group(tmp=eq[:, :, :], pos=pos[:, :], slot=slot[:, :], kept=kept[:, :])
                slots_of(dve, link, b, pre[:, :, :], hot[:, :, :], index[:, :], net.tab("trash")[:, 0:NT], C1,
                         scatter[:, :], gather[:, :], acc[:, :])
                link(dve.tensor_tensor(gate[:, :], gate[:, :], acc[:, :], ALU.mult))
                dve.nop().then_inc(s.slots.sem, 1)
                for j in range(STEPS):
                    dve.wait_ge(s.silu.sem, s.silu.at(0, j + 1))
                    dve.wait_ge(s.u_ps.sem, s.u_ps.at(0, j + 1))
                    if j >= 2:
                        dve.wait_ge(s.y_ps.sem, s.y_ps.at(0, j - 1))
                    dve.tensor_tensor(hid[:, j % 2, :], act_g[:, j % 2, :], bank[2 + j % 2][:, 0:4 * C1], ALU.mult).then_inc(s.hid.sem, 1)
                dve.wait_ge(fetched, 16 * NT)
                for t in range(NT):
                    dve.tensor_scalar(yg[:, t, :], yg[:, t, :], gate[:, t:t + 1], None, ALU.mult).then_inc(s.combined.sem, 1)
                dve.wait_ge(s.combined.sem, s.combined.at(0, NT))
                flat = yg[:, :, :].rearrange("p t d -> p (t d)")
                dve.scalar_tensor_tensor(flat, net.x_tok[:, :], 2.0, flat, ALU.mult, ALU.add).then_inc(s.combined.sem, 1)
                dve.wait_ge(s.combined.sem, s.combined.at(0, NT + 1))
                with dve.Fori(0, B) as i:
                    norm_dve(dve, s, n, i, yg[:, bass.ds(TPB * i, TPB), :])

            @block.gpsimd
            def _(pool):
                pool.wait_ge(s.slots.sem, s.slots.at(0, 1))
                pool.wait_ge(net.zeroed, net.zero_ready)
                for t in range(NT):
                    pool.indirect_dma_start(net.slots[0], bass.IndirectOffsetOnAxis(ap=scatter[:, t:t + 1], axis=0),
                                            net.x_tok[:, t * P:(t + 1) * P], None).then_inc(moved, 16)
                pool.wait_ge(stored, 16)
                for t in range(NT):
                    pool.indirect_dma_start(yg[:, t, :], None, net.slots_out[0],
                                            bass.IndirectOffsetOnAxis(ap=gather[:, t:t + 1], axis=0)).then_inc(fetched, 16)
                with pool.Fori(0, B) as i:
                    norm_pool(pool, s, n, i)

            @block.sync
            def _(sp):
                with nc.allow_non_contiguous_dma(reason="biases, one to a partition"):
                    for to, of, done in net.loads2:
                        sp.dma_start(to, of).then_inc(done, 16)
                sp.wait_ge(moved, 16 * NT)
                sp.dma_start(rows[:, :, :], net.slots[0][0:SLOTS, :].rearrange("(k p) d -> p k d", p=P)).then_inc(net.rows_in, 16)
                sp.wait_ge(s.y_sb.sem, s.y_sb.at(0, STEPS))
                sp.dma_start(net.slots_out[0].rearrange("(e c) d -> c e d", c=C1), y[0:C1, :, :]).then_inc(stored, 16)
    close_stage(nc, net.pool)


def stage_mha(nc, net, w, mask, src, dst, load=()):
    with ExitStack() as ctx:
        sb = lambda name, shape: ctx.enter_context(nc.sbuf_tensor(net.name(name), shape, F32))
        K = 4
        TURNS = T // (K * P)
        BL = P // NL
        HW = AH * NL
        RING = 6 * K
        qk_w, vp_w = sb("wk_wq", [P, AH, D]), sb("wv_wp", [P, AH, D])
        w_res = sb("residual", [P, D])
        U, Z = sb("U", [P, 2, AH, P]), sb("Z", [P, AH, P])
        turned = U[:, :, :, :].rearrange("p a h t -> p (a h t)")
        xs, x_tok = sb("xs", [P, K, P]), sb("x_rows", [P, 2, D])
        S, A = sb("prob", [P, AH, NL]), sb("probT", [P, 2, HW])
        top, tot, inv = sb("top", [P, AH]), sb("total", [P, AH]), sb("inv", [P, AH])
        st, mv, ve, rstd, xn = sb("st", [P, 6]), sb("mv", [P, 2, 2]), sb("ve", [P, 2]), sb("rstd", [P, 2]), sb("xn", [P, 2, D])
        s = open_stage(nc, net.pool, f"settled:0 w_ps:6 w_act:6 m_ps:8 m_act:4 m_dve:4 sum_ps:1 w_res:1 xs_ready:{K} ring_ps:{RING} ring:{RING} "
                       f"scored:{K} masked:{K} top:{K} shifted:{K} exped:{K} total:{K} inv:{K} prob:{K} probT:{K} "
                       f"z_ps:{BL * K} z_act:{2 * K} z_dve:{2 * K} y_ready:{K} stats:{K} agg:{K} var_eps:{K} rstd:{K} xn_ready:{K}")
        bank, ident = net.bank, net.tab("ident")

        def items(k, first, last):
            here = [] if last and k + 1 >= K else [("u", k + 1, g) for g in range(5)]
            if not (first and k < 2):
                here.append(("n", k - 2, 0))
            at = 5 * (k + 1) if first and k < 2 else 6 * k + 3 if k < K else 6 * (K - 1) + 4 + k - K
            return [(at + d, *item) for d, item in enumerate(here)]

        u_end = lambda k, first: items(k - 1, first, False)[4][0] + 1
        def turns(eng, turn):
            turn(0, True, False)
            with eng.Fori(1, TURNS - 1) as i:
                turn(i, False, False)
            turn(TURNS - 1, False, True)

        per_head = lambda ap: ap.unsqueeze(2).to_broadcast([P, AH, NL])
        with nc.Block() as block:
            @block.sync
            def _(sp):
                with nc.allow_non_contiguous_dma(reason="biases, one to a partition, and a small router"):
                    for to, of, done in load:
                        sp.dma_start(to, of).then_inc(done, 16)

            @block.gpsimd
            def _(pool):
                with pool.Fori(0, TURNS) as i:
                    for k in range(K):
                        pool.wait_ge(s.agg.sem, s.agg.at(i, k + 1))
                        pool.tensor_tensor(ve[:, k % 2:k % 2 + 1], mv[:, k % 2, 1:2], net.eps[:, 0:1], ALU.add).then_inc(s.var_eps.sem, 1)
                        pool.wait_ge(s.var_eps.sem, s.var_eps.at(i, k + 1))
                        pool.tensor_tensor(rstd[:, k % 2:k % 2 + 1], ve[:, k % 2:k % 2 + 1], net.neghalf[:, 0:1], ALU.pow).then_inc(s.rstd.sem, 1)

            @block.tensor
            def _(pe):
                pe.wait_ge(net.ld_w2, net.w2_ready)
                for j, wt in enumerate((w.q, w.k, w.v)):
                    for b in range(2):
                        for c in range(4):
                            last = pe.transpose(bank[2 * j + b][:, c * P:(c + 1) * P], wt[:, (4 * b + c) * P:(4 * b + c + 1) * P], ident)
                        last.then_inc(s.w_ps.sem, 1)
                pe.wait_ge(s.w_act.sem, s.w_act.at(0, 6))
                row = lambda h: slice(ADK * (h % 2), ADK * (h % 2) + ADK)
                part = lambda j, h: turned[row(h), (8 * j + h // 2) * P:(8 * j + h // 2 + 1) * P]
                for q in range(8):
                    for m in range(4):
                        h = 2 * (4 * (q % 2) + m) + (q // 2) % 2
                        if q < 4:
                            last = pe.matmul(bank[q][:, m * P:(m + 1) * P], part(1, h), part(0, h), start=True, stop=True)
                        else:
                            last = pe.matmul(bank[q][:, m * P:(m + 1) * P], part(2, h), w.p[row(h), h // 2, :], start=True, stop=True)
                    last.then_inc(s.m_ps.sem, 1)
                pe.wait_ge(s.m_act.sem, s.m_act.at(0, 4))
                for c in range(AH // 2):
                    last = pe.matmul(bank[0][:, 0:D], turned[:, (16 + c) * P:(17 + c) * P], w.p[:, c, :], start=(c == 0), stop=(c == AH // 2 - 1))
                last.then_inc(s.sum_ps.sem, 1)
                pe.wait_ge(s.w_res.sem, s.w_res.at(0, 1))

                def ring(i, k, first, last):
                    for n, what, m, g in items(k, first, last):
                        to = bank[n % 2]
                        pe.wait_ge(s.ring.sem, s.ring.at(i, n - 1 if n or not first else 0))
                        if what == "n":
                            pe.wait_ge(s.xn_ready.sem, s.xn_ready.at(i, m + 1))
                            last_ins = pe.transpose(to[:, 0:P], xn[:, m % 2, :], ident)
                        elif g == 0:
                            pe.wait_ge(s.xs_ready.sem, s.xs_ready.at(i, m + 1))
                            last_ins = pe.transpose(to[:, 0:P], xs[:, m % K, :], ident)
                        else:
                            for h in range(4):
                                last_ins = pe.matmul(to[:, h * P:(h + 1) * P], qk_w[:, 4 * (g - 1) + h, :], xs[:, m % K, :], start=True, stop=True)
                        last_ins.then_inc(s.ring_ps.sem, 1)

                def project(i, j):
                    pe.wait_ge(s.z_act.sem, s.z_act.at(i, 2 * j + 2))
                    pe.wait_ge(s.z_dve.sem, s.z_dve.at(i, 2 * j + 2))
                    pe.wait_ge(s.xn_ready.sem, s.xn_ready.at(i, j))
                    for h in range(AH):
                        pe.matmul(bank[3][:, 0:D], Z[:, h, :], vp_w[:, h, :], start=(h == 0), stop=False)
                    pe.matmul(bank[3][:, 0:D], net.tab("ones")[0:1, :], w.pb[:, :], start=False, stop=False)
                    pe.matmul(bank[3][:, 0:D], xs[:, j % K, :], w_res[:, :], start=False, stop=True).then_inc(s.y_ready.sem, 1)

                def turn(i, first, last):
                    if first:
                        ring(i, -1, first, last)
                    for k in range(K):
                        pe.wait_ge(s.ring.sem, s.ring.at(i, u_end(k, first)))
                        pe.wait_ge(s.shifted.sem, s.shifted.at(i, k))
                        for b in range(BL):
                            blk = slice(NL * b, NL * (b + 1))
                            last_ins = pe.matmul(bank[2][blk, :], xs[:, k, blk], U[:, k % 2, :, blk], start=True, stop=True)
                        last_ins.then_inc(s.scored.sem, 1)
                        ring(i, k, first, last)
                        if not (first and k == 0):
                            project(i, k - 1)
                        pe.wait_ge(s.probT.sem, s.probT.at(i, k + 1))
                        pe.wait_ge(s.z_act.sem, s.z_act.at(i, 2 * k))
                        pe.wait_ge(s.z_dve.sem, s.z_dve.at(i, 2 * k))
                        for b in range(BL):
                            blk = slice(NL * b, NL * (b + 1))
                            pe.matmul(bank[4 + b][:, :], x_tok[blk, k % 2, :], A[blk, k % 2, :], start=True, stop=True).then_inc(s.z_ps.sem, 1)
                    if last:
                        ring(i, K, first, last)
                        project(i, K - 1)
                        ring(i, K + 1, first, last)
                turns(pe, turn)

            @block.scalar
            def _(act):
                for n in range(6):
                    act.wait_ge(s.w_ps.sem, s.w_ps.at(0, n + 1))
                    act.activation(turned[:, n * 512:(n + 1) * 512], bank[n][:, :], ACT.Copy).then_inc(s.w_act.sem, 1)
                for q in range(4):
                    act.wait_ge(s.m_ps.sem, s.m_ps.at(0, q + 1))
                    h = 8 * (q % 2) + q // 2
                    act.activation(qk_w[:, h:h + 7:2, :], bank[q][:, :].rearrange("p (m d) -> p m d", m=4), ACT.Copy).then_inc(s.m_act.sem, 1)

                def load_x(i, k):
                    settle(act, s)
                    act.activation(xs[:, k % K, :], src[:, bass.ds(i * K * P + k * P, P)], ACT.Copy).then_inc(s.xs_ready.sem, 1)

                def ring(i, here):
                    for n, what, m, g in here:
                        act.wait_ge(s.ring_ps.sem, s.ring_ps.at(i, n + 1))
                        if what == "n":
                            settle(act, s)
                            act.activation(dst[:, bass.ds(i * K * P + m * P, P)], bank[n % 2][:, 0:P], ACT.Identity,
                                           scale=w.g[:, :], bias=w.b[:, :]).then_inc(s.ring.sem, 1)
                        elif g == 0:
                            act.activation(x_tok[:, m % 2, :], bank[n % 2][:, 0:P], ACT.Copy).then_inc(s.ring.sem, 1)
                        else:
                            act.activation(U[:, m % 2, 4 * (g - 1):4 * g, :], bank[n % 2][:, :].rearrange("p (h t) -> p h t", h=4), ACT.Copy)\
                                .then_inc(s.ring.sem, 1)

                def turn(i, first, last):
                    if first:
                        load_x(i, 0)
                        load_x(i, 1)
                        ring(i, items(-1, first, last))
                    for k in range(K):
                        if not (last and k + 2 >= K):
                            if not (first and k < 2):
                                act.wait_ge(s.y_ready.sem, s.y_ready.at(i, k - 1))
                            load_x(i, k + 2)
                        here = items(k, first, last)
                        ring(i, here[0:2])
                        act.wait_ge(s.shifted.sem, s.shifted.at(i, k + 1))
                        act.activation(S[:, :, :], S[:, :, :], ACT.Exp, scale=ADK ** -0.5).then_inc(s.exped.sem, 1)
                        ring(i, here[2:])
                        for b in range(2):
                            act.wait_ge(s.z_ps.sem, s.z_ps.at(i, BL * k + b + 1))
                            act.activation(Z[:, :, NL * b:NL * (b + 1)], bank[4 + b][:, :].rearrange("p (h q) -> p h q", h=AH), ACT.Copy)\
                                .then_inc(s.z_act.sem, 1)
                    if last:
                        ring(i, items(K, first, last))
                        ring(i, items(K + 1, first, last))
                turns(act, turn)

            @block.vector
            def _(dve):
                for q in range(4):
                    dve.wait_ge(s.m_ps.sem, s.m_ps.at(0, q + 5))
                    h = 8 * (q % 2) + q // 2
                    dve.tensor_copy(vp_w[:, h:h + 7:2, :], bank[4 + q][:, :].rearrange("p (m d) -> p m d", m=4)).then_inc(s.m_dve.sem, 1)
                dve.wait_ge(s.sum_ps.sem, s.sum_ps.at(0, 1))
                dve.tensor_tensor(w_res[:, :], ident, bank[0][:, 0:D], ALU.subtract).then_inc(s.w_res.sem, 1)

                def turn(i, first, last):
                    for k in range(K + 1 if last else K):
                        behind = not (first and k == 0)
                        if k < K:
                            scores = bank[2][:, :].rearrange("p (h q) -> p h q", h=AH)
                            dve.wait_ge(s.scored.sem, s.scored.at(i, k + 1))
                            if mask is not None:
                                dve.tensor_tensor(S[:, :, :], scores, mask.unsqueeze(1).to_broadcast([P, AH, NL]), ALU.add).then_inc(s.masked.sem, 1)
                                dve.wait_ge(s.masked.sem, s.masked.at(i, k + 1))
                                scores = S[:, :, :]
                            dve.tensor_reduce(top[:, :], scores, AX.X, ALU.max).then_inc(s.top.sem, 1)
                            dve.wait_ge(s.top.sem, s.top.at(i, k + 1))
                            dve.tensor_tensor(S[:, :, :], scores, per_head(top[:, :]), ALU.subtract).then_inc(s.shifted.sem, 1)
                            dve.wait_ge(s.exped.sem, s.exped.at(i, k + 1))
                            dve.tensor_reduce(tot[:, :], S[:, :, :], AX.X, ALU.add).then_inc(s.total.sem, 1)
                            dve.wait_ge(s.total.sem, s.total.at(i, k + 1))
                            dve.reciprocal(inv[:, :], tot[:, :]).then_inc(s.inv.sem, 1)
                            dve.wait_ge(s.inv.sem, s.inv.at(i, k + 1))
                            dve.tensor_tensor(S[:, :, :], S[:, :, :], per_head(inv[:, :]), ALU.mult).then_inc(s.prob.sem, 1)
                            dve.wait_ge(s.prob.sem, s.prob.at(i, k + 1))
                            dve.transpose(A[:, k % 2, :], S[:, :, :].rearrange("p h q -> p (h q)")).then_inc(s.probT.sem, 1)
                        if behind:
                            j = k - 1
                            dve.wait_ge(s.y_ready.sem, s.y_ready.at(i, j + 1))
                            dve.bn_stats(st[:, :], bank[3][:, 0:D]).then_inc(s.stats.sem, 1)
                            dve.wait_ge(s.stats.sem, s.stats.at(i, j + 1))
                            settle(dve, s)
                            dve.bn_aggr(mv[:, j % 2, :], st[:, :]).then_inc(s.agg.sem, 1)
                        if k < K:
                            for b in range(2, BL):
                                dve.wait_ge(s.z_ps.sem, s.z_ps.at(i, BL * k + b + 1))
                                dve.tensor_copy(Z[:, :, NL * b:NL * (b + 1)], bank[4 + b][:, :].rearrange("p (h q) -> p h q", h=AH)).then_inc(s.z_dve.sem, 1)
                        if behind:
                            dve.wait_ge(s.rstd.sem, s.rstd.at(i, j + 1))
                            dve.tensor_scalar(xn[:, j % 2, :], bank[3][:, 0:D], mv[:, j % 2, 0:1], rstd[:, j % 2:j % 2 + 1], ALU.subtract, ALU.mult)\
                                .then_inc(s.xn_ready.sem, 1)
                turns(dve, turn)
    close_stage(nc, net.pool)


def stage_relu_mlp(nc, net, w, x, final, order, order_to):
    with ExitStack() as ctx:
        sb = lambda name, shape: ctx.enter_context(nc.sbuf_tensor(net.name(name), shape, F32))
        n, nf = norm_buffers(ctx, nc, net), norm_buffers(ctx, nc, net, keep=True)
        C = DI // P
        xs, x0, z, hid = sb("xs", [P, L]), sb("x0", [P, L]), sb("z", [P, L]), sb("hid", [P, C, L])
        s = open_stage(nc, net.pool, f"xs_ready:1 x0_ready:1 h_ps:{C} hid:{C} " + NORM + " " + prefixed("f_", NORM))
        f = part(s, "f_")
        bank, ident = net.bank, net.tab("ident")
        y_bank, yT_bank, z_bank, zT_bank = bank[4:8]
        tiles = lambda bank: bank[:, 0:L].rearrange("p (t d) -> p t d", d=D)
        with nc.Block() as block:
            @block.gpsimd
            def _(pool):
                def turn(i, ahead, own, behind):
                    if own:
                        norm_pool(pool, s, n, i)
                    if behind:
                        norm_pool(pool, f, nf, i - 1)
                skewed(pool, turn, final)

            @block.tensor
            def _(pe):
                pe.wait_ge(net.ld_w2, net.w2_ready)

                def turn(i, ahead, own, behind):
                    if ahead:
                        pe.wait_ge(s.xs_ready.sem, s.xs_ready.at(i + 1, 1))
                        pe.wait_ge(s.hid.sem, s.hid.at(i + 1, 0))
                        for c in range(C):
                            pe.matmul(bank[c][:, 0:L], w.w1[:, c * P:(c + 1) * P], xs[:, :], start=True, stop=True).then_inc(s.h_ps.sem, 1)
                    if behind:
                        pe.wait_ge(s.x_updated.sem, s.x_updated.at(i - 1, 1))
                        pe.wait_ge(s.x0_ready.sem, s.x0_ready.at(i - 1, 1))
                        pe.wait_ge(f.xn_ready.sem, f.xn_ready.at(i - 1, 0))
                        for t in range(TPB):
                            tok = slice(t * P, (t + 1) * P)
                            pe.matmul(z_bank[:, tok], z[:, tok], ident, start=True, stop=False)
                            last = pe.matmul(z_bank[:, tok], x0[:, tok], ident, start=False, stop=True)
                        last.then_inc(f.y_ready.sem, 1)
                    if own:
                        pe.wait_ge(s.x_updated.sem, s.x_updated.at(i, 0))
                        norm_pe(pe, s, n, i, yT_bank[:, 0:L])
                    if ahead:
                        pe.wait_ge(s.xn_ready.sem, s.xn_ready.at(i + 1, 0))
                        pe.wait_ge(s.hid.sem, s.hid.at(i + 1, C))
                        for t in range(TPB):
                            tok = slice(t * P, (t + 1) * P)
                            for c in range(C):
                                pe.matmul(y_bank[:, tok], hid[:, c, tok], w.w2[:, c, :], start=(c == 0), stop=False)
                            pe.matmul(y_bank[:, tok], net.tab("ones")[0:1, :], w.b2[:, :], start=False, stop=False)
                            last = pe.matmul(y_bank[:, tok], xs[:, tok], ident, start=False, stop=True)
                        last.then_inc(s.y_ready.sem, 1)
                    if behind:
                        pe.wait_ge(f.x_updated.sem, f.x_updated.at(i - 1, 0))
                        norm_pe(pe, f, nf, i - 1, zT_bank[:, 0:L])
                skewed(pe, turn, final)

            @block.scalar
            def _(act):
                act.wait_ge(net.ld_w2, net.w2_ready)

                def turn(i, ahead, own, behind):
                    if ahead:
                        act.wait_ge(s.y_ready.sem, s.y_ready.at(i + 1, 0))
                        settle(act, s)
                        act.activation(xs[:, :], x[:, bass.ds((i + 1) * L, L)], ACT.Copy).then_inc(s.xs_ready.sem, 1)
                        for c in range(C):
                            act.wait_ge(s.h_ps.sem, s.h_ps.at(i + 1, c + 1))
                            act.activation(hid[:, c, :], bank[c][:, 0:L], ACT.Relu, bias=w.b1[:, c:c + 1]).then_inc(s.hid.sem, 1)
                    if own and final:
                        act.wait_ge(f.y_ready.sem, f.y_ready.at(i, 0))
                        settle(act, s)
                        act.activation(x0[:, :], net.xT[:, bass.ds(i * L, L)], ACT.Copy).then_inc(s.x0_ready.sem, 1)
                    if own:
                        dst = z[:, :] if final else x[:, bass.ds(i * L, L)]
                        norm_act(act, s, i, order(yT_bank[:, 0:L]), order_to(dst), w.g[:, :], w.b[:, :])
                    if behind:
                        norm_act(act, f, i - 1, zT_bank[:, 0:L], net.xT[:, bass.ds((i - 1) * L, L)])
                skewed(act, turn, final)

            @block.vector
            def _(dve):
                def turn(i, ahead, own, behind):
                    if own:
                        norm_stats(dve, s, n, i, tiles(y_bank))
                    if behind:
                        norm_stats(dve, f, nf, i - 1, tiles(z_bank))
                    if own:
                        norm_apply(dve, s, n, i, tiles(y_bank))
                    if behind:
                        norm_apply(dve, f, nf, i - 1, tiles(z_bank))
                skewed(dve, turn, final)
    close_stage(nc, net.pool)


def stage_top2_experts(nc, net, io):
    with ExitStack() as ctx:
        sb = lambda name, shape, dt=F32: ctx.enter_context(nc.sbuf_tensor(net.name(name), shape, dt))
        n = norm_buffers(ctx, nc, net, in_psum=False)
        prob, rest, eq, hot1, hot2, pre = (sb(k, [P, NT, E2]) for k in ("prob", "rest", "equal", "hot1", "hot2", "pre"))
        (top, tot, inv, p1, p2, i1, i2, acc1, acc2, pos, slot, kept, ms, rms) = (sb(k, [P, NT]) for k in (
            "top", "total", "inv", "p1", "p2", "index1", "index2", "acc1", "acc2", "pos", "slot", "kept", "mean_sq", "rms"))
        scatter, gather = sb("scatter", [P, 2, NT], I32), sb("gather", [P, 2, NT], I32)
        sq = sb("square", [P, D])
        KT = SLOTS // P
        rows, rowsT = sb("rows", [P, KT, D]), sb("rowsT", [P, SLOTS])
        FC = IR // P
        act_g, hid = sb("act_g", [P, 2, C2]), sb("hid", [P, 2, FC, C2])
        yg1, yg2 = sb("y_first", [P, NT, D]), sb("y_second", [P, NT, D])
        y = sb("y", [P, 2, 3, D])
        SC = IS // P
        sgate, shid = sb("shared_gate", [P, 2, L]), sb("shared_hid", [P, SC, L])
        xs, z = sb("xs", [P, L]), sb("z", [P, TPB, D])
        shared = sb("shared", [P, NT, D])
        parts = ((0, B // 2), (B // 2, B))
        MS = [(0, P), (P, P), (2 * P, C2 - 2 * P)]
        s = open_stage(nc, net.pool, f"v:120 logits:1 squares:{NT} mean:1 rms:1 shifted:1 exp:1 hot:1 counts:1 slots:1 rowsT_ps:5 rowsT:5 "
                       f"g_ps:{E2 * FC} u_ps:{E2 * FC} silu:{E2 * FC} hid:{E2 * FC} y_ps:{E2} y_sb:{E2} "
                       f"xs_ready:1 sg_ps:{SC} su_ps:{SC} s_silu:{SC} s_hid:{SC} shared_ps:1 shared:1 z_ready:1 " + NORM)
        bank = net.bank
        b3 = lambda k: bank[k][:, 0:NT * E2].rearrange("p (t e) -> p t e", e=E2)
        wide = lambda ap: ap.unsqueeze(2).to_broadcast([P, NT, E2])
        iota = net.tab("iota32")[:, 0:E2].unsqueeze(1).to_broadcast([P, NT, E2])
        rg, ru = (net.moe_w[k][:, :, :].rearrange("p e f -> p (e f)").rearrange("p (e i) -> p e i", e=E2) for k in range(2))
        rd = net.moe_w[2][:, :, :].rearrange("p (e c) d -> p e c d", e=E2)
        moved, stored, fetched = net.moved2, net.stored2, net.fetched2
        with nc.Block() as block:
            gate_bank, up_bank = (lambda c: bank[3 + c % 2]), (lambda c: bank[5 + c % 2])

            def down(pe, e):
                pe.wait_ge(s.hid.sem, s.hid.at(0, FC * (e + 1)))
                if e >= 1:
                    pe.wait_ge(s.y_sb.sem, s.y_sb.at(0, e))
                for m, (at, w) in enumerate(MS):
                    for c in range(FC):
                        last = pe.matmul(bank[4][0:w, m * P:(m + 1) * P], hid[:, e % 2, c, at:at + w], rd[:, e, c, :], start=(c == 0), stop=(c == FC - 1))
                last.then_inc(s.y_ps.sem, 1)

            @block.tensor
            def _(pe):
                pe.wait_ge(net.ld_w3, net.w3_ready)
                for t in range(NT):
                    last = pe.matmul(bank[0][:, t * E2:(t + 1) * E2], net.xT[:, t * P:(t + 1) * P], net.router2[:, :], start=True, stop=True)
                last.then_inc(s.logits.sem, 1)
                pe.wait_ge(s.hot.sem, s.hot.at(0, 1))
                flat = eq[:, :, :].rearrange("p t e -> p (t e)")
                pe.matmul(bank[1][:, 0:NT * E2], net.tab("tri"), flat, start=True, stop=True)
                pe.matmul(bank[2][:, 0:NT * E2], net.tab("ones"), flat, start=True, stop=True).then_inc(s.counts.sem, 1)

                def shared_expert(part):
                    with pe.Fori(*parts[part]) as i:
                        pe.wait_ge(s.xs_ready.sem, s.xs_ready.at(i, 1))
                        for c in range(SC):
                            pe.wait_ge(s.s_hid.sem, s.s_hid.at(i, max(0, c - 1)))
                            for w, to, done in ((net.sg, gate_bank(c), s.sg_ps), (net.su, up_bank(c), s.su_ps)):
                                pe.matmul(to[:, 0:L], w[:, c * P:(c + 1) * P], xs[:, :], start=True, stop=True).then_inc(done.sem, 1)
                        pe.wait_ge(s.s_hid.sem, s.s_hid.at(i, SC))
                        pe.wait_ge(s.shared.sem, s.shared.at(i, 0))
                        for t in range(TPB):
                            tok = slice(t * P, (t + 1) * P)
                            for c in range(SC):
                                pe.matmul(bank[7][:, tok], shid[:, c, tok], net.sd[:, c, :], start=(c == 0), stop=False)
                            last = pe.matmul(bank[7][:, tok], xs[:, tok], net.tab("ident"), start=False, stop=True)
                        last.then_inc(s.shared_ps.sem, 1)

                shared_expert(0)
                pe.wait_ge(net.rows_in, 32)
                pe.wait_ge(s.slots.sem, s.slots.at(0, 1))
                for g in range(KT // 4):
                    for k in range(4):
                        last = pe.transpose(bank[g][:, k * P:(k + 1) * P], rows[:, 4 * g + k, :], net.tab("ident"))
                    last.then_inc(s.rowsT_ps.sem, 1)
                pe.wait_ge(s.rowsT.sem, s.rowsT.at(0, 5))
                for e in range(E2):
                    x = rowsT[:, e * C2:(e + 1) * C2]
                    for c in range(FC):
                        j = FC * e + c
                        for w, ps, done in ((rg, 0, s.g_ps), (ru, 2, s.u_ps)):
                            if j >= 2:
                                pe.wait_ge(s.hid.sem, s.hid.at(0, j - 1))
                            pe.matmul(bank[ps + j % 2][:, 0:C2], w[:, e, c * P:(c + 1) * P], x, start=True, stop=True).then_inc(done.sem, 1)
                    if e >= 1:
                        down(pe, e - 1)
                down(pe, E2 - 1)
                pe.wait_ge(s.y_sb.sem, s.y_sb.at(0, E2))
                shared_expert(1)
                with pe.Fori(0, B) as i:
                    pe.wait_ge(s.x_updated.sem, s.x_updated.at(i, 0))
                    norm_pe(pe, s, n, i, bank[1][:, 0:L])

            def copy_y(act, e):
                act.wait_ge(s.y_ps.sem, s.y_ps.at(0, e + 1))
                if e >= 2:
                    act.wait_ge(stored[e % 2], 16 * 2 * (e // 2))
                act.activation(y[:, e % 2, 0:2, :], bank[4][:, 0:2 * P].rearrange("p (k d) -> p k d", d=D), ACT.Copy)
                act.activation(y[0:C2 - 2 * P, e % 2, 2, :], bank[4][0:C2 - 2 * P, 2 * P:3 * P], ACT.Copy).then_inc(s.y_sb.sem, 1)

            @block.scalar
            def _(act):
                for t in range(NT):
                    act.activation(sq[:, :], net.x_tok[:, t * P:(t + 1) * P], ACT.Square, accum_out=ms[:, t:t + 1]).then_inc(s.squares.sem, 1)
                    act.wait_ge(s.squares.sem, s.squares.at(0, t + 1))
                act.wait_ge(s.shifted.sem, s.shifted.at(0, 1))
                act.activation(prob[:, :, :], prob[:, :, :], ACT.Exp).then_inc(s.exp.sem, 1)

                def shared_expert(part):
                    with act.Fori(*parts[part]) as i:
                        act.wait_ge(s.shared_ps.sem, s.shared_ps.at(i, 0))
                        settle(act, s)
                        act.activation(xs[:, :], net.xT[:, bass.ds(i * L, L)], ACT.Copy).then_inc(s.xs_ready.sem, 1)
                        for c in range(SC):
                            act.wait_ge(s.sg_ps.sem, s.sg_ps.at(i, c + 1))
                            act.wait_ge(s.s_hid.sem, s.s_hid.at(i, max(0, c - 1)))
                            act.activation(sgate[:, c % 2, :], gate_bank(c)[:, 0:L], ACT.Silu).then_inc(s.s_silu.sem, 1)
                        act.wait_ge(s.shared_ps.sem, s.shared_ps.at(i, 1))
                        settle(act, s)
                        act.activation(shared[:, bass.ds(TPB * i, TPB), :], bank[7][:, 0:L].rearrange("p (t d) -> p t d", d=D), ACT.Copy)\
                            .then_inc(s.shared.sem, 1)

                shared_expert(0)
                for g in range(KT // 4):
                    act.wait_ge(s.rowsT_ps.sem, s.rowsT_ps.at(0, g + 1))
                    act.activation(rowsT[:, g * 512:(g + 1) * 512], bank[g][:, :], ACT.Copy).then_inc(s.rowsT.sem, 1)
                for e in range(E2):
                    for c in range(FC):
                        j = FC * e + c
                        act.wait_ge(s.g_ps.sem, s.g_ps.at(0, j + 1))
                        if j >= 2:
                            act.wait_ge(s.hid.sem, s.hid.at(0, j - 1))
                        act.activation(act_g[:, j % 2, :], bank[j % 2][:, 0:C2], ACT.Silu).then_inc(s.silu.sem, 1)
                    if e >= 1:
                        copy_y(act, e - 1)
                copy_y(act, E2 - 1)
                shared_expert(1)
                with act.Fori(0, B) as i:
                    norm_act(act, s, i, bank[1][:, 0:L], net.xT[:, bass.ds(i * L, L)])

            @block.vector
            def _(dve):
                count = [0]

                def link(ins):
                    count[0] += 1
                    ins.then_inc(s.v.sem, 1)
                    dve.wait_ge(s.v.sem, s.v.at(0, count[0]))

                dve.wait_ge(s.squares.sem, s.squares.at(0, NT))
                dve.tensor_scalar(ms[:, :], ms[:, :], 1.0 / D, float(np.finfo(np.float32).eps), ALU.mult, ALU.add).then_inc(s.mean.sem, 1)
                dve.wait_ge(s.logits.sem, s.logits.at(0, 1))
                dve.wait_ge(s.rms.sem, s.rms.at(0, 1))
                link(dve.tensor_tensor(prob[:, :, :], b3(0), wide(rms[:, :]), ALU.mult))
                link(dve.tensor_reduce(top[:, :], prob[:, :, :], AX.X, ALU.max))
                dve.tensor_tensor(prob[:, :, :], prob[:, :, :], wide(top[:, :]), ALU.subtract).then_inc(s.shifted.sem, 1)
                dve.wait_ge(s.exp.sem, s.exp.at(0, 1))
                link(dve.tensor_reduce(tot[:, :], prob[:, :, :], AX.X, ALU.add))
                link(dve.reciprocal(inv[:, :], tot[:, :]))
                link(dve.tensor_tensor(prob[:, :, :], prob[:, :, :], wide(inv[:, :]), ALU.mult))
                choose_first(dve, link, prob[:, :, :], iota, p1[:, :], eq[:, :, :], i1[:, :], hot1[:, :, :], E2)
                link(dve.scalar_tensor_tensor(rest[:, :, :], hot1[:, :, :], -2.0, prob[:, :, :], ALU.mult, ALU.add))
                choose_first(dve, link, rest[:, :, :], iota, p2[:, :], eq[:, :, :], i2[:, :], hot2[:, :, :], E2)
                link(dve.tensor_tensor(eq[:, :, :], hot1[:, :, :], hot2[:, :, :], ALU.add))
                dve.nop().then_inc(s.hot.sem, 1)
                link(dve.tensor_tensor(tot[:, :], p1[:, :], p2[:, :], ALU.add))
                link(dve.reciprocal(inv[:, :], tot[:, :]))
                dve.wait_ge(s.counts.sem, s.counts.at(0, 1))
                running_count(dve, link, net, pre, b3(1), b3(2), E2)
                b = group(tmp=eq[:, :, :], pos=pos[:, :], slot=slot[:, :], kept=kept[:, :])
                for k, (hot, index, acc, p) in enumerate(((hot1, i1, acc1, p1), (hot2, i2, acc2, p2))):
                    slots_of(dve, link, b, pre[:, :, :], hot[:, :, :], index[:, :], net.tab("trash")[:, k * NT:(k + 1) * NT], C2,
                             scatter[:, k, :], gather[:, k, :], acc[:, :])
                    link(dve.tensor_tensor(p[:, :], p[:, :], inv[:, :], ALU.mult))
                    link(dve.tensor_tensor(p[:, :], p[:, :], acc[:, :], ALU.mult))
                dve.nop().then_inc(s.slots.sem, 1)

                def shared_batch(i):
                    for c in range(SC):
                        dve.wait_ge(s.s_silu.sem, s.s_silu.at(i, c + 1))
                        dve.wait_ge(s.su_ps.sem, s.su_ps.at(i, c + 1))
                        dve.wait_ge(s.shared_ps.sem, s.shared_ps.at(i, 0))
                        dve.tensor_tensor(shid[:, c, :], sgate[:, c % 2, :], up_bank(c)[:, 0:L], ALU.mult).then_inc(s.s_hid.sem, 1)

                with dve.Fori(*parts[0]) as i:
                    shared_batch(i)
                for e in range(E2):
                    for c in range(FC):
                        j = FC * e + c
                        dve.wait_ge(s.silu.sem, s.silu.at(0, j + 1))
                        dve.wait_ge(s.u_ps.sem, s.u_ps.at(0, j + 1))
                        if e >= 2:
                            dve.wait_ge(s.y_ps.sem, s.y_ps.at(0, e - 1))
                        dve.tensor_tensor(hid[:, e % 2, c, :], act_g[:, j % 2, :], bank[2 + j % 2][:, 0:C2], ALU.mult).then_inc(s.hid.sem, 1)
                with dve.Fori(parts[1][0], B - 1) as i:
                    shared_batch(i)
                dve.wait_ge(fetched, 16 * 2 * NT)
                wide_d = lambda ap: ap.unsqueeze(2).to_broadcast([P, NT, D])
                link(dve.tensor_tensor(yg1[:, :, :], yg1[:, :, :], wide_d(p1[:, :]), ALU.mult))
                link(dve.tensor_tensor(yg2[:, :, :], yg2[:, :, :], wide_d(p2[:, :]), ALU.mult))
                link(dve.tensor_tensor(yg1[:, :, :], yg1[:, :, :], yg2[:, :, :], ALU.add))
                shared_batch(B - 1)
                dve.wait_ge(s.shared.sem, s.shared.at(B - 1, 1))
                with dve.Fori(0, B) as i:
                    dve.wait_ge(s.xn_ready.sem, s.xn_ready.at(i, 0))
                    dve.tensor_tensor(z[:, :, :], shared[:, bass.ds(TPB * i, TPB), :], yg1[:, bass.ds(TPB * i, TPB), :], ALU.add)\
                        .then_inc(s.z_ready.sem, 1)
                    dve.wait_ge(s.z_ready.sem, s.z_ready.at(i, 1))
                    settle(dve, s)
                    norm_dve(dve, s, n, i, z[:, :, :])

            @block.gpsimd
            def _(pool):
                pool.wait_ge(s.mean.sem, s.mean.at(0, 1))
                pool.tensor_tensor(rms[:, :], ms[:, :], net.neghalf[:, 0:NT], ALU.pow).then_inc(s.rms.sem, 1)
                pool.wait_ge(s.slots.sem, s.slots.at(0, 1))
                pool.wait_ge(net.zeroed, net.zero_ready)
                for k in range(2):
                    for t in range(NT):
                        pool.indirect_dma_start(net.slots[1], bass.IndirectOffsetOnAxis(ap=scatter[:, k, t:t + 1], axis=0),
                                                net.x_tok[:, t * P:(t + 1) * P], None).then_inc(moved, 16)
                for half in stored:
                    pool.wait_ge(half, 16 * 2 * E2 // 2)
                for k, to in enumerate((yg1, yg2)):
                    for t in range(NT):
                        pool.indirect_dma_start(to[:, t, :], None, net.slots_out[1],
                                                bass.IndirectOffsetOnAxis(ap=gather[:, k, t:t + 1], axis=0)).then_inc(fetched, 16)
                with pool.Fori(0, B) as i:
                    norm_pool(pool, s, n, i)

            @block.sync
            def _(sp):
                sp.wait_ge(moved, 16 * 2 * NT)
                sp.dma_start(rows[:, :, :], net.slots[1][0:SLOTS, :].rearrange("(k p) d -> p k d", p=P)).then_inc(net.rows_in, 16)
                for e in range(E2):
                    sp.wait_ge(s.y_sb.sem, s.y_sb.at(0, e + 1))
                    at = e * C2
                    sp.dma_start(net.slots_out[1][at:at + 2 * P, :].rearrange("(k p) d -> p k d", p=P), y[:, e % 2, 0:2, :]).then_inc(stored[e % 2], 16)
                    sp.dma_start(net.slots_out[1][at + 2 * P:at + C2, :], y[0:C2 - 2 * P, e % 2, 2, :]).then_inc(stored[e % 2], 16)
    close_stage(nc, net.pool)


def stage_decayed_attention(nc, net, io):
    with ExitStack() as ctx:
        sb = lambda name, shape: ctx.enter_context(nc.sbuf_tensor(net.name(name), shape, F32))
        a = attend_buffers(ctx, nc, net, RH, RDH, RDH ** -0.5, net.tab("causal").rearrange("p (t k) -> p t k", t=TPB), net.cmask16,
                           ring=(2, 3, 4), out=(6,), tail=1, scores=(0, 1, 5), causal=True)
        n = norm_buffers(ctx, nc, net)
        xs, x_old = sb("xs", [P, L]), sb("x_old", [P, L])
        xi, rate = sb("xi", [P, RH]), sb("rate", [P, RH // 2])
        W, CH = 32, RH // HPG
        EARLY = 7
        qk = sb("qk_wide", [P, TPB, 2, RH, W])
        prod = sb("prod", [P, 4, 8, 2, RDH // 2])
        q16, k16 = (ctx.enter_context(nc.sbuf_tensor(net.name(k), [P, CH, L], BF16)) for k in ("q16", "k16"))
        v = sb("v", [P, 2, TPB, RH, RDH + 1])
        free = [w[:, :, :].rearrange("p e f -> p (e f)") for w in net.moe_w]
        kT = [free[p][:, 0:HPG * CH * L].rearrange("p (y c t) -> p y c t", y=HPG, c=CH) for p in range(2)]
        qT = [free[2][:, p * CH * L:(p + 1) * CH * L].rearrange("p (c t) -> p c t", c=CH) for p in range(2)]
        o, oT = sb("o", [P, TPB, D]), sb("oT", [P, L])
        s = open_stage(nc, net.pool, "clear:1 rate0:1 rate:1 decay:1 xs_ready:1 x_old:1 front_ps:6 plain:2 v_ready:2 products:2 wide:2 "
                       "qkT:4 oT_ps:1 oT_ready:1 " + attend_spec(RH) + NORM.replace("settled:0 ", ""))
        bank, ident = net.bank, net.tab("ident")
        front_bank = lambda k: bank[(0, 1, 5)[k % 3]]
        oT_bank, y_bank = bank[5], bank[7]
        tiles = lambda k: net.tab(k).rearrange("p (t k) -> p t k", t=TPB)
        rcos, rsin = tiles("rcos"), tiles("rsin")
        with nc.Block() as block:
            @block.sync
            def _(sp):
                sp.dma_start(xi[:, :], io["L3_attn_log_xi"].partition_broadcast(P)).then_inc(net.ld_xi, 16)

            @block.gpsimd
            def _(pool):
                pool.memset(qk[:, :, :, :, :], 0.0).then_inc(s.clear.sem, 1)
                pool.memset(v[:, :, :, :, RDH:RDH + 1], 1.0)
                pool.memset(a.top_parts[:, :, :], 0.0)
                pool.memset(kT[0][:, :, :, :], 0.0)
                pool.memset(kT[1][:, :, :, :], 0.0).then_inc(s.clear.sem, 1)
                with pool.Fori(0, B) as i:
                    norm_pool(pool, s, n, i)

            @block.tensor
            def _(pe):
                pe.wait_ge(net.ld_w3, net.w3_ready)

                def project(i, t, follows=True):
                    if follows:
                        pe.wait_ge(s.top_parts.sem, s.top_parts.at(i - 1, 1))
                    pe.wait_ge(s.xs_ready.sem, s.xs_ready.at(i, 1))
                    pe.matmul(front_bank(t)[:, 0:3 * D], xs[:, t * P:(t + 1) * P], net.w_qkv3[:, :], start=True, stop=True)\
                        .then_inc(s.front_ps.sem, 1)

                def turn(i, t, first=False):
                    pe.wait_ge(s.wide.sem, s.wide.at(i, t + 1))
                    pe.wait_ge(s.v_ready.sem, s.v_ready.at(i, TPB))
                    pe.wait_ge(s.products.sem, s.products.at(i, TPB))
                    for j in range(2):
                        if t == 1 and j == 1:
                            pe.wait_ge(s.qkT.sem, s.qkT.at(i, 1))
                        if t == 0 and j == 0 and not first:
                            pe.wait_ge(s.oT_ready.sem, s.oT_ready.at(i - 1, 0))
                        to = front_bank(2 + 2 * t + j)
                        for c in range(CH):
                            last = pe.transpose(to[:, c * P:(c + 1) * P], qk[:, t, j, HPG * c:HPG * (c + 1), :].rearrange("p h w -> p (h w)"), ident)
                        last.then_inc(s.front_ps.sem, 1)

                row = lambda h: slice(W * (h % HPG), W * (h % HPG) + W)
                q16_at = lambda h, at, w: q16[row(h), h // HPG, at:at + w]
                k16_at = lambda h, at, w: k16[row(h), h // HPG, at:at + w]

                def front(i):
                    for t in range(TPB):
                        project(i, t, False)
                    for t in range(TPB):
                        turn(i, t, True)
                    pe.wait_ge(s.qkT.sem, s.qkT.at(i, 4))
                    for h in range(RH):
                        scores_pe(pe, s, a, net, i, h, q16_at, k16_at)
                    top_pe(pe, s, a, net, i)
                    for t in range(TPB):
                        project(i + 1, t)

                def turn_output(i):
                    pe.wait_ge(s.o_ready.sem, s.o_ready.at(i, 1))
                    for t in range(TPB):
                        last = pe.transpose(oT_bank[:, t * P:(t + 1) * P], o[:, t, :], ident)
                    last.then_inc(s.oT_ps.sem, 1)

                def output(i):
                    pe.wait_ge(s.oT_ready.sem, s.oT_ready.at(i, 1))
                    pe.wait_ge(s.x_old.sem, s.x_old.at(i, 1))
                    pe.wait_ge(s.x_updated.sem, s.x_updated.at(i, 0))
                    for t in range(TPB):
                        tok = slice(t * P, (t + 1) * P)
                        pe.matmul(y_bank[:, tok], oT[:, tok], net.w_o3[:, :], start=True, stop=False)
                        last = pe.matmul(y_bank[:, tok], x_old[:, tok], ident, start=False, stop=True)
                    last.then_inc(s.y_ready.sem, 1)

                def run(i, p, ahead, behind):
                    q_at = lambda h, at, w: qT[p][:, h // HPG, at:at + w]
                    k_at = lambda h, at, w: kT[p][:, h % HPG, h // HPG, at:at + w]
                    v_at = lambda kb, h: v[:, p, kb, h, :]
                    pe.wait_ge(s.v_ready.sem, s.v_ready.at(i, TPB))
                    for k in range(3 * a.R):
                        shifted_pe(pe, s, a, net, i, k, (), q_at, k_at)
                        if behind and k == 0:
                            turn_output(i - 1)
                        if behind and k == 3:
                            output(i - 1)
                        if ahead and k in (2, 4):
                            turn(i + 1, (k - 2) // 2)
                        if k in (5, 8, 11):
                            mix_pe(pe, s, a, i, (k - 5) // 3, v_at)
                        if behind and k == 7:
                            norm_pe(pe, s, n, i - 1, y_bank[:, L:2 * L])
                        if ahead and k >= EARLY:
                            pe.wait_ge(s.qkT.sem, s.qkT.at(i + 1, 4))
                            for h in range(3 * (k - EARLY), 3 * (k - EARLY) + 3):
                                scores_pe(pe, s, a, net, i + 1, h, q16_at, k16_at)
                    mix_pe(pe, s, a, i, a.R - 1, v_at)
                    if ahead:
                        for h in range(3 * (3 * a.R - EARLY), RH):
                            scores_pe(pe, s, a, net, i + 1, h, q16_at, k16_at)
                        top_pe(pe, s, a, net, i + 1)
                    if ahead == 2:
                        for t in range(TPB):
                            project(i + 2, t)

                front(0)
                run(0, 0, 2, False)
                with pe.Fori(0, B // 2 - 2) as j:
                    run(2 * j + 1, 1, 2, True)
                    run(2 * j + 2, 0, 2, True)
                run(B - 3, 1, 2, True)
                run(B - 2, 0, 1, True)
                run(B - 1, 1, 0, True)
                turn_output(B - 1)
                output(B - 1)
                norm_pe(pe, s, n, B - 1, y_bank[:, L:2 * L])

            @block.scalar
            def _(act):
                act.wait_ge(net.ld_xi, 16)
                act.activation(xi[:, :], xi[:, :], ACT.Exp, scale=-1.0).then_inc(s.rate0.sem, 1)
                act.wait_ge(s.clear.sem, s.clear.at(0, 2))

                def load_x(i):
                    act.activation(xs[:, :], net.xT[:, bass.ds(i * L, L)], ACT.Copy).then_inc(s.xs_ready.sem, 1)

                def take(i, p):
                    act.wait_ge(s.front_ps.sem, s.front_ps.at(i, 0))
                    for t in range(TPB):
                        act.wait_ge(s.front_ps.sem, s.front_ps.at(i, t + 1))
                        src = front_bank(t)[:, 0:2 * D].rearrange("p (g y d) -> p g y d", y=HPG, d=RDH)
                        dst = qk[:, t, :, :, 0:RDH].rearrange("p j (g y) d -> p (j g) y d", y=HPG)
                        for y in range(2):
                            last = act.activation(dst[:, :, y, :], src[:, :, y, :], ACT.Copy)
                        last.then_inc(s.plain.sem, 1)
                        act.activation(v[:, p, t, :, 0:RDH], front_bank(t)[:, 2 * D:3 * D].rearrange("p (h d) -> p h d", d=RDH), ACT.Copy)\
                            .then_inc(s.v_ready.sem, 1)

                def copy_qk(i, p, t, j):
                    tok = slice(t * P, (t + 1) * P)
                    act.wait_ge(s.front_ps.sem, s.front_ps.at(i, 3 + 2 * t + j))
                    of = front_bank(2 + 2 * t + j)[:, :].rearrange("p (c t) -> p c t", t=P)
                    if j == 0:
                        act.activation(q16[:, :, tok], of, ACT.Copy)
                        last = act.activation(qT[p][:, :, tok], of, ACT.Copy)
                    else:
                        act.activation(k16[:, :, tok], of, ACT.Copy)
                        for y in range(HPG):
                            row = slice(W * y, W * (y + 1))
                            last = act.activation(kT[p][row, y, :, tok], of[row], ACT.Copy)
                    last.then_inc(s.qkT.sem, 1)

                def front(i, p):
                    load_x(i)
                    take(i, p)
                    load_x(i + 1)
                    for t in range(TPB):
                        for j in range(2):
                            copy_qk(i, p, t, j)
                    top_row_act(act, s, a, i)
                    take(i + 1, 1 - p)

                def keep_old(i):
                    act.wait_ge(s.y_ready.sem, s.y_ready.at(i, 0))
                    settle(act, s)
                    act.activation(x_old[:, :], net.xT[:, bass.ds(i * L, L)], ACT.Copy).then_inc(s.x_old.sem, 1)

                def copy_output(i):
                    act.wait_ge(s.oT_ps.sem, s.oT_ps.at(i, 1))
                    act.activation(oT[:, :], oT_bank[:, 0:L], ACT.Copy).then_inc(s.oT_ready.sem, 1)

                def run(i, p, ahead, behind):
                    if behind:
                        keep_old(i - 1)
                    for k in range(3 * a.R):
                        exp_act(act, s, a, i, k)
                        if behind and k == 0:
                            copy_output(i - 1)
                        if ahead and k in (2, 3, 4, 5):
                            copy_qk(i + 1, 1 - p, (k - 2) // 2, (k - 2) % 2)
                        if behind and k == 8:
                            norm_act(act, s, i - 1, y_bank[:, L:2 * L], net.xT[:, bass.ds((i - 1) * L, L)])
                    if ahead == 2:
                        load_x(i + 2)
                    if ahead:
                        top_row_act(act, s, a, i + 1)
                    if ahead == 2:
                        take(i + 2, p)

                front(0, 0)
                run(0, 0, 2, False)
                with act.Fori(0, B // 2 - 2) as j:
                    run(2 * j + 1, 1, 2, True)
                    run(2 * j + 2, 0, 2, True)
                run(B - 3, 1, 2, True)
                run(B - 2, 0, 1, True)
                run(B - 1, 1, 0, True)
                keep_old(B - 1)
                copy_output(B - 1)
                norm_act(act, s, B - 1, y_bank[:, L:2 * L], net.xT[:, (B - 1) * L:B * L])

            @block.vector
            def _(dve):
                dve.wait_ge(s.rate0.sem, s.rate0.at(0, 1))
                dve.tensor_scalar(rate[:, :], xi[:, 1:RH:2], RDH ** 0.5, None, ALU.mult).then_inc(s.rate.sem, 1)
                dve.wait_ge(s.rate.sem, s.rate.at(0, 1))
                dve.wait_ge(s.clear.sem, s.clear.at(0, 1))
                for t in range(TPB):
                    pos = net.tab("pos")[:, t:t + 1]
                    dve.tensor_scalar(qk[:, t, 0, 1:RH:2, RDH + 1], rate[:, :], pos, -1.0, ALU.mult, ALU.mult)
                    dve.tensor_scalar(qk[:, t, 1, 1:RH:2, RDH], rate[:, :], pos, None, ALU.mult)
                    dve.memset(qk[:, t, 0, 1:RH:2, RDH], 1.0)
                    last = dve.memset(qk[:, t, 1, 1:RH:2, RDH + 1], 1.0)
                last.then_inc(s.decay.sem, 1)
                dve.wait_ge(s.decay.sem, s.decay.at(0, 1))
                HR = RDH // 2
                y = y_bank[:, 0:L].rearrange("p (t d) -> p t d", d=D)

                def rotate(i):
                    dve.wait_ge(s.front_ps.sem, s.front_ps.at(i, 0))
                    for t in range(TPB):
                        dve.wait_ge(s.v_ready.sem, s.v_ready.at(i, t + 1))
                        src = front_bank(t)[:, 0:2 * D].rearrange("p (g y e x) -> p g y e x", g=8, y=HPG, x=2)
                        ev, od = src[:, :, 2:4, :, 0], src[:, :, 2:4, :, 1]
                        cos, sin = (x[:, t, :].unsqueeze(1).unsqueeze(1).to_broadcast([P, 8, 2, HR]) for x in (rcos, rsin))
                        dve.wait_ge(s.wide.sem, s.wide.at(i, t))
                        dve.tensor_tensor(prod[:, 0, :, :, :], ev, cos, ALU.mult)
                        dve.tensor_tensor(prod[:, 1, :, :, :], od, sin, ALU.mult)
                        dve.tensor_tensor(prod[:, 2, :, :, :], ev, sin, ALU.mult)
                        dve.tensor_tensor(prod[:, 3, :, :, :], od, cos, ALU.mult).then_inc(s.products.sem, 1)
                        dve.wait_ge(s.products.sem, s.products.at(i, t + 1))
                        dst = qk[:, t, :, :, 0:RDH].rearrange("p j h (e x) -> p (j h) e x", x=2).rearrange("p (g y) e x -> p g y e x", y=HPG)
                        dve.tensor_tensor(dst[:, :, 2:4, :, 0], prod[:, 0, :, :, :], prod[:, 1, :, :, :], ALU.subtract)
                        dve.tensor_tensor(dst[:, :, 2:4, :, 1], prod[:, 2, :, :, :], prod[:, 3, :, :, :], ALU.add).then_inc(s.wide.sem, 1)

                def run(i, p, ahead, behind):
                    if ahead:
                        rotate(i + 1)
                    if behind:
                        norm_dve(dve, s, n, i - 1, y)
                    if ahead:
                        scores_dve(dve, s, a, net, i + 1)
                    normalise_dve(dve, s, a, i, o[:, :, :].rearrange("p t (h d) -> p (t h) d", h=RH), s.oT_ps)

                rotate(0)
                scores_dve(dve, s, a, net, 0)
                run(0, 0, 2, False)
                with dve.Fori(0, B // 2 - 2) as j:
                    run(2 * j + 1, 1, 2, True)
                    run(2 * j + 2, 0, 2, True)
                run(B - 3, 1, 2, True)
                run(B - 2, 0, 1, True)
                run(B - 1, 1, 0, True)
                norm_dve(dve, s, n, B - 1, y)
    close_stage(nc, net.pool)


def stage_ternary(nc, net, io, out):
    with ExitStack() as ctx:
        sb = lambda name, shape: ctx.enter_context(nc.sbuf_tensor(net.name(name), shape, F32))
        n = norm_buffers(ctx, nc, net, keep=True)
        w, pos, neg, mag, wT = (sb(k, [P, P]) for k in ("weight", "above", "below", "magnitude", "ternaryT"))
        xs = sb("xs", [P, 2, L])
        part_sum, delta, mdelta, alpha, bias = sb("abs_sum", [P, 1]), sb("delta", [P, 1]), sb("minus_delta", [P, 1]), sb("alpha", [P, 1]), sb("bias", [1, D])
        s = open_stage(nc, net.pool, "mag:1 v:8 mean_ps:1 tern:1 wT_ps:1 wT:1 xs_ready:1 " + NORM)
        bank, ident = net.bank, net.tab("ident")
        y_bank = lambda p: bank[2 + p]
        with nc.Block() as block:
            @block.sync
            def _(sp):
                sp.dma_start(w[:, :], io["L3_ffn_weight"]).then_inc(net.ld_t, 16)
                sp.dma_start(alpha[:, :], io["L3_ffn_alpha"].partition_broadcast(P)).then_inc(net.ld_t, 16)
                sp.dma_start(bias[:, :], io["L3_ffn_bias"].rearrange("(o d) -> o d", o=1)).then_inc(net.ld_t, 16)
                sp.wait_ge(s.kept.sem, s.kept.at(B - 1, 1))
                sp.dma_start(out.rearrange("b (t p) d -> p (b t) d", p=P), net.x_tok[:, :].rearrange("p (t d) -> p t d", d=D)).then_inc(net.out_done, 16)
                sp.wait_ge(net.out_done, 16)

            @block.gpsimd
            def _(pool):
                with pool.Fori(0, B) as i:
                    norm_rstd(pool, s, n, i)

            @block.scalar
            def _(act):
                act.wait_ge(net.ld_t, 48)
                act.activation(mag[:, :], w[:, :], ACT.Abs, accum_out=part_sum[:, :]).then_inc(s.mag.sem, 1)
                act.wait_ge(s.wT_ps.sem, s.wT_ps.at(0, 1))
                act.activation(wT[:, :], bank[1][:, 0:P], ACT.Copy).then_inc(s.wT.sem, 1)

                def load_x(i, p):
                    settle(act, s)
                    act.activation(xs[:, p, :], net.xT[:, bass.ds(i * L, L)], ACT.Copy).then_inc(s.xs_ready.sem, 1)

                def keep(i):
                    act.wait_ge(s.xn_ready.sem, s.xn_ready.at(i, 1))
                    settle(act, s)
                    act.activation(net.x_tok[:, bass.ds(i * L, L)], n.xn[:, :, :].rearrange("p t d -> p (t d)"), ACT.Copy).then_inc(s.kept.sem, 1)

                load_x(0, 0)
                load_x(1, 1)
                with act.Fori(0, B // 2 - 1) as j:
                    for p in range(2):
                        keep(2 * j + p)
                        act.wait_ge(s.y_ready.sem, s.y_ready.at(2 * j + p, 1))
                        load_x(2 * j + p + 2, p)
                keep(B - 2)
                keep(B - 1)

            @block.tensor
            def _(pe):
                pe.wait_ge(s.mag.sem, s.mag.at(0, 1))
                pe.matmul(bank[0][:, 0:1], net.tab("ones"), part_sum[:, :], start=True, stop=True).then_inc(s.mean_ps.sem, 1)
                pe.wait_ge(s.tern.sem, s.tern.at(0, 1))
                pe.transpose(bank[1][:, 0:P], pos[:, :], ident).then_inc(s.wT_ps.sem, 1)
                pe.wait_ge(s.wT.sem, s.wT.at(0, 1))

                def project(i, p):
                    pe.wait_ge(s.xs_ready.sem, s.xs_ready.at(i, 1))
                    for t in range(TPB):
                        tok = slice(t * P, (t + 1) * P)
                        pe.matmul(y_bank(p)[:, tok], xs[:, p, tok], wT[:, :], start=True, stop=False)
                        pe.matmul(y_bank(p)[:, tok], net.tab("ones")[0:1, :], bias[:, :], start=False, stop=False)
                        last = pe.matmul(y_bank(p)[:, tok], xs[:, p, tok], ident, start=False, stop=True)
                    last.then_inc(s.y_ready.sem, 1)

                project(0, 0)
                project(1, 1)
                with pe.Fori(1, B // 2) as j:
                    for p in range(2):
                        pe.wait_ge(s.xn_ready.sem, s.xn_ready.at(2 * j + p - 1, 0))
                        project(2 * j + p, p)

            @block.vector
            def _(dve):
                dve.wait_ge(s.mean_ps.sem, s.mean_ps.at(0, 1))
                v = s.v
                dve.tensor_scalar(delta[:, :], bank[0][:, 0:1], 1.0 / (D * D), 0.7, ALU.mult, ALU.mult)
                dve.tensor_scalar(mdelta[:, :], bank[0][:, 0:1], 1.0 / (D * D), -0.7, ALU.mult, ALU.mult).then_inc(v.sem, 1)
                dve.wait_ge(v.sem, v.at(0, 1))
                dve.tensor_scalar(pos[:, :], w[:, :], delta[:, :], None, ALU.is_gt)
                dve.tensor_scalar(neg[:, :], w[:, :], mdelta[:, :], None, ALU.is_lt).then_inc(v.sem, 1)
                dve.wait_ge(v.sem, v.at(0, 2))
                dve.tensor_tensor(pos[:, :], pos[:, :], neg[:, :], ALU.subtract).then_inc(v.sem, 1)
                dve.wait_ge(v.sem, v.at(0, 3))
                dve.tensor_scalar(pos[:, :], pos[:, :], alpha[:, :], None, ALU.mult).then_inc(s.tern.sem, 1)
                with dve.Fori(0, B // 2) as j:
                    for p in range(2):
                        norm_dve(dve, s, n, 2 * j + p, y_bank(p)[:, 0:L].rearrange("p (t d) -> p t d", d=D), turned=False)
    close_stage(nc, net.pool)


def network(nc, io, out):
    at, width = table_layout()
    with ExitStack() as ctx:
        sb = lambda name, shape: ctx.enter_context(nc.sbuf_tensor(name, shape, F32))
        net = Shared()
        net.count = 0

        def name(base):
            net.count += 1
            return f"{base}_{net.count}"
        net.name = name
        net.tabs = sb("tabs", [P, width])
        net.tab = lambda n: net.tabs[:, at[n][0]:at[n][0] + at[n][1]]
        net.xT, net.x_tok = sb("xT", [P, T]), sb("x_tok", [P, T])
        net.neghalf, net.eps = sb("neghalf", [P, 64]), sb("eps", [P, 64])
        net.ident16, net.lmask16, net.cmask16 = (ctx.enter_context(nc.sbuf_tensor(k, [P, w], BF16)) for k, w in (
            ("ident16", P), ("lmask16", L + P), ("cmask16", L + P)))
        net.pick16 = ctx.enter_context(nc.sbuf_tensor("pick16", [P, PART], BF16))
        net.bank = [ctx.enter_context(nc.psum_tensor(f"bank{k}", [P, 512], F32)) for k in range(8)]
        sem = lambda name: ctx.enter_context(nc.semaphore(name))
        net.ld_x, net.ld_w, net.ld_moe, net.ld_a, net.out_done = (sem(n) for n in ("ld_x", "ld_w", "ld_moe", "ld_a", "out_done"))
        net.pool = [sem(f"stage_signal_{k}") for k in range(60)]
        net.loads_sp, net.loads_moe = [], []
        net.ld_s, net.ld_s_count = sem("ld_s"), 0
        net.xw = sb("x_work", [P, T])
        col = lambda ap: ap.rearrange("(c p) -> p c", p=P)
        small = {}
        for l in range(DEPTH):
            for key, width_ in (("ln_g", 1), ("ln_b", 1), ("b1a", 3), ("b1g", 3), ("b2", 1)):
                small[key, l] = sb(f"{key}_{l}", [P, width_])
            for key, nm in (("ln_g", "L0_ffn_ln_g"), ("ln_b", "L0_ffn_ln_b"), ("b2", "L0_ffn_b2")):
                net.loads_sp.append((small[key, l][:, :], col(io[nm][l])))
            for c, (a0, w) in enumerate(HCH):
                for key, off in (("b1a", 0), ("b1g", HID)):
                    net.loads_sp.append((small[key, l][0:w, c:c + 1], io["L0_ffn_b1"][l, off + a0:off + a0 + w].rearrange("(w o) -> w o", o=1)))
        net.small = lambda key, l: small[key, l][:, :]
        net.w_in, net.w_out, net.w_xproj = sb("w_in", [P, 2 * DIN]), sb("w_out", [P, 2, D]), sb("w_xproj", [P, 2, XP])
        net.conv_w, net.conv_b, net.w_dt = sb("conv_w", [P, 2, NCONV]), sb("conv_b", [P, 2]), sb("w_dt", [1, DIN])
        net.b_dt, net.a_log, net.d_par = sb("b_dt", [P, 2]), sb("a_log", [P, 2, NS]), sb("d_par", [P, 2])
        halves = lambda ap: ap.rearrange("(c p) n -> p c n", p=P)
        net.loads_sp += [(net.w_in[:, :], io["L1_attn_W_in"]), (net.w_out[:, :, :], halves(io["L1_attn_W_out"])),
                         (net.w_xproj[:, :, :], halves(io["L1_attn_W_xproj"])),
                         (net.conv_w[:, :, :], halves(io["L1_attn_conv_w"].rearrange("d o k -> d (o k)"))),
                         (net.conv_b[:, :], col(io["L1_attn_conv_b"])), (net.b_dt[:, :], col(io["L1_attn_b_dt"])),
                         (net.d_par[:, :], col(io["L1_attn_D_param"])), (net.a_log[:, :, :], halves(io["L1_attn_A_log"])),
                         (net.w_dt[:, :], io["L1_attn_w_dt"].rearrange("(o d) -> o d", o=1))]
        net.w_router = sb("w_router", [P, E1])
        net.loads_sp.append((net.w_router[:, :], io["L1_ffn_w_router"]))
        net.moe_w = [sb(f"moe_w{k}", [P, E1, P]) for k in range(3)]
        net.loads_moe = [(net.moe_w[k][:, :, :], io[nm].rearrange("e h f -> h e f"))
                         for k, nm in enumerate(("L1_ffn_w_gate", "L1_ffn_w_up", "L1_ffn_w_down"))]
        net.moved, net.stored, net.fetched, net.rows_in, net.zeroed = (sem(k) for k in ("moved", "stored", "fetched", "rows_in", "zeroed"))
        net.slots = [nc.dram_tensor(f"slots{k}", [SLOTS + (k + 1) * T, D], F32, kind="Internal").ap() for k in range(2)]
        net.slots_out = [nc.dram_tensor(f"slots_out{k}", [SLOTS, D], F32, kind="Internal").ap() for k in range(2)]
        net.zero = sb("zero", [P, 512])
        net.loads2, net.loads3 = [], []
        net.ld_w2, net.ld_w3, net.moved2, net.fetched2, net.ld_xi, net.ld_t = (
            sem(k) for k in ("ld_w2", "ld_w3", "moved2", "fetched2", "ld_xi", "ld_t"))
        net.stored2 = [sem(f"stored2_{k}") for k in range(2)]
        net.zero_ready = 16 * 2 * (SLOTS // 512)
        first_layer = ExitStack()
        fb = lambda name, shape: first_layer.enter_context(nc.sbuf_tensor(name, shape, F32))
        net.wqkv = [fb(f"wqkv{l}", [P, 3 * INNER]) for l in range(DEPTH)]
        net.wo = [fb(f"wo{l}", [P, INNER // P, D]) for l in range(DEPTH)]
        for l in range(DEPTH):
            net.loads_sp += [(net.wqkv[l][:, :], io["L0_ffn_wqkv"][l]),
                             (net.wo[l][:, :, :], io["L0_ffn_wo"][l].rearrange("(c p) d -> p c d", p=P))]
        net.gates = [fb(k, [P, P]) for k in ("ig_blocks", "ag_blocks")] + [fb(k, [P, 1]) for k in ("ig_b", "ag_b", "a_par")]
        net.w1 = [fb(f"w1_{l}", [P, 2 * HID]) for l in range(DEPTH)]
        net.w2 = [fb(f"w2_{l}", [P, len(HCH), D]) for l in range(DEPTH)]
        for l in range(DEPTH):
            net.loads_sp.append((net.w1[l][:, :], io["L0_ffn_w1"][l]))
            for c, (a0, w) in enumerate(HCH):
                net.loads_sp.append((net.w2[l][0:w, c, :], io["L0_ffn_w2"][l, a0:a0 + w, :]))
        net.w_ready = 16 * len(net.loads_sp)
        stage_load(nc, net, io)
        stage_recurrence(nc, net, io)
        stage_local_attention(nc, net, io, 0, net.xT, net.xw)
        stage_gated_mlp(nc, net, io, 0, net.xw, False)
        stage_local_attention(nc, net, io, 1, net.xw, net.xw)
        stage_gated_mlp(nc, net, io, 1, net.xw, True)
        first_layer.close()
        with ExitStack() as scope:
            xc, sz = (scope.enter_context(nc.sbuf_tensor(k, [P, 2, T], F32)) for k in ("xc", "silu_z"))
            stage_scan_inputs(nc, net, io, xc, sz)
            stage_scan(nc, net, io, xc, sz)
        net.router2, net.sg, net.su, net.sd = sb("router2", [P, E2]), sb("sg", [P, IS]), sb("su", [P, IS]), sb("sd", [P, IS // P, D])
        net.w_qkv3, net.w_o3 = sb("w_qkv3", [P, 3 * D]), sb("w_o3", [P, D])
        second = ExitStack()
        w = second_weights(nc, net, io, second)
        stage_switch_experts(nc, net, io)
        split = lambda ap: ap.rearrange("p (s j) -> p j s", j=NL)
        joined = lambda ap: ap.rearrange("p (j s) -> p j s", j=NL)
        back = lambda ap: ap.rearrange("p (j s) -> p s j", j=NL)
        rows = lambda ap: ap.rearrange("p (s j) -> p s j", j=NL)
        stage_mha(nc, net, w["la"], None, net.xT, net.xw, net.loads3)
        stage_relu_mlp(nc, net, w["lf"], net.xw, False, split, joined)
        stage_mha(nc, net, w["sa"], net.tab("blk8"), net.xw, net.xw)
        stage_relu_mlp(nc, net, w["pf"], net.xw, True, back, rows)
        second.close()
        stage_top2_experts(nc, net, io)
        stage_decayed_attention(nc, net, io)
        stage_ternary(nc, net, io, out)


def second_weights(nc, net, io, scope):
    sb = lambda name, shape: scope.enter_context(nc.sbuf_tensor(name, shape, F32))
    col = lambda ap: ap.rearrange("(c p) -> p c", p=P)
    row = lambda ap: ap.rearrange("(o d) -> o d", o=1)
    pre = "L2_attn_"
    w = {}
    for k in ("la", "sa"):
        w[k] = m = group(q=sb(k + "_q", [P, AH * ADK]), k=sb(k + "_k", [P, AH * ADK]), v=sb(k + "_v", [P, AH * ADK]),
                                   p=sb(k + "_p", [P, AH * ADK // P, D]), pb=sb(k + "_pb", [1, D]), g=sb(k + "_g", [P, 1]), b=sb(k + "_b", [P, 1]))
        for to, nm in ((m.q, "_wqs"), (m.k, "_wks"), (m.v, "_wvs")):
            net.loads2.append((to[:, :].rearrange("d (h k) -> d h k", h=AH), io[pre + k + nm].rearrange("h d k -> d h k")))
        net.loads2 += [(m.p[:, :, :], io[pre + k + "_pw"].rearrange("(c p) d -> p c d", p=P)), (m.pb[:, :], row(io[pre + k + "_pb"]))]
    for k in ("lf", "pf"):
        w[k] = m = group(w1=sb(k + "_w1", [P, DI]), w2=sb(k + "_w2", [P, DI // P, D]), b1=sb(k + "_b1", [P, DI // P]),
                                   b2=sb(k + "_b2", [1, D]), g=sb(k + "_g", [P, 1]), b=sb(k + "_b", [P, 1]))
        net.loads2 += [(m.w1[:, :], io[pre + k + "_w1"]), (m.w2[:, :, :], io[pre + k + "_w2"].rearrange("(c p) d -> p c d", p=P)),
                       (m.b1[:, :], col(io[pre + k + "_b1"])), (m.b2[:, :], row(io[pre + k + "_b2"]))]
    for k, m in w.items():
        net.loads2 += [(m.g[:, :], col(io[pre + k + "_g"])), (m.b[:, :], col(io[pre + k + "_b"]))]
    net.loads2 = [(a, b, net.ld_w2) for a, b in net.loads2]
    net.w2_ready = 16 * len(net.loads2)
    f = "L2_ffn_"
    flat = lambda k: net.moe_w[k][:, :, :].rearrange("p e f -> p (e f)").rearrange("p (e i) -> p e i", e=E2)
    net.loads3 = [(flat(0), io[f + "rg"].rearrange("e h i -> h e i")), (flat(1), io[f + "ru"].rearrange("e h i -> h e i")),
                  (net.moe_w[2][:, :, :], io[f + "rd"].rearrange("e (c p) d -> p (e c) d", p=P)),
                  (net.router2[:, :], io[f + "router_w"].rearrange("e h -> h e")),
                  (net.sg[:, :], io[f + "sg"]), (net.su[:, :], io[f + "su"]),
                  (net.sd[:, :, :], io[f + "sd"].rearrange("(c p) d -> p c d", p=P)),
                  (net.w_qkv3[:, :], io["L3_attn_w_qkv"]), (net.w_o3[:, :], io["L3_attn_w_o"])]
    net.loads3 = [(a, b, net.ld_w3) for a, b in net.loads3]
    net.w3_ready = 16 * len(net.loads3)
    return w


_INS = [
    "L0_attn_x", "L0_attn_ig_w", "L0_attn_ig_b", "L0_attn_ag_w", "L0_attn_ag_b", "L0_attn_a_param",
    "L0_ffn_wqkv", "L0_ffn_q_scale", "L0_ffn_k_scale", "L0_ffn_wo", "L0_ffn_ln_g", "L0_ffn_ln_b", "L0_ffn_w1", "L0_ffn_b1",
    "L0_ffn_w2", "L0_ffn_b2",
    "L1_attn_W_in", "L1_attn_conv_w", "L1_attn_conv_b", "L1_attn_W_xproj", "L1_attn_w_dt", "L1_attn_b_dt", "L1_attn_A_log",
    "L1_attn_D_param", "L1_attn_W_out",
    "L1_ffn_w_router", "L1_ffn_w_gate", "L1_ffn_w_up", "L1_ffn_w_down",
    *(f"L2_attn_{a}_{k}" for a, ks in (("la", "wqs wks wvs pw pb g b"), ("lf", "w1 b1 w2 b2 g b"),
                                      ("sa", "wqs wks wvs pw pb g b"), ("pf", "w1 b1 w2 b2 g b")) for k in ks.split()),
    "L2_ffn_router_w", "L2_ffn_rg", "L2_ffn_ru", "L2_ffn_rd", "L2_ffn_sg", "L2_ffn_su", "L2_ffn_sd",
    "L3_attn_w_qkv", "L3_attn_w_o", "L3_attn_log_xi", "L3_ffn_weight", "L3_ffn_alpha", "L3_ffn_bias",
]


def kernel(**inputs):
    import numpy as _np
    import concourse.bacc as _bacc
    from concourse import mybir as _mybir
    from concourse.bass_utils import run_bass_kernel_spmd as _run

    nc = _bacc.Bacc("TRN2", target_bir_lowering=False, num_devices=1)
    arrays, io = {}, {}
    given = {name: inputs[name] for name in _INS}
    given["tables"] = _np.concatenate(list(tables().values()), axis=1)
    for name, a in given.items():
        a = _np.ascontiguousarray(a)
        arrays[f"in_{name}_dram"] = a
        io[name] = nc.dram_tensor(f"in_{name}_dram", a.shape, _mybir.dt.from_np(a.dtype), kind="ExternalInput").ap()
    out = nc.dram_tensor("out_0_dram", (B, L, D), _mybir.dt.float32, kind="ExternalOutput").ap()
    network(nc, io, out)
    r = _run(nc, [arrays], core_ids=[0])
    return r.results[0]["out_0_dram"]
```
